# Optimizing a Trainium2 kernel written in Bass

```python
import numpy as np
import jax
import jax.numpy as jnp

def _softmax(x, axis=-1):
    return jax.nn.softmax(x, axis=axis)

def _gelu(x):
    return jax.nn.gelu(x, approximate=True)

def _silu(x):
    return jax.nn.silu(x)

def _sigmoid(x):
    return jax.nn.sigmoid(x)

def _layernorm(x, axis=-1, eps=1e-05):
    m = jnp.mean(x, axis=axis, keepdims=True)
    v = jnp.var(x, axis=axis, keepdims=True)
    return (x - m) / jnp.sqrt(v + eps)

def _scatter_add(tgt, idx, src, axis=0):
    return tgt.at[idx].add(src)

def _segment_sum(src, seg, n):
    return jax.ops.segment_sum(src, seg, n)
kernel_name = 'mk_gnn_ffn_d2_gnn_r64_ae7209'

def setup_inputs(seed: int=0):
    np.random.seed(seed)
    _w = jnp.asarray

    def _rec_inputs():
        import jax
        import jax.numpy as jnp
        _gk = jax.random.key(seed)
        x = -8.776e-05 + 1 * jax.random.normal(jax.random.fold_in(_gk, 1), (10000, 512), jnp.float32)
        src = jax.random.randint(jax.random.fold_in(_gk, 2), (2500,), 0, 10000, jnp.int32)
        dst = jax.random.randint(jax.random.fold_in(_gk, 3), (2500,), 0, 10000, jnp.int32)
        _o = jnp.argsort(dst, stable=True)
        src = src[_o]
        dst = dst[_o]
        edge_attr_8 = jax.random.uniform(jax.random.fold_in(_gk, 12), (2500, 8), jnp.float32, 0.0, 0.999999)
        edge_weight = jax.random.uniform(jax.random.fold_in(_gk, 14), (2500,), jnp.float32, 0.0, 0.0999999)
        node_vec = jax.random.uniform(jax.random.fold_in(_gk, 15), (10000,), jnp.float32, 0.0, 0.999988)
        return (x, src, dst, edge_attr_8, edge_weight, node_vec)
    x, src, dst, edge_attr_8, edge_weight, node_vec = _rec_inputs()

    def _L0_gnn_setup():
        import jax, jax.numpy as jnp
        import numpy as np
        N, E, D, H = (10000, 2500, 512, 8)
        HD = D // H
        SCALE = HD ** (-0.5)

        def _layernorm(x, g, b):
            mu = jnp.mean(x, axis=-1, keepdims=True)
            var = jnp.mean(jnp.square(x - mu), axis=-1, keepdims=True)
            return (x - mu) * jax.lax.rsqrt(var + 1e-05) * g + b
        key = jax.random.key(seed)
        ks = jax.random.split(key, 12)
        s = D ** (-0.5)
        return {'x': jax.random.normal(ks[0], (N, D), jnp.float32), 'edge_index': jax.random.randint(ks[1], (2, E), 0, N, jnp.int64), 'edge_weights': jax.random.uniform(ks[2], (E, H), jnp.float32), 'ln_g': jnp.ones((D,), jnp.float32), 'ln_b': jnp.zeros((D,), jnp.float32), 'Wq': jax.random.normal(ks[3], (D, D), jnp.float32) * s, 'bq': jnp.zeros((D,), jnp.float32), 'Wk': jax.random.normal(ks[4], (D, D), jnp.float32) * s, 'bk': jnp.zeros((D,), jnp.float32), 'Wv': jax.random.normal(ks[5], (D, D), jnp.float32) * s, 'bv': jnp.zeros((D,), jnp.float32), 'W1': jax.random.normal(ks[6], (D, D), jnp.float32) * s, 'b1': jnp.zeros((D,), jnp.float32), 'W2': jax.random.normal(ks[7], (D, D), jnp.float32) * s, 'b2': jnp.zeros((D,), jnp.float32)}
    _L0_gnn_all = _L0_gnn_setup()
    _L0_gnn_in = {k: v for k, v in _L0_gnn_all.items() if k in ('ln_g', 'ln_b', 'Wq', 'bq', 'Wk', 'bk', 'Wv', 'bv', 'W1', 'b1', 'W2', 'b2')}
    del _L0_gnn_all

    def _L0_ffn_setup():
        import jax, jax.numpy as jnp
        import numpy as np
        G = 4
        EPG = 4
        E = 16
        KG = 2
        K = 2
        GTP = 0.9
        TP = 0.9
        SCALE = 1.0 / float(np.sqrt(G))

        def _routing_weights(xf, Wr, br, Wgate, bgate):
            N = xf.shape[0]
            gp = jax.nn.softmax(xf @ Wr + br, axis=-1)
            order = jnp.argsort(-gp, axis=-1)
            sp_k = jnp.take_along_axis(gp, order, axis=-1)[:, :KG]
            idx_k = order[:, :KG]
            act = jnp.cumsum(sp_k, axis=-1) <= GTP
            act = act.at[:, 0].set(True)
            mp = sp_k * act
            rn = mp / (jnp.sum(mp, axis=-1, keepdims=True) + 1e-09)
            w_group = jnp.zeros((N, G), xf.dtype).at[jnp.arange(N)[:, None], idx_k].set(rn)
            ep = jax.nn.softmax(jnp.einsum('nd,gde->nge', xf, Wgate) + bgate, axis=-1)
            eorder = jnp.argsort(-ep, axis=-1)
            esp = jnp.take_along_axis(ep, eorder, axis=-1)[:, :, :K]
            eidx = eorder[:, :, :K]
            eact = jnp.cumsum(esp, axis=-1) <= TP
            eact = eact.at[:, :, 0].set(True)
            emp = esp * eact
            ern = emp / (jnp.sum(emp, axis=-1, keepdims=True) + 1e-09)
            w_exp = jnp.zeros((N, G, EPG), xf.dtype).at[jnp.arange(N)[:, None, None], jnp.arange(G)[None, :, None], eidx].set(ern)
            return (w_group[:, :, None] * w_exp * SCALE).reshape(N, E)
        key = jax.random.key(seed)
        ks = jax.random.split(key, 6)
        B, T, D, H = (2, 1024, 512, 32)
        x = jax.random.normal(ks[0], (B, T, D), jnp.float32)
        Wr = jax.random.normal(ks[1], (D, G), jnp.float32) * 0.02
        br = jnp.zeros((G,), jnp.float32)
        Wgate = jax.random.normal(ks[2], (G, D, EPG), jnp.float32) * 0.02
        bgate = jnp.zeros((G, EPG), jnp.float32)
        W1 = jax.random.normal(ks[3], (E, D, H), jnp.float32) * 0.02
        W3 = jax.random.normal(ks[4], (E, D, H), jnp.float32) * 0.02
        W2 = jax.random.normal(ks[5], (E, H, D), jnp.float32) * 0.02
        return {'x': x, 'Wr': Wr, 'br': br, 'Wgate': Wgate, 'bgate': bgate, 'W1': W1, 'W3': W3, 'W2': W2}
    _L0_ffn_all = _L0_ffn_setup()
    _L0_ffn_in = {k: v for k, v in _L0_ffn_all.items() if k in ('Wr', 'br', 'Wgate', 'bgate', 'W1', 'W3', 'W2')}
    del _L0_ffn_all

    def _L1_gnn_setup():
        import jax, jax.numpy as jnp
        import numpy as np
        N_NODES = 50000
        N_EDGES = 6250
        DIM = 512

        def _graph_conv(x, W0, W1, b, diag, edge_vals, edge_src, edge_dst):
            n = x.shape[0]
            self_term = diag[:, None] * (x @ W0)
            msgs = edge_vals[:, None] * (x @ W1)[edge_src]
            neigh = jax.ops.segment_sum(msgs, edge_dst, num_segments=n)
            return jax.nn.relu(self_term + neigh + b)
        key = jax.random.key(seed)
        ks = jax.random.split(key, 10)
        scale = 1.0 / np.sqrt(DIM)
        return {'x': jax.random.normal(ks[0], (N_NODES, DIM), jnp.float32), 'W0_1': jax.random.normal(ks[1], (DIM, DIM), jnp.float32) * scale, 'W1_1': jax.random.normal(ks[2], (DIM, DIM), jnp.float32) * scale, 'b1': jnp.zeros((DIM,), jnp.float32), 'W0_2': jax.random.normal(ks[3], (DIM, DIM), jnp.float32) * scale, 'W1_2': jax.random.normal(ks[4], (DIM, DIM), jnp.float32) * scale, 'b2': jnp.zeros((DIM,), jnp.float32), 'diag': jax.random.uniform(ks[5], (N_NODES,), jnp.float32), 'edge_vals': jax.random.uniform(ks[6], (N_EDGES,), jnp.float32) * 0.1, 'edge_src': jax.random.randint(ks[7], (N_EDGES,), 0, N_NODES, jnp.int32), 'edge_dst': jax.random.randint(ks[8], (N_EDGES,), 0, N_NODES, jnp.int32)}
    _L1_gnn_all = _L1_gnn_setup()
    _L1_gnn_in = {k: v for k, v in _L1_gnn_all.items() if k in ('W0_1', 'W1_1', 'b1', 'W0_2', 'W1_2', 'b2')}
    del _L1_gnn_all

    def _L1_ffn_setup():
        import jax, jax.numpy as jnp
        import numpy as np
        K = 2
        EPS = 1e-06

        def _layernorm(x, gamma, beta):
            mu = jnp.mean(x, axis=-1, keepdims=True)
            var = jnp.mean(jnp.square(x - mu), axis=-1, keepdims=True)
            return (x - mu) * jax.lax.rsqrt(var + EPS) * gamma + beta
        key = jax.random.key(seed)
        ks = jax.random.split(key, 5)
        B, S, D, F, E = (8, 32, 512, 32, 8)
        x = jax.random.normal(ks[0], (B, S, D), dtype=jnp.float32)
        router_w = jax.random.normal(ks[1], (D, E), dtype=jnp.float32) * 0.02
        w1 = jax.random.normal(ks[2], (E, D, F), dtype=jnp.float32) * 0.02
        b1 = jnp.zeros((E, F), dtype=jnp.float32)
        w2 = jax.random.normal(ks[3], (E, F, D), dtype=jnp.float32) * 0.02
        b2 = jnp.zeros((E, D), dtype=jnp.float32)
        gamma = jnp.ones((E, D), dtype=jnp.float32)
        beta = jnp.zeros((E, D), dtype=jnp.float32)
        return {'x': x, 'router_w': router_w, 'w1': w1, 'b1': b1, 'w2': w2, 'b2': b2, 'gamma': gamma, 'beta': beta}
    _L1_ffn_all = _L1_ffn_setup()
    _L1_ffn_in = {k: v for k, v in _L1_ffn_all.items() if k in ('router_w', 'w1', 'b1', 'w2', 'b2', 'gamma', 'beta')}
    del _L1_ffn_all
    return {'x': x, 'src': src, 'dst': dst, 'edge_attr_8': edge_attr_8, 'edge_weight': edge_weight, 'node_vec': node_vec, 'L0_gnn_ln_g': _L0_gnn_in['ln_g'], 'L0_gnn_ln_b': _L0_gnn_in['ln_b'], 'L0_gnn_Wq': _L0_gnn_in['Wq'], 'L0_gnn_bq': _L0_gnn_in['bq'], 'L0_gnn_Wk': _L0_gnn_in['Wk'], 'L0_gnn_bk': _L0_gnn_in['bk'], 'L0_gnn_Wv': _L0_gnn_in['Wv'], 'L0_gnn_bv': _L0_gnn_in['bv'], 'L0_gnn_W1': _L0_gnn_in['W1'], 'L0_gnn_b1': _L0_gnn_in['b1'], 'L0_gnn_W2': _L0_gnn_in['W2'], 'L0_gnn_b2': _L0_gnn_in['b2'], 'L0_ffn_Wr': _L0_ffn_in['Wr'], 'L0_ffn_br': _L0_ffn_in['br'], 'L0_ffn_Wgate': _L0_ffn_in['Wgate'], 'L0_ffn_bgate': _L0_ffn_in['bgate'], 'L0_ffn_W1': _L0_ffn_in['W1'], 'L0_ffn_W3': _L0_ffn_in['W3'], 'L0_ffn_W2': _L0_ffn_in['W2'], 'L1_gnn_W0_1': _L1_gnn_in['W0_1'], 'L1_gnn_W1_1': _L1_gnn_in['W1_1'], 'L1_gnn_b1': _L1_gnn_in['b1'], 'L1_gnn_W0_2': _L1_gnn_in['W0_2'], 'L1_gnn_W1_2': _L1_gnn_in['W1_2'], 'L1_gnn_b2': _L1_gnn_in['b2'], 'L1_ffn_router_w': _L1_ffn_in['router_w'], 'L1_ffn_w1': _L1_ffn_in['w1'], 'L1_ffn_b1': _L1_ffn_in['b1'], 'L1_ffn_w2': _L1_ffn_in['w2'], 'L1_ffn_b2': _L1_ffn_in['b2'], 'L1_ffn_gamma': _L1_ffn_in['gamma'], 'L1_ffn_beta': _L1_ffn_in['beta']}

def reference(x, src, dst, edge_attr_8, edge_weight, node_vec, L0_gnn_ln_g, L0_gnn_ln_b, L0_gnn_Wq, L0_gnn_bq, L0_gnn_Wk, L0_gnn_bk, L0_gnn_Wv, L0_gnn_bv, L0_gnn_W1, L0_gnn_b1, L0_gnn_W2, L0_gnn_b2, L0_ffn_Wr, L0_ffn_br, L0_ffn_Wgate, L0_ffn_bgate, L0_ffn_W1, L0_ffn_W3, L0_ffn_W2, L1_gnn_W0_1, L1_gnn_W1_1, L1_gnn_b1, L1_gnn_W0_2, L1_gnn_W1_2, L1_gnn_b2, L1_ffn_router_w, L1_ffn_w1, L1_ffn_b1, L1_ffn_w2, L1_ffn_b2, L1_ffn_gamma, L1_ffn_beta):
    import jax
    import jax.numpy as jnp

    def _L0_gnn_ref(x, edge_index, edge_weights, ln_g, ln_b, Wq, bq, Wk, bk, Wv, bv, W1, b1, W2, b2):
        import jax, jax.numpy as jnp
        import numpy as np
        N, E, D, H = (10000, 2500, 512, 8)
        HD = D // H
        SCALE = HD ** (-0.5)

        def _layernorm(x, g, b):
            mu = jnp.mean(x, axis=-1, keepdims=True)
            var = jnp.mean(jnp.square(x - mu), axis=-1, keepdims=True)
            return (x - mu) * jax.lax.rsqrt(var + 1e-05) * g + b
        origin, destination = (edge_index[0], edge_index[1])
        x_norm = _layernorm(x, ln_g, ln_b)
        q = (x_norm @ Wq + bq).reshape(N, H, HD)
        k = (x_norm @ Wk + bk).reshape(N, H, HD)
        v = (x_norm @ Wv + bv).reshape(N, H, HD)
        scores = jnp.einsum('ehd,ehd->eh', q[origin], k[destination]) * SCALE
        ws = scores * edge_weights
        seg_max = jax.ops.segment_max(ws, origin, num_segments=N)
        seg_max = jnp.where(jnp.isfinite(seg_max), seg_max, 0.0)
        e = jnp.exp(ws - seg_max[origin])
        denom = jax.ops.segment_sum(e, origin, num_segments=N)
        att = e / (denom[origin] + 1e-16)
        weighted_values = att[:, :, None] * v[destination]
        values = jax.ops.segment_sum(weighted_values, origin, num_segments=N)
        values = values.reshape(N, D)
        values = (values @ W1 + b1) @ W2 + b2
        return x + values

    def _L0_ffn_ref(x, Wr, br, Wgate, bgate, W1, W3, W2):
        import jax, jax.numpy as jnp
        import numpy as np
        G = 4
        EPG = 4
        E = 16
        KG = 2
        K = 2
        GTP = 0.9
        TP = 0.9
        SCALE = 1.0 / float(np.sqrt(G))

        def _routing_weights(xf, Wr, br, Wgate, bgate):
            N = xf.shape[0]
            gp = jax.nn.softmax(xf @ Wr + br, axis=-1)
            order = jnp.argsort(-gp, axis=-1)
            sp_k = jnp.take_along_axis(gp, order, axis=-1)[:, :KG]
            idx_k = order[:, :KG]
            act = jnp.cumsum(sp_k, axis=-1) <= GTP
            act = act.at[:, 0].set(True)
            mp = sp_k * act
            rn = mp / (jnp.sum(mp, axis=-1, keepdims=True) + 1e-09)
            w_group = jnp.zeros((N, G), xf.dtype).at[jnp.arange(N)[:, None], idx_k].set(rn)
            ep = jax.nn.softmax(jnp.einsum('nd,gde->nge', xf, Wgate) + bgate, axis=-1)
            eorder = jnp.argsort(-ep, axis=-1)
            esp = jnp.take_along_axis(ep, eorder, axis=-1)[:, :, :K]
            eidx = eorder[:, :, :K]
            eact = jnp.cumsum(esp, axis=-1) <= TP
            eact = eact.at[:, :, 0].set(True)
            emp = esp * eact
            ern = emp / (jnp.sum(emp, axis=-1, keepdims=True) + 1e-09)
            w_exp = jnp.zeros((N, G, EPG), xf.dtype).at[jnp.arange(N)[:, None, None], jnp.arange(G)[None, :, None], eidx].set(ern)
            return (w_group[:, :, None] * w_exp * SCALE).reshape(N, E)
        B, T, D = x.shape
        xf = x.reshape(-1, D)
        tw = _routing_weights(xf, Wr, br, Wgate, bgate)
        out = jnp.zeros_like(xf)
        for e in range(E):
            h = jax.nn.silu(xf @ W1[e]) * (xf @ W3[e])
            out = out + tw[:, e:e + 1] * (h @ W2[e])
        return out.reshape(B, T, D)

    def _L1_gnn_ref(x, W0_1, W1_1, b1, W0_2, W1_2, b2, diag, edge_vals, edge_src, edge_dst):
        import jax, jax.numpy as jnp
        import numpy as np
        N_NODES = 50000
        N_EDGES = 6250
        DIM = 512

        def _graph_conv(x, W0, W1, b, diag, edge_vals, edge_src, edge_dst):
            n = x.shape[0]
            self_term = diag[:, None] * (x @ W0)
            msgs = edge_vals[:, None] * (x @ W1)[edge_src]
            neigh = jax.ops.segment_sum(msgs, edge_dst, num_segments=n)
            return jax.nn.relu(self_term + neigh + b)
        h = _graph_conv(x, W0_1, W1_1, b1, diag, edge_vals, edge_src, edge_dst)
        h = _graph_conv(h, W0_2, W1_2, b2, diag, edge_vals, edge_src, edge_dst)
        return (h + x) * 0.5

    def _L1_ffn_ref(x, router_w, w1, b1, w2, b2, gamma, beta):
        import jax, jax.numpy as jnp
        import numpy as np
        K = 2
        EPS = 1e-06

        def _layernorm(x, gamma, beta):
            mu = jnp.mean(x, axis=-1, keepdims=True)
            var = jnp.mean(jnp.square(x - mu), axis=-1, keepdims=True)
            return (x - mu) * jax.lax.rsqrt(var + EPS) * gamma + beta
        B, S, D = x.shape
        E = w1.shape[0]
        xf = x.reshape(-1, D)
        logits = xf @ router_w
        gate_vals, idx = jax.lax.top_k(logits, K)
        gates = jax.nn.softmax(gate_vals, axis=-1)
        out = jnp.zeros_like(xf)
        for e in range(E):
            h = jax.nn.relu(xf @ w1[e] + b1[e]) @ w2[e] + b2[e]
            y = _layernorm(xf + h, gamma[e], beta[e])
            w = jnp.sum(jnp.where(idx == e, gates, 0.0), axis=-1)
            out = out + w[:, None] * y
        return out.reshape(B, S, D)
    edge_index = jnp.stack([src, dst])
    x = x + _L0_gnn_ref(_layernorm(x, axis=-1), edge_index, edge_attr_8, L0_gnn_ln_g, L0_gnn_ln_b, L0_gnn_Wq, L0_gnn_bq, L0_gnn_Wk, L0_gnn_bk, L0_gnn_Wv, L0_gnn_bv, L0_gnn_W1, L0_gnn_b1, L0_gnn_W2, L0_gnn_b2)
    x = x + _L0_ffn_ref(_layernorm(x, axis=-1)[None], L0_ffn_Wr, L0_ffn_br, L0_ffn_Wgate, L0_ffn_bgate, L0_ffn_W1, L0_ffn_W3, L0_ffn_W2)[0]
    x = x + _L1_gnn_ref(_layernorm(x, axis=-1), L1_gnn_W0_1, L1_gnn_W1_1, L1_gnn_b1, L1_gnn_W0_2, L1_gnn_W1_2, L1_gnn_b2, node_vec, edge_weight, src, dst)
    x = x + _L1_ffn_ref(_layernorm(x, axis=-1)[None], L1_ffn_router_w, L1_ffn_w1, L1_ffn_b1, L1_ffn_w2, L1_ffn_b2, L1_ffn_gamma, L1_ffn_beta)[0]
    return x

_drawn_inputs = setup_inputs


def setup_inputs(seed=0):
    import zlib

    import numpy as np

    out = dict(_drawn_inputs(seed))
    spreads = {'L0_gnn_ln_g': (1.0, 0.2),
     'L0_gnn_ln_b': (0.0, 0.39),
     'L0_gnn_bq': (0.0, 0.8),
     'L0_gnn_bk': (0.0, 0.8),
     'L0_gnn_bv': (0.0, 0.355),
     'L0_gnn_b1': (0.0, 0.1),
     'L0_gnn_b2': (0.0, 0.1),
     'L0_ffn_br': (0.0, 0.8),
     'L0_ffn_bgate': (0.0, 0.8),
     'L1_gnn_b1': (0.0, 0.8),
     'L1_gnn_b2': (0.0, 0.544),
     'L1_ffn_b1': (0.0, 2.0),
     'L1_ffn_b2': (0.0, 1.37),
     'L1_ffn_gamma': (1.0, 0.596),
     'L1_ffn_beta': (0.0, 0.411)}
    factors = {'edge_attr_8': 5.808,
     'edge_weight': 8.0,
     'L0_gnn_Wq': 2.831,
     'L0_gnn_Wk': 2.699,
     'L0_ffn_Wr': 8.0,
     'L0_ffn_Wgate': 8.0,
     'L0_ffn_W1': 8.0,
     'L0_ffn_W3': 8.0,
     'L0_ffn_W2': 8.0,
     'L1_gnn_W1_1': 8.0,
     'L1_gnn_W1_2': 8.0,
     'L1_ffn_w1': 8.0,
     'L1_ffn_w2': 7.476}
    for name, (base, spread) in spreads.items():
        noise = np.random.default_rng([zlib.crc32(name.encode()), seed]).standard_normal(out[name].shape)
        drawn = base * np.exp(spread * noise) if base else spread * noise
        out[name] = jnp.asarray(drawn.astype(out[name].dtype))
    for name, factor in factors.items():
        out[name] = (out[name] * factor).astype(out[name].dtype)
    return out
```

```python
from contextlib import ExitStack

import concourse.bass as bass
from concourse import mybir

F32 = mybir.dt.float32
F32R = mybir.dt.float32r
BF16 = mybir.dt.bfloat16
I32 = mybir.dt.int32
ALU = mybir.AluOpType
ACT = mybir.ActivationFunctionType
X_AXIS = mybir.AxisListType.X

P = 128
D = 512
KC = D // P
N = 10000
NG = 20
T = 4
GR = T * P
NT = NG * T
NPAD = NG * GR
E = 2500
ET = 20
EG = ET // T
EP = ET * P
HEADS = 8
HD = D // HEADS
NO_SLOT = 1 << 20
REC_S = 12
REC_D = 4
EXPERTS0 = 16
SETS = 5
EXPERTS1 = 8
HID1 = 32
FC1 = EXPERTS1 * HID1 // P


def ds(a, n):
    return bass.ds(a, n)


def split3(te, out, lhs, rhs, first=True, last=True):
    te.matmul(out, lhs[0], rhs[0], start=first, stop=False, skip_group_check=True)
    te.matmul(out, lhs[0], rhs[1], start=False, stop=False, skip_group_check=True)
    return te.matmul(out, lhs[1], rhs[0], start=False, stop=last, skip_group_check=True)


def hold(eng):
    eng.nop(nofuse=True)


class Steps:

    def __init__(self, eng, sem, base=0):
        self.eng, self.sem, self.base, self.n = eng, sem, base, 0

    def __call__(self, ins):
        ins.then_inc(self.sem, 1)
        self.n += 1
        return ins

    def settle(self):
        self.eng.wait_ge(self.sem, self.base + self.n)

    def link(self, ins):
        self(ins)
        self.settle()


class Core:

    def __init__(self, nc, stack, tag):
        self.nc, self.stack, self.tag = nc, stack, tag
        self.sems = []
        stack.callback(self.release)

    def sb(self, name, shape, dt=F32):
        return self.stack.enter_context(self.nc.sbuf_tensor(f"{self.tag}_{name}", shape, dt))

    def ps(self, name):
        return self.stack.enter_context(self.nc.psum_tensor(f"{self.tag}_{name}", [P, D], F32))

    def sem(self, name):
        self.sems.append(self.nc.alloc_semaphore(name=f"{self.tag}_{name}"))
        return self.sems[-1]

    def release(self):
        if self.sems:
            self.nc.clear_and_free_semaphores(self.sems)
            self.nc.all_engine_barrier()



def sort_phase(nc, a, k):
    with ExitStack() as stack:
        c = Core(nc, stack, "sort")
        raw = {x: c.sb(f"raw_{x}", [P, EP], I32) for x in "sd"}
        row = {x: c.sb(f"row_{x}", [P, EP]) for x in "sd"}
        col_i = {x: c.sb(f"col_i_{x}", [P, ET], I32) for x in "sd"}
        col = {x: c.sb(f"col_{x}", [P, ET]) for x in "sd"}
        lower = c.sb("lower", [P, ET])
        upper = c.sb("upper", [P, ET])
        middle = c.sb("middle", [P, ET])
        tri = c.sb("tri", [P, P])
        diag = {x: c.sb(f"diag_{x}", [P, ET, P]) for x in "sd"}
        mask = {x: c.sb(f"mask_{x}", [P, 4, EP], BF16) for x in "sd"}
        ones = c.sb("ones", [P, 1], BF16)
        one = c.sb("one", [1, 1])
        rank_row = {x: c.sb(f"rank_row_{x}", [1, EP]) for x in "sd"}
        rank = {x: c.sb(f"rank_{x}", [P, ET], I32) for x in "sd"}
        rec = {"s": c.sb("rec_s", [P, ET, REC_S], I32), "d": c.sb("rec_d", [P, ET, REC_D], I32)}
        attr = c.sb("attr", [P, ET, HEADS])
        edge_w = c.sb("edge_w", [P, ET])
        no_slot = c.sb("no_slot", [P, NPAD // P], I32)
        counts = [c.ps(f"counts{n}") for n in range(EP // D)]
        rank_cols = c.ps("rank_cols")
        keys_in, tri_made = c.sem("keys_in"), c.sem("tri_made")
        rec_in, rec_made = c.sem("rec_in"), c.sem("rec_made")
        dve, act = c.sem("dve"), c.sem("act")
        mask_made = {x: c.sem(f"mask_made_{x}") for x in "sd"}
        mask_used = {x: c.sem(f"mask_used_{x}") for x in "sd"}
        row_made = c.sem("row_made")
        cols_made = c.sem("cols_made")
        rank_made = c.sem("rank_made")
        tails_made, stored, scattered = c.sem("tails_made"), c.sem("stored"), c.sem("scattered")
        block = stack.enter_context(nc.Block())

        @block.sync
        def _(sp):
            for x in "sd":
                sp.dma_start(raw[x][:], a[f"key_{x}"].broadcast_to([P, EP])).then_inc(keys_in, 16)
                sp.dma_start(col_i[x][:], a[f"col_{x}"]).then_inc(keys_in, 16)
            sp.dma_start(attr[:], a["attr"]).then_inc(rec_in, 16)
            sp.dma_start(edge_w[:], a["edge_w"]).then_inc(rec_in, 16)
            sp.wait_ge(tails_made, 1)
            sp.dma_start(k.rec_s[EP:EP + 1, :], no_slot[0:1, 0:REC_S]).then_inc(stored, 16)
            sp.dma_start(k.rec_d[EP:EP + 1, :], no_slot[0:1, 0:REC_D]).then_inc(stored, 16)
            for x in "sd":
                sp.dma_start(k.slots[x].rearrange("(p n) o -> p (n o)", p=P), no_slot[:]).then_inc(stored, 16)
            sp.wait_ge(stored, 16 * 4)

        @block.gpsimd
        def _(pool):
            pool.memset(tri[:], 0.5).then_inc(tri_made, 1)
            pool.wait_ge(tri_made, 1)
            pool.affine_select(out=tri[:], in_=tri[:], compare_op=ALU.is_gt, fill=0.0, base=0,
                               pattern=[[1, P]], channel_multiplier=-1).then_inc(tri_made, 1)
            pool.memset(no_slot[:], NO_SLOT).then_inc(tails_made, 1)
            pool.memset(k.ident[:], 0.0).then_inc(tri_made, 1)
            pool.wait_ge(tri_made, 3)
            pool.affine_select(out=k.ident[:], in_=k.ident[:], compare_op=ALU.not_equal, fill=1.0,
                               base=0, pattern=[[-1, P]], channel_multiplier=1).then_inc(tri_made, 1)
            r = Steps(pool, rec_made)
            r(pool.memset(rec["s"][:, :, 2 + HEADS:REC_S], 0))
            r(pool.memset(rec["d"][:, :, 3:REC_D], 0))
            pool.wait_ge(keys_in, 64)
            pool.wait_ge(rec_in, 32)
            for x in "sd":
                r(pool.tensor_copy(rec[x][:, :, 0], col_i["s"][:]))
                r(pool.tensor_copy(rec[x][:, :, 1], col_i["d"][:]))
            r(pool.tensor_copy(rec["s"][:, :, 2:2 + HEADS].bitcast(F32), attr[:]))
            r(pool.tensor_copy(rec["d"][:, :, 2].bitcast(F32), edge_w[:]))
            r.settle()
            for n, (x, out) in enumerate((("s", k.rec_s), ("d", k.rec_d))):
                pool.wait_ge(rank_made, n + 1)
                for t in range(ET):
                    pool.indirect_dma_start(out[:, :], bass.IndirectOffsetOnAxis(ap=rank[x][:, t:t + 1], axis=0),
                                            rec[x][:, t, :], None, bounds_check=EP - 1,
                                            oob_is_err=False).then_inc(scattered, 16)
            pool.wait_ge(scattered, 2 * ET * 16)

        def mask_pieces(j):
            return (0, j * P), (j * P + P, EP), (j * P, j * P + P)

        @block.vector
        def _(v):
            s = Steps(v, dve)
            s(v.memset(ones[:], 1.0))
            s(v.memset(one[:], 1.0))
            v.wait_ge(keys_in, 64)
            for x in "sd":
                s(v.tensor_copy(row[x][:], raw[x][:]))
                s(v.tensor_copy(col[x][:], col_i[x][:]))
            s.settle()
            s(v.tensor_scalar(lower[:], col["d"][:], -1.0, -0.5, ALU.mult, ALU.add))
            s(v.tensor_scalar(upper[:], col["d"][:], -1.0, 0.5, ALU.mult, ALU.add))
            s(v.tensor_scalar(middle[:], col["d"][:], -1.0, -0.25, ALU.mult, ALU.add))
            v.wait_ge(tri_made, 2)
            for x in "ds":
                s(v.tensor_tensor(diag[x][:], row[x][:].rearrange("p (t n) -> p t n", n=P),
                                  tri[:].unsqueeze(1).broadcast_to([P, ET, P]), ALU.add))
            s.settle()
            assert s.n == 11
            for j in range(ET):
                key = col["s"][:, j:j + 1]
                before, after, own = mask_pieces(j)
                if j >= 4:
                    v.wait_ge(mask_used["s"], j - 3)
                if before[1]:
                    v.tensor_scalar(mask["s"][:, j % 4, before[0]:before[1]], row["s"][:, before[0]:before[1]],
                                    key, None, ALU.is_gt)
                if after[0] < EP:
                    v.tensor_scalar(mask["s"][:, j % 4, after[0]:after[1]], row["s"][:, after[0]:after[1]],
                                    key, None, ALU.is_ge)
                v.tensor_scalar(mask["s"][:, j % 4, own[0]:own[1]], diag["s"][:, j, :], key, None,
                                ALU.is_gt).then_inc(mask_made["s"], 1)
            v.wait_ge(mask_used["s"], ET)
            for n in range(EP // D):
                v.tensor_copy(rank_row["s"][:, n * D:n * D + D], counts[n][0:1, :]).then_inc(row_made, 1)
            v.wait_ge(cols_made, 1)
            v.tensor_copy(rank["s"][:], rank_cols[:, 0:ET]).then_inc(rank_made, 1)
            v.wait_ge(mask_used["d"], ET)
            for n in range(EP // D):
                v.tensor_scalar(rank_row["d"][:, n * D:n * D + D], counts[n][0:1, :], 0.5, EP / 2,
                                ALU.mult, ALU.add).then_inc(row_made, 1)
            v.wait_ge(cols_made, 2)
            v.tensor_copy(rank["d"][:], rank_cols[:, 0:ET]).then_inc(rank_made, 1)
            v.wait_ge(rank_made, 2)

        @block.scalar
        def _(act_):
            act_.wait_ge(dve, 11)
            for j in range(ET):
                before, after, own = mask_pieces(j)
                if j >= 4:
                    act_.wait_ge(mask_used["d"], j - 3)
                if before[1]:
                    act_.activation(mask["d"][:, j % 4, before[0]:before[1]], row["d"][:, before[0]:before[1]],
                                    ACT.Sign, bias=lower[:, j:j + 1])
                if after[0] < EP:
                    act_.activation(mask["d"][:, j % 4, after[0]:after[1]], row["d"][:, after[0]:after[1]],
                                    ACT.Sign, bias=upper[:, j:j + 1])
                act_.activation(mask["d"][:, j % 4, own[0]:own[1]], diag["d"][:, j, :], ACT.Sign,
                                bias=middle[:, j:j + 1]).then_inc(mask_made["d"], 1)

        @block.tensor
        def _(pe):
            pe.wait_ge(dve, 2)
            for n, x in enumerate("sd"):
                if n:
                    pe.wait_ge(row_made, 5)
                for j in range(ET):
                    pe.wait_ge(mask_made[x], j + 1)
                    for m in range(EP // D):
                        last = pe.matmul(counts[m][0:1, :], ones[:], mask[x][:, j % 4, m * D:m * D + D],
                                         start=j == 0, stop=j == ET - 1)
                    last.then_inc(mask_used[x], 1)
                pe.wait_ge(row_made, 5 * (n + 1))
                if n:
                    pe.wait_ge(rank_made, 1)
                for t in range(ET):
                    last = pe.matmul(rank_cols[:, t:t + 1], rank_row[x][:, t * P:t * P + P], one[:],
                                     start=True, stop=True)
                last.then_inc(cols_made, 1)



def edge_columns(v, s, k, x, rec_cols, next_key, places, slot_at):
    key = rec_cols
    s.link(v.tensor_tensor(places[:, 0:ET], key, next_key, ALU.is_equal))
    s(v.tensor_scalar(places[:, ET:2 * ET], key, 7, None, ALU.logical_shift_right))
    s.link(v.tensor_scalar(places[:, 2 * ET:3 * ET], key, 127, None, ALU.bitwise_and))
    s.link(v.tensor_scalar(places[:, 2 * ET:3 * ET], places[:, 2 * ET:3 * ET], NT, None, ALU.mult))
    s.link(v.tensor_tensor(places[:, ET:2 * ET], places[:, ET:2 * ET], places[:, 2 * ET:3 * ET], ALU.add))
    s.link(v.tensor_scalar(places[:, 0:ET], places[:, 0:ET], NO_SLOT, None, ALU.mult))
    s.link(v.tensor_tensor(slot_at, places[:, ET:2 * ET], places[:, 0:ET], ALU.add))


def attention_phase(nc, a, k):
    with ExitStack() as stack:
        c = Core(nc, stack, "att")
        same, rec = k.same, k.rec
        hi = {n: c.sb(f"{n}_hi", [P, KC, D], F32R) for n in ("wq", "wk", "wv", "w12")}
        lo = {n: c.sb(f"{n}_lo", [P, KC, D], F32R) for n in ("wq", "wk", "wv", "w12")}
        ln_g, ln_b = c.sb("ln_g", [P, KC]), c.sb("ln_b", [P, KC])
        bias_in = c.sb("bias_in", [P, 3, KC])
        bias = c.sb("bias", [P, 3, KC])
        headsel = c.sb("headsel", [P, KC, HEADS])
        headsel2 = c.sb("headsel2", [HEADS, D])
        flags_ready = c.sem("flags_ready")

        recs_in, made, chain = c.sem("recs_in"), c.sem("made"), c.sem("chain")
        keyt, keyc = c.sem("keyt"), c.sem("keyc")
        stage_in = [c.sem(f"stage_in{n}") for n in range(2)]
        stage_free, hi_made, prep = c.sem("stage_free"), c.sem("hi_made"), c.sem("prep")
        small_in, w12_done, b12_done, bias_done = (c.sem(n) for n in ("small_in", "w12_done", "b12_done", "bias_done"))
        slots_out = c.sem("slots_out")
        w_scaled = c.sem("w_scaled")
        split_done = c.sem("split_done")
        slots_in = c.sem("slots_in")

        with ExitStack() as inner:
            ci = Core(nc, inner, "prep")
            stage = [ci.sb(f"stage{n}", [P, KC, D]) for n in range(2)]
            next_key = {x: ci.sb(f"next_key_{x}", [P, ET], I32) for x in "sd"}
            places = ci.sb("places", [P, 3 * ET], I32)
            slot_at = {x: ci.sb(f"slot_at_{x}", [P, ET], I32) for x in "sd"}
            own_place = ci.sb("own_place", [P, ET], I32)
            key_f = ci.sb("key_f", [P, ET])
            key_diag = ci.sb("key_diag", [P, 2, P])
            key_row = ci.sb("key_row", [P, 2, GR + 1])
            b1_col = ci.sb("b1_col", [P, KC])
            b1_wide = ci.sb("b1_wide", [P, KC, P])
            b2_row = ci.sb("b2_row", [1, D])
            ones_row = ci.sb("ones_row", [1, P])
            w1t = ci.sb("w1t", [P, KC, D])
            w2 = ci.sb("w2", [P, KC, D])
            w12 = ci.sb("w12", [P, KC, D])
            pk = [ci.ps(f"pk{n}") for n in range(2)]
            pb = ci.ps("pb")
            pw = [ci.ps(f"pw{n}") for n in range(2)]
            names = ("wq", "wk", "wv")
            w1_in = ci.sem("w1_in")
            rows_made = ci.sem("rows_made")
            block = inner.enter_context(nc.Block())

            @block.sync
            def _(sp):
                for x, t, w in (("s", k.rec_s, REC_S), ("d", k.rec_d, REC_D)):
                    sp.dma_start(rec[x][:], t[0:EP, :].rearrange("(t p) w -> p t w", p=P)).then_inc(recs_in, 16)
                    kk = 0 if x == "s" else 1
                    with nc.allow_non_contiguous_dma(reason="one word of each record"):
                        sp.dma_start(next_key[x][:], t[1:EP + 1, kk:kk + 1].rearrange("(t p) w -> p (t w)", p=P))\
                          .then_inc(recs_in, 16)
                for t, s in ((ln_g, "ln_g"), (ln_b, "ln_b"), (b1_col, "b1_col"), (b2_row, "b2_row")):
                    sp.dma_start(t[:], a[s]).then_inc(small_in, 16)
                for n, s in enumerate(("bq", "bk", "bv")):
                    sp.dma_start(bias_in[:, n, :], a[s]).then_inc(small_in, 16)
                sp.dma_start(w1t[:], a["w1t"].rearrange("(c p) n -> p c n", p=P)).then_inc(w1_in, 16)
                sp.dma_start(w2[:], a["w2"].rearrange("(c p) n -> p c n", p=P)).then_inc(w1_in, 16)
                for n, name in enumerate(names):
                    if n >= 2:
                        sp.wait_ge(split_done, n - 1)
                    sp.dma_start(stage[n % 2][:], a[name].rearrange("(c p) n -> p c n", p=P)).then_inc(stage_in[n % 2], 16)
                sp.wait_ge(slots_out, 2 * ET * 16)
                for x in "sd":
                    sp.dma_start(k.slot[x][:], k.slots[x].rearrange("(p n) o -> p (n o)", p=P)).then_inc(slots_in, 16)
                sp.wait_ge(slots_in, 32)

            @block.gpsimd
            def _(pool):
                s = Steps(pool, made)
                s(pool.iota(own_place[:], pattern=[[P, ET]], base=0, channel_multiplier=1))
                s(pool.memset(headsel[:], HD ** -0.5))
                s(pool.memset(headsel2[:], 1.0))
                s(pool.memset(ones_row[:], 1.0))
                s(pool.memset(k.zeros[:], 0.0))
                s(pool.memset(k.ones[:], 1.0))
                s(pool.memset(k.half_neg[:], -0.5))
                s.settle()
                s.link(pool.affine_select(out=headsel[:], in_=headsel[:], compare_op=ALU.is_ge, fill=0.0, base=0,
                                          pattern=[[P, KC], [-HD, HEADS]], channel_multiplier=1))
                s.link(pool.affine_select(out=headsel[:], in_=headsel[:], compare_op=ALU.is_ge, fill=0.0, base=HD - 1,
                                          pattern=[[-P, KC], [HD, HEADS]], channel_multiplier=-1))
                s.link(pool.affine_select(out=headsel2[:], in_=headsel2[:], compare_op=ALU.is_ge, fill=0.0, base=0,
                                          pattern=[[1, D]], channel_multiplier=-HD))
                s.link(pool.affine_select(out=headsel2[:], in_=headsel2[:], compare_op=ALU.is_ge, fill=0.0,
                                          base=HD - 1, pattern=[[-1, D]], channel_multiplier=HD))
                for n, x in enumerate("sd"):
                    pool.wait_ge(chain, 7 * (n + 1))
                    for t in range(ET):
                        pool.indirect_dma_start(k.slots[x][:, :],
                                                bass.IndirectOffsetOnAxis(ap=slot_at[x][:, t:t + 1], axis=0),
                                                own_place[:, t:t + 1], None, bounds_check=NPAD - 1,
                                                oob_is_err=False).then_inc(slots_out, 16)

            @block.vector
            def _(v):
                s = Steps(v, chain)
                v.wait_ge(recs_in, 64)
                for n, x in enumerate("sd"):
                    edge_columns(v, s, k, x, rec[x][:, :, n], next_key[x][:], places, slot_at[x][:])
                v.wait_ge(small_in, 7 * 16)
                for kc in range(KC):
                    s(v.tensor_copy(b1_wide[:, kc, :], b1_col[:, kc:kc + 1].broadcast_to([P, P])))
                s.settle()
                assert s.n == 18
                q = Steps(v, rows_made)
                for n, x in enumerate("sd"):
                    q.link(v.tensor_copy(key_f[:], rec[x][:, :, n]))
                    q.link(v.memset(key_row[:, 1, GR:GR + 1], -1.0))
                    for g in range(EG):
                        for t in range(T):
                            i = (n * EG + g) * T + t
                            if i >= 2:
                                v.wait_ge(keyt, i - 1)
                            v.tensor_scalar(key_diag[:, i % 2, :], k.ident[:], key_f[:, g * T + t:g * T + t + 1], None,
                                            ALU.mult).then_inc(keyc, 1)
                        v.wait_ge(keyt, (n * EG + g + 1) * T)
                        q(v.tensor_copy(key_row[:, g % 2, 0:1], key_row[:, (g + 1) % 2, GR:GR + 1]))
                        q.link(v.tensor_copy(key_row[:, g % 2, 1:GR + 1], pk[g % 2][:]))
                        q.link(v.tensor_tensor(same[x][:, g * GR:g * GR + GR], key_row[:, g % 2, 1:GR + 1],
                                               key_row[:, g % 2, 0:GR], ALU.is_equal))
                    q.link(v.memset(same[x][:, EP:EP + 1], 0.0))
                for n in range(3):
                    v.wait_ge(stage_in[n % 2], 16 * (n // 2 + 1))
                    v.wait_ge(bias_done, n + 1)
                    for kc in range(KC):
                        ins = v.tensor_scalar(stage[n % 2][:, kc, :], stage[n % 2][:, kc, :], ln_g[:, kc:kc + 1], None,
                                              ALU.mult)
                    ins.then_inc(w_scaled, 1)
                    v.wait_ge(hi_made, n + 1)
                    v.tensor_tensor(lo[names[n]][:], stage[n % 2][:], hi[names[n]][:].bitcast(F32), ALU.subtract)\
                     .then_inc(split_done, 1)
                v.wait_ge(bias_done, 3)
                q.link(v.tensor_tensor(bias[:], bias_in[:], pb[:, 0:3 * KC].rearrange("p (n c) -> p n c", n=3), ALU.add))
                for c4 in range(KC):
                    v.wait_ge(w12_done, c4 + 1)
                    v.tensor_copy(w12[:, c4, :], pw[c4 % 2][:]).then_inc(w_scaled, 1)
                v.wait_ge(hi_made, 4)
                v.tensor_tensor(lo["w12"][:], w12[:], hi["w12"][:].bitcast(F32), ALU.subtract).then_inc(split_done, 1)
                v.wait_ge(b12_done, 1)
                v.tensor_copy(k.b12[:], pw[0][:]).then_inc(split_done, 1)
                v.wait_ge(split_done, 5)

            @block.scalar
            def _(act_):
                act_.wait_ge(small_in, 7 * 16)
                for n in range(3):
                    act_.wait_ge(w_scaled, n + 1)
                    act_.activation(hi[names[n]][:], stage[n % 2][:], ACT.Copy).then_inc(hi_made, 1)
                act_.wait_ge(w_scaled, 7)
                act_.activation(hi["w12"][:], w12[:], ACT.Copy).then_inc(hi_made, 1)

            @block.tensor
            def _(pe):
                pe.wait_ge(made, 7)
                for i in range(2 * ET):
                    g = i // T
                    if g >= 2 and i % T == 0:
                        n, gg = divmod(g, EG)
                        pe.wait_ge(rows_made, n * (3 + 3 * EG) + 2 + 3 * gg - 3 if gg else 3 + 3 * EG)
                    pe.wait_ge(keyc, i + 1)
                    pe.matmul(pk[(g % EG) % 2][:, (i % T) * P:(i % T) * P + P], k.ones[:], key_diag[:, i % 2, :],
                              start=True, stop=True).then_inc(keyt, 1)
                for n in range(3):
                    pe.wait_ge(stage_in[n % 2], 16 * (n // 2 + 1))
                    for dc in range(KC):
                        for kc in range(KC):
                            last = pe.matmul(pb[:, n * KC + dc:n * KC + dc + 1], stage[n % 2][:, kc, dc * P:dc * P + P],
                                             ln_b[:, kc:kc + 1], start=kc == 0, stop=kc == KC - 1)
                    last.then_inc(bias_done, 1)
                pe.wait_ge(w1_in, 32)
                for ic in range(KC):
                    if ic >= 2:
                        pe.wait_ge(w_scaled, 3 + ic - 1)
                    for kc in range(KC):
                        last = pe.matmul(pw[ic % 2][:], w1t[:, kc, ic * P:ic * P + P], w2[:, kc, :],
                                         start=kc == 0, stop=kc == KC - 1)
                    last.then_inc(w12_done, 1)
                pe.wait_ge(w_scaled, 6)
                for kc in range(KC):
                    pe.matmul(pw[0][:], b1_wide[:, kc, :], w2[:, kc, :], start=kc == 0, stop=False)
                pe.matmul(pw[0][:], ones_row[:], b2_row[:], start=False, stop=True).then_inc(b12_done, 1)

        qkv_and_softmax(nc, a, k, stack, c, hi, lo, bias, headsel, headsel2)


def qkv_and_softmax(nc, a, k, outer, co, hi, lo, bias, headsel, headsel2):
    with ExitStack() as stack:
        c = Core(nc, stack, "edge")
        scores = c.sb("scores", [HEADS, EP])
        value = c.sb("value", [P, KC, EP + 1])
        with ExitStack() as inner:
            project_edges(nc, a, k, inner, hi, lo, bias, headsel, scores, value)
        with ExitStack() as inner:
            aggregate_values(nc, a, k, inner, hi, lo, headsel2, scores, value)


def project_edges(nc, a, k, stack, hi, lo, bias, headsel, scores, value):
    c = Core(nc, stack, "qkv")
    rows = {x: c.sb(f"rows_{x}", [P, T, D]) for x in "sd"}
    at = {x: c.sb(f"at_{x}", [P, T], I32) for x in "sd"}
    st = {x: c.sb(f"st_{x}", [P, T, 6]) for x in "sd"}
    mv = {x: c.sb(f"mv_{x}", [P, T, 2]) for x in "sd"}
    ve = {x: c.sb(f"ve_{x}", [P, T]) for x in "sd"}
    r1 = {x: c.sb(f"r1_{x}", [P, T]) for x in "sd"}
    r2 = {x: c.sb(f"r2_{x}", [P, T]) for x in "sd"}
    shift = {x: c.sb(f"shift_{x}", [P, T]) for x in "sd"}
    xh = {x: c.sb(f"xh_{x}", [P, KC, GR], F32R) for x in "sd"}
    xl = {x: c.sb(f"xl_{x}", [P, KC, GR], F32R) for x in "sd"}
    qs = c.sb("qs", [P, KC, GR])
    prod = c.sb("prod", [P, 2, GR])
    attr = c.sb("attr", [P, T, 8])
    attr_t = c.sb("attr_t", [P, GR])
    pp = [c.ps(f"pp{n}") for n in range(2)]
    tr = [c.ps(f"tr{n}") for n in range(2)]
    p_score, p_attr = c.ps("p_score"), c.ps("p_attr")
    at_made, attr_made = c.sem("at_made"), c.sem("attr_made")
    rows_in = {x: [c.sem(f"rows_in_{x}{t}") for t in range(T)] for x in "sd"}
    stats = {x: c.sem(f"stats_{x}") for x in "sd"}
    pow_done = {x: c.sem(f"pow_done_{x}") for x in "sd"}
    normed = {x: c.sem(f"normed_{x}") for x in "sd"}
    turned = {x: c.sem(f"turned_{x}") for x in "sd"}
    hi_made = {x: c.sem(f"hi_made_{x}") for x in "sd"}
    lo_made = {x: c.sem(f"lo_made_{x}") for x in "sd"}
    q_done, k_done, v_done, q_out, k_out, v_out = (c.sem(n) for n in ("q_done", "k_done", "v_done", "q_out", "k_out", "v_out"))
    score_done, score_out, attr_turned, attr_out = (c.sem(n) for n in ("score_done", "score_out", "attr_turned", "attr_out"))
    value0 = c.sem("value0")
    block = stack.enter_context(nc.Block())
    NST = 9

    def gather(pool, g):
        for n, x in enumerate("sd"):
            pool.wait_ge(turned[x], 4 * g + 4)
            hold(pool)
            pool.tensor_copy(at[x][:], k.rec["s"][:, ds(4 * g, T), n]).then_inc(at_made, 1)
            pool.wait_ge(at_made, 3 * g + n + 1)
            hold(pool)
            for t in range(T):
                pool.indirect_dma_start(rows[x][:, t, :], None, a["x"][:, :],
                                        bass.IndirectOffsetOnAxis(ap=at[x][:, t:t + 1], axis=0),
                                        bounds_check=NPAD - 1, oob_is_err=False).then_inc(rows_in[x][t], 16)
        pool.wait_ge(attr_turned, g + 1)
        hold(pool)
        pool.tensor_copy(attr[:], k.rec["s"][:, ds(4 * g, T), 2:10].bitcast(F32)).then_inc(at_made, 1)

    def powers(pool, g):
        for x in "sd":
            for n, r in enumerate((r1, r2)):
                pool.wait_ge(stats[x], NST * g + (4 if n == 0 else 7))
                pool.tensor_tensor(r[x][:], ve[x][:], k.half_neg[:, 0:T], ALU.pow).then_inc(pow_done[x], 1)

    @block.gpsimd
    def _(pool):
        gather(pool, 0)
        powers(pool, 0)
        with pool.Fori(0, EG - 1) as g:
            gather(pool, g + 1)
            powers(pool, g + 1)

    def statistics(v, g, x):
        s = Steps(v, stats[x], NST * g)
        for t in range(T):
            v.wait_ge(rows_in[x][t], 16 * g + 16)
            hold(v)
            ins = v.bn_stats(st[x][:, t, :], rows[x][:, t, :])
            if t == T - 1:
                s.link(ins)
        for t in range(T):
            if t == 0:
                hold(v)
            ins = v.bn_aggr(mv[x][:, t, :], st[x][:, t, :])
            if t == T - 1:
                s.link(ins)
        var, mean = mv[x][:, :, 1], mv[x][:, :, 0]
        s(v.tensor_scalar(shift[x][:], mean, -1.0, None, ALU.mult))
        s(v.tensor_scalar(ve[x][:], var, 1e-5, None, ALU.add))
        v.wait_ge(pow_done[x], 2 * g + 1)
        s.link(v.tensor_tensor(ve[x][:], var, r1[x][:], ALU.mult))
        s.link(v.tensor_tensor(ve[x][:], ve[x][:], r1[x][:], ALU.mult))
        s(v.tensor_scalar(ve[x][:], ve[x][:], 1e-5, None, ALU.add))
        v.wait_ge(pow_done[x], 2 * g + 2)
        s.link(v.tensor_tensor(r2[x][:], r1[x][:], r2[x][:], ALU.mult))
        s(v.tensor_tensor(shift[x][:], shift[x][:], r2[x][:], ALU.mult))
        assert s.n == NST

    def split_lo(v, g, x, t, turn):
        v.wait_ge(hi_made[x], 4 * g + t + 1)
        v.tensor_tensor(xl[x][:, :, t * P:t * P + P], tr[turn][:].rearrange("p (c n) -> p c n", n=P),
                        xh[x][:, :, t * P:t * P + P].bitcast(F32), ALU.subtract).then_inc(lo_made[x], 1)

    @block.vector
    def _(v):
        v.sem_inc(k_out, 1)
        v.sem_inc(score_out, 1)
        v.memset(value[:, :, 0:1], 0.0).then_inc(value0, 1)
        statistics(v, 0, "s")
        statistics(v, 0, "d")
        for t in range(T):
            split_lo(v, 0, "s", t, t % 2)

        def body(g, last):
            for t in range(T):
                split_lo(v, g, "d", t, t % 2)
            for cc in range(KC):
                v.wait_ge(k_done, 4 * g + cc + 1)
                v.wait_ge(q_out, 4 * g + cc + 1)
                v.wait_ge(score_done, 4 * g + cc + 1)
                v.scalar_tensor_tensor(prod[:, cc % 2, :], pp[cc % 2][:], bias[:, 1, cc:cc + 1], qs[:, cc, :],
                                       ALU.add, ALU.mult).then_inc(k_out, 1)
            if not last:
                statistics(v, g + 1, "s")
            v.wait_ge(attr_out, g + 1)
            v.wait_ge(score_done, 4 * g + 4 + 2)
            v.tensor_tensor(scores[:, ds(g * GR, GR)], p_score[0:HEADS, :], attr_t[0:HEADS, :], ALU.mult)\
             .then_inc(score_out, 1)
            if not last:
                for t in range(T):
                    split_lo(v, g + 1, "s", t, t % 2)
                statistics(v, g + 1, "d")

        with v.Fori(0, EG - 1) as g:
            body(g, False)
        body(EG - 1, True)
        v.wait_ge(score_out, EG + 1)

    def norm(act_, g, x, t):
        if t == 0:
            act_.wait_ge(stats[x], NST * g + NST)
        act_.activation(rows[x][:, t, :], rows[x][:, t, :], ACT.Identity, bias=shift[x][:, t:t + 1],
                        scale=r2[x][:, t:t + 1]).then_inc(normed[x], 1)

    def split_hi(act_, g, x, t, turn):
        act_.wait_ge(turned[x], 4 * g + t + 1 + 4)
        act_.activation(xh[x][:, :, t * P:t * P + P], tr[turn][:].rearrange("p (c n) -> p c n", n=P),
                        ACT.Copy).then_inc(hi_made[x], 1)

    @block.scalar
    def _(act_):
        act_.sem_inc(v_out, 4)
        for x in "sd":
            for t in range(T):
                norm(act_, 0, x, t)
        for t in range(T):
            split_hi(act_, 0, "s", t, t % 2)

        def body(g, last):
            for cc in range(KC):
                act_.wait_ge(q_done, 4 * g + cc + 1)
                if cc == 0:
                    act_.wait_ge(k_out, 4 * g + 1)
                act_.activation(qs[:, cc, :], pp[cc % 2][:], ACT.Identity, bias=bias[:, 0, cc:cc + 1])\
                    .then_inc(q_out, 1)
                split_hi(act_, g, "d", cc, cc % 2)
            act_.wait_ge(attr_turned, g + 2)
            act_.wait_ge(score_out, g + 1)
            act_.activation(attr_t[0:HEADS, :], p_attr[0:HEADS, :], ACT.Copy).then_inc(attr_out, 1)
            if not last:
                for t in range(T):
                    norm(act_, g + 1, "s", t)
            for cc in range(KC):
                if not last:
                    split_hi(act_, g + 1, "s", cc, cc % 2)
                act_.wait_ge(v_done, 4 * g + cc + 1)
                act_.activation(value[:, cc, ds(g * GR + 1, GR)], pp[cc % 2][:], ACT.Identity,
                                bias=bias[:, 2, cc:cc + 1]).then_inc(v_out, 1)
            if not last:
                for t in range(T):
                    norm(act_, g + 1, "d", t)

        with act_.Fori(0, EG - 1) as g:
            body(g, False)
        body(EG - 1, True)

    def turn(pe, g, x, t):
        pe.wait_ge(normed[x], 4 * g + t + 1)
        for kc in range(KC):
            last = pe.transpose(tr[t % 2][:, kc * P:kc * P + P], rows[x][:, t, kc * P:kc * P + P], k.ident[:])
        last.then_inc(turned[x], 1)

    def project(pe, x, name, cc):
        for kc in range(KC):
            w = [z[name][:, kc, cc * P:cc * P + P] for z in (hi, lo)]
            last = split3(pe, pp[cc % 2][:], w, (xh[x][:, kc, :], xl[x][:, kc, :]), kc == 0, kc == KC - 1)
        return last

    @block.tensor
    def _(pe):
        pe.sem_inc(attr_turned, 1)
        pe.sem_inc(score_done, 2)
        pe.sem_inc(turned["s"], 4)
        pe.sem_inc(turned["d"], 4)
        for t in range(T):
            if t >= 2:
                pe.wait_ge(lo_made["s"], t - 1)
            turn(pe, 0, "s", t)

        def body(g, last_group):
            pe.wait_ge(lo_made["s"], 4 * g + 4)
            for cc in range(KC):
                if cc >= 2:
                    pe.wait_ge(q_out, 4 * g + cc - 1)
                else:
                    pe.wait_ge(v_out, 4 * g + cc + 1 + 2)
                project(pe, "s", "wq", cc).then_inc(q_done, 1)
                if cc >= 2:
                    pe.wait_ge(lo_made["d"], 4 * g + cc - 1)
                turn(pe, g, "d", cc)
            pe.wait_ge(lo_made["d"], 4 * g + 4)
            for cc in range(KC):
                if cc >= 2:
                    pe.wait_ge(k_out, 4 * g + cc - 1 + 1)
                else:
                    pe.wait_ge(q_out, 4 * g + cc + 3)
                project(pe, "d", "wk", cc).then_inc(k_done, 1)
                if cc == 0:
                    pe.wait_ge(score_out, g + 1)
                if cc >= 1:
                    score(pe, g, cc - 1)
            pe.wait_ge(at_made, 3 * g + 3)
            for t in range(T):
                last = pe.matmul(p_attr[0:HEADS, t * P:t * P + P], attr[:, t, :], k.ident[:], start=True, stop=True)
            last.then_inc(attr_turned, 1)
            for cc in range(KC):
                if cc == 1:
                    score(pe, g, KC - 1)
                if not last_group:
                    if cc >= 2:
                        pe.wait_ge(lo_made["s"], 4 * g + 4 + cc - 1)
                    turn(pe, g + 1, "s", cc)
                if cc < 2:
                    pe.wait_ge(k_out, 4 * g + cc + 4)
                else:
                    pe.wait_ge(v_out, 4 * g + cc + 3)
                project(pe, "d", "wv", cc).then_inc(v_done, 1)

        def score(pe, g, cc):
            pe.wait_ge(k_out, 4 * g + cc + 1 + 1)
            pe.matmul(p_score[0:HEADS, :], headsel[:, cc, :], prod[:, cc % 2, :], start=cc == 0,
                      stop=cc == KC - 1, skip_group_check=True).then_inc(score_done, 1)

        with pe.Fori(0, EG - 1) as g:
            body(g, False)
        body(EG - 1, True)



def aggregate_values(nc, a, k, stack, hi, lo, headsel2, scores, value):
    c = Core(nc, stack, "agg")
    pen = c.sb("pen", [HEADS, EP + 1])
    best = c.sb("best", [HEADS, EP])
    expo = c.sb("expo", [HEADS, EP])
    ah, al = c.sb("ah", [P, KC, GR], F32R), c.sb("al", [P, KC, GR], F32R)
    out = c.sb("out", [P, 2, D])
    pa = [c.ps(f"pa{n}") for n in range(KC)]
    po = [c.ps(f"po{n}") for n in range(2)]
    chain, exp_done, att_ready = c.sem("chain"), c.sem("exp_done"), c.sem("att_ready")
    spread, weighted, summed, hi_made, lo_made = (c.sem(n) for n in ("spread", "weighted", "summed", "hi_made", "lo_made"))
    row_done, row_out = c.sem("row_done"), c.sem("row_out")
    stored = [c.sem(f"stored{n}") for n in range(2)]
    same = k.same["s"]
    block = stack.enter_context(nc.Block())

    @block.vector
    def _(v):
        v.sem_inc(weighted, KC)
        s = Steps(v, chain)
        s.link(v.tensor_scalar(pen[:], same[0:HEADS, :], -1.0, 1e30, ALU.add, ALU.mult))
        s.link(v.tensor_tensor_scan(best[:], pen[:, 0:EP], scores[:], 0.0, ALU.add, ALU.max))
        s.link(v.tensor_tensor_scan(best[:, ::-1], pen[:, EP:0:-1], best[:, ::-1], -1e30, ALU.add, ALU.max))
        s(v.tensor_tensor(scores[:], scores[:], best[:], ALU.subtract))
        v.wait_ge(exp_done, 1)
        s.link(v.tensor_tensor_scan(best[:], same[0:HEADS, 0:EP], expo[:], 0.0, ALU.mult, ALU.add))
        s.link(v.tensor_tensor_scan(best[:, ::-1], same[0:HEADS, EP:0:-1], best[:, ::-1], 0.0, ALU.mult, ALU.max))
        s.link(v.tensor_scalar(best[:], best[:], 1e-16, None, ALU.add))
        s.link(v.reciprocal(best[:], best[:]))
        v.tensor_tensor(scores[:], expo[:], best[:], ALU.mult).then_inc(att_ready, 1)

        with v.Fori(0, EG) as g:
            for cc in range(KC):
                v.wait_ge(spread, 4 * g + cc + 1)
                cols = value[:, cc, ds(g * GR + 1, GR)]
                v.tensor_tensor(cols, cols, pa[cc][:], ALU.mult).then_inc(weighted, 1)
                v.wait_ge(weighted, 4 * g + cc + 1 + KC)
                v.tensor_tensor_scan(cols, same[:, ds(g * GR, GR)], cols, value[:, cc, ds(g * GR, 1)],
                                     ALU.mult, ALU.add).then_inc(summed, 1)
            for cc in range(KC):
                v.wait_ge(hi_made, 4 * g + cc + 1)
                v.tensor_tensor(al[:, cc, :], value[:, cc, ds(g * GR + 1, GR)], ah[:, cc, :].bitcast(F32),
                                ALU.subtract).then_inc(lo_made, 1)
            for t in range(T):
                v.wait_ge(row_done, 4 * g + t + 1)
                v.wait_ge(stored[t % 2], 32 * g + 16 * (t // 2) + 16)
                v.tensor_tensor(out[:, t % 2, :], po[t % 2][:], k.b12[:], ALU.add).then_inc(row_out, 1)

    @block.scalar
    def _(act_):
        act_.wait_ge(chain, 4)
        act_.activation(expo[:], scores[:], ACT.Exp).then_inc(exp_done, 1)
        with act_.Fori(0, EG) as g:
            for cc in range(KC):
                act_.wait_ge(summed, 4 * g + cc + 1)
                if cc == 0:
                    act_.wait_ge(row_out, 4 * g + 2)
                act_.activation(ah[:, cc, :], value[:, cc, ds(g * GR + 1, GR)], ACT.Copy).then_inc(hi_made, 1)

    @block.tensor
    def _(pe):
        pe.wait_ge(att_ready, 1)

        def spread_weights(g):
            for cc in range(KC):
                pe.wait_ge(weighted, 4 * g + cc + 1)
                hold(pe)
                pe.matmul(pa[cc][:], headsel2[:, cc * P:cc * P + P], scores[:, ds(g * GR, GR)], start=True,
                          stop=True).then_inc(spread, 1)

        with pe.Fori(0, EG) as g:
            spread_weights(g)
            for t in range(T):
                pe.wait_ge(row_out, 4 * g + t + 1)
                for cc in range(KC):
                    if t == 0:
                        pe.wait_ge(lo_made, 4 * g + cc + 1)
                    sl = slice(t * P, t * P + P)
                    last = split3(pe, po[t % 2][:], (ah[:, cc, sl], al[:, cc, sl]),
                                  (hi["w12"][:, cc, :], lo["w12"][:, cc, :]), cc == 0, cc == KC - 1)
                last.then_inc(row_done, 1)

    @block.sync
    def _(sp):
        for n in range(2):
            sp.sem_inc(stored[n], 16)
        sp.sem_inc(row_out, 2)
        with sp.Fori(0, EG) as g:
            for t in range(T):
                sp.wait_ge(row_out, 4 * g + t + 3)
                sp.dma_start(k.values[ds(g * GR + t * P, P), :], out[:, t % 2, :]).then_inc(stored[t % 2], 16)
        for n in range(2):
            sp.wait_ge(stored[n], 16 + 16 * ET // 2)



def split_weights(nc, k, jobs):
    with ExitStack() as stack:
        c = Core(nc, stack, f"split{nc.next_id()}")
        stage = [c.sb(f"stage{n}", [P, KC * D]) for n in range(2)]
        loaded = [c.sem(f"loaded{n}") for n in range(2)]
        hi_made, lo_made = c.sem("hi_made"), c.sem("lo_made")
        block = stack.enter_context(nc.Block())

        def view(n, like):
            return stage[n % 2][:, 0:like.shape[1] * like.shape[2]].rearrange("p (c n) -> p c n", c=like.shape[1])

        @block.sync
        def _(sp):
            for n, (source, hi, _) in enumerate(jobs):
                if n >= 2:
                    sp.wait_ge(lo_made, n - 1)
                sp.dma_start(view(n, hi), source).then_inc(loaded[n % 2], 16)

        @block.scalar
        def _(act_):
            for n, (_, hi, _) in enumerate(jobs):
                act_.wait_ge(loaded[n % 2], 16 * (n // 2 + 1))
                act_.activation(hi[:], view(n, hi), ACT.Copy).then_inc(hi_made, 1)

        @block.vector
        def _(v):
            for n, (_, hi, lo) in enumerate(jobs):
                v.wait_ge(hi_made, n + 1)
                v.tensor_tensor(lo[:], view(n, hi), hi[:].bitcast(F32), ALU.subtract).then_inc(lo_made, 1)
            v.wait_ge(lo_made, len(jobs))


def chunks(source):
    return source.rearrange("(c p) n -> p c n", p=P)



def dense0_phase(nc, a, k):
    with ExitStack() as stack:
        c = Core(nc, stack, "d0")
        w = {n: [c.sb(f"{n}_{h}", [P, KC, D], F32R) for h in ("hi", "lo")] for n in ("w1", "w3", "w2")}
        wr = [c.sb(f"wr_{h}", [P, KC, SETS * 4], F32R) for h in ("hi", "lo")]
        split_weights(nc, k, [(chunks(a["e_w1"]), *w["w1"]), (chunks(a["e_w3"]), *w["w3"]),
                              (chunks(a["e_w2"]), *w["w2"]), (chunks(a["e_wr"]), *wr)])
        x = [c.sb(f"x{n}", [P, T, D]) for n in range(2)]
        val = c.sb("val", [P, T, D])
        at = c.sb("at", [P, T], I32)
        xf = c.sb("xf", [P, 2, D])
        xh, xl = (c.sb(n, [P, KC, GR], F32R) for n in ("xh", "xl"))
        act_out = c.sb("act_out", [P, 2, GR])
        hh, hl = (c.sb(n, [P, KC, GR], F32R) for n in ("hh", "hl"))
        y = c.sb("y", [P, 2, D])
        st = [c.sb(f"st{n}", [P, T, 6]) for n in range(3)]
        mv = [c.sb(f"mv{n}", [P, T, 2]) for n in range(3)]
        ve = [c.sb(f"ve{n}", [P, T]) for n in range(3)]
        rs = [c.sb(f"rs{n}", [P, T]) for n in range(3)]
        shift = [c.sb(f"shift{n}", [P, T]) for n in range(3)]
        gain = c.sb("gain", [P, T])
        rbias = c.sb("rbias", [P, SETS * 4])
        before = c.sb("before", [P, 4, 4])
        expert = c.sb("expert", [2 * EXPERTS0, D])
        expert2 = c.sb("expert2", [2 * EXPERTS0, D])
        expert_r = c.sb("expert_r", [2 * EXPERTS0, D], F32R)
        NS = T * SETS
        prob, one_hot, second, rank = (c.sb(n, [P, NS, 4]) for n in ("prob", "one_hot", "second", "rank"))
        total = c.sb("total", [P, NS])
        wins, ties = (c.sb(n, [P, NS, 4, 4]) for n in ("wins", "ties"))
        mix = c.sb("mix", [P, T, EXPERTS0])
        parts = c.sb("parts", [P, T, P], F32R)
        mix_t = c.sb("mix_t", [2 * EXPERTS0, GR], F32R)
        pa, pc, po = ([c.ps(f"{n}{i}") for i in range(2)] for n in ("pa", "pc", "po"))
        ptr, pmix = c.ps("ptr"), c.ps("pmix")
        bank = [ptr, pa[0], pc[0], ptr]

        consts, routed_in = c.sem("consts"), c.sem("routed_in")
        x_in = [c.sem(f"x_in{n}") for n in range(2)]
        val_in = [c.sem(f"val_in{n}") for n in range(T)]
        y_out = [c.sem(f"y_out{n}") for n in range(2)]
        at_made, val_made = c.sem("at_made"), c.sem("val_made")
        stats = [c.sem(f"stats{n}") for n in range(3)]
        shift_made = [c.sem(f"shift_made{n}") for n in range(2)]
        dev_made = c.sem("dev_made")
        pow_done = [c.sem(f"pow_done{n}") for n in range(3)]
        x0_normed, x1_made, x1_normed, x2_made, y_made = (c.sem(n) for n in ("x0_normed", "x1_made", "x1_normed", "x2_made", "y_made"))
        turned, xh_made, xl_made = (c.sem(n) for n in ("turned", "xh_made", "xl_made"))
        up_done, gate_done, mixed, tanh_done = (c.sem(n) for n in ("up_done", "gate_done", "mixed", "tanh_done"))
        gated, hidden, hh_made, hl_made = (c.sem(n) for n in ("gated", "hidden", "hh_made", "hl_made"))
        down_done, logits_done = c.sem("down_done"), c.sem("logits_done")
        route, exp_done, mix_turned, mix_out = (c.sem(n) for n in ("route", "exp_done", "mix_turned", "mix_out"))
        block = stack.enter_context(nc.Block())
        NSTAT, NROUTE = 4, 25

        @block.sync
        def _(sp):
            sp.sem_inc(y_out[0], 16)
            sp.sem_inc(y_out[1], 16)
            sp.dma_start(rbias[:], a["e_br"].broadcast_to([P, SETS * 4])).then_inc(routed_in, 16)

            def load(g, u):
                sp.wait_ge(y_made, 4 * g + 4)
                sp.dma_start(x[u][:], a["x"][ds(g * GR, GR), :].rearrange("(t p) n -> p t n", p=P))\
                  .then_inc(x_in[u], 16)

            def store(g):
                for t in range(T):
                    sp.wait_ge(y_made, 4 * g + t + 9)
                    sp.dma_start(k.y[ds(g * GR + t * P, P), :], y[:, t % 2, :]).then_inc(y_out[t % 2], 16)

            load(0, 0)
            load(1, 1)
            with sp.Fori(0, NG // 2 - 1) as i:
                store(i * 2)
                load(i * 2 + 2, 0)
                store(i * 2 + 1)
                load(i * 2 + 3, 1)
            store(NG - 2)
            store(NG - 1)
            for n in range(2):
                sp.wait_ge(y_out[n], 16 + 16 * NT // 2)

        @block.gpsimd
        def _(pool):
            s = Steps(pool, consts)
            s(pool.memset(before[:], 1.0))
            s(pool.memset(expert[:], 0.25))
            s(pool.memset(expert2[:], 0.25))
            s.settle()
            s(pool.affine_select(out=before[:], in_=before[:], compare_op=ALU.is_gt, fill=0.0, base=0,
                                 pattern=[[1, 4], [-1, 4]], channel_multiplier=0))
            for m, off in ((expert, 0), (expert2, EXPERTS0 * HID1)):
                s.link(pool.affine_select(out=m[:], in_=m[:], compare_op=ALU.is_ge, fill=0.0, base=off,
                                          pattern=[[1, D]], channel_multiplier=-HID1))
                s.link(pool.affine_select(out=m[:], in_=m[:], compare_op=ALU.is_ge, fill=0.0,
                                          base=HID1 - 1 - off, pattern=[[-1, D]], channel_multiplier=HID1))

            def power(g, n):
                pool.wait_ge(stats[n], NSTAT * g + 4 if n < 2 else 5 * g + 4)
                pool.tensor_tensor(rs[n][:], ve[n][:], k.half_neg[:, 0:T], ALU.pow).then_inc(pow_done[n], 1)

            def gather(g, t):
                if t == 0:
                    pool.wait_ge(x1_made, 4 * g + 4)
                    hold(pool)
                    pool.tensor_copy(at[:], k.slot["s"][:, ds(T * g, T)]).then_inc(at_made, 1)
                pool.tensor_tensor(val[:, t, :], k.b12[:], k.zeros[:], ALU.add).then_inc(val_made, 1)
                pool.wait_ge(val_made, 4 * g + t + 1)
                pool.wait_ge(at_made, g + 1)
                hold(pool)
                pool.indirect_dma_start(val[:, t, :], None, k.values[:, :],
                                        bass.IndirectOffsetOnAxis(ap=at[:, t:t + 1], axis=0),
                                        bounds_check=EP - 1, oob_is_err=False).then_inc(val_in[t], 16)

            def low(g, cc):
                if cc == 0:
                    pool.wait_ge(down_done, 4 * g + 4)
                pool.wait_ge(hh_made, 4 * g + cc + 1)
                pool.tensor_tensor(hl[:, cc, :], act_out[:, cc % 2, :], hh[:, cc, :].bitcast(F32), ALU.subtract)\
                    .then_inc(hl_made, 1)

            def body(g, last):
                if not last:
                    power(g + 1, 0)
                    gather(g + 1, 0)
                low(g, 0)
                if not last:
                    gather(g + 1, 1)
                    gather(g + 1, 2)
                low(g, 1)
                if not last:
                    gather(g + 1, 3)
                    power(g + 1, 1)
                low(g, 2)
                low(g, 3)
                power(g, 2)

            pool.sem_inc(hl_made, 2)
            power(0, 0)
            for t in range(T):
                gather(0, t)
            power(0, 1)
            with pool.Fori(0, NG // 2 - 1) as i:
                body(i * 2, False)
                body(i * 2 + 1, False)
            body(NG - 2, False)
            body(NG - 1, True)

        def statistics(v, g, u, n):
            s = Steps(v, stats[n], (NSTAT if n < 2 else 5) * g)
            for t in range(T):
                ins = v.bn_stats(st[n][:, t, :], x[u][:, t, :])
            s.link(ins)
            hold(v)
            for t in range(T):
                ins = v.bn_aggr(mv[n][:, t, :], st[n][:, t, :])
            s.link(ins)
            s(v.tensor_scalar(shift[n][:], mv[n][:, :, 0], -1.0, None, ALU.mult))
            s(v.tensor_scalar(ve[n][:], mv[n][:, :, 1], 1e-5, None, ALU.add))
            return s

        @block.vector
        def _(v):
            v.sem_inc(x1_made, 4)
            v.sem_inc(hidden, 2)
            v.sem_inc(x2_made, 2)
            v.wait_ge(consts, 8)
            v.tensor_tensor(expert_r[:], expert[:], expert2[:], ALU.add).then_inc(consts, 1)
            v.memset(parts[:, :, 2 * EXPERTS0:P].bitcast(F32), 0.0).then_inc(consts, 1)
            v.wait_ge(routed_in, 16)

            def front0_end(g):
                v.wait_ge(pow_done[0], g + 1)
                v.tensor_scalar(gain[:], rs[0][:], 1.0, None, ALU.add).then_inc(shift_made[0], 1)
                v.tensor_tensor(shift[0][:], shift[0][:], rs[0][:], ALU.mult).then_inc(shift_made[0], 1)

            def front1(g, u):
                for t in range(T):
                    v.wait_ge(x0_normed, 4 * g + t + 1)
                    v.wait_ge(val_in[t], 16 * g + 16)
                    v.tensor_tensor(x[u][:, t, :], x[u][:, t, :], val[:, t, :], ALU.add).then_inc(x1_made, 1)
                v.wait_ge(x1_made, 4 * g + 4 + 4)
                hold(v)
                statistics(v, g, u, 1)

            def front1_end(g):
                v.wait_ge(pow_done[1], g + 1)
                v.tensor_tensor(shift[1][:], shift[1][:], rs[1][:], ALU.mult).then_inc(shift_made[1], 1)

            def low(g, t):
                v.wait_ge(xh_made, 4 * g + t + 1)
                v.tensor_tensor(xl[:, :, t * P:t * P + P], bank[t][:].rearrange("p (c n) -> p c n", n=P),
                                xh[:, :, t * P:t * P + P].bitcast(F32), ALU.subtract).then_inc(xl_made, 1)

            def chunk(g, cc):
                h = act_out[:, cc % 2, :]
                v.wait_ge(tanh_done, 4 * g + cc + 1)
                v.scalar_tensor_tensor(h, h, 1.0, pa[cc % 2][:], ALU.add, ALU.mult).then_inc(gated, 1)
                v.wait_ge(gated, 8 * g + 2 * cc + 1)
                v.wait_ge(gate_done, 4 * g + cc + 1)
                v.tensor_tensor(h, h, pc[cc % 2][:], ALU.mult).then_inc(gated, 1)
                v.wait_ge(gated, 8 * g + 2 * cc + 2)
                v.wait_ge(mixed, 4 * g + cc + 1)
                v.tensor_tensor(h, h, pmix[:], ALU.mult).then_inc(hidden, 1)

            def back(g, u, t):
                v.wait_ge(down_done, 4 * g + t + 1 + 4)
                v.tensor_tensor(x[u][:, t, :], x[u][:, t, :], po[t % 2][:], ALU.add).then_inc(x2_made, 1)

            def back_stats(g, u):
                v.wait_ge(x2_made, 4 * g + 4 + 2)
                hold(v)
                s = statistics(v, g, u, 2)
                v.tensor_copy(k.mean[:, ds(T * g, T)], mv[2][:, :, 0])
                v.wait_ge(pow_done[2], g + 1)
                s(v.tensor_tensor(shift[2][:], shift[2][:], rs[2][:], ALU.mult))
                v.tensor_tensor(k.dev[:, ds(T * g, T)], ve[2][:], rs[2][:], ALU.mult).then_inc(dev_made, 1)

            def routing(g):
                s = Steps(v, route, NROUTE * g)
                v.wait_ge(logits_done, g + 1)
                s.link(v.tensor_tensor(prob[:].rearrange("p (t s) e -> p t (s e)", t=T),
                                       pmix[:, 0:T * SETS * 4].rearrange("p (t n) -> p t n", t=T),
                                       rbias[:].unsqueeze(1).broadcast_to([P, T, SETS * 4]), ALU.add))
                s.link(v.tensor_reduce(total[:], prob[:], X_AXIS, ALU.max))
                s(v.tensor_tensor(prob[:], prob[:], total[:].unsqueeze(2).broadcast_to([P, NS, 4]), ALU.subtract))
                v.wait_ge(exp_done, g + 1)
                s.link(v.tensor_reduce(total[:], prob[:], X_AXIS, ALU.add))
                s.link(v.reciprocal(total[:], total[:]))
                s.link(v.tensor_tensor(prob[:], prob[:], total[:].unsqueeze(2).broadcast_to([P, NS, 4]), ALU.mult))
                other = prob[:].unsqueeze(2).broadcast_to([P, NS, 4, 4])
                own = prob[:].unsqueeze(3).broadcast_to([P, NS, 4, 4])
                s(v.tensor_tensor(wins[:], other, own, ALU.is_gt))
                s.link(v.tensor_tensor(ties[:], other, own, ALU.is_equal))
                s.link(v.tensor_tensor(ties[:], ties[:], before[:].unsqueeze(1).broadcast_to([P, NS, 4, 4]), ALU.mult))
                s.link(v.tensor_tensor(wins[:], wins[:], ties[:], ALU.add))
                s.link(v.tensor_reduce(rank[:], wins[:], X_AXIS, ALU.add))
                s(v.scalar_tensor_tensor(one_hot[:], rank[:], 0.0, prob[:], ALU.is_equal, ALU.mult))
                s.link(v.scalar_tensor_tensor(second[:], rank[:], 1.0, prob[:], ALU.is_equal, ALU.mult))
                s.link(v.tensor_tensor(prob[:], one_hot[:], second[:], ALU.add))
                s.link(v.tensor_reduce(total[:], prob[:], X_AXIS, ALU.add))
                s.link(v.tensor_scalar(total[:], total[:], 0.9, None, ALU.is_le))
                s.link(v.tensor_tensor(second[:], second[:], total[:].unsqueeze(2).broadcast_to([P, NS, 4]), ALU.mult))
                s.link(v.tensor_tensor(prob[:], one_hot[:], second[:], ALU.add))
                s.link(v.tensor_reduce(total[:], prob[:], X_AXIS, ALU.add))
                s.link(v.tensor_scalar(total[:], total[:], 1e-9, None, ALU.add))
                s.link(v.reciprocal(total[:], total[:]))
                s.link(v.tensor_tensor(prob[:], prob[:], total[:].unsqueeze(2).broadcast_to([P, NS, 4]), ALU.mult))
                sets = prob[:].rearrange("p (t s) e -> p t s e", t=T)
                for t in range(T):
                    ins = v.tensor_tensor(mix[:, t, :].rearrange("p (s e) -> p s e", e=4), sets[:, t, 1:SETS, :],
                                          sets[:, t, 0, :].unsqueeze(2).broadcast_to([P, 4, 4]), ALU.mult)
                s.link(ins)
                v.wait_ge(mix_turned, g + 1)
                s.link(v.tensor_copy(parts[:, :, 0:EXPERTS0], mix[:]))
                s(v.tensor_tensor(parts[:, :, EXPERTS0:2 * EXPERTS0], mix[:], parts[:, :, 0:EXPERTS0].bitcast(F32),
                                  ALU.subtract))
                assert s.n == NROUTE

            def body(g, u, last, xc):
                n = 1 - u
                if not last:
                    v.wait_ge(x_in[n], xc)
                    hold(v)
                    statistics(v, g + 1, n, 0)
                chunk(g, 0)
                if not last:
                    front0_end(g + 1)
                chunk(g, 1)
                if not last:
                    front1(g + 1, n)
                chunk(g, 2)
                if not last:
                    front1_end(g + 1)
                chunk(g, 3)
                if not last:
                    for t in range(T):
                        low(g + 1, t)
                back(g, u, 0)
                back(g, u, 1)
                if not last:
                    routing(g + 1)
                back(g, u, 2)
                back(g, u, 3)
                back_stats(g, u)

            v.wait_ge(x_in[0], 16)
            statistics(v, 0, 0, 0)
            front0_end(0)
            front1(0, 0)
            front1_end(0)
            for t in range(T):
                low(0, t)
            routing(0)
            with v.Fori(0, NG // 2 - 1) as i:
                body(i * 2, 0, False, i * 16 + 16)
                body(i * 2 + 1, 1, False, i * 16 + 32)
            body(NG - 2, 0, False, 16 * (NG // 2))
            body(NG - 1, 1, True, 0)
            v.wait_ge(dev_made, NG)

        @block.scalar
        def _(act_):
            act_.sem_inc(y_made, 8)

            def norm0(g, u):
                act_.wait_ge(shift_made[0], 2 * g + 2)
                for t in range(T):
                    act_.activation(x[u][:, t, :], x[u][:, t, :], ACT.Identity, bias=shift[0][:, t:t + 1],
                                    scale=gain[:, t:t + 1]).then_inc(x0_normed, 1)

            def norm1(g, u, t):
                act_.wait_ge(shift_made[1], g + 1)
                act_.wait_ge(turned, 4 * g + t + 1)
                act_.activation(xf[:, t % 2, :], x[u][:, t, :], ACT.Identity, bias=shift[1][:, t:t + 1],
                                scale=rs[1][:, t:t + 1]).then_inc(x1_normed, 1)

            def high(g, t):
                act_.wait_ge(turned, 4 * g + t + 1 + 2)
                act_.activation(xh[:, :, t * P:t * P + P], bank[t][:].rearrange("p (c n) -> p c n", n=P), ACT.Copy)\
                    .then_inc(xh_made, 1)

            def tanh(g, cc):
                act_.wait_ge(up_done, 4 * g + cc + 1)
                act_.wait_ge(hl_made, 4 * g + cc + 1)
                act_.activation(act_out[:, cc % 2, :], pa[cc % 2][:], ACT.Tanh, scale=0.5).then_inc(tanh_done, 1)

            def split(g, cc):
                act_.wait_ge(hidden, 4 * g + cc + 1 + 2)
                if cc == 0:
                    act_.wait_ge(down_done, 4 * g + 4)
                act_.activation(hh[:, cc, :], act_out[:, cc % 2, :], ACT.Copy).then_inc(hh_made, 1)

            def softmax_exp(g):
                act_.wait_ge(route, NROUTE * g + 3)
                act_.activation(prob[:], prob[:], ACT.Exp).then_inc(exp_done, 1)

            def mix_copy(g):
                act_.wait_ge(mix_turned, g + 2)
                act_.activation(mix_t[:], ptr[0:2 * EXPERTS0, :], ACT.Copy).then_inc(mix_out, 1)

            def finish(g, u):
                act_.wait_ge(stats[2], 5 * g + 5)
                for t in range(T):
                    act_.wait_ge(y_out[t % 2], 32 * g + 16 * (t // 2) + 16)
                    act_.activation(y[:, t % 2, :], x[u][:, t, :], ACT.Identity, bias=shift[2][:, t:t + 1],
                                    scale=rs[2][:, t:t + 1]).then_inc(y_made, 1)

            def body(g, u, last):
                n = 1 - u
                tanh(g, 0)
                if not last:
                    norm0(g + 1, n)
                split(g, 0)
                tanh(g, 1)
                split(g, 1)
                tanh(g, 2)
                split(g, 2)
                if not last:
                    norm1(g + 1, n, 0)
                    norm1(g + 1, n, 1)
                tanh(g, 3)
                split(g, 3)
                if not last:
                    high(g + 1, 0)
                    norm1(g + 1, n, 2)
                    high(g + 1, 1)
                    norm1(g + 1, n, 3)
                    high(g + 1, 2)
                    high(g + 1, 3)
                    softmax_exp(g + 1)
                finish(g, u)
                if not last:
                    mix_copy(g + 1)

            norm0(0, 0)
            norm1(0, 0, 0)
            norm1(0, 0, 1)
            high(0, 0)
            norm1(0, 0, 2)
            high(0, 1)
            norm1(0, 0, 3)
            high(0, 2)
            high(0, 3)
            softmax_exp(0)
            mix_copy(0)
            with act_.Fori(0, NG // 2 - 1) as i:
                body(i * 2, 0, False)
                body(i * 2 + 1, 1, False)
            body(NG - 2, 0, False)
            body(NG - 1, 1, True)

        @block.tensor
        def _(pe):
            pe.sem_inc(turned, 2)
            pe.sem_inc(down_done, 4)
            pe.sem_inc(mix_turned, 1)
            pe.wait_ge(consts, 10)

            def turn(g):
                for t in range(T):
                    pe.wait_ge(x1_normed, 4 * g + t + 1)
                    if t == 3:
                        pe.wait_ge(xl_made, 4 * g + 1)
                    for kc in range(KC):
                        last = pe.transpose(bank[t][:, kc * P:kc * P + P], xf[:, t % 2, kc * P:kc * P + P], k.ident[:])
                    last.then_inc(turned, 1)

            def logits(g):
                pe.wait_ge(xl_made, 4 * g + 4)
                pe.wait_ge(hidden, 4 * g + 2)
                for t in range(T):
                    for kc in range(KC):
                        sl = slice(t * P, t * P + P)
                        last = split3(pe, pmix[:, t * SETS * 4:(t + 1) * SETS * 4], (xh[:, kc, sl], xl[:, kc, sl]),
                                      (wr[0][:, kc, :], wr[1][:, kc, :]), kc == 0, kc == KC - 1)
                last.then_inc(logits_done, 1)

            def up(g, cc):
                pe.wait_ge(hidden, 4 * g + cc + 1)
                for name, out, done in (("w1", pa, up_done), ("w3", pc, gate_done)):
                    for kc in range(KC):
                        sl = slice(cc * P, cc * P + P)
                        last = split3(pe, out[cc % 2][:], (w[name][0][:, kc, sl], w[name][1][:, kc, sl]),
                                      (xh[:, kc, :], xl[:, kc, :]), kc == 0, kc == KC - 1)
                    last.then_inc(done, 1)

            def spread(g, cc):
                pe.wait_ge(hidden, 4 * g + cc + 2)
                pe.matmul(pmix[:], expert_r[:, cc * P:cc * P + P], mix_t[:], start=True, stop=True).then_inc(mixed, 1)

            def turn_mix(g):
                pe.wait_ge(route, NROUTE * g + NROUTE)
                for t in range(T):
                    last = pe.transpose(ptr[:, t * P:t * P + P], parts[:, t, :].bitcast(F32), k.ident[:])
                last.then_inc(mix_turned, 1)

            def down(g, t, ccs):
                sl = slice(t * P, t * P + P)
                for cc in ccs:
                    if cc == 0:
                        pe.wait_ge(x2_made, 4 * g + t + 1)
                    pe.wait_ge(hl_made, 4 * g + cc + 1 + 2)
                    last = split3(pe, po[t % 2][:], (hh[:, cc, sl], hl[:, cc, sl]),
                                  (w["w2"][0][:, cc, :], w["w2"][1][:, cc, :]), cc == 0, cc == KC - 1)
                    if cc == KC - 1:
                        last.then_inc(down_done, 1)

            def body(g, last):
                for cc in range(KC):
                    up(g, cc)
                    if cc == 0:
                        turn_mix(g)
                        pe.wait_ge(mix_out, g + 1)
                    spread(g, cc)
                if not last:
                    turn(g + 1)
                down(g, 0, (0, 1, 2))
                down(g, 1, (0, 1, 2))
                down(g, 0, (3,))
                down(g, 1, (3,))
                if not last:
                    logits(g + 1)
                down(g, 2, range(KC))
                down(g, 3, range(KC))

            turn(0)
            logits(0)
            with pe.Fori(0, NG // 2 - 1) as i:
                body(i * 2, False)
                body(i * 2 + 1, False)
            body(NG - 2, False)
            body(NG - 1, True)



def messages(nc, k, tag, source, weight, table):
    with ExitStack() as stack:
        c = Core(nc, stack, tag)
        at = c.sb("at", [P, T], I32)
        weights = c.sb("weights", [P, T])
        rows = c.sb("rows", [P, T, D])
        sums = c.sb("sums", [P, T, D])
        sh, sl = (c.sb(n, [P, 2, D], F32R) for n in ("sh", "sl"))
        out = c.sb("out", [P, 2, D])
        ptr = [c.ps(f"ptr{n}") for n in range(2)]
        po = [c.ps(f"po{n}") for n in range(2)]
        at_made = c.sem("at_made")
        rows_in = [c.sem(f"rows_in{t}") for t in range(T)]
        scaled, turned, summed, hi_made, lo_made, done, row_out = (
            c.sem(n) for n in ("scaled", "turned", "summed", "hi_made", "lo_made", "done", "row_out"))
        stored = [c.sem(f"stored{n}") for n in range(2)]
        block = stack.enter_context(nc.Block())
        same = k.same["d"]

        @block.gpsimd
        def _(pool):
            with pool.Fori(0, EG) as g:
                pool.wait_ge(turned, 4 * g + 4)
                hold(pool)
                pool.tensor_copy(at[:], k.rec["d"][:, ds(T * g, T), 0]).then_inc(at_made, 1)
                pool.tensor_copy(weights[:], k.rec["d"][:, ds(T * g, T), 2].bitcast(F32)).then_inc(at_made, 1)
                pool.wait_ge(at_made, 2 * g + 2)
                hold(pool)
                for t in range(T):
                    pool.indirect_dma_start(rows[:, t, :], None, source[:, :],
                                            bass.IndirectOffsetOnAxis(ap=at[:, t:t + 1], axis=0),
                                            bounds_check=NPAD - 1, oob_is_err=False).then_inc(rows_in[t], 16)

        def copy_row(act_, g, t):
            act_.wait_ge(done, 4 * g + t + 1 + 2)
            act_.wait_ge(stored[t % 2], 32 * g + 16 * (t // 2) + 16)
            act_.activation(out[:, t % 2, :], po[t % 2][:], ACT.Copy).then_inc(row_out, 1)

        @block.scalar
        def _(act_):
            act_.sem_inc(row_out, 2)

            def scale(g, t):
                act_.wait_ge(rows_in[t], 16 * g + 16)
                act_.wait_ge(at_made, 2 * g + 2)
                act_.activation(rows[:, t, :], rows[:, t, :], ACT.Copy, scale=weights[:, t:t + 1]).then_inc(scaled, 1)

            with act_.Fori(0, EG) as g:
                for t in range(T):
                    scale(g, t)
                for t in range(T):
                    act_.wait_ge(summed, 4 * g + t + 1 + 4)
                    act_.wait_ge(done, 4 * g + t + 1)
                    act_.activation(sh[:, t % 2, :], sums[:, t, :], ACT.Copy).then_inc(hi_made, 1)
                    if t:
                        copy_row(act_, g, t - 1)
                copy_row(act_, g, T - 1)

        @block.vector
        def _(v):
            v.sem_inc(lo_made, 4)
            v.memset(sums[:], 0.0).then_inc(summed, 4)
            with v.Fori(0, EG) as g:
                for t in range(T):
                    v.wait_ge(turned, 4 * g + t + 1 + 4)
                    v.wait_ge(summed, 4 * g + t + 4)
                    v.wait_ge(lo_made, 4 * g + t + 1)
                    hold(v)
                    for kc in range(KC):
                        own = slice(kc * P, kc * P + P)
                        last = v.tensor_tensor_scan(sums[:, t, own], same[:, ds(g * GR + t * P, P)], ptr[t % 2][:, own],
                                                    sums[:, (t - 1) % T, kc * P + P - 1:kc * P + P], ALU.mult, ALU.add)
                    last.then_inc(summed, 1)
                    v.wait_ge(hi_made, 4 * g + t + 1)
                    v.tensor_tensor(sl[:, t % 2, :], sums[:, t, :], sh[:, t % 2, :].bitcast(F32), ALU.subtract)\
                     .then_inc(lo_made, 1)

        @block.tensor
        def _(pe):
            pe.sem_inc(turned, 4)
            pe.sem_inc(done, 2)

            def turn(g, t):
                pe.wait_ge(scaled, 4 * g + t + 1)
                pe.wait_ge(summed, 4 * g + t - 1 + 4)
                for kc in range(KC):
                    own = slice(kc * P, kc * P + P)
                    last = pe.transpose(ptr[t % 2][:, own], rows[:, t, own], k.ident[:])
                last.then_inc(turned, 1)

            def product(g, t):
                pe.wait_ge(lo_made, 4 * g + t + 1 + 4)
                pe.wait_ge(row_out, 4 * g + t + 1)
                for kc in range(KC):
                    own = slice(kc * P, kc * P + P)
                    last = split3(pe, po[t % 2][:], (sh[:, t % 2, own], sl[:, t % 2, own]),
                                  (weight[0][:, kc, :], weight[1][:, kc, :]), kc == 0, kc == KC - 1)
                last.then_inc(done, 1)

            with pe.Fori(0, EG) as g:
                turn(g, 0)
                turn(g, 1)
                product(g, 0)
                turn(g, 2)
                product(g, 1)
                turn(g, 3)
                product(g, 2)
                product(g, 3)

        @block.sync
        def _(sp):
            sp.sem_inc(stored[0], 16)
            sp.sem_inc(stored[1], 16)
            with sp.Fori(0, EG) as g:
                for t in range(T):
                    sp.wait_ge(row_out, 4 * g + t + 3)
                    sp.dma_start(table[ds(g * GR + t * P, P), :], out[:, t % 2, :]).then_inc(stored[t % 2], 16)
            for n in range(2):
                sp.wait_ge(stored[n], 16 + 16 * ET // 2)



def conv_phase(nc, a, k):
    with ExitStack() as stack:
        c = Core(nc, stack, "conv")
        w = {n: [c.sb(f"{n}_{h}", [P, KC, D], F32R) for h in ("hi", "lo")] for n in ("w11", "w01", "w02")}
        split_weights(nc, k, [(chunks(a[f"g_{n}"]), *w[n]) for n in ("w11", "w01", "w02")])
        messages(nc, k, "msg1", k.y, w["w11"], k.message1)
        yin = c.sb("yin", [P, T, D])
        msg = c.sb("msg", [P, T, D])
        at = c.sb("at", [P, T], I32)
        diag = c.sb("diag", [P, NT])
        dg, dg2 = c.sb("dg", [P, T]), c.sb("dg2", [P, T])
        bias = [c.sb(f"bias{n}", [P, D]) for n in range(2)]
        yh, yl, hh, hl = (c.sb(n, [P, 2, D], F32R) for n in ("yh", "yl", "hh", "hl"))
        h = c.sb("h", [P, T, D])
        own = c.sb("own", [P, 2, D])
        pty, pth, p1, p2 = ([c.ps(f"{n}{i}") for i in range(2)] for n in ("pty", "pth", "p1", "p2"))
        consts = c.sem("consts")
        y_in, msg_in, h_out = ([c.sem(f"{n}{t}") for t in range(T)] for n in ("y_in", "msg_in", "h_out"))
        own_out = [c.sem(f"own_out{n}") for n in range(2)]
        added = c.sem("added")
        at_made, msg_made, dg_made = c.sem("at_made"), c.sem("msg_made"), c.sem("dg_made")
        y_turned, yh_made, yl_made, one_done, summed, h_made = (
            c.sem(n) for n in ("y_turned", "yh_made", "yl_made", "one_done", "summed", "h_made"))
        h_turned, hh_made, hl_made, two_done, own_made = (
            c.sem(n) for n in ("h_turned", "hh_made", "hl_made", "two_done", "own_made"))
        block = stack.enter_context(nc.Block())

        @block.sync
        def _(sp):
            for t in range(T):
                sp.sem_inc(h_out[t], 16)
            for n in range(2):
                sp.sem_inc(own_out[n], 16)
            sp.dma_start(diag[:], a["diag"]).then_inc(consts, 16)
            for n in range(2):
                sp.dma_start(bias[n][:], a[f"g_b{n + 1}"].broadcast_to([P, D])).then_inc(consts, 16)

            def load(g, t):
                sp.wait_ge(y_turned, 4 * g + t + 1)
                sp.dma_start(yin[:, t, :], k.y[ds(g * GR + t * P, P), :]).then_inc(y_in[t], 16)

            def store_h(g, t):
                sp.wait_ge(h_made, 4 * g + t + 1)
                sp.dma_start(k.h[ds(g * GR + t * P, P), :], h[:, t, :]).then_inc(h_out[t], 16)

            def store_own(g, t):
                sp.wait_ge(own_made, 4 * g + t + 1 + 2)
                sp.dma_start(k.own[ds(g * GR + t * P, P), :], own[:, t % 2, :]).then_inc(own_out[t % 2], 16)

            for t in range(T):
                load(0, t)
            with sp.Fori(0, NG - 1) as g:
                for t in range(T):
                    store_h(g, t)
                    load(g + 1, t)
                    if t:
                        store_own(g, t - 1)
                store_own(g, T - 1)
            for t in range(T):
                store_h(NG - 1, t)
            for t in range(T):
                store_own(NG - 1, t)
            for t in range(T):
                sp.wait_ge(h_out[t], 16 + 16 * NG)
            for n in range(2):
                sp.wait_ge(own_out[n], 16 + 32 * NG)

        @block.gpsimd
        def _(pool):
            with pool.Fori(0, NG) as g:
                pool.wait_ge(summed, 4 * g + 4)
                hold(pool)
                pool.tensor_copy(at[:], k.slot["d"][:, ds(T * g, T)]).then_inc(at_made, 1)
                pool.memset(msg[:], 0.0).then_inc(msg_made, 1)
                pool.wait_ge(msg_made, g + 1)
                pool.wait_ge(at_made, g + 1)
                hold(pool)
                for t in range(T):
                    pool.indirect_dma_start(msg[:, t, :], None, k.message1[:, :],
                                            bass.IndirectOffsetOnAxis(ap=at[:, t:t + 1], axis=0),
                                            bounds_check=EP - 1, oob_is_err=False).then_inc(msg_in[t], 16)

        def nxt(g, t):
            return (g, t + 1) if t < T - 1 else (g + 1, 0)

        def prv(g, t):
            return (g, t - 1) if t else (g - 1, T - 1)

        def low(v, g, t, bank, hi, lo, made, ready):
            v.wait_ge(ready, 4 * g + t + 1)
            v.tensor_tensor(lo[:, t % 2, :], bank[t % 2][:], hi[:, t % 2, :].bitcast(F32), ALU.subtract)\
             .then_inc(made, 1)

        @block.vector
        def _(v):
            v.sem_inc(summed, 4)
            v.sem_inc(own_made, 2)
            v.wait_ge(consts, 48)

            def step(g, t, first=False, last=False):
                if not last:
                    low(v, *nxt(g, t), pty, yh, yl, yl_made, yh_made)
                v.wait_ge(one_done, 4 * g + t + 1)
                v.wait_ge(msg_in[t], 16 * g + 16)
                v.wait_ge(h_out[t], 16 * g + 16)
                v.scalar_tensor_tensor(h[:, t, :], p1[t % 2][:], dg[:, t:t + 1], msg[:, t, :], ALU.mult, ALU.add)\
                 .then_inc(added, 1)
                v.wait_ge(added, 4 * g + t + 1)
                v.tensor_tensor(h[:, t, :], h[:, t, :], bias[0][:], ALU.add).then_inc(summed, 1)
                if not first:
                    behind(*prv(g, t))

            def behind(g, t):
                low(v, g, t, pth, hh, hl, hl_made, hh_made)
                v.wait_ge(two_done, 4 * g + t + 1)
                v.wait_ge(own_out[t % 2], 32 * g + 16 * (t // 2) + 16)
                v.scalar_tensor_tensor(own[:, t % 2, :], p2[t % 2][:], dg2[:, t:t + 1], bias[1][:], ALU.mult, ALU.add)\
                 .then_inc(own_made, 1)

            def group(g, first=False, last=False):
                for t in range(T):
                    if t == 0:
                        v.tensor_copy(dg[:], diag[:, ds(T * g, T)]).then_inc(dg_made, 1)
                        v.wait_ge(dg_made, 2 * g + 1)
                    step(g, t, first and t == 0, last and t == T - 1)
                    if t == 0:
                        v.wait_ge(own_made, 4 * g + 2)
                        hold(v)
                        v.tensor_copy(dg2[:], diag[:, ds(T * g, T)]).then_inc(dg_made, 1)
                        v.wait_ge(dg_made, 2 * g + 2)

            low(v, 0, 0, pty, yh, yl, yl_made, yh_made)
            group(0, first=True)
            with v.Fori(1, NG - 1) as g:
                group(g)
            group(NG - 1, last=True)
            behind(NG - 1, T - 1)
            v.wait_ge(own_made, NT + 2)

        @block.scalar
        def _(act_):
            def high(g, t, bank, hi, made, ready):
                act_.wait_ge(ready, 4 * g + t + 1)
                act_.activation(hi[:, t % 2, :], bank[t % 2][:], ACT.Copy).then_inc(made, 1)

            def step(g, t, first=False, last=False):
                if not last:
                    n = nxt(g, t)
                    act_.wait_ge(y_turned, 4 * n[0] + n[1] + 1 + 4)
                    act_.activation(yh[:, n[1] % 2, :], pty[n[1] % 2][:], ACT.Copy).then_inc(yh_made, 1)
                if not first:
                    high(*prv(g, t), pth, hh, hh_made, h_turned)
                act_.wait_ge(summed, 4 * g + t + 1 + 4)
                act_.activation(h[:, t, :], h[:, t, :], ACT.Relu).then_inc(h_made, 1)

            act_.wait_ge(y_turned, 5)
            act_.activation(yh[:, 0, :], pty[0][:], ACT.Copy).then_inc(yh_made, 1)
            for t in range(T):
                step(0, t, t == 0)
            with act_.Fori(1, NG - 1) as g:
                for t in range(T):
                    step(g, t)
            for t in range(T):
                step(NG - 1, t, False, t == T - 1)
            high(NG - 1, T - 1, pth, hh, hh_made, h_turned)

        @block.tensor
        def _(pe):
            pe.sem_inc(y_turned, 4)

            def turn(bank, src, t, done):
                for kc in range(KC):
                    own_ = slice(kc * P, kc * P + P)
                    last = pe.transpose(bank[t % 2][:, own_], src[:, t, own_], k.ident[:])
                last.then_inc(done, 1)

            def product(bank, hi, lo, name, t, done):
                for kc in range(KC):
                    own_ = slice(kc * P, kc * P + P)
                    last = split3(pe, bank[t % 2][:], (hi[:, t % 2, own_], lo[:, t % 2, own_]),
                                  (w[name][0][:, kc, :], w[name][1][:, kc, :]), kc == 0, kc == KC - 1)
                last.then_inc(done, 1)

            def turn_y(g, t, wait=True):
                pe.wait_ge(y_in[t], 16 * g + 16)
                if wait:
                    pe.wait_ge(yl_made, 4 * g + t - 1)
                turn(pty, yin, t, y_turned)

            def product_y(g, t, wait=True):
                pe.wait_ge(yl_made, 4 * g + t + 1)
                if wait:
                    pe.wait_ge(summed, 4 * g + t - 1 + 4)
                product(p1, yh, yl, "w01", t, one_done)

            def turn_h(g, t, wait=True):
                pe.wait_ge(h_made, 4 * g + t + 1)
                if wait:
                    pe.wait_ge(hl_made, 4 * g + t - 1)
                turn(pth, h, t, h_turned)

            def product_h(g, t, wait=True):
                pe.wait_ge(hl_made, 4 * g + t + 1)
                if wait:
                    pe.wait_ge(own_made, 4 * g + t - 1 + 2)
                product(p2, hh, hl, "w02", t, two_done)

            def step(g, t, start=False, last=False):
                n, b = nxt(g, t), prv(g, t)
                if not last:
                    turn_y(*n, not (start and t == 0))
                if not (start and t == 0):
                    turn_h(*b, not (start and t < 3))
                product_y(g, t, not (start and t < 2))
                if not (start and t == 0):
                    product_h(*b, not (start and t < 3))

            turn_y(0, 0, False)
            for t in range(T):
                step(0, t, True)
            with pe.Fori(1, NG - 1) as g:
                for t in range(T):
                    step(g, t)
            for t in range(T):
                step(NG - 1, t, False, t == T - 1)
            turn_h(NG - 1, T - 1)
            product_h(NG - 1, T - 1)



class Experts:
    pass


def expert_weights(nc, a, k, c, x):
    x.w1, x.w2t = ([c.sb(f"{n}_{h}", [P, KC, FC1 * P], F32R) for h in ("hi", "lo")] for n in ("w1", "w2t"))
    x.gram = [c.sb(f"gram_{h}", [P, FC1, P], F32R) for h in ("hi", "lo")]
    x.w2g = [c.sb(f"w2g_{h}", [P, FC1, D], F32R) for h in ("hi", "lo")]
    x.route = [c.sb(f"route_{h}", [P, KC, 16], F32R) for h in ("hi", "lo")]
    x.rows_x, x.rows_1 = c.sb("rows_x", [48, D], F32R), c.sb("rows_1", [48, D], F32R)
    x.b1 = c.sb("b1", [P, FC1])
    x.cross = c.sb("cross", [P, FC1])
    x.square = c.sb("square", [P, EXPERTS1])
    x.expert = c.sb("expert", [P, FC1, EXPERTS1], F32R)
    x.spread = c.sb("spread", [48, FC1 * P], F32R)
    x.earlier = c.sb("earlier", [P, EXPERTS1, EXPERTS1])
    with ExitStack() as stack:
        ci = Core(nc, stack, "ew")
        w1 = ci.sb("w1", [P, KC, FC1 * P])
        w2, b2r, gr = (ci.sb(n, [P, FC1, D]) for n in ("w2", "b2r", "gr"))
        scratch = ci.sb("scratch", [P, D])
        mean = ci.sb("mean", [P, 2 * FC1 + 1])
        route = ci.sb("route", [P, KC, 16])
        w2t = ci.sb("w2t", [P, KC, FC1 * P])
        gram = ci.sb("gram", [P, FC1, P])
        g48, b48, beta48, t48 = (ci.sb(n, [48, D]) for n in ("g48", "b48", "beta48", "t48"))
        lo48 = ci.sb("lo48", [48, D])
        hi48 = ci.sb("hi48", [48, D], F32R)
        is_lo, is_lo2, is_hi = (ci.sb(n, [48, 1]) for n in ("is_lo", "is_lo2", "is_hi"))
        blocks = ci.sb("blocks", [P, P // HID1, HID1])
        ex, sp1, sp2 = ci.sb("ex", [P, FC1, EXPERTS1]), ci.sb("sp1", [48, FC1 * P]), ci.sb("sp2", [48, FC1 * P])
        pt, pg, psq = ci.ps("pt"), ci.ps("pg"), ci.ps("psq")
        arrived, chain, consts, turned, evac, gram_done, square_done, zeroed = (
            ci.sem(n) for n in ("arrived", "chain", "consts", "turned", "evac", "gram_done", "square_done", "zeroed"))
        rows_arrived, hi_made = ci.sem("rows_arrived"), ci.sem("hi_made")
        block = stack.enter_context(nc.Block())
        per = P // HID1

        @block.sync
        def _(sp):
            sp.dma_start(w1[:], chunks(a["f_w1"])).then_inc(arrived, 16)
            sp.dma_start(w2[:], chunks(a["f_w2"])).then_inc(arrived, 16)
            sp.dma_start(x.b1[:], a["f_b1"]).then_inc(arrived, 16)
            with nc.allow_non_contiguous_dma(reason="router columns"):
                sp.dma_start(route[:, :, 0:8], a["f_router"].rearrange("(c p) n -> p c n", p=P)).then_inc(arrived, 16)
            for e in range(EXPERTS1):
                at = slice((e % per) * HID1, (e % per + 1) * HID1)
                for t, n in ((b2r, "f_b2"), (gr, "f_gamma")):
                    sp.dma_start(t[at, e // per, :], a[n][e:e + 1, :].broadcast_to([HID1, D])).then_inc(arrived, 16)
            sp.wait_ge(zeroed, 3)
            for r in range(3):
                at = slice(r * EXPERTS1, (r + 1) * EXPERTS1)
                sp.dma_start(g48[at, :], a["f_gamma"]).then_inc(rows_arrived, 16)
                sp.dma_start(b48[at, :], a["f_b2"]).then_inc(rows_arrived, 16)
                sp.dma_start(beta48[24 + r * EXPERTS1:24 + (r + 1) * EXPERTS1, :], a["f_beta"]).then_inc(rows_arrived, 16)
            sp.wait_ge(rows_arrived, 9 * 16)

        @block.gpsimd
        def _(pool):
            z = Steps(pool, zeroed)
            for t in (g48, b48, beta48):
                z(pool.memset(t[:], 0.0))
            s = Steps(pool, consts)
            for t in (is_lo, is_lo2, blocks, ex, sp1, sp2, x.earlier):
                s(pool.memset(t[:], 1.0))
            s.settle()

            def band(m, base, pattern, mult, width):
                s.link(pool.affine_select(out=m, in_=m, compare_op=ALU.is_ge, fill=0.0, base=base,
                                          pattern=pattern, channel_multiplier=mult))
                s.link(pool.affine_select(out=m, in_=m, compare_op=ALU.is_ge, fill=0.0, base=width - 1 - base,
                                          pattern=[[-q, n] for q, n in pattern], channel_multiplier=-mult))

            band(is_lo[:], -8, [[0, 1]], 1, 8)
            band(is_lo2[:], -32, [[0, 1]], 1, 8)
            band(blocks[:], 0, [[-HID1, per], [0, HID1]], 1, HID1)
            band(ex[:], 0, [[P, FC1], [-HID1, EXPERTS1]], 1, HID1)
            band(sp1[:], 0, [[1, FC1 * P]], -HID1, HID1)
            band(sp2[:], 16 * HID1, [[1, FC1 * P]], -HID1, HID1)
            s(pool.affine_select(out=x.earlier[:], in_=x.earlier[:], compare_op=ALU.is_gt, fill=0.0, base=0,
                                 pattern=[[1, EXPERTS1], [-1, EXPERTS1]], channel_multiplier=0))

        @block.vector
        def _(v):
            s = Steps(v, chain)
            v.wait_ge(consts, 20)
            s(v.tensor_copy(x.expert[:], ex[:]))
            s(v.tensor_tensor(x.spread[:], sp1[:], sp2[:], ALU.add))
            s.link(v.tensor_tensor(is_lo[:], is_lo[:], is_lo2[:], ALU.add))
            s(v.tensor_scalar(is_hi[:], is_lo[:], -1.0, 1.0, ALU.mult, ALU.add))
            v.wait_ge(arrived, 16 * 20)
            s(v.tensor_copy(x.w1[0][:], w1[:]))
            for fc in range(FC1):
                s(v.tensor_reduce(mean[:, fc:fc + 1], w2[:, fc, :], X_AXIS, ALU.add))
                s(v.tensor_reduce(mean[:, FC1 + fc:FC1 + fc + 1], b2r[:, fc, :], X_AXIS, ALU.add))
            s.settle()
            s(v.tensor_tensor(x.w1[1][:], w1[:], x.w1[0][:].bitcast(F32), ALU.subtract))
            s.link(v.tensor_scalar(mean[:, 0:2 * FC1], mean[:, 0:2 * FC1], -1.0 / D, None, ALU.mult))
            for fc in range(FC1):
                s(v.tensor_scalar(w2[:, fc, :], w2[:, fc, :], mean[:, fc:fc + 1], None, ALU.add))
                s(v.tensor_scalar(b2r[:, fc, :], b2r[:, fc, :], mean[:, FC1 + fc:FC1 + fc + 1], None, ALU.add))
            s.settle()
            for fc in range(FC1):
                s.link(v.scalar_tensor_tensor(scratch[:], w2[:, fc, :], 2.0, b2r[:, fc, :], ALU.mult, ALU.mult,
                                              accum_out=x.cross[:, fc:fc + 1]))
            s.link(v.tensor_tensor(gr[:], gr[:], w2[:], ALU.mult))
            s.link(v.tensor_copy(x.w2g[0][:], gr[:]))
            s(v.tensor_tensor(x.w2g[1][:], gr[:], x.w2g[0][:].bitcast(F32), ALU.subtract))
            v.wait_ge(rows_arrived, 9 * 16)
            s.link(v.tensor_reduce(mean[0:48, 2 * FC1:2 * FC1 + 1], b48[:], X_AXIS, ALU.add))
            s.link(v.tensor_scalar(mean[0:48, 2 * FC1:2 * FC1 + 1], mean[0:48, 2 * FC1:2 * FC1 + 1], -1.0 / D, None,
                                   ALU.mult))
            s.link(v.tensor_scalar(b48[:], b48[:], mean[0:48, 2 * FC1:2 * FC1 + 1], None, ALU.add))
            centred = s.n
            assert centred == 23, centred
            for kc in range(KC):
                v.wait_ge(turned, kc + 1)
                s(v.tensor_scalar(w2t[:, kc, :], pt[:, 0:FC1 * P], 2.0, None, ALU.mult))
                s.link(v.tensor_scalar(route[:, kc, 8:16], pt[:, FC1 * P:FC1 * P + 8], 2.0, None, ALU.mult))
            s(v.tensor_copy(x.w2t[0][:], w2t[:]))
            s.link(v.tensor_copy(x.route[0][:], route[:]))
            s(v.tensor_tensor(x.w2t[1][:], w2t[:], x.w2t[0][:].bitcast(F32), ALU.subtract))
            s(v.tensor_tensor(x.route[1][:], route[:], x.route[0][:].bitcast(F32), ALU.subtract))
            s(v.tensor_tensor(scratch[:, 0:KC * 8].rearrange("p (c n) -> p c n", c=KC), route[:, :, 8:16],
                              route[:, :, 8:16], ALU.mult))
            assert s.n == 36, s.n
            v.wait_ge(gram_done, 1)
            s.settle()
            for fc in range(FC1):
                s(v.scalar_tensor_tensor(gram[:, fc, :], pg[:, fc * P:fc * P + P], 0.25,
                                         blocks[:].rearrange("p a b -> p (a b)"), ALU.mult, ALU.mult))
            s.settle()
            s.link(v.tensor_copy(x.gram[0][:], gram[:]))
            s(v.tensor_tensor(x.gram[1][:], gram[:], x.gram[0][:].bitcast(F32), ALU.subtract))
            v.wait_ge(square_done, 1)
            s(v.tensor_scalar(x.square[:], psq[:, 0:8], 0.25, None, ALU.mult))
            s.link(v.tensor_tensor(t48[:], b48[:], g48[:], ALU.mult))
            s.link(v.tensor_tensor(t48[:], t48[:], beta48[:], ALU.add))
            for src, dst in ((g48, x.rows_x), (t48, x.rows_1)):
                s.link(v.tensor_copy(hi48[:], src[:]))
                s.link(v.tensor_tensor(lo48[:], src[:], hi48[:].bitcast(F32), ALU.subtract))
                s.link(v.tensor_scalar(lo48[:], lo48[:], is_lo[:], None, ALU.mult))
                s.link(v.scalar_tensor_tensor(dst[:], hi48[:].bitcast(F32), is_hi[:], lo48[:], ALU.mult, ALU.add))

        @block.tensor
        def _(pe):
            for kc in range(KC):
                pe.wait_ge(chain, 23 + 2 * kc)
                for fc in range(FC1):
                    pe.transpose(pt[:, fc * P:fc * P + P], w2[:, fc, kc * P:kc * P + P], k.ident[:])
                pe.matmul(pt[:, FC1 * P:FC1 * P + 8], b48[0:8, kc * P:kc * P + P], k.ident[0:8, 0:8],
                          start=True, stop=True).then_inc(turned, 1)
            pe.wait_ge(chain, 36)
            for fc in range(FC1):
                for kc in range(KC):
                    part = w2t[:, kc, fc * P:fc * P + P]
                    last = pe.matmul(pg[:, fc * P:fc * P + P], part, part, start=kc == 0, stop=kc == KC - 1)
            last.then_inc(gram_done, 1)
            for kc in range(KC):
                last = pe.matmul(psq[:, 0:8], k.ones[:], scratch[:, kc * 8:kc * 8 + 8], start=kc == 0,
                                 stop=kc == KC - 1)
            last.then_inc(square_done, 1)



def dense1_phase(nc, a, k, out):
    with ExitStack() as stack:
        c = Core(nc, stack, "d1")
        w12 = [c.sb(f"w12_{h}", [P, KC, D], F32R) for h in ("hi", "lo")]
        ex = Experts()
        split_weights(nc, k, [(chunks(a["g_w12"]), *w12)])
        messages(nc, k, "msg2", k.h, w12, k.message2)
        expert_weights(nc, a, k, c, ex)
        x3 = [c.sb(f"x3{n}", [P, T, D]) for n in range(2)]
        own, msg = (c.sb(n, [P, T, D]) for n in ("own", "msg"))
        at = c.sb("at", [P, T], I32)
        gain, middle = c.sb("gain", [P, T]), c.sb("middle", [P, T])
        xf = [c.sb(f"xf{n}", [P, T, D]) for n in range(2)]
        xh, xl = (c.sb(n, [P, KC, GR], F32R) for n in ("xh", "xl"))
        hid = c.sb("hid", [P, FC1, GR])
        quad = c.sb("quad", [P, FC1, GR])
        hh, hl, qh, ql = (c.sb(n, [P, FC1, GR], F32R) for n in ("hh", "hl", "qh", "ql"))
        st, mv = c.sb("st", [P, T, 6]), c.sb("mv", [P, T, 2])
        ve, rs, shift, power_in = (c.sb(n, [P, T]) for n in ("ve", "rs", "shift", "power_in"))
        msq = c.sb("msq", [P, T])
        S3 = [P, T, EXPERTS1]
        logit = c.sb("logit", [P, T, 16])
        prob, rank, gate, var, rse, coef = (c.sb(n, S3) for n in ("prob", "rank", "gate", "var", "rse", "coef"))
        top, total = c.sb("top", [P, T]), c.sb("total", [P, T])
        wins, ties = (c.sb(n, [P, T, EXPERTS1, EXPERTS1]) for n in ("wins", "ties"))
        parts = c.sb("parts", [P, T, P], F32R)
        coef_t = c.sb("coef_t", [48, GR], F32R)
        ptr = [c.ps(f"ptr{n}") for n in range(2)]
        pu, pq = ([c.ps(f"{n}{i}") for i in range(2)] for n in ("pu", "pq"))
        psm, pb = c.ps("psm"), c.ps("pb")
        pox, po1 = [ptr[0], ptr[1]], [pu[0], pu[1]]

        NS_, NR, EXP_STEP, VAR_STEP = 4, 25, 4, 18
        relu_done = c.sem("relu_done")
        consts = c.sem("consts")
        y_in, own_in = ([c.sem(f"{n}{t}") for t in range(T)] for n in ("y_in", "own_in"))
        msg_in = [c.sem(f"msg_in{t}") for t in range(T)]
        out_done = [c.sem(f"out_done{n}") for n in range(T)]
        at_made, msg_made, added, halved, affine, x3_made = (
            c.sem(n) for n in ("at_made", "msg_made", "added", "halved", "affine", "x3_made"))
        gains, stats, pow_done, shifted, normed = (c.sem(n) for n in ("gains", "stats", "pow_done", "shifted", "normed"))
        turned, xh_made, xl_made = (c.sem(n) for n in ("turned", "xh_made", "xl_made"))
        logits_done, up_done, hid_made, hh_made, hl_made = (
            c.sem(n) for n in ("logits_done", "up_done", "hid_made", "hh_made", "hl_made"))
        cross_done, quad_made, qh_made, ql_made, square_done = (
            c.sem(n) for n in ("cross_done", "quad_made", "qh_made", "ql_made", "square_done"))
        route, exp_done, pow2_done, coef_turned, coef_out, spread_done, scaled = (
            c.sem(n) for n in ("route", "exp_done", "pow2_done", "coef_turned", "coef_out", "spread_done", "scaled"))
        ch_made, cl_made, x_done, one_done, finished, mul_done = (
            c.sem(n) for n in ("ch_made", "cl_made", "x_done", "one_done", "finished", "mul_done"))
        block = stack.enter_context(nc.Block())

        @block.sync
        def _(sp):
            def load(g, u, t):
                sp.wait_ge(out_done[t], 16 * g + 16)
                sp.dma_start(x3[u][:, t, :], k.y[ds(g * GR + t * P, P), :]).then_inc(y_in[t], 16)
                sp.wait_ge(halved, 4 * g + t + 1)
                sp.dma_start(own[:, t, :], k.own[ds(g * GR + t * P, P), :]).then_inc(own_in[t], 16)

            def store(g, u, t):
                sp.wait_ge(finished, 4 * g + t + 1)
                sp.dma_start(out[ds(g * GR + t * P, P), :], x3[u][:, t, :]).then_inc(out_done[t], 16)

            for t in range(T):
                sp.sem_inc(out_done[t], 32)
            for t in range(T):
                load(0, 0, t)
            for t in range(T):
                load(1, 1, t)
            with sp.Fori(0, NG // 2 - 1) as i:
                for u in range(2):
                    for t in range(T):
                        store(i * 2 + u, u, t)
                        load(i * 2 + u + 2, u, t)
            for u in range(2):
                for t in range(T):
                    store(NG - 2 + u, u, t)
            for t in range(T):
                sp.wait_ge(out_done[t], 32 + 16 * NG)

        @block.gpsimd
        def _(pool):
            def gather(g):
                pool.wait_ge(halved, 4 * g + 4)
                hold(pool)
                pool.tensor_copy(at[:], k.slot["d"][:, ds(T * g, T)]).then_inc(at_made, 1)
                pool.memset(msg[:], 0.0).then_inc(msg_made, 1)
                pool.wait_ge(msg_made, g + 1)
                pool.wait_ge(at_made, g + 1)
                hold(pool)
                for t in range(T):
                    pool.indirect_dma_start(msg[:, t, :], None, k.message2[:, :],
                                            bass.IndirectOffsetOnAxis(ap=at[:, t:t + 1], axis=0),
                                            bounds_check=EP - 1, oob_is_err=False).then_inc(msg_in[t], 16)

            def add(g):
                for t in range(T):
                    pool.wait_ge(own_in[t], 16 * g + 16)
                    pool.wait_ge(msg_in[t], 16 * g + 16)
                    pool.tensor_tensor(msg[:, t, :], msg[:, t, :], own[:, t, :], ALU.add).then_inc(added, 1)

            def power(g):
                pool.wait_ge(stats, NS_ * g + 4)
                pool.tensor_tensor(rs[:], ve[:], k.half_neg[:, 0:T], ALU.pow).then_inc(pow_done, 1)

            def low(g, fc, src, hi, lo, ready, made):
                pool.wait_ge(ready, FC1 * g + fc + 1)
                pool.tensor_tensor(lo[:, fc, :], src[:, fc, :], hi[:, fc, :].bitcast(F32), ALU.subtract)\
                    .then_inc(made, 1)

            def power2(g):
                pool.wait_ge(route, NR * g + VAR_STEP)
                pool.tensor_tensor(rse[:].rearrange("p t e -> p (t e)"), var[:].rearrange("p t e -> p (t e)"),
                                   k.half_neg[:, 0:T * EXPERTS1], ALU.pow).then_inc(pow2_done, 1)

            def body(g, last):
                if not last:
                    gather(g + 1)
                low(g, 0, hid, hh, hl, hh_made, hl_made)
                low(g, 1, hid, hh, hl, hh_made, hl_made)
                low(g, 0, quad, qh, ql, qh_made, ql_made)
                low(g, 1, quad, qh, ql, qh_made, ql_made)
                if not last:
                    add(g + 1)
                power2(g)
                if not last:
                    power(g + 1)
                low(g, 0, quad, qh, ql, ch_made, cl_made)
                low(g, 1, quad, qh, ql, ch_made, cl_made)

            gather(0)
            add(0)
            power(0)
            with pool.Fori(0, NG // 2 - 1) as i:
                body(i * 2, False)
                body(i * 2 + 1, False)
            body(NG - 2, False)
            body(NG - 1, True)

        @block.scalar
        def _(act_):
            def halves(g, u, t):
                act_.wait_ge(added, 4 * g + t + 1)
                act_.activation(msg[:, t, :], msg[:, t, :], ACT.Relu, scale=0.5).then_inc(relu_done, 1)
                act_.wait_ge(y_in[t], 16 * g + 16)
                act_.wait_ge(gains, 2 * g + 2)
                act_.activation(x3[u][:, t, :], x3[u][:, t, :], ACT.Identity, bias=middle[:, t:t + 1],
                                scale=gain[:, t:t + 1]).then_inc(affine, 1)

            def norm(g, u, t):
                act_.wait_ge(shifted, 2 * g + 2)
                act_.activation(xf[u][:, t, :], x3[u][:, t, :], ACT.Identity, bias=shift[:, t:t + 1],
                                scale=rs[:, t:t + 1]).then_inc(normed, 1)

            def high(g, t):
                act_.wait_ge(turned, 4 * g + t + 1)
                act_.activation(xh[:, :, t * P:t * P + P], ptr[t % 2][:].rearrange("p (c n) -> p c n", n=P), ACT.Copy)\
                    .then_inc(xh_made, 1)

            def hidden(g, fc):
                act_.wait_ge(up_done, FC1 * g + fc + 1)
                act_.activation(hid[:, fc, :], pu[fc][:], ACT.Relu, bias=ex.b1[:, fc:fc + 1]).then_inc(hid_made, 1)
                act_.wait_ge(hid_made, FC1 * g + fc + 1)
                act_.activation(hh[:, fc, :], hid[:, fc, :], ACT.Copy).then_inc(hh_made, 1)

            def part(g, fc, ready, made):
                act_.wait_ge(ready, FC1 * g + fc + 1)
                act_.activation(qh[:, fc, :], quad[:, fc, :], ACT.Copy).then_inc(made, 1)

            def body(g, u, last):
                n = 1 - u
                hidden(g, 0)
                hidden(g, 1)
                part(g, 0, quad_made, qh_made)
                part(g, 1, quad_made, qh_made)
                act_.wait_ge(route, NR * g + EXP_STEP)
                act_.activation(prob[:], prob[:], ACT.Exp).then_inc(exp_done, 1)
                if not last:
                    for t in range(T):
                        halves(g + 1, n, t)
                act_.wait_ge(coef_turned, g + 1)
                act_.activation(coef_t[:], ptr[1][0:48, :], ACT.Copy).then_inc(coef_out, 1)
                part(g, 0, scaled, ch_made)
                part(g, 1, scaled, ch_made)
                if not last:
                    for t in range(T):
                        norm(g + 1, n, t)
                    for t in range(T):
                        high(g + 1, t)

            for t in range(T):
                halves(0, 0, t)
            for t in range(T):
                norm(0, 0, t)
            for t in range(T):
                high(0, t)
            with act_.Fori(0, NG // 2 - 1) as i:
                body(i * 2, 0, False)
                body(i * 2 + 1, 1, False)
            body(NG - 2, 0, False)
            body(NG - 1, 1, True)

        @block.vector
        def _(v):
            v.sem_inc(halved, 4)
            v.memset(parts[:, :, 48:P].bitcast(F32), 0.0).then_inc(consts, 1)

            def gains_of(g):
                v.tensor_scalar(gain[:], k.dev[:, ds(T * g, T)], 0.5, None, ALU.add).then_inc(gains, 1)
                v.tensor_copy(middle[:], k.mean[:, ds(T * g, T)]).then_inc(gains, 1)

            def sums(g, u):
                for t in range(T):
                    v.wait_ge(relu_done, 4 * g + t + 1)
                    v.wait_ge(affine, 4 * g + t + 1)
                    v.tensor_tensor(x3[u][:, t, :], x3[u][:, t, :], msg[:, t, :], ALU.add).then_inc(halved, 1)

            def statistics(g, u):
                s = Steps(v, stats, NS_ * g)
                v.wait_ge(halved, 4 * g + 4 + 4)
                hold(v)
                for t in range(T):
                    ins = v.bn_stats(st[:, t, :], x3[u][:, t, :])
                s.link(ins)
                hold(v)
                for t in range(T):
                    ins = v.bn_aggr(mv[:, t, :], st[:, t, :])
                s.link(ins)
                s(v.tensor_scalar(shift[:], mv[:, :, 0], -1.0, None, ALU.mult))
                s(v.tensor_scalar(ve[:], mv[:, :, 1], 1e-5, None, ALU.add))

            def shifts(g):
                v.wait_ge(pow_done, g + 1)
                v.tensor_tensor(shift[:], shift[:], rs[:], ALU.mult).then_inc(shifted, 1)
                v.tensor_tensor(power_in[:], mv[:, :, 1], rs[:], ALU.mult).then_inc(shifted, 1)
                v.wait_ge(shifted, 2 * g + 2)

            def low(g, t):
                v.wait_ge(xh_made, 4 * g + t + 1)
                v.tensor_tensor(xl[:, :, t * P:t * P + P], ptr[t % 2][:].rearrange("p (c n) -> p c n", n=P),
                                xh[:, :, t * P:t * P + P].bitcast(F32), ALU.subtract).then_inc(xl_made, 1)

            def quadratic(g, fc):
                v.wait_ge(cross_done, FC1 * g + fc + 1)
                v.scalar_tensor_tensor(quad[:, fc, :], pq[fc][:], ex.cross[:, fc:fc + 1], hid[:, fc, :], ALU.add,
                                       ALU.mult).then_inc(quad_made, 1)

            def wide(t_):
                return t_.unsqueeze(2).broadcast_to(S3)

            def routing(g):
                s = Steps(v, route, NR * g)
                v.wait_ge(logits_done, g + 1)
                s(v.tensor_tensor(msq[:], power_in[:], rs[:], ALU.mult))
                s.link(v.tensor_copy(logit[:], psm[:, 0:T * 16].rearrange("p (t n) -> p t n", t=T)))
                choice = logit[:, :, 0:EXPERTS1]
                s.link(v.tensor_reduce(top[:], choice, X_AXIS, ALU.max))
                s(v.tensor_tensor(prob[:], choice, wide(top[:]), ALU.subtract))
                assert s.n == EXP_STEP
                other = choice.unsqueeze(2).broadcast_to([P, T, EXPERTS1, EXPERTS1])
                mine = choice.unsqueeze(3).broadcast_to([P, T, EXPERTS1, EXPERTS1])
                s(v.tensor_tensor(wins[:], other, mine, ALU.is_gt))
                s.link(v.tensor_tensor(ties[:], other, mine, ALU.is_equal))
                s.link(v.tensor_tensor(ties[:], ties[:],
                                       ex.earlier[:].unsqueeze(1).broadcast_to([P, T, EXPERTS1, EXPERTS1]), ALU.mult))
                s.link(v.tensor_tensor(wins[:], wins[:], ties[:], ALU.add))
                s.link(v.tensor_reduce(rank[:], wins[:], X_AXIS, ALU.add))
                v.wait_ge(exp_done, g + 1)
                s.link(v.scalar_tensor_tensor(gate[:], rank[:], 1.0, prob[:], ALU.is_le, ALU.mult))
                s.link(v.tensor_reduce(total[:], gate[:], X_AXIS, ALU.add))
                s.link(v.reciprocal(total[:], total[:]))
                s(v.tensor_tensor(gate[:], gate[:], wide(total[:]), ALU.mult))
                v.wait_ge(square_done, g + 1)
                s.link(v.tensor_tensor(var[:], psm[:, 128:128 + T * EXPERTS1].rearrange("p (t n) -> p t n", t=T),
                                       logit[:, :, EXPERTS1:16], ALU.add))
                s.link(v.tensor_tensor(var[:], var[:], ex.square[:].unsqueeze(1).broadcast_to(S3), ALU.add))
                s.link(v.tensor_scalar(var[:], var[:], 1.0 / D, None, ALU.mult))
                s.link(v.tensor_tensor(var[:], var[:], wide(msq[:]), ALU.add))
                s(v.tensor_scalar(var[:], var[:], 0.0, 1e-6, ALU.max, ALU.add))
                assert s.n == VAR_STEP
                v.wait_ge(pow2_done, g + 1)
                s.link(v.tensor_tensor(coef[:], gate[:], rse[:], ALU.mult))
                E1 = EXPERTS1
                for n, src in ((0, coef), (3 * E1, gate)):
                    s(v.tensor_copy(parts[:, :, n:n + E1], src[:]))
                    s.link(v.tensor_copy(parts[:, :, n + E1:n + 2 * E1], src[:]))
                    s(v.tensor_tensor(parts[:, :, n + 2 * E1:n + 3 * E1], src[:],
                                      parts[:, :, n:n + E1].bitcast(F32), ALU.subtract))
                assert s.n == NR

            def scale(g, fc):
                v.wait_ge(spread_done, FC1 * g + fc + 1)
                v.wait_ge(ql_made, FC1 * g + FC1)
                v.tensor_tensor(quad[:, fc, :], hid[:, fc, :], pb[:], ALU.mult).then_inc(scaled, 1)

            def finish(g, u, t):
                v.wait_ge(x_done, 4 * g + t + 1)
                v.tensor_tensor(xf[u][:, t, :], xf[u][:, t, :], pox[t % 2][:], ALU.mult).then_inc(mul_done, 1)
                v.wait_ge(one_done, 4 * g + t + 1)
                v.tensor_tensor(x3[u][:, t, :], x3[u][:, t, :], po1[t % 2][:], ALU.add).then_inc(mul_done, 1)
                v.wait_ge(mul_done, 8 * g + 2 * t + 2)
                v.tensor_tensor(x3[u][:, t, :], x3[u][:, t, :], xf[u][:, t, :], ALU.add).then_inc(finished, 1)

            def body(g, u, last):
                n = 1 - u
                if not last:
                    gains_of(g + 1)
                quadratic(g, 0)
                quadratic(g, 1)
                routing(g)
                if not last:
                    sums(g + 1, n)
                    statistics(g + 1, n)
                scale(g, 0)
                scale(g, 1)
                if not last:
                    shifts(g + 1)
                for t in range(T):
                    finish(g, u, t)
                if not last:
                    for t in range(T):
                        low(g + 1, t)

            gains_of(0)
            sums(0, 0)
            statistics(0, 0)
            shifts(0)
            for t in range(T):
                low(0, t)
            with v.Fori(0, NG // 2 - 1) as i:
                body(i * 2, 0, False)
                body(i * 2 + 1, 1, False)
            body(NG - 2, 0, False)
            body(NG - 1, 1, True)

        @block.tensor
        def _(pe):
            pe.wait_ge(consts, 1)

            def turn(g, u):
                for t in range(T):
                    pe.wait_ge(normed, 4 * g + t + 1)
                    if t >= 2:
                        pe.wait_ge(xl_made, 4 * g + t - 1)
                    for kc in range(KC):
                        own_ = slice(kc * P, kc * P + P)
                        last = pe.transpose(ptr[t % 2][:, own_], xf[u][:, t, own_], k.ident[:])
                    last.then_inc(turned, 1)

            def logits(g):
                for t in range(T):
                    pe.wait_ge(xl_made, 4 * g + t + 1)
                    sl = slice(t * P, t * P + P)
                    for kc in range(KC):
                        last = split3(pe, psm[:, t * 16:t * 16 + 16], (xh[:, kc, sl], xl[:, kc, sl]),
                                      (ex.route[0][:, kc, :], ex.route[1][:, kc, :]), kc == 0, kc == KC - 1)
                last.then_inc(logits_done, 1)

            def up(g, fc):
                sl = slice(fc * P, fc * P + P)
                for kc in range(KC):
                    last = split3(pe, pu[fc][:], (ex.w1[0][:, kc, sl], ex.w1[1][:, kc, sl]),
                                  (xh[:, kc, :], xl[:, kc, :]), kc == 0, kc == KC - 1)
                last.then_inc(up_done, 1)

            def cross(g, fc):
                sl = slice(fc * P, fc * P + P)
                for kc in range(KC):
                    split3(pe, pq[fc][:], (ex.w2t[0][:, kc, sl], ex.w2t[1][:, kc, sl]),
                           (xh[:, kc, :], xl[:, kc, :]), kc == 0, False)

            def gram(g, fc):
                pe.wait_ge(hl_made, FC1 * g + fc + 1)
                split3(pe, pq[fc][:], (ex.gram[0][:, fc, :], ex.gram[1][:, fc, :]), (hh[:, fc, :], hl[:, fc, :]),
                       False, True).then_inc(cross_done, 1)

            def squares(g):
                pe.wait_ge(ql_made, FC1 * g + FC1)
                pe.wait_ge(route, NR * g + 2)
                for t in range(T):
                    sl = slice(t * P, t * P + P)
                    for fc in range(FC1):
                        for n, q in enumerate((qh, ql)):
                            last = pe.matmul(psm[:, 128 + t * EXPERTS1:128 + (t + 1) * EXPERTS1], q[:, fc, sl],
                                             ex.expert[:, fc, :], start=fc == 0 and n == 0,
                                             stop=fc == FC1 - 1 and n == 1, skip_group_check=True)
                last.then_inc(square_done, 1)

            def turn_coef(g):
                pe.wait_ge(route, NR * g + NR)
                for t in range(T):
                    last = pe.transpose(ptr[1][:, t * P:t * P + P], parts[:, t, :].bitcast(F32), k.ident[:])
                last.then_inc(coef_turned, 1)

            def spread(g, fc):
                pe.wait_ge(coef_out, g + 1)
                if fc:
                    pe.wait_ge(scaled, FC1 * g + fc)
                pe.matmul(pb[:], ex.spread[:, fc * P:fc * P + P], coef_t[:], start=True, stop=True)\
                  .then_inc(spread_done, 1)

            def product(g, t):
                sl = slice(t * P, t * P + P)
                if t >= 2:
                    pe.wait_ge(mul_done, 8 * g + 2 * t - 2)
                pe.matmul(pox[t % 2][:], coef_t[:, sl], ex.rows_x[:], start=True, stop=True).then_inc(x_done, 1)
                pe.matmul(po1[t % 2][:], coef_t[:, sl], ex.rows_1[:], start=True, stop=False, skip_group_check=True)
                for fc in range(FC1):
                    pe.wait_ge(cl_made, FC1 * g + fc + 1)
                    last = split3(pe, po1[t % 2][:], (qh[:, fc, sl], ql[:, fc, sl]),
                                  (ex.w2g[0][:, fc, :], ex.w2g[1][:, fc, :]), False, fc == FC1 - 1)
                last.then_inc(one_done, 1)

            def body(g, u, last):
                logits(g)
                up(g, 0)
                up(g, 1)
                cross(g, 0)
                gram(g, 0)
                cross(g, 1)
                gram(g, 1)
                squares(g)
                turn_coef(g)
                spread(g, 0)
                spread(g, 1)
                for t in range(T):
                    product(g, t)
                if not last:
                    pe.wait_ge(mul_done, 8 * g + 8)
                    turn(g + 1, 1 - u)

            turn(0, 0)
            with pe.Fori(0, NG // 2 - 1) as i:
                body(i * 2, 0, False)
                body(i * 2 + 1, 1, False)
            body(NG - 2, 0, False)
            body(NG - 1, 1, True)


class Tables:
    pass


def program(nc, a, out):
    with ExitStack() as stack:
        c = Core(nc, stack, "net")
        k = Tables()

        def dram(name, shape, dt=F32):
            return nc.dram_tensor(name, shape, dt).ap()

        k.rec_s, k.rec_d = dram("rec_s", [EP + 1, REC_S], I32), dram("rec_d", [EP + 1, REC_D], I32)
        k.slots = {x: dram(f"slots_{x}", [NPAD, 1], I32) for x in "sd"}
        k.values = dram("values", [EP, D])
        k.ident = c.sb("ident", [P, P])
        k.ones = c.sb("ones", [P, P])
        k.zeros = c.sb("zeros", [P, D])
        k.half_neg = c.sb("half_neg", [P, 32])
        k.b12 = c.sb("b12", [P, D])
        k.slot = {x: c.sb(f"slot_{x}", [P, NT], I32) for x in "sd"}
        k.same = {x: c.sb(f"same_{x}", [P, EP + 1], BF16) for x in "sd"}
        k.rec = {"s": c.sb("rec_s_sb", [P, ET, REC_S], I32), "d": c.sb("rec_d_sb", [P, ET, REC_D], I32)}
        k.y = dram("y", [NPAD, D])
        k.message2 = dram("message2", [EP, D])
        k.message1, k.h, k.own = dram("message1", [EP, D]), dram("h", [NPAD, D]), dram("own", [NPAD, D])
        k.mean, k.dev = c.sb("mean", [P, NT]), c.sb("dev", [P, NT])
        sort_phase(nc, a, k)
        attention_phase(nc, a, k)
        dense0_phase(nc, a, k)
        conv_phase(nc, a, k)
        dense1_phase(nc, a, k, out)


def columns(v):
    return v.reshape(-1, P, *v.shape[1:]).swapaxes(0, 1)


def kernel(x, src, dst, edge_attr_8, edge_weight, node_vec, L0_gnn_ln_g, L0_gnn_ln_b, L0_gnn_Wq, L0_gnn_bq,
           L0_gnn_Wk, L0_gnn_bk, L0_gnn_Wv, L0_gnn_bv, L0_gnn_W1, L0_gnn_b1, L0_gnn_W2, L0_gnn_b2, L0_ffn_Wr,
           L0_ffn_br, L0_ffn_Wgate, L0_ffn_bgate, L0_ffn_W1, L0_ffn_W3, L0_ffn_W2, L1_gnn_W0_1, L1_gnn_W1_1,
           L1_gnn_b1, L1_gnn_W0_2, L1_gnn_W1_2, L1_gnn_b2, L1_ffn_router_w, L1_ffn_w1, L1_ffn_b1, L1_ffn_w2,
           L1_ffn_b2, L1_ffn_gamma, L1_ffn_beta):
    import numpy as np
    import concourse.bacc as bacc
    from concourse.bass_utils import run_bass_kernel_spmd

    def padded(v, rows, fill):
        v = np.asarray(v)
        return np.concatenate([v, np.full((rows - len(v),) + v.shape[1:], fill, v.dtype)])

    def row(v):
        return np.asarray(v).reshape(1, -1)

    def column(v):
        return columns(np.asarray(v))

    src, dst = padded(src, EP, N), padded(dst, EP, N)
    arrays = {
        "x": padded(x, NPAD, 0), "key_s": row(src), "key_d": row(dst), "col_s": column(src), "col_d": column(dst),
        "attr": column(padded(edge_attr_8, EP, 0)), "edge_w": column(padded(edge_weight, EP, 0)),
        "diag": column(padded(node_vec, NPAD, 0)),
        "ln_g": column(L0_gnn_ln_g), "ln_b": column(L0_gnn_ln_b),
        "wq": L0_gnn_Wq, "wk": L0_gnn_Wk, "wv": L0_gnn_Wv,
        "bq": column(L0_gnn_bq), "bk": column(L0_gnn_bk), "bv": column(L0_gnn_bv),
        "w1t": np.asarray(L0_gnn_W1).T, "w2": L0_gnn_W2, "b1_col": column(L0_gnn_b1), "b2_row": row(L0_gnn_b2),
        "e_w1": np.asarray(L0_ffn_W1).transpose(1, 0, 2).reshape(D, -1),
        "e_w3": np.asarray(L0_ffn_W3).transpose(1, 0, 2).reshape(D, -1),
        "e_w2": np.asarray(L0_ffn_W2).reshape(-1, D),
        "e_wr": np.concatenate([L0_ffn_Wr, np.asarray(L0_ffn_Wgate).transpose(1, 0, 2).reshape(D, -1)], 1),
        "e_br": row(np.concatenate([L0_ffn_br, np.asarray(L0_ffn_bgate).reshape(-1)])),
        "g_w01": L1_gnn_W0_1, "g_w11": L1_gnn_W1_1, "g_w02": L1_gnn_W0_2, "g_w12": L1_gnn_W1_2,
        "g_b1": row(L1_gnn_b1), "g_b2": row(L1_gnn_b2),
        "f_w1": np.asarray(L1_ffn_w1).transpose(1, 0, 2).reshape(D, -1),
        "f_w2": np.asarray(L1_ffn_w2).reshape(-1, D), "f_b1": np.asarray(L1_ffn_b1).reshape(-1, P).T,
        "f_router": L1_ffn_router_w, "f_b2": L1_ffn_b2, "f_gamma": L1_ffn_gamma, "f_beta": L1_ffn_beta,
    }
    arrays = {f"in_{name}": np.ascontiguousarray(v) for name, v in arrays.items()}

    nc = bacc.Bacc("TRN2", target_bir_lowering=False, num_devices=1)
    a = {name[3:]: nc.dram_tensor(name, v.shape, mybir.dt.from_np(v.dtype), kind="ExternalInput").ap()
         for name, v in arrays.items()}
    out = nc.dram_tensor("out", [NPAD, D], F32, kind="ExternalOutput").ap()
    program(nc, a, out)
    result = run_bass_kernel_spmd(nc, [arrays], core_ids=[0])
    return result.results[0]["out"][:N]
```

```python
from contextlib import ExitStack

import concourse.bass as bass
from concourse import mybir

F32 = mybir.dt.float32
F32R = mybir.dt.float32r
BF16 = mybir.dt.bfloat16
I32 = mybir.dt.int32
ALU = mybir.AluOpType
ACT = mybir.ActivationFunctionType
X_AXIS = mybir.AxisListType.X

P = 128
D = 512
KC = D // P
N = 10000
NG = 20
T = 4
GR = T * P
NT = NG * T
NPAD = NG * GR
E = 2500
ET = 20
EG = ET // T
EP = ET * P
HEADS = 8
HD = D // HEADS
NO_SLOT = 1 << 20
REC_S = 12
REC_D = 4
EXPERTS0 = 16
XS = 4
SETS = 5
EXPERTS1 = 8
HID1 = 32
LOGITS = 2 * EXPERTS1
SMALL = 3 * EXPERTS1
FC1 = EXPERTS1 * HID1 // P


def ds(a, n):
    return bass.ds(a, n)


def split3(te, out, lhs, rhs, first=True, last=True):
    te.matmul(out, lhs[0], rhs[0], start=first, stop=False, skip_group_check=True)
    te.matmul(out, lhs[0], rhs[1], start=False, stop=False, skip_group_check=True)
    return te.matmul(out, lhs[1], rhs[0], start=False, stop=last, skip_group_check=True)


def hold(eng):
    eng.nop(nofuse=True)


class Steps:

    def __init__(self, eng, sem, base=0):
        self.eng, self.sem, self.base, self.n = eng, sem, base, 0

    def __call__(self, ins):
        ins.then_inc(self.sem, 1)
        self.n += 1
        return ins

    def settle(self):
        self.eng.wait_ge(self.sem, self.base + self.n)

    def link(self, ins):
        self(ins)
        self.settle()


class Core:

    def __init__(self, nc, stack, tag):
        self.nc, self.stack, self.tag = nc, stack, tag
        self.sems = []
        stack.callback(self.release)

    def sb(self, name, shape, dt=F32):
        return self.stack.enter_context(self.nc.sbuf_tensor(f"{self.tag}_{name}", shape, dt))

    def ps(self, name):
        return self.stack.enter_context(self.nc.psum_tensor(f"{self.tag}_{name}", [P, D], F32))

    def sem(self, name):
        self.sems.append(self.nc.alloc_semaphore(name=f"{self.tag}_{name}"))
        return self.sems[-1]

    def release(self):
        if self.sems:
            self.nc.clear_and_free_semaphores(self.sems)
            self.nc.all_engine_barrier()



def sort_phase(nc, a, k):
    with ExitStack() as stack:
        c = Core(nc, stack, "sort")
        raw = {x: c.sb(f"raw_{x}", [P, EP], I32) for x in "sd"}
        row = {x: c.sb(f"row_{x}", [P, EP]) for x in "sd"}
        col_i = {x: c.sb(f"col_i_{x}", [P, ET], I32) for x in "sd"}
        col = {x: c.sb(f"col_{x}", [P, ET]) for x in "sd"}
        lower = c.sb("lower", [P, ET])
        upper = c.sb("upper", [P, ET])
        middle = c.sb("middle", [P, ET])
        tri = c.sb("tri", [P, P])
        diag = {x: c.sb(f"diag_{x}", [P, ET, P]) for x in "sd"}
        mask = {x: c.sb(f"mask_{x}", [P, 4, EP], BF16) for x in "sd"}
        ones = c.sb("ones", [P, 1], BF16)
        one = c.sb("one", [1, 1])
        rank_row = {x: c.sb(f"rank_row_{x}", [1, EP]) for x in "sd"}
        rank = {x: c.sb(f"rank_{x}", [P, ET], I32) for x in "sd"}
        rec = {"s": c.sb("rec_s", [P, ET, REC_S], I32), "d": c.sb("rec_d", [P, ET, REC_D], I32)}
        attr = c.sb("attr", [P, ET, HEADS])
        edge_w = c.sb("edge_w", [P, ET])
        no_slot = c.sb("no_slot", [P, NPAD // P], I32)
        counts = [c.ps(f"counts{n}") for n in range(EP // D)]
        rank_cols = c.ps("rank_cols")
        keys_in, tri_made = c.sem("keys_in"), c.sem("tri_made")
        rec_in, rec_made = c.sem("rec_in"), c.sem("rec_made")
        dve, act = c.sem("dve"), c.sem("act")
        mask_made = {x: c.sem(f"mask_made_{x}") for x in "sd"}
        mask_used = {x: c.sem(f"mask_used_{x}") for x in "sd"}
        row_made = c.sem("row_made")
        cols_made = c.sem("cols_made")
        rank_made = c.sem("rank_made")
        tails_made, stored, scattered = c.sem("tails_made"), c.sem("stored"), c.sem("scattered")
        block = stack.enter_context(nc.Block())

        @block.sync
        def _(sp):
            for x in "sd":
                sp.dma_start(raw[x][:], a[f"key_{x}"].broadcast_to([P, EP])).then_inc(keys_in, 16)
                sp.dma_start(col_i[x][:], a[f"col_{x}"]).then_inc(keys_in, 16)
            sp.dma_start(attr[:], a["attr"]).then_inc(rec_in, 16)
            sp.dma_start(edge_w[:], a["edge_w"]).then_inc(rec_in, 16)
            sp.wait_ge(tails_made, 1)
            sp.dma_start(k.rec_s[EP:EP + 1, :], no_slot[0:1, 0:REC_S]).then_inc(stored, 16)
            sp.dma_start(k.rec_d[EP:EP + 1, :], no_slot[0:1, 0:REC_D]).then_inc(stored, 16)
            for x in "sd":
                sp.dma_start(k.slots[x].rearrange("(p n) o -> p (n o)", p=P), no_slot[:]).then_inc(stored, 16)
            sp.wait_ge(stored, 16 * 4)

        @block.gpsimd
        def _(pool):
            pool.memset(tri[:], 0.5).then_inc(tri_made, 1)
            pool.wait_ge(tri_made, 1)
            pool.affine_select(out=tri[:], in_=tri[:], compare_op=ALU.is_gt, fill=0.0, base=0,
                               pattern=[[1, P]], channel_multiplier=-1).then_inc(tri_made, 1)
            pool.memset(no_slot[:], NO_SLOT).then_inc(tails_made, 1)
            pool.memset(k.ident[:], 0.0).then_inc(tri_made, 1)
            pool.wait_ge(tri_made, 3)
            pool.affine_select(out=k.ident[:], in_=k.ident[:], compare_op=ALU.not_equal, fill=1.0,
                               base=0, pattern=[[-1, P]], channel_multiplier=1).then_inc(tri_made, 1)
            r = Steps(pool, rec_made)
            r(pool.memset(rec["s"][:, :, 2 + HEADS:REC_S], 0))
            r(pool.memset(rec["d"][:, :, 3:REC_D], 0))
            pool.wait_ge(keys_in, 64)
            pool.wait_ge(rec_in, 32)
            for x in "sd":
                r(pool.tensor_copy(rec[x][:, :, 0], col_i["s"][:]))
                r(pool.tensor_copy(rec[x][:, :, 1], col_i["d"][:]))
            r(pool.tensor_copy(rec["s"][:, :, 2:2 + HEADS].bitcast(F32), attr[:]))
            r(pool.tensor_copy(rec["d"][:, :, 2].bitcast(F32), edge_w[:]))
            r.settle()
            for n, (x, out) in enumerate((("s", k.rec_s), ("d", k.rec_d))):
                pool.wait_ge(rank_made, n + 1)
                for t in range(ET):
                    pool.indirect_dma_start(out[:, :], bass.IndirectOffsetOnAxis(ap=rank[x][:, t:t + 1], axis=0),
                                            rec[x][:, t, :], None, bounds_check=EP - 1,
                                            oob_is_err=False).then_inc(scattered, 16)
            pool.wait_ge(scattered, 2 * ET * 16)

        def mask_pieces(j):
            return (0, j * P), (j * P + P, EP), (j * P, j * P + P)

        @block.vector
        def _(v):
            s = Steps(v, dve)
            s(v.memset(ones[:], 1.0))
            s(v.memset(one[:], 1.0))
            v.wait_ge(keys_in, 64)
            for x in "sd":
                s(v.tensor_copy(row[x][:], raw[x][:]))
                s(v.tensor_copy(col[x][:], col_i[x][:]))
            s.settle()
            s(v.tensor_scalar(lower[:], col["d"][:], -1.0, -0.5, ALU.mult, ALU.add))
            s(v.tensor_scalar(upper[:], col["d"][:], -1.0, 0.5, ALU.mult, ALU.add))
            s(v.tensor_scalar(middle[:], col["d"][:], -1.0, -0.25, ALU.mult, ALU.add))
            v.wait_ge(tri_made, 2)
            for x in "ds":
                s(v.tensor_tensor(diag[x][:], row[x][:].rearrange("p (t n) -> p t n", n=P),
                                  tri[:].unsqueeze(1).broadcast_to([P, ET, P]), ALU.add))
            s.settle()
            assert s.n == 11
            for j in range(ET):
                key = col["s"][:, j:j + 1]
                before, after, own = mask_pieces(j)
                if j >= 4:
                    v.wait_ge(mask_used["s"], j - 3)
                if before[1]:
                    v.tensor_scalar(mask["s"][:, j % 4, before[0]:before[1]], row["s"][:, before[0]:before[1]],
                                    key, None, ALU.is_gt)
                if after[0] < EP:
                    v.tensor_scalar(mask["s"][:, j % 4, after[0]:after[1]], row["s"][:, after[0]:after[1]],
                                    key, None, ALU.is_ge)
                v.tensor_scalar(mask["s"][:, j % 4, own[0]:own[1]], diag["s"][:, j, :], key, None,
                                ALU.is_gt).then_inc(mask_made["s"], 1)
            v.wait_ge(mask_used["s"], ET)
            for n in range(EP // D):
                v.tensor_copy(rank_row["s"][:, n * D:n * D + D], counts[n][0:1, :]).then_inc(row_made, 1)
            v.wait_ge(cols_made, 1)
            v.tensor_copy(rank["s"][:], rank_cols[:, 0:ET]).then_inc(rank_made, 1)
            v.wait_ge(mask_used["d"], ET)
            for n in range(EP // D):
                v.tensor_scalar(rank_row["d"][:, n * D:n * D + D], counts[n][0:1, :], 0.5, EP / 2,
                                ALU.mult, ALU.add).then_inc(row_made, 1)
            v.wait_ge(cols_made, 2)
            v.tensor_copy(rank["d"][:], rank_cols[:, 0:ET]).then_inc(rank_made, 1)
            v.wait_ge(rank_made, 2)

        @block.scalar
        def _(act_):
            act_.wait_ge(dve, 11)
            for j in range(ET):
                before, after, own = mask_pieces(j)
                if j >= 4:
                    act_.wait_ge(mask_used["d"], j - 3)
                if before[1]:
                    act_.activation(mask["d"][:, j % 4, before[0]:before[1]], row["d"][:, before[0]:before[1]],
                                    ACT.Sign, bias=lower[:, j:j + 1])
                if after[0] < EP:
                    act_.activation(mask["d"][:, j % 4, after[0]:after[1]], row["d"][:, after[0]:after[1]],
                                    ACT.Sign, bias=upper[:, j:j + 1])
                act_.activation(mask["d"][:, j % 4, own[0]:own[1]], diag["d"][:, j, :], ACT.Sign,
                                bias=middle[:, j:j + 1]).then_inc(mask_made["d"], 1)

        @block.tensor
        def _(pe):
            pe.wait_ge(dve, 2)
            for n, x in enumerate("sd"):
                if n:
                    pe.wait_ge(row_made, 5)
                for j in range(ET):
                    pe.wait_ge(mask_made[x], j + 1)
                    for m in range(EP // D):
                        last = pe.matmul(counts[m][0:1, :], ones[:], mask[x][:, j % 4, m * D:m * D + D],
                                         start=j == 0, stop=j == ET - 1)
                    last.then_inc(mask_used[x], 1)
                pe.wait_ge(row_made, 5 * (n + 1))
                if n:
                    pe.wait_ge(rank_made, 1)
                for t in range(ET):
                    last = pe.matmul(rank_cols[:, t:t + 1], rank_row[x][:, t * P:t * P + P], one[:],
                                     start=True, stop=True)
                last.then_inc(cols_made, 1)



def edge_columns(v, s, k, x, rec_cols, next_key, places, slot_at):
    key = rec_cols
    s.link(v.tensor_tensor(places[:, 0:ET], key, next_key, ALU.is_equal))
    s(v.tensor_scalar(places[:, ET:2 * ET], key, 7, None, ALU.logical_shift_right))
    s.link(v.tensor_scalar(places[:, 2 * ET:3 * ET], key, 127, None, ALU.bitwise_and))
    s.link(v.tensor_scalar(places[:, 2 * ET:3 * ET], places[:, 2 * ET:3 * ET], NT, None, ALU.mult))
    s.link(v.tensor_tensor(places[:, ET:2 * ET], places[:, ET:2 * ET], places[:, 2 * ET:3 * ET], ALU.add))
    s.link(v.tensor_scalar(places[:, 0:ET], places[:, 0:ET], NO_SLOT, None, ALU.mult))
    s.link(v.tensor_tensor(slot_at, places[:, ET:2 * ET], places[:, 0:ET], ALU.add))


def attention_phase(nc, a, k):
    with ExitStack() as stack:
        c = Core(nc, stack, "att")
        same, rec = k.same, k.rec
        hi = {n: c.sb(f"{n}_hi", [P, KC, D], F32R) for n in ("wq", "wk", "wv", "w12")}
        lo = {n: c.sb(f"{n}_lo", [P, KC, D], F32R) for n in ("wq", "wk", "wv", "w12")}
        ln_g, ln_b = c.sb("ln_g", [P, KC]), c.sb("ln_b", [P, KC])
        bias_in = c.sb("bias_in", [P, 3, KC])
        bias = c.sb("bias", [P, 3, KC])
        headsel = c.sb("headsel", [P, KC, HEADS])
        headsel2 = c.sb("headsel2", [HEADS, D])
        flags_ready = c.sem("flags_ready")

        recs_in, made, chain = c.sem("recs_in"), c.sem("made"), c.sem("chain")
        keyt, keyc = c.sem("keyt"), c.sem("keyc")
        stage_in = [c.sem(f"stage_in{n}") for n in range(2)]
        stage_free, hi_made, prep = c.sem("stage_free"), c.sem("hi_made"), c.sem("prep")
        small_in, w12_done, b12_done, bias_done = (c.sem(n) for n in ("small_in", "w12_done", "b12_done", "bias_done"))
        slots_out = c.sem("slots_out")
        w_scaled = c.sem("w_scaled")
        split_done = c.sem("split_done")
        slots_in = c.sem("slots_in")

        with ExitStack() as inner:
            ci = Core(nc, inner, "prep")
            stage = [ci.sb(f"stage{n}", [P, KC, D]) for n in range(2)]
            next_key = {x: ci.sb(f"next_key_{x}", [P, ET], I32) for x in "sd"}
            places = ci.sb("places", [P, 3 * ET], I32)
            slot_at = {x: ci.sb(f"slot_at_{x}", [P, ET], I32) for x in "sd"}
            own_place = ci.sb("own_place", [P, ET], I32)
            key_f = ci.sb("key_f", [P, ET])
            key_diag = ci.sb("key_diag", [P, 2, P])
            key_row = ci.sb("key_row", [P, 2, GR + 1])
            b1_col = ci.sb("b1_col", [P, KC])
            b1_wide = ci.sb("b1_wide", [P, KC, P])
            b2_row = ci.sb("b2_row", [1, D])
            ones_row = ci.sb("ones_row", [1, P])
            w1t = ci.sb("w1t", [P, KC, D])
            w2 = ci.sb("w2", [P, KC, D])
            w12 = ci.sb("w12", [P, KC, D])
            pk = [ci.ps(f"pk{n}") for n in range(2)]
            pb = ci.ps("pb")
            pw = [ci.ps(f"pw{n}") for n in range(2)]
            names = ("wq", "wk", "wv")
            w1_in = ci.sem("w1_in")
            rows_made = ci.sem("rows_made")
            block = inner.enter_context(nc.Block())

            @block.sync
            def _(sp):
                for x, t, w in (("s", k.rec_s, REC_S), ("d", k.rec_d, REC_D)):
                    sp.dma_start(rec[x][:], t[0:EP, :].rearrange("(t p) w -> p t w", p=P)).then_inc(recs_in, 16)
                    kk = 0 if x == "s" else 1
                    with nc.allow_non_contiguous_dma(reason="one word of each record"):
                        sp.dma_start(next_key[x][:], t[1:EP + 1, kk:kk + 1].rearrange("(t p) w -> p (t w)", p=P))\
                          .then_inc(recs_in, 16)
                for t, s in ((ln_g, "ln_g"), (ln_b, "ln_b"), (b1_col, "b1_col"), (b2_row, "b2_row")):
                    sp.dma_start(t[:], a[s]).then_inc(small_in, 16)
                for n, s in enumerate(("bq", "bk", "bv")):
                    sp.dma_start(bias_in[:, n, :], a[s]).then_inc(small_in, 16)
                sp.dma_start(w1t[:], a["w1t"].rearrange("(c p) n -> p c n", p=P)).then_inc(w1_in, 16)
                sp.dma_start(w2[:], a["w2"].rearrange("(c p) n -> p c n", p=P)).then_inc(w1_in, 16)
                for n, name in enumerate(names):
                    if n >= 2:
                        sp.wait_ge(split_done, n - 1)
                    sp.dma_start(stage[n % 2][:], a[name].rearrange("(c p) n -> p c n", p=P)).then_inc(stage_in[n % 2], 16)
                sp.wait_ge(slots_out, 2 * ET * 16)
                for x in "sd":
                    sp.dma_start(k.slot[x][:], k.slots[x].rearrange("(p n) o -> p (n o)", p=P)).then_inc(slots_in, 16)
                sp.wait_ge(slots_in, 32)

            @block.gpsimd
            def _(pool):
                s = Steps(pool, made)
                s(pool.iota(own_place[:], pattern=[[P, ET]], base=0, channel_multiplier=1))
                s(pool.memset(headsel[:], HD ** -0.5))
                s(pool.memset(headsel2[:], 1.0))
                s(pool.memset(ones_row[:], 1.0))
                s(pool.memset(k.zeros[:], 0.0))
                s(pool.memset(k.ones[:], 1.0))
                s(pool.memset(k.half_neg[:], -0.5))
                s.settle()
                s.link(pool.affine_select(out=headsel[:], in_=headsel[:], compare_op=ALU.is_ge, fill=0.0, base=0,
                                          pattern=[[P, KC], [-HD, HEADS]], channel_multiplier=1))
                s.link(pool.affine_select(out=headsel[:], in_=headsel[:], compare_op=ALU.is_ge, fill=0.0, base=HD - 1,
                                          pattern=[[-P, KC], [HD, HEADS]], channel_multiplier=-1))
                s.link(pool.affine_select(out=headsel2[:], in_=headsel2[:], compare_op=ALU.is_ge, fill=0.0, base=0,
                                          pattern=[[1, D]], channel_multiplier=-HD))
                s.link(pool.affine_select(out=headsel2[:], in_=headsel2[:], compare_op=ALU.is_ge, fill=0.0,
                                          base=HD - 1, pattern=[[-1, D]], channel_multiplier=HD))
                for n, x in enumerate("sd"):
                    pool.wait_ge(chain, 7 * (n + 1))
                    for t in range(ET):
                        pool.indirect_dma_start(k.slots[x][:, :],
                                                bass.IndirectOffsetOnAxis(ap=slot_at[x][:, t:t + 1], axis=0),
                                                own_place[:, t:t + 1], None, bounds_check=NPAD - 1,
                                                oob_is_err=False).then_inc(slots_out, 16)

            @block.vector
            def _(v):
                s = Steps(v, chain)
                v.wait_ge(recs_in, 64)
                for n, x in enumerate("sd"):
                    edge_columns(v, s, k, x, rec[x][:, :, n], next_key[x][:], places, slot_at[x][:])
                v.wait_ge(small_in, 7 * 16)
                for kc in range(KC):
                    s(v.tensor_copy(b1_wide[:, kc, :], b1_col[:, kc:kc + 1].broadcast_to([P, P])))
                s.settle()
                assert s.n == 18
                q = Steps(v, rows_made)
                for n, x in enumerate("sd"):
                    q.link(v.tensor_copy(key_f[:], rec[x][:, :, n]))
                    q.link(v.memset(key_row[:, 1, GR:GR + 1], -1.0))
                    for g in range(EG):
                        for t in range(T):
                            i = (n * EG + g) * T + t
                            if i >= 2:
                                v.wait_ge(keyt, i - 1)
                            v.tensor_scalar(key_diag[:, i % 2, :], k.ident[:], key_f[:, g * T + t:g * T + t + 1], None,
                                            ALU.mult).then_inc(keyc, 1)
                        v.wait_ge(keyt, (n * EG + g + 1) * T)
                        q(v.tensor_copy(key_row[:, g % 2, 0:1], key_row[:, (g + 1) % 2, GR:GR + 1]))
                        q.link(v.tensor_copy(key_row[:, g % 2, 1:GR + 1], pk[g % 2][:]))
                        q.link(v.tensor_tensor(same[x][:, g * GR:g * GR + GR], key_row[:, g % 2, 1:GR + 1],
                                               key_row[:, g % 2, 0:GR], ALU.is_equal))
                    q.link(v.memset(same[x][:, EP:EP + 1], 0.0))
                for n in range(3):
                    v.wait_ge(stage_in[n % 2], 16 * (n // 2 + 1))
                    v.wait_ge(bias_done, n + 1)
                    for kc in range(KC):
                        ins = v.tensor_scalar(stage[n % 2][:, kc, :], stage[n % 2][:, kc, :], ln_g[:, kc:kc + 1], None,
                                              ALU.mult)
                    ins.then_inc(w_scaled, 1)
                    v.wait_ge(hi_made, n + 1)
                    v.tensor_tensor(lo[names[n]][:], stage[n % 2][:], hi[names[n]][:].bitcast(F32), ALU.subtract)\
                     .then_inc(split_done, 1)
                v.wait_ge(bias_done, 3)
                q.link(v.tensor_tensor(bias[:], bias_in[:], pb[:, 0:3 * KC].rearrange("p (n c) -> p n c", n=3), ALU.add))
                for c4 in range(KC):
                    v.wait_ge(w12_done, c4 + 1)
                    v.tensor_copy(w12[:, c4, :], pw[c4 % 2][:]).then_inc(w_scaled, 1)
                v.wait_ge(hi_made, 4)
                v.tensor_tensor(lo["w12"][:], w12[:], hi["w12"][:].bitcast(F32), ALU.subtract).then_inc(split_done, 1)
                v.wait_ge(b12_done, 1)
                v.tensor_copy(k.b12[:], pw[0][:]).then_inc(split_done, 1)
                v.wait_ge(split_done, 5)

            @block.scalar
            def _(act_):
                act_.wait_ge(small_in, 7 * 16)
                for n in range(3):
                    act_.wait_ge(w_scaled, n + 1)
                    act_.activation(hi[names[n]][:], stage[n % 2][:], ACT.Copy).then_inc(hi_made, 1)
                act_.wait_ge(w_scaled, 7)
                act_.activation(hi["w12"][:], w12[:], ACT.Copy).then_inc(hi_made, 1)

            @block.tensor
            def _(pe):
                pe.wait_ge(made, 7)
                for i in range(2 * ET):
                    g = i // T
                    if g >= 2 and i % T == 0:
                        n, gg = divmod(g, EG)
                        pe.wait_ge(rows_made, n * (3 + 3 * EG) + 2 + 3 * gg - 3 if gg else 3 + 3 * EG)
                    pe.wait_ge(keyc, i + 1)
                    pe.matmul(pk[(g % EG) % 2][:, (i % T) * P:(i % T) * P + P], k.ones[:], key_diag[:, i % 2, :],
                              start=True, stop=True).then_inc(keyt, 1)
                for n in range(3):
                    pe.wait_ge(stage_in[n % 2], 16 * (n // 2 + 1))
                    for dc in range(KC):
                        for kc in range(KC):
                            last = pe.matmul(pb[:, n * KC + dc:n * KC + dc + 1], stage[n % 2][:, kc, dc * P:dc * P + P],
                                             ln_b[:, kc:kc + 1], start=kc == 0, stop=kc == KC - 1)
                    last.then_inc(bias_done, 1)
                pe.wait_ge(w1_in, 32)
                for ic in range(KC):
                    if ic >= 2:
                        pe.wait_ge(w_scaled, 3 + ic - 1)
                    for kc in range(KC):
                        last = pe.matmul(pw[ic % 2][:], w1t[:, kc, ic * P:ic * P + P], w2[:, kc, :],
                                         start=kc == 0, stop=kc == KC - 1)
                    last.then_inc(w12_done, 1)
                pe.wait_ge(w_scaled, 6)
                for kc in range(KC):
                    pe.matmul(pw[0][:], b1_wide[:, kc, :], w2[:, kc, :], start=kc == 0, stop=False)
                pe.matmul(pw[0][:], ones_row[:], b2_row[:], start=False, stop=True).then_inc(b12_done, 1)

        qkv_and_softmax(nc, a, k, stack, c, hi, lo, bias, headsel, headsel2)


def qkv_and_softmax(nc, a, k, outer, co, hi, lo, bias, headsel, headsel2):
    with ExitStack() as stack:
        c = Core(nc, stack, "edge")
        scores = c.sb("scores", [HEADS, EP])
        value = c.sb("value", [P, KC, EP + 1])
        with ExitStack() as inner:
            project_edges(nc, a, k, inner, hi, lo, bias, headsel, scores, value)
        with ExitStack() as inner:
            aggregate_values(nc, a, k, inner, hi, lo, headsel2, scores, value)


def project_edges(nc, a, k, stack, hi, lo, bias, headsel, scores, value):
    c = Core(nc, stack, "qkv")
    rows = {x: c.sb(f"rows_{x}", [P, T, D]) for x in "sd"}
    at = {x: c.sb(f"at_{x}", [P, T], I32) for x in "sd"}
    st = {x: c.sb(f"st_{x}", [P, T, 6]) for x in "sd"}
    mv = {x: c.sb(f"mv_{x}", [P, T, 2]) for x in "sd"}
    ve = {x: c.sb(f"ve_{x}", [P, T]) for x in "sd"}
    r1 = {x: c.sb(f"r1_{x}", [P, T]) for x in "sd"}
    r2 = {x: c.sb(f"r2_{x}", [P, T]) for x in "sd"}
    shift = {x: c.sb(f"shift_{x}", [P, T]) for x in "sd"}
    xh = {x: c.sb(f"xh_{x}", [P, KC, GR], F32R) for x in "sd"}
    xl = {x: c.sb(f"xl_{x}", [P, KC, GR], F32R) for x in "sd"}
    qs = c.sb("qs", [P, KC, GR])
    prod = c.sb("prod", [P, 2, GR])
    attr = c.sb("attr", [P, T, 8])
    attr_t = c.sb("attr_t", [P, GR])
    pp = [c.ps(f"pp{n}") for n in range(2)]
    tr = [c.ps(f"tr{n}") for n in range(2)]
    p_score, p_attr = c.ps("p_score"), c.ps("p_attr")
    at_made, attr_made = c.sem("at_made"), c.sem("attr_made")
    rows_in = {x: [c.sem(f"rows_in_{x}{t}") for t in range(T)] for x in "sd"}
    stats = {x: c.sem(f"stats_{x}") for x in "sd"}
    pow_done = {x: c.sem(f"pow_done_{x}") for x in "sd"}
    normed = {x: c.sem(f"normed_{x}") for x in "sd"}
    turned = {x: c.sem(f"turned_{x}") for x in "sd"}
    hi_made = {x: c.sem(f"hi_made_{x}") for x in "sd"}
    lo_made = {x: c.sem(f"lo_made_{x}") for x in "sd"}
    q_done, k_done, v_done, q_out, k_out, v_out = (c.sem(n) for n in ("q_done", "k_done", "v_done", "q_out", "k_out", "v_out"))
    score_done, score_out, attr_turned, attr_out = (c.sem(n) for n in ("score_done", "score_out", "attr_turned", "attr_out"))
    value0 = c.sem("value0")
    block = stack.enter_context(nc.Block())
    NST = 9

    def gather(pool, g):
        for n, x in enumerate("sd"):
            pool.wait_ge(turned[x], 4 * g + 4)
            hold(pool)
            pool.tensor_copy(at[x][:], k.rec["s"][:, ds(4 * g, T), n]).then_inc(at_made, 1)
            pool.wait_ge(at_made, 3 * g + n + 1)
            hold(pool)
            for t in range(T):
                pool.indirect_dma_start(rows[x][:, t, :], None, a["x"][:, :],
                                        bass.IndirectOffsetOnAxis(ap=at[x][:, t:t + 1], axis=0),
                                        bounds_check=NPAD - 1, oob_is_err=False).then_inc(rows_in[x][t], 16)
        pool.wait_ge(attr_turned, g + 1)
        hold(pool)
        pool.tensor_copy(attr[:], k.rec["s"][:, ds(4 * g, T), 2:10].bitcast(F32)).then_inc(at_made, 1)

    def powers(pool, g):
        for x in "sd":
            for n, r in enumerate((r1, r2)):
                pool.wait_ge(stats[x], NST * g + (4 if n == 0 else 7))
                pool.tensor_tensor(r[x][:], ve[x][:], k.half_neg[:, 0:T], ALU.pow).then_inc(pow_done[x], 1)

    @block.gpsimd
    def _(pool):
        gather(pool, 0)
        powers(pool, 0)
        with pool.Fori(0, EG - 1) as g:
            gather(pool, g + 1)
            powers(pool, g + 1)

    def statistics(v, g, x):
        s = Steps(v, stats[x], NST * g)
        for t in range(T):
            v.wait_ge(rows_in[x][t], 16 * g + 16)
            hold(v)
            ins = v.bn_stats(st[x][:, t, :], rows[x][:, t, :])
            if t == T - 1:
                s.link(ins)
        for t in range(T):
            if t == 0:
                hold(v)
            ins = v.bn_aggr(mv[x][:, t, :], st[x][:, t, :])
            if t == T - 1:
                s.link(ins)
        var, mean = mv[x][:, :, 1], mv[x][:, :, 0]
        s(v.tensor_scalar(shift[x][:], mean, -1.0, None, ALU.mult))
        s(v.tensor_scalar(ve[x][:], var, 1e-5, None, ALU.add))
        v.wait_ge(pow_done[x], 2 * g + 1)
        s.link(v.tensor_tensor(ve[x][:], var, r1[x][:], ALU.mult))
        s.link(v.tensor_tensor(ve[x][:], ve[x][:], r1[x][:], ALU.mult))
        s(v.tensor_scalar(ve[x][:], ve[x][:], 1e-5, None, ALU.add))
        v.wait_ge(pow_done[x], 2 * g + 2)
        s.link(v.tensor_tensor(r2[x][:], r1[x][:], r2[x][:], ALU.mult))
        s(v.tensor_tensor(shift[x][:], shift[x][:], r2[x][:], ALU.mult))
        assert s.n == NST

    def split_lo(v, g, x, t, turn):
        v.wait_ge(hi_made[x], 4 * g + t + 1)
        v.tensor_tensor(xl[x][:, :, t * P:t * P + P], tr[turn][:].rearrange("p (c n) -> p c n", n=P),
                        xh[x][:, :, t * P:t * P + P].bitcast(F32), ALU.subtract).then_inc(lo_made[x], 1)

    @block.vector
    def _(v):
        v.sem_inc(k_out, 1)
        v.sem_inc(score_out, 1)
        v.memset(value[:, :, 0:1], 0.0).then_inc(value0, 1)
        statistics(v, 0, "s")
        statistics(v, 0, "d")
        for t in range(T):
            split_lo(v, 0, "s", t, t % 2)

        def body(g, last):
            for t in range(T):
                split_lo(v, g, "d", t, t % 2)
            for cc in range(KC):
                v.wait_ge(k_done, 4 * g + cc + 1)
                v.wait_ge(q_out, 4 * g + cc + 1)
                v.wait_ge(score_done, 4 * g + cc + 1)
                v.scalar_tensor_tensor(prod[:, cc % 2, :], pp[cc % 2][:], bias[:, 1, cc:cc + 1], qs[:, cc, :],
                                       ALU.add, ALU.mult).then_inc(k_out, 1)
            if not last:
                statistics(v, g + 1, "s")
            v.wait_ge(attr_out, g + 1)
            v.wait_ge(score_done, 4 * g + 4 + 2)
            v.tensor_tensor(scores[:, ds(g * GR, GR)], p_score[0:HEADS, :], attr_t[0:HEADS, :], ALU.mult)\
             .then_inc(score_out, 1)
            if not last:
                for t in range(T):
                    split_lo(v, g + 1, "s", t, t % 2)
                statistics(v, g + 1, "d")

        with v.Fori(0, EG - 1) as g:
            body(g, False)
        body(EG - 1, True)
        v.wait_ge(score_out, EG + 1)

    def norm(act_, g, x, t):
        if t == 0:
            act_.wait_ge(stats[x], NST * g + NST)
        act_.activation(rows[x][:, t, :], rows[x][:, t, :], ACT.Identity, bias=shift[x][:, t:t + 1],
                        scale=r2[x][:, t:t + 1]).then_inc(normed[x], 1)

    def split_hi(act_, g, x, t, turn):
        act_.wait_ge(turned[x], 4 * g + t + 1 + 4)
        act_.activation(xh[x][:, :, t * P:t * P + P], tr[turn][:].rearrange("p (c n) -> p c n", n=P),
                        ACT.Copy).then_inc(hi_made[x], 1)

    @block.scalar
    def _(act_):
        act_.sem_inc(v_out, 4)
        for x in "sd":
            for t in range(T):
                norm(act_, 0, x, t)
        for t in range(T):
            split_hi(act_, 0, "s", t, t % 2)

        def body(g, last):
            for cc in range(KC):
                act_.wait_ge(q_done, 4 * g + cc + 1)
                if cc == 0:
                    act_.wait_ge(k_out, 4 * g + 1)
                act_.activation(qs[:, cc, :], pp[cc % 2][:], ACT.Identity, bias=bias[:, 0, cc:cc + 1])\
                    .then_inc(q_out, 1)
                split_hi(act_, g, "d", cc, cc % 2)
            act_.wait_ge(attr_turned, g + 2)
            act_.wait_ge(score_out, g + 1)
            act_.activation(attr_t[0:HEADS, :], p_attr[0:HEADS, :], ACT.Copy).then_inc(attr_out, 1)
            if not last:
                for t in range(T):
                    norm(act_, g + 1, "s", t)
            for cc in range(KC):
                if not last:
                    split_hi(act_, g + 1, "s", cc, cc % 2)
                act_.wait_ge(v_done, 4 * g + cc + 1)
                act_.activation(value[:, cc, ds(g * GR + 1, GR)], pp[cc % 2][:], ACT.Identity,
                                bias=bias[:, 2, cc:cc + 1]).then_inc(v_out, 1)
            if not last:
                for t in range(T):
                    norm(act_, g + 1, "d", t)

        with act_.Fori(0, EG - 1) as g:
            body(g, False)
        body(EG - 1, True)

    def turn(pe, g, x, t):
        pe.wait_ge(normed[x], 4 * g + t + 1)
        for kc in range(KC):
            last = pe.transpose(tr[t % 2][:, kc * P:kc * P + P], rows[x][:, t, kc * P:kc * P + P], k.ident[:])
        last.then_inc(turned[x], 1)

    def project(pe, x, name, cc):
        for kc in range(KC):
            w = [z[name][:, kc, cc * P:cc * P + P] for z in (hi, lo)]
            last = split3(pe, pp[cc % 2][:], w, (xh[x][:, kc, :], xl[x][:, kc, :]), kc == 0, kc == KC - 1)
        return last

    @block.tensor
    def _(pe):
        pe.sem_inc(attr_turned, 1)
        pe.sem_inc(score_done, 2)
        pe.sem_inc(turned["s"], 4)
        pe.sem_inc(turned["d"], 4)
        for t in range(T):
            if t >= 2:
                pe.wait_ge(lo_made["s"], t - 1)
            turn(pe, 0, "s", t)

        def body(g, last_group):
            pe.wait_ge(lo_made["s"], 4 * g + 4)
            for cc in range(KC):
                if cc >= 2:
                    pe.wait_ge(q_out, 4 * g + cc - 1)
                else:
                    pe.wait_ge(v_out, 4 * g + cc + 1 + 2)
                project(pe, "s", "wq", cc).then_inc(q_done, 1)
                if cc >= 2:
                    pe.wait_ge(lo_made["d"], 4 * g + cc - 1)
                turn(pe, g, "d", cc)
            pe.wait_ge(lo_made["d"], 4 * g + 4)
            for cc in range(KC):
                if cc >= 2:
                    pe.wait_ge(k_out, 4 * g + cc - 1 + 1)
                else:
                    pe.wait_ge(q_out, 4 * g + cc + 3)
                project(pe, "d", "wk", cc).then_inc(k_done, 1)
                if cc == 0:
                    pe.wait_ge(score_out, g + 1)
                if cc >= 1:
                    score(pe, g, cc - 1)
            pe.wait_ge(at_made, 3 * g + 3)
            for t in range(T):
                last = pe.matmul(p_attr[0:HEADS, t * P:t * P + P], attr[:, t, :], k.ident[:], start=True, stop=True)
            last.then_inc(attr_turned, 1)
            for cc in range(KC):
                if cc == 1:
                    score(pe, g, KC - 1)
                if not last_group:
                    if cc >= 2:
                        pe.wait_ge(lo_made["s"], 4 * g + 4 + cc - 1)
                    turn(pe, g + 1, "s", cc)
                if cc < 2:
                    pe.wait_ge(k_out, 4 * g + cc + 4)
                else:
                    pe.wait_ge(v_out, 4 * g + cc + 3)
                project(pe, "d", "wv", cc).then_inc(v_done, 1)

        def score(pe, g, cc):
            pe.wait_ge(k_out, 4 * g + cc + 1 + 1)
            pe.matmul(p_score[0:HEADS, :], headsel[:, cc, :], prod[:, cc % 2, :], start=cc == 0,
                      stop=cc == KC - 1, skip_group_check=True).then_inc(score_done, 1)

        with pe.Fori(0, EG - 1) as g:
            body(g, False)
        body(EG - 1, True)



def aggregate_values(nc, a, k, stack, hi, lo, headsel2, scores, value):
    c = Core(nc, stack, "agg")
    pen = c.sb("pen", [HEADS, EP + 1])
    best = c.sb("best", [HEADS, EP])
    expo = c.sb("expo", [HEADS, EP])
    ah, al = c.sb("ah", [P, KC, GR], F32R), c.sb("al", [P, KC, GR], F32R)
    out = c.sb("out", [P, 2, D])
    pa = [c.ps(f"pa{n}") for n in range(KC)]
    po = [c.ps(f"po{n}") for n in range(2)]
    chain, exp_done, att_ready = c.sem("chain"), c.sem("exp_done"), c.sem("att_ready")
    spread, weighted, summed, hi_made, lo_made = (c.sem(n) for n in ("spread", "weighted", "summed", "hi_made", "lo_made"))
    row_done, row_out = c.sem("row_done"), c.sem("row_out")
    stored = [c.sem(f"stored{n}") for n in range(2)]
    same = k.same["s"]
    block = stack.enter_context(nc.Block())

    @block.vector
    def _(v):
        v.sem_inc(weighted, KC)
        s = Steps(v, chain)
        s.link(v.tensor_scalar(pen[:], same[0:HEADS, :], -1.0, 1e30, ALU.add, ALU.mult))
        s.link(v.tensor_tensor_scan(best[:], pen[:, 0:EP], scores[:], 0.0, ALU.add, ALU.max))
        s.link(v.tensor_tensor_scan(best[:, ::-1], pen[:, EP:0:-1], best[:, ::-1], -1e30, ALU.add, ALU.max))
        s(v.tensor_tensor(scores[:], scores[:], best[:], ALU.subtract))
        v.wait_ge(exp_done, 1)
        s.link(v.tensor_tensor_scan(best[:], same[0:HEADS, 0:EP], expo[:], 0.0, ALU.mult, ALU.add))
        s.link(v.tensor_tensor_scan(best[:, ::-1], same[0:HEADS, EP:0:-1], best[:, ::-1], 0.0, ALU.mult, ALU.max))
        s.link(v.tensor_scalar(best[:], best[:], 1e-16, None, ALU.add))
        s.link(v.reciprocal(best[:], best[:]))
        v.tensor_tensor(scores[:], expo[:], best[:], ALU.mult).then_inc(att_ready, 1)

        with v.Fori(0, EG) as g:
            for cc in range(KC):
                v.wait_ge(spread, 4 * g + cc + 1)
                cols = value[:, cc, ds(g * GR + 1, GR)]
                v.tensor_tensor(cols, cols, pa[cc][:], ALU.mult).then_inc(weighted, 1)
                v.wait_ge(weighted, 4 * g + cc + 1 + KC)
                v.tensor_tensor_scan(cols, same[:, ds(g * GR, GR)], cols, value[:, cc, ds(g * GR, 1)],
                                     ALU.mult, ALU.add).then_inc(summed, 1)
            for cc in range(KC):
                v.wait_ge(hi_made, 4 * g + cc + 1)
                v.tensor_tensor(al[:, cc, :], value[:, cc, ds(g * GR + 1, GR)], ah[:, cc, :].bitcast(F32),
                                ALU.subtract).then_inc(lo_made, 1)
            for t in range(T):
                v.wait_ge(row_done, 4 * g + t + 1)
                v.wait_ge(stored[t % 2], 32 * g + 16 * (t // 2) + 16)
                v.tensor_tensor(out[:, t % 2, :], po[t % 2][:], k.b12[:], ALU.add).then_inc(row_out, 1)

    @block.scalar
    def _(act_):
        act_.wait_ge(chain, 4)
        act_.activation(expo[:], scores[:], ACT.Exp).then_inc(exp_done, 1)
        with act_.Fori(0, EG) as g:
            for cc in range(KC):
                act_.wait_ge(summed, 4 * g + cc + 1)
                if cc == 0:
                    act_.wait_ge(row_out, 4 * g + 2)
                act_.activation(ah[:, cc, :], value[:, cc, ds(g * GR + 1, GR)], ACT.Copy).then_inc(hi_made, 1)

    @block.tensor
    def _(pe):
        pe.wait_ge(att_ready, 1)

        def spread_weights(g):
            for cc in range(KC):
                pe.wait_ge(weighted, 4 * g + cc + 1)
                hold(pe)
                pe.matmul(pa[cc][:], headsel2[:, cc * P:cc * P + P], scores[:, ds(g * GR, GR)], start=True,
                          stop=True).then_inc(spread, 1)

        with pe.Fori(0, EG) as g:
            spread_weights(g)
            for t in range(T):
                pe.wait_ge(row_out, 4 * g + t + 1)
                for cc in range(KC):
                    if t == 0:
                        pe.wait_ge(lo_made, 4 * g + cc + 1)
                    sl = slice(t * P, t * P + P)
                    last = split3(pe, po[t % 2][:], (ah[:, cc, sl], al[:, cc, sl]),
                                  (hi["w12"][:, cc, :], lo["w12"][:, cc, :]), cc == 0, cc == KC - 1)
                last.then_inc(row_done, 1)

    @block.sync
    def _(sp):
        for n in range(2):
            sp.sem_inc(stored[n], 16)
        sp.sem_inc(row_out, 2)
        with sp.Fori(0, EG) as g:
            for t in range(T):
                sp.wait_ge(row_out, 4 * g + t + 3)
                sp.dma_start(k.values[ds(g * GR + t * P, P), :], out[:, t % 2, :]).then_inc(stored[t % 2], 16)
        for n in range(2):
            sp.wait_ge(stored[n], 16 + 16 * ET // 2)



def split_weights(nc, k, jobs):
    with ExitStack() as stack:
        c = Core(nc, stack, f"split{nc.next_id()}")
        stage = [c.sb(f"stage{n}", [P, KC * D]) for n in range(2)]
        loaded = [c.sem(f"loaded{n}") for n in range(2)]
        hi_made, lo_made = c.sem("hi_made"), c.sem("lo_made")
        block = stack.enter_context(nc.Block())

        def view(n, like):
            return stage[n % 2][:, 0:like.shape[1] * like.shape[2]].rearrange("p (c n) -> p c n", c=like.shape[1])

        @block.sync
        def _(sp):
            for n, (source, hi, _) in enumerate(jobs):
                if n >= 2:
                    sp.wait_ge(lo_made, n - 1)
                sp.dma_start(view(n, hi), source).then_inc(loaded[n % 2], 16)

        @block.scalar
        def _(act_):
            for n, (_, hi, _) in enumerate(jobs):
                act_.wait_ge(loaded[n % 2], 16 * (n // 2 + 1))
                act_.activation(hi[:], view(n, hi), ACT.Copy).then_inc(hi_made, 1)

        @block.vector
        def _(v):
            for n, (_, hi, lo) in enumerate(jobs):
                v.wait_ge(hi_made, n + 1)
                v.tensor_tensor(lo[:], view(n, hi), hi[:].bitcast(F32), ALU.subtract).then_inc(lo_made, 1)
            v.wait_ge(lo_made, len(jobs))


def chunks(source):
    return source.rearrange("(c p) n -> p c n", p=P)



def dense0_phase(nc, a, k):
    with ExitStack() as stack:
        c = Core(nc, stack, "d0")
        w = {n: [c.sb(f"{n}_{h}", [P, KC, D], F32R) for h in ("hi", "lo")] for n in ("w1", "w3", "w2")}
        wr = [c.sb(f"wr_{h}", [P, KC, P], F32R) for h in ("hi", "lo")]
        split_weights(nc, k, [(chunks(a["e_w1"]), *w["w1"]), (chunks(a["e_w3"]), *w["w3"]),
                              (chunks(a["e_w2"]), *w["w2"]), (chunks(a["e_wr"]), wr[0][:, :, 0:SETS * 4], wr[1][:, :, 0:SETS * 4])])
        x = [c.sb(f"x{n}", [P, T, D]) for n in range(XS)]
        val = c.sb("val", [P, T, D])
        at = c.sb("at", [P, T], I32)
        xf = c.sb("xf", [P, T, D])
        xh, xl = ([c.sb(f"{n}{i}", [P, KC, GR], F32R) for i in range(2)] for n in ("xh", "xl"))
        logit_t = c.sb("logit_t", [SETS * 4, GR])
        act_out = c.sb("act_out", [P, 2, GR])
        hh, hl = (c.sb(n, [P, KC, GR], F32R) for n in ("hh", "hl"))
        y = c.sb("y", [P, 2, D])
        st = [c.sb(f"st{n}", [P, T, 6]) for n in range(3)]
        mv = [c.sb(f"mv{n}", [P, T, 2]) for n in range(3)]
        ve = [c.sb(f"ve{n}", [P, T]) for n in range(3)]
        rs = [c.sb(f"rs{n}", [P, T]) for n in range(3)]
        shift = [c.sb(f"shift{n}", [P, T]) for n in range(3)]
        gain = c.sb("gain", [P, T])
        rbias = c.sb("rbias", [P, SETS * 4])
        before = c.sb("before", [P, 4, 4])
        expert = c.sb("expert", [2 * EXPERTS0, D])
        expert2 = c.sb("expert2", [2 * EXPERTS0, D])
        expert_r = c.sb("expert_r", [2 * EXPERTS0, D], F32R)
        NS = T * SETS
        prob, one_hot, second, rank = (c.sb(n, [P, NS, 4]) for n in ("prob", "one_hot", "second", "rank"))
        total = c.sb("total", [P, NS])
        wins, ties = (c.sb(n, [P, NS, 4, 4]) for n in ("wins", "ties"))
        mix = c.sb("mix", [P, T, EXPERTS0])
        parts = c.sb("parts", [P, T, P], F32R)
        mix_t = c.sb("mix_t", [2 * EXPERTS0, GR], F32R)
        pa, pc, po = ([c.ps(f"{n}{i}") for i in range(2)] for n in ("pa", "pc", "po"))
        ptr, pmix = c.ps("ptr"), c.ps("pmix")

        consts, routed_in = c.sem("consts"), c.sem("routed_in")
        x_in = [c.sem(f"x_in{n}") for n in range(XS)]
        val_in = [c.sem(f"val_in{n}") for n in range(T)]
        y_out = [c.sem(f"y_out{n}") for n in range(2)]
        at_made, val_made = c.sem("at_made"), c.sem("val_made")
        stats = [c.sem(f"stats{n}") for n in range(3)]
        shift_made = [c.sem(f"shift_made{n}") for n in range(2)]
        dev_made = c.sem("dev_made")
        pow_done = [c.sem(f"pow_done{n}") for n in range(3)]
        x0_normed, x1_made, x1_normed, x2_made, y_made = (c.sem(n) for n in ("x0_normed", "x1_made", "x1_normed", "x2_made", "y_made"))
        turned, xh_made, xl_made = (c.sem(n) for n in ("turned", "xh_made", "xl_made"))
        up_done, gate_done, mixed, tanh_done = (c.sem(n) for n in ("up_done", "gate_done", "mixed", "tanh_done"))
        gated, hidden, hh_made, hl_made = (c.sem(n) for n in ("gated", "hidden", "hh_made", "hl_made"))
        down_done, logits_done, logits_out, logits_turned = (
            c.sem(n) for n in ("down_done", "logits_done", "logits_out", "logits_turned"))
        route, exp_done, mix_turned, mix_out = (c.sem(n) for n in ("route", "exp_done", "mix_turned", "mix_out"))
        block = stack.enter_context(nc.Block())
        NSTAT, NROUTE = 4, 25

        def bodies(eng, body):
            body(0, 0)
            with eng.Fori(0, (NG - XS) // XS) as i:
                for c_ in range(1, XS + 1):
                    body(i, c_)
            for c_ in range(NG - XS + 1, NG):
                body(0, c_)

        def in_range(i, c_, ahead):
            return not isinstance(i, int) or 0 <= c_ + ahead < NG

        @block.sync
        def _(sp):
            sp.sem_inc(y_out[0], 16)
            sp.sem_inc(y_out[1], 16)
            sp.dma_start(rbias[:], a["e_br"].broadcast_to([P, SETS * 4])).then_inc(routed_in, 16)

            def load(g, u):
                sp.dma_start(x[u][:], a["x"][ds(g * GR, GR), :].rearrange("(t p) n -> p t n", p=P))\
                  .then_inc(x_in[u], 16)

            def body(i, c_):
                if not in_range(i, c_, -1):
                    return
                g = i * XS + c_ - 1
                for t in range(T):
                    sp.wait_ge(y_made, 4 * g + t + 1)
                    sp.dma_start(k.y[ds(g * GR + t * P, P), :], y[:, t % 2, :]).then_inc(y_out[t % 2], 16)
                if in_range(i, c_, XS - 1):
                    load(g + XS, (c_ - 1) % XS)

            for g in range(XS):
                load(g, g)
            bodies(sp, body)
            body(0, NG)
            for n in range(2):
                sp.wait_ge(y_out[n], 16 + 16 * NT // 2)

        @block.gpsimd
        def _(pool):
            s = Steps(pool, consts)
            s(pool.memset(before[:], 1.0))
            s(pool.memset(expert[:], 0.25))
            s(pool.memset(expert2[:], 0.25))
            s.settle()
            s(pool.affine_select(out=before[:], in_=before[:], compare_op=ALU.is_gt, fill=0.0, base=0,
                                 pattern=[[1, 4], [-1, 4]], channel_multiplier=0))
            for m, off in ((expert, 0), (expert2, EXPERTS0 * HID1)):
                s.link(pool.affine_select(out=m[:], in_=m[:], compare_op=ALU.is_ge, fill=0.0, base=off,
                                          pattern=[[1, D]], channel_multiplier=-HID1))
                s.link(pool.affine_select(out=m[:], in_=m[:], compare_op=ALU.is_ge, fill=0.0,
                                          base=HID1 - 1 - off, pattern=[[-1, D]], channel_multiplier=HID1))

            def power(g, n):
                pool.wait_ge(stats[n], NSTAT * g + 4 if n < 2 else 5 * g + 4)
                pool.tensor_tensor(rs[n][:], ve[n][:], k.half_neg[:, 0:T], ALU.pow).then_inc(pow_done[n], 1)

            def gather(g, t):
                if t == 0:
                    pool.wait_ge(x1_made, 4 * g + 4)
                    hold(pool)
                    pool.tensor_copy(at[:], k.slot["s"][:, ds(T * g, T)]).then_inc(at_made, 1)
                pool.tensor_tensor(val[:, t, :], k.b12[:], k.zeros[:], ALU.add).then_inc(val_made, 1)
                pool.wait_ge(val_made, 4 * g + t + 1)
                pool.wait_ge(at_made, g + 1)
                hold(pool)
                pool.indirect_dma_start(val[:, t, :], None, k.values[:, :],
                                        bass.IndirectOffsetOnAxis(ap=at[:, t:t + 1], axis=0),
                                        bounds_check=EP - 1, oob_is_err=False).then_inc(val_in[t], 16)

            def add(g, u, t):
                pool.wait_ge(x0_normed, 4 * g + t + 1)
                pool.wait_ge(val_in[t], 16 * g + 16)
                pool.tensor_tensor(x[u][:, t, :], x[u][:, t, :], val[:, t, :], ALU.add).then_inc(x1_made, 1)

            def low(g, cc):
                if cc == 0:
                    pool.wait_ge(down_done, 4 * g + 4)
                pool.wait_ge(hh_made, 4 * g + cc + 1)
                pool.tensor_tensor(hl[:, cc, :], act_out[:, cc % 2, :], hh[:, cc, :].bitcast(F32), ALU.subtract)\
                    .then_inc(hl_made, 1)

            def body(i, c_):
                g, u2 = i * XS + c_, (c_ + 2) % XS
                front = in_range(i, c_, 2)
                if in_range(i, c_, -1):
                    power(g - 1, 2)
                if front:
                    power(g + 2, 0)
                low(g, 0)
                if front:
                    add(g + 2, u2, 0)
                    add(g + 2, u2, 1)
                low(g, 1)
                if front:
                    add(g + 2, u2, 2)
                    add(g + 2, u2, 3)
                low(g, 2)
                if front:
                    power(g + 2, 1)
                if in_range(i, c_, 3):
                    gather(g + 3, 0)
                low(g, 3)
                if in_range(i, c_, 3):
                    gather(g + 3, 1)
                    gather(g + 3, 2)
                    gather(g + 3, 3)

            pool.sem_inc(hl_made, 2)
            pool.sem_inc(x1_made, 4)
            for t in range(T):
                gather(0, t)
            for g in range(2):
                power(g, 0)
                for t in range(T):
                    add(g, g, t)
                for t in range(T):
                    gather(g + 1, t)
                power(g, 1)
            bodies(pool, body)
            power(NG - 1, 2)

        def statistics(v, g, u, n):
            s = Steps(v, stats[n], (NSTAT if n < 2 else 5) * g)
            for t in range(T):
                ins = v.bn_stats(st[n][:, t, :], x[u][:, t, :])
            s.link(ins)
            hold(v)
            for t in range(T):
                ins = v.bn_aggr(mv[n][:, t, :], st[n][:, t, :])
            s.link(ins)
            s(v.tensor_scalar(shift[n][:], mv[n][:, :, 0], -1.0, None, ALU.mult))
            s(v.tensor_scalar(ve[n][:], mv[n][:, :, 1], 1e-5, None, ALU.add))

        @block.vector
        def _(v):
            v.sem_inc(hidden, 2)
            v.sem_inc(x2_made, 2)
            v.wait_ge(consts, 8)
            v.tensor_tensor(expert_r[:], expert[:], expert2[:], ALU.add).then_inc(consts, 1)
            for part in wr:
                v.memset(part[:, :, SETS * 4:P].bitcast(F32), 0.0).then_inc(consts, 1)
            v.memset(parts[:, :, 2 * EXPERTS0:P].bitcast(F32), 0.0).then_inc(consts, 1)
            v.wait_ge(routed_in, 16)

            def front0(i, c_):
                g = i * XS + c_
                v.wait_ge(x_in[c_ % XS], i * 16 + 16 * (c_ // XS + 1))
                if in_range(i, c_, -1):
                    v.wait_ge(x0_normed, 4 * g)
                hold(v)
                statistics(v, g, c_ % XS, 0)

            def front0_end(g):
                v.wait_ge(pow_done[0], g + 1)
                v.tensor_scalar(gain[:], rs[0][:], 1.0, None, ALU.add).then_inc(shift_made[0], 1)
                v.tensor_tensor(shift[0][:], shift[0][:], rs[0][:], ALU.mult).then_inc(shift_made[0], 1)

            def front1(i, c_):
                g = i * XS + c_
                v.wait_ge(x1_made, 4 * g + 4 + 4)
                if in_range(i, c_, -1):
                    v.wait_ge(x1_normed, 4 * g)
                hold(v)
                statistics(v, g, c_ % XS, 1)

            def front1_end(g):
                v.wait_ge(pow_done[1], g + 1)
                v.tensor_tensor(shift[1][:], shift[1][:], rs[1][:], ALU.mult).then_inc(shift_made[1], 1)

            def low(g, n, t):
                v.wait_ge(xh_made, 4 * g + t + 1)
                v.tensor_tensor(xl[n][:, :, t * P:t * P + P], ptr[:].rearrange("p (c n) -> p c n", n=P),
                                xh[n][:, :, t * P:t * P + P].bitcast(F32), ALU.subtract).then_inc(xl_made, 1)

            def chunk(g, cc):
                h = act_out[:, cc % 2, :]
                v.wait_ge(tanh_done, 4 * g + cc + 1)
                v.scalar_tensor_tensor(h, h, 1.0, pa[cc % 2][:], ALU.add, ALU.mult).then_inc(gated, 1)
                v.wait_ge(gated, 8 * g + 2 * cc + 1)
                v.wait_ge(gate_done, 4 * g + cc + 1)
                v.tensor_tensor(h, h, pc[cc % 2][:], ALU.mult).then_inc(gated, 1)
                v.wait_ge(gated, 8 * g + 2 * cc + 2)
                v.wait_ge(mixed, 4 * g + cc + 1)
                v.tensor_tensor(h, h, pmix[:], ALU.mult).then_inc(hidden, 1)

            def back(g, u, t):
                v.wait_ge(down_done, 4 * g + t + 1 + 4)
                v.tensor_tensor(x[u][:, t, :], x[u][:, t, :], po[t % 2][:], ALU.add).then_inc(x2_made, 1)

            def back_stats(i, c_):
                g = i * XS + c_
                v.wait_ge(x2_made, 4 * g + 4 + 2)
                if in_range(i, c_, -1):
                    v.wait_ge(y_made, 4 * g)
                hold(v)
                statistics(v, g, c_ % XS, 2)
                v.tensor_copy(k.mean[:, ds(T * g, T)], mv[2][:, :, 0])

            def back_end(g):
                v.wait_ge(pow_done[2], g + 1)
                v.tensor_tensor(shift[2][:], shift[2][:], rs[2][:], ALU.mult).then_inc(stats[2], 1)
                v.tensor_tensor(k.dev[:, ds(T * g, T)], ve[2][:], rs[2][:], ALU.mult).then_inc(dev_made, 1)

            def routing(g, between):
                s = Steps(v, route, NROUTE * g)

                def link(ins):
                    s.link(ins)
                    if s.n in between:
                        between[s.n]()
                        s.settle()

                v.wait_ge(logits_turned, g + 1)
                link(v.tensor_tensor(prob[:].rearrange("p (t s) e -> p t (s e)", t=T),
                                     ptr[:, 0:T * SETS * 4].rearrange("p (t n) -> p t n", t=T),
                                     rbias[:].unsqueeze(1).broadcast_to([P, T, SETS * 4]), ALU.add))
                link(v.tensor_reduce(total[:], prob[:], X_AXIS, ALU.max))
                s(v.tensor_tensor(prob[:], prob[:], total[:].unsqueeze(2).broadcast_to([P, NS, 4]), ALU.subtract))
                v.wait_ge(exp_done, g + 1)
                link(v.tensor_reduce(total[:], prob[:], X_AXIS, ALU.add))
                link(v.reciprocal(total[:], total[:]))
                link(v.tensor_tensor(prob[:], prob[:], total[:].unsqueeze(2).broadcast_to([P, NS, 4]), ALU.mult))
                other = prob[:].unsqueeze(2).broadcast_to([P, NS, 4, 4])
                own = prob[:].unsqueeze(3).broadcast_to([P, NS, 4, 4])
                s(v.tensor_tensor(wins[:], other, own, ALU.is_gt))
                link(v.tensor_tensor(ties[:], other, own, ALU.is_equal))
                link(v.tensor_tensor(ties[:], ties[:], before[:].unsqueeze(1).broadcast_to([P, NS, 4, 4]), ALU.mult))
                link(v.tensor_tensor(wins[:], wins[:], ties[:], ALU.add))
                link(v.tensor_reduce(rank[:], wins[:], X_AXIS, ALU.add))
                s(v.scalar_tensor_tensor(one_hot[:], rank[:], 0.0, prob[:], ALU.is_equal, ALU.mult))
                link(v.scalar_tensor_tensor(second[:], rank[:], 1.0, prob[:], ALU.is_equal, ALU.mult))
                link(v.tensor_tensor(prob[:], one_hot[:], second[:], ALU.add))
                link(v.tensor_reduce(total[:], prob[:], X_AXIS, ALU.add))
                link(v.tensor_scalar(total[:], total[:], 0.9, None, ALU.is_le))
                link(v.tensor_tensor(second[:], second[:], total[:].unsqueeze(2).broadcast_to([P, NS, 4]), ALU.mult))
                link(v.tensor_tensor(prob[:], one_hot[:], second[:], ALU.add))
                link(v.tensor_reduce(total[:], prob[:], X_AXIS, ALU.add))
                link(v.tensor_scalar(total[:], total[:], 1e-9, None, ALU.add))
                link(v.reciprocal(total[:], total[:]))
                link(v.tensor_tensor(prob[:], prob[:], total[:].unsqueeze(2).broadcast_to([P, NS, 4]), ALU.mult))
                sets = prob[:].rearrange("p (t s) e -> p t s e", t=T)
                for t in range(T):
                    ins = v.tensor_tensor(mix[:, t, :].rearrange("p (s e) -> p s e", e=4), sets[:, t, 1:SETS, :],
                                          sets[:, t, 0, :].unsqueeze(2).broadcast_to([P, 4, 4]), ALU.mult)
                link(ins)
                v.wait_ge(mix_turned, g + 1)
                link(v.tensor_copy(parts[:, :, 0:EXPERTS0], mix[:]))
                s(v.tensor_tensor(parts[:, :, EXPERTS0:2 * EXPERTS0], mix[:], parts[:, :, 0:EXPERTS0].bitcast(F32),
                                  ALU.subtract))
                assert s.n == NROUTE

            def body(i, c_):
                g, u, n1 = i * XS + c_, c_ % XS, (c_ + 1) % 2
                front, mid, behind = in_range(i, c_, 2), in_range(i, c_, 1), in_range(i, c_, -1)
                if behind:
                    back_stats(i, c_ - 1)
                if behind:
                    back_end(g - 1)
                chunk(g, 0)
                if mid:
                    low(g + 1, n1, 0)
                if front:
                    front0(i, c_ + 2)
                if mid:
                    low(g + 1, n1, 1)
                if front:
                    front0_end(g + 2)
                chunk(g, 1)
                if mid:
                    low(g + 1, n1, 2)
                    low(g + 1, n1, 3)
                chunk(g, 2)
                if front:
                    front1(i, c_ + 2)
                chunk(g, 3)
                if front:
                    front1_end(g + 2)
                if mid:
                    routing(g + 1, {10: lambda: back(g, u, 0), 18: lambda: back(g, u, 1)})
                else:
                    back(g, u, 0)
                    back(g, u, 1)
                back(g, u, 2)
                back(g, u, 3)

            for g in range(2):
                front0(0, g)
                front0_end(g)
                front1(0, g)
                front1_end(g)
                if g == 0:
                    for t in range(T):
                        low(0, 0, t)
                    routing(0, {})
            bodies(v, body)
            back_stats(0, NG - 1)
            back_end(NG - 1)
            v.wait_ge(dev_made, NG)

        @block.scalar
        def _(act_):
            def norm0(g, u, t):
                if t == 0:
                    act_.wait_ge(shift_made[0], 2 * g + 2)
                act_.activation(x[u][:, t, :], x[u][:, t, :], ACT.Identity, bias=shift[0][:, t:t + 1],
                                scale=gain[:, t:t + 1]).then_inc(x0_normed, 1)

            def norm1(g, u):
                act_.wait_ge(shift_made[1], g + 1)
                for t in range(T):
                    act_.wait_ge(turned, 4 * g + t + 1)
                    act_.activation(xf[:, t, :], x[u][:, t, :], ACT.Identity, bias=shift[1][:, t:t + 1],
                                    scale=rs[1][:, t:t + 1]).then_inc(x1_normed, 1)

            def high(g, n, t):
                act_.wait_ge(turned, 4 * g + t + 1 + 4)
                act_.activation(xh[n][:, :, t * P:t * P + P], ptr[:].rearrange("p (c n) -> p c n", n=P), ACT.Copy)\
                    .then_inc(xh_made, 1)

            def tanh(g, cc):
                act_.wait_ge(up_done, 4 * g + cc + 1)
                act_.wait_ge(hl_made, 4 * g + cc + 1)
                act_.activation(act_out[:, cc % 2, :], pa[cc % 2][:], ACT.Tanh, scale=0.5).then_inc(tanh_done, 1)

            def split(g, cc):
                act_.wait_ge(hidden, 4 * g + cc + 1 + 2)
                if cc == 0:
                    act_.wait_ge(down_done, 4 * g + 4)
                act_.activation(hh[:, cc, :], act_out[:, cc % 2, :], ACT.Copy).then_inc(hh_made, 1)

            def logits_copy(g):
                act_.wait_ge(logits_done, g + 1)
                act_.activation(logit_t[:], ptr[0:SETS * 4, :], ACT.Copy).then_inc(logits_out, 1)

            def softmax_exp(g):
                act_.wait_ge(route, NROUTE * g + 3)
                act_.activation(prob[:], prob[:], ACT.Exp).then_inc(exp_done, 1)

            def mix_copy(g):
                act_.wait_ge(mix_turned, g + 2)
                act_.activation(mix_t[:], ptr[0:2 * EXPERTS0, :], ACT.Copy).then_inc(mix_out, 1)

            def finish(g, u, t):
                if t == 0:
                    act_.wait_ge(stats[2], 5 * g + 5)
                act_.wait_ge(y_out[t % 2], 32 * g + 16 * (t // 2) + 16)
                act_.activation(y[:, t % 2, :], x[u][:, t, :], ACT.Identity, bias=shift[2][:, t:t + 1],
                                scale=rs[2][:, t:t + 1]).then_inc(y_made, 1)

            def body(i, c_):
                g, n1 = i * XS + c_, (c_ + 1) % 2
                u, u1, u2 = (c_ - 1) % XS, (c_ + 1) % XS, (c_ + 2) % XS
                front, mid, behind = in_range(i, c_, 2), in_range(i, c_, 1), in_range(i, c_, -1)
                if mid:
                    norm1(g + 1, u1)
                tanh(g, 0)
                mix_copy(g)
                if mid:
                    high(g + 1, n1, 0)
                split(g, 0)
                if behind:
                    finish(g - 1, u, 0)
                if mid:
                    high(g + 1, n1, 1)
                tanh(g, 1)
                if behind:
                    finish(g - 1, u, 1)
                if front:
                    norm0(g + 2, u2, 0)
                if mid:
                    high(g + 1, n1, 2)
                split(g, 1)
                if front:
                    norm0(g + 2, u2, 1)
                    norm0(g + 2, u2, 2)
                tanh(g, 2)
                if mid:
                    high(g + 1, n1, 3)
                if front:
                    norm0(g + 2, u2, 3)
                if behind:
                    finish(g - 1, u, 2)
                    finish(g - 1, u, 3)
                split(g, 2)
                tanh(g, 3)
                if mid:
                    logits_copy(g + 1)
                split(g, 3)
                if mid:
                    softmax_exp(g + 1)

            for g in range(2):
                for t in range(T):
                    norm0(g, g, t)
                if g == 0:
                    norm1(0, 0)
                    for t in range(T):
                        high(0, 0, t)
                    logits_copy(0)
                    softmax_exp(0)
            bodies(act_, body)
            for t in range(T):
                finish(NG - 1, (NG - 1) % XS, t)

        @block.tensor
        def _(pe):
            pe.sem_inc(turned, 4)
            pe.sem_inc(down_done, 4)
            pe.sem_inc(mix_turned, 1)
            pe.wait_ge(consts, 12)

            def turn(g, t, first=False):
                pe.wait_ge(x1_normed, 4 * g + t + 1)
                if t:
                    pe.wait_ge(xl_made, 4 * g + t)
                elif not first:
                    pe.wait_ge(mix_out, g)
                for kc in range(KC):
                    last = pe.transpose(ptr[:, kc * P:kc * P + P], xf[:, t, kc * P:kc * P + P], k.ident[:])
                last.then_inc(turned, 1)

            def logits(g, n):
                pe.wait_ge(xl_made, 4 * g + 4)
                for kc in range(KC):
                    last = split3(pe, ptr[:], (wr[0][:, kc, :], wr[1][:, kc, :]), (xh[n][:, kc, :], xl[n][:, kc, :]),
                                  kc == 0, kc == KC - 1)
                last.then_inc(logits_done, 1)

            def turn_logits(g):
                pe.wait_ge(logits_out, g + 1)
                for t in range(T):
                    last = pe.matmul(ptr[:, t * SETS * 4:(t + 1) * SETS * 4], logit_t[:, t * P:t * P + P],
                                     k.ident[0:SETS * 4, 0:SETS * 4], start=True, stop=True)
                last.then_inc(logits_turned, 1)

            def up(g, n, cc, name, out, done):
                if name == "w1":
                    pe.wait_ge(hidden, 4 * g + cc + 1)
                sl = slice(cc * P, cc * P + P)
                for kc in range(KC):
                    last = split3(pe, out[cc % 2][:], (w[name][0][:, kc, sl], w[name][1][:, kc, sl]),
                                  (xh[n][:, kc, :], xl[n][:, kc, :]), kc == 0, kc == KC - 1)
                last.then_inc(done, 1)

            def spread(g, cc):
                pe.wait_ge(hidden, 4 * g + cc + 2)
                pe.matmul(pmix[:], expert_r[:, cc * P:cc * P + P], mix_t[:], start=True, stop=True).then_inc(mixed, 1)

            def turn_mix(g):
                pe.wait_ge(route, NROUTE * g + NROUTE)
                for t in range(T):
                    last = pe.transpose(ptr[:, t * P:t * P + P], parts[:, t, :].bitcast(F32), k.ident[:])
                last.then_inc(mix_turned, 1)

            def down(g, t, ccs):
                sl = slice(t * P, t * P + P)
                for cc in ccs:
                    if cc == 0:
                        pe.wait_ge(x2_made, 4 * g + t + 1)
                    pe.wait_ge(hl_made, 4 * g + cc + 1 + 2)
                    last = split3(pe, po[t % 2][:], (hh[:, cc, sl], hl[:, cc, sl]),
                                  (w["w2"][0][:, cc, :], w["w2"][1][:, cc, :]), cc == 0, cc == KC - 1)
                    if cc == KC - 1:
                        last.then_inc(down_done, 1)

            def body(i, c_):
                g, n, n1 = i * XS + c_, c_ % 2, (c_ + 1) % 2
                mid = in_range(i, c_, 1)
                up(g, n, 0, "w1", pa, up_done)
                turn_mix(g)
                up(g, n, 0, "w3", pc, gate_done)
                pe.wait_ge(mix_out, g + 1)
                spread(g, 0)
                if mid:
                    turn(g + 1, 0)
                up(g, n, 1, "w1", pa, up_done)
                if mid:
                    turn(g + 1, 1)
                up(g, n, 1, "w3", pc, gate_done)
                spread(g, 1)
                if mid:
                    turn(g + 1, 2)
                up(g, n, 2, "w1", pa, up_done)
                if mid:
                    turn(g + 1, 3)
                up(g, n, 2, "w3", pc, gate_done)
                spread(g, 2)
                up(g, n, 3, "w1", pa, up_done)
                if mid:
                    logits(g + 1, n1)
                up(g, n, 3, "w3", pc, gate_done)
                spread(g, 3)
                if mid:
                    turn_logits(g + 1)
                down(g, 0, (0, 1, 2))
                down(g, 1, (0, 1, 2))
                down(g, 0, (3,))
                down(g, 1, (3,))
                down(g, 2, range(KC))
                down(g, 3, range(KC))

            for t in range(T):
                turn(0, t, True)
            logits(0, 0)
            turn_logits(0)
            bodies(pe, body)



def messages(nc, k, tag, source, weight, table):
    with ExitStack() as stack:
        c = Core(nc, stack, tag)
        at = c.sb("at", [P, T], I32)
        weights = c.sb("weights", [P, T])
        rows = c.sb("rows", [P, T, D])
        sums = c.sb("sums", [P, T, D])
        sh, sl = (c.sb(n, [P, 2, D], F32R) for n in ("sh", "sl"))
        out = c.sb("out", [P, 2, D])
        ptr = [c.ps(f"ptr{n}") for n in range(2)]
        po = [c.ps(f"po{n}") for n in range(2)]
        at_made = c.sem("at_made")
        rows_in = [c.sem(f"rows_in{t}") for t in range(T)]
        scaled, turned, summed, hi_made, lo_made, done, row_out = (
            c.sem(n) for n in ("scaled", "turned", "summed", "hi_made", "lo_made", "done", "row_out"))
        stored = [c.sem(f"stored{n}") for n in range(2)]
        block = stack.enter_context(nc.Block())
        same = k.same["d"]

        @block.gpsimd
        def _(pool):
            with pool.Fori(0, EG) as g:
                pool.wait_ge(turned, 4 * g + 4)
                hold(pool)
                pool.tensor_copy(at[:], k.rec["d"][:, ds(T * g, T), 0]).then_inc(at_made, 1)
                pool.tensor_copy(weights[:], k.rec["d"][:, ds(T * g, T), 2].bitcast(F32)).then_inc(at_made, 1)
                pool.wait_ge(at_made, 2 * g + 2)
                hold(pool)
                for t in range(T):
                    pool.indirect_dma_start(rows[:, t, :], None, source[:, :],
                                            bass.IndirectOffsetOnAxis(ap=at[:, t:t + 1], axis=0),
                                            bounds_check=NPAD - 1, oob_is_err=False).then_inc(rows_in[t], 16)

        def copy_row(act_, g, t):
            act_.wait_ge(done, 4 * g + t + 1 + 2)
            act_.wait_ge(stored[t % 2], 32 * g + 16 * (t // 2) + 16)
            act_.activation(out[:, t % 2, :], po[t % 2][:], ACT.Copy).then_inc(row_out, 1)

        @block.scalar
        def _(act_):
            act_.sem_inc(row_out, 2)

            def scale(g, t):
                act_.wait_ge(rows_in[t], 16 * g + 16)
                act_.wait_ge(at_made, 2 * g + 2)
                act_.activation(rows[:, t, :], rows[:, t, :], ACT.Copy, scale=weights[:, t:t + 1]).then_inc(scaled, 1)

            with act_.Fori(0, EG) as g:
                for t in range(T):
                    scale(g, t)
                for t in range(T):
                    act_.wait_ge(summed, 4 * g + t + 1 + 4)
                    act_.wait_ge(done, 4 * g + t + 1)
                    act_.activation(sh[:, t % 2, :], sums[:, t, :], ACT.Copy).then_inc(hi_made, 1)
                    if t:
                        copy_row(act_, g, t - 1)
                copy_row(act_, g, T - 1)

        @block.vector
        def _(v):
            v.sem_inc(lo_made, 4)
            v.memset(sums[:], 0.0).then_inc(summed, 4)
            with v.Fori(0, EG) as g:
                for t in range(T):
                    v.wait_ge(turned, 4 * g + t + 1 + 4)
                    v.wait_ge(summed, 4 * g + t + 4)
                    v.wait_ge(lo_made, 4 * g + t + 1)
                    hold(v)
                    for kc in range(KC):
                        own = slice(kc * P, kc * P + P)
                        last = v.tensor_tensor_scan(sums[:, t, own], same[:, ds(g * GR + t * P, P)], ptr[t % 2][:, own],
                                                    sums[:, (t - 1) % T, kc * P + P - 1:kc * P + P], ALU.mult, ALU.add)
                    last.then_inc(summed, 1)
                    v.wait_ge(hi_made, 4 * g + t + 1)
                    v.tensor_tensor(sl[:, t % 2, :], sums[:, t, :], sh[:, t % 2, :].bitcast(F32), ALU.subtract)\
                     .then_inc(lo_made, 1)

        @block.tensor
        def _(pe):
            pe.sem_inc(turned, 4)
            pe.sem_inc(done, 2)

            def turn(g, t):
                pe.wait_ge(scaled, 4 * g + t + 1)
                pe.wait_ge(summed, 4 * g + t - 1 + 4)
                for kc in range(KC):
                    own = slice(kc * P, kc * P + P)
                    last = pe.transpose(ptr[t % 2][:, own], rows[:, t, own], k.ident[:])
                last.then_inc(turned, 1)

            def product(g, t):
                pe.wait_ge(lo_made, 4 * g + t + 1 + 4)
                pe.wait_ge(row_out, 4 * g + t + 1)
                for kc in range(KC):
                    own = slice(kc * P, kc * P + P)
                    last = split3(pe, po[t % 2][:], (sh[:, t % 2, own], sl[:, t % 2, own]),
                                  (weight[0][:, kc, :], weight[1][:, kc, :]), kc == 0, kc == KC - 1)
                last.then_inc(done, 1)

            with pe.Fori(0, EG) as g:
                turn(g, 0)
                turn(g, 1)
                product(g, 0)
                turn(g, 2)
                product(g, 1)
                turn(g, 3)
                product(g, 2)
                product(g, 3)

        @block.sync
        def _(sp):
            sp.sem_inc(stored[0], 16)
            sp.sem_inc(stored[1], 16)
            with sp.Fori(0, EG) as g:
                for t in range(T):
                    sp.wait_ge(row_out, 4 * g + t + 3)
                    sp.dma_start(table[ds(g * GR + t * P, P), :], out[:, t % 2, :]).then_inc(stored[t % 2], 16)
            for n in range(2):
                sp.wait_ge(stored[n], 16 + 16 * ET // 2)



def conv_phase(nc, a, k):
    with ExitStack() as stack:
        c = Core(nc, stack, "conv")
        w = {n: [c.sb(f"{n}_{h}", [P, KC, D], F32R) for h in ("hi", "lo")] for n in ("w11", "w01", "w02")}
        split_weights(nc, k, [(chunks(a[f"g_{n}"]), *w[n]) for n in ("w11", "w01", "w02")])
        messages(nc, k, "msg1", k.y, w["w11"], k.message1)
        yin = c.sb("yin", [P, T, D])
        msg = c.sb("msg", [P, T, D])
        at = c.sb("at", [P, T], I32)
        diag = c.sb("diag", [P, NT])
        dg, dg2 = c.sb("dg", [P, T]), c.sb("dg2", [P, T])
        bias = [c.sb(f"bias{n}", [P, D]) for n in range(2)]
        yh, yl, hh, hl = (c.sb(n, [P, 2, D], F32R) for n in ("yh", "yl", "hh", "hl"))
        h = c.sb("h", [P, T, D])
        own = c.sb("own", [P, 2, D])
        pty, pth, p1, p2 = ([c.ps(f"{n}{i}") for i in range(2)] for n in ("pty", "pth", "p1", "p2"))
        consts = c.sem("consts")
        y_in, msg_in, h_out = ([c.sem(f"{n}{t}") for t in range(T)] for n in ("y_in", "msg_in", "h_out"))
        own_out = [c.sem(f"own_out{n}") for n in range(2)]
        added = c.sem("added")
        at_made, msg_made, dg_made = c.sem("at_made"), c.sem("msg_made"), c.sem("dg_made")
        y_turned, yh_made, yl_made, one_done, summed, h_made = (
            c.sem(n) for n in ("y_turned", "yh_made", "yl_made", "one_done", "summed", "h_made"))
        h_turned, hh_made, hl_made, two_done, own_made = (
            c.sem(n) for n in ("h_turned", "hh_made", "hl_made", "two_done", "own_made"))
        block = stack.enter_context(nc.Block())

        @block.sync
        def _(sp):
            for t in range(T):
                sp.sem_inc(h_out[t], 16)
            for n in range(2):
                sp.sem_inc(own_out[n], 16)
            sp.dma_start(diag[:], a["diag"]).then_inc(consts, 16)
            for n in range(2):
                sp.dma_start(bias[n][:], a[f"g_b{n + 1}"].broadcast_to([P, D])).then_inc(consts, 16)

            def load(g, t):
                sp.wait_ge(y_turned, 4 * g + t + 1)
                sp.dma_start(yin[:, t, :], k.y[ds(g * GR + t * P, P), :]).then_inc(y_in[t], 16)

            def store_h(g, t):
                sp.wait_ge(h_made, 4 * g + t + 1)
                sp.dma_start(k.h[ds(g * GR + t * P, P), :], h[:, t, :]).then_inc(h_out[t], 16)

            def store_own(g, t):
                sp.wait_ge(own_made, 4 * g + t + 1 + 2)
                sp.dma_start(k.own[ds(g * GR + t * P, P), :], own[:, t % 2, :]).then_inc(own_out[t % 2], 16)

            for t in range(T):
                load(0, t)
            with sp.Fori(0, NG - 1) as g:
                for t in range(T):
                    store_h(g, t)
                    load(g + 1, t)
                    if t:
                        store_own(g, t - 1)
                store_own(g, T - 1)
            for t in range(T):
                store_h(NG - 1, t)
            for t in range(T):
                store_own(NG - 1, t)
            for t in range(T):
                sp.wait_ge(h_out[t], 16 + 16 * NG)
            for n in range(2):
                sp.wait_ge(own_out[n], 16 + 32 * NG)

        @block.gpsimd
        def _(pool):
            with pool.Fori(0, NG) as g:
                pool.wait_ge(summed, 4 * g + 4)
                hold(pool)
                pool.tensor_copy(at[:], k.slot["d"][:, ds(T * g, T)]).then_inc(at_made, 1)
                pool.memset(msg[:], 0.0).then_inc(msg_made, 1)
                pool.wait_ge(msg_made, g + 1)
                pool.wait_ge(at_made, g + 1)
                hold(pool)
                for t in range(T):
                    pool.indirect_dma_start(msg[:, t, :], None, k.message1[:, :],
                                            bass.IndirectOffsetOnAxis(ap=at[:, t:t + 1], axis=0),
                                            bounds_check=EP - 1, oob_is_err=False).then_inc(msg_in[t], 16)

        def nxt(g, t):
            return (g, t + 1) if t < T - 1 else (g + 1, 0)

        def prv(g, t):
            return (g, t - 1) if t else (g - 1, T - 1)

        def low(v, g, t, bank, hi, lo, made, ready):
            v.wait_ge(ready, 4 * g + t + 1)
            v.tensor_tensor(lo[:, t % 2, :], bank[t % 2][:], hi[:, t % 2, :].bitcast(F32), ALU.subtract)\
             .then_inc(made, 1)

        @block.vector
        def _(v):
            v.sem_inc(summed, 4)
            v.sem_inc(own_made, 2)
            v.wait_ge(consts, 48)

            def own_term(g, t):
                v.wait_ge(two_done, 4 * g + t + 1)
                v.wait_ge(own_out[t % 2], 32 * g + 16 * (t // 2) + 16)
                v.scalar_tensor_tensor(own[:, t % 2, :], p2[t % 2][:], dg2[:, t:t + 1], bias[1][:], ALU.mult, ALU.add)\
                 .then_inc(own_made, 1)

            def step(g, t, behind=2, last=False):
                if not last:
                    low(v, *nxt(g, t), pty, yh, yl, yl_made, yh_made)
                if behind >= 1:
                    low(v, *prv(g, t), pth, hh, hl, hl_made, hh_made)
                if behind >= 2:
                    own_term(*prv(*prv(g, t)))
                v.wait_ge(one_done, 4 * g + t + 1)
                v.wait_ge(msg_in[t], 16 * g + 16)
                v.wait_ge(h_out[t], 16 * g + 16)
                v.scalar_tensor_tensor(h[:, t, :], p1[t % 2][:], dg[:, t:t + 1], msg[:, t, :], ALU.mult, ALU.add)\
                 .then_inc(added, 1)
                v.wait_ge(added, 4 * g + t + 1)
                v.tensor_tensor(h[:, t, :], h[:, t, :], bias[0][:], ALU.add).then_inc(summed, 1)

            def group(g, first=False, last=False):
                for t in range(T):
                    if t == 0:
                        v.tensor_copy(dg[:], diag[:, ds(T * g, T)]).then_inc(dg_made, 1)
                        v.wait_ge(dg_made, 2 * g + 1)
                    step(g, t, t if first else 2, last and t == T - 1)
                    if t == 1:
                        v.wait_ge(own_made, 4 * g + 2)
                        hold(v)
                        v.tensor_copy(dg2[:], diag[:, ds(T * g, T)]).then_inc(dg_made, 1)
                        v.wait_ge(dg_made, 2 * g + 2)

            low(v, 0, 0, pty, yh, yl, yl_made, yh_made)
            group(0, first=True)
            with v.Fori(1, NG - 1) as g:
                group(g)
            group(NG - 1, last=True)
            low(v, NG - 1, T - 1, pth, hh, hl, hl_made, hh_made)
            own_term(NG - 1, T - 2)
            own_term(NG - 1, T - 1)
            v.wait_ge(own_made, NT + 2)

        @block.scalar
        def _(act_):
            def high(g, t, bank, hi, made, ready):
                act_.wait_ge(ready, 4 * g + t + 1)
                act_.activation(hi[:, t % 2, :], bank[t % 2][:], ACT.Copy).then_inc(made, 1)

            def step(g, t, first=False, last=False):
                if not last:
                    n = nxt(g, t)
                    act_.wait_ge(y_turned, 4 * n[0] + n[1] + 1 + 4)
                    act_.activation(yh[:, n[1] % 2, :], pty[n[1] % 2][:], ACT.Copy).then_inc(yh_made, 1)
                if not first:
                    high(*prv(g, t), pth, hh, hh_made, h_turned)
                act_.wait_ge(summed, 4 * g + t + 1 + 4)
                act_.activation(h[:, t, :], h[:, t, :], ACT.Relu).then_inc(h_made, 1)

            act_.wait_ge(y_turned, 5)
            act_.activation(yh[:, 0, :], pty[0][:], ACT.Copy).then_inc(yh_made, 1)
            for t in range(T):
                step(0, t, t == 0)
            with act_.Fori(1, NG - 1) as g:
                for t in range(T):
                    step(g, t)
            for t in range(T):
                step(NG - 1, t, False, t == T - 1)
            high(NG - 1, T - 1, pth, hh, hh_made, h_turned)

        @block.tensor
        def _(pe):
            pe.sem_inc(y_turned, 4)

            def turn(bank, src, t, done):
                for kc in range(KC):
                    own_ = slice(kc * P, kc * P + P)
                    last = pe.transpose(bank[t % 2][:, own_], src[:, t, own_], k.ident[:])
                last.then_inc(done, 1)

            def product(bank, hi, lo, name, t, done):
                for kc in range(KC):
                    own_ = slice(kc * P, kc * P + P)
                    last = split3(pe, bank[t % 2][:], (hi[:, t % 2, own_], lo[:, t % 2, own_]),
                                  (w[name][0][:, kc, :], w[name][1][:, kc, :]), kc == 0, kc == KC - 1)
                last.then_inc(done, 1)

            def turn_y(g, t, wait=True):
                pe.wait_ge(y_in[t], 16 * g + 16)
                if wait:
                    pe.wait_ge(yl_made, 4 * g + t - 1)
                turn(pty, yin, t, y_turned)

            def product_y(g, t, wait=True):
                pe.wait_ge(yl_made, 4 * g + t + 1)
                if wait:
                    pe.wait_ge(summed, 4 * g + t - 1 + 4)
                product(p1, yh, yl, "w01", t, one_done)

            def turn_h(g, t, wait=True):
                pe.wait_ge(h_made, 4 * g + t + 1)
                if wait:
                    pe.wait_ge(hl_made, 4 * g + t - 1)
                turn(pth, h, t, h_turned)

            def product_h(g, t, wait=True):
                pe.wait_ge(hl_made, 4 * g + t + 1)
                if wait:
                    pe.wait_ge(own_made, 4 * g + t - 1 + 2)
                product(p2, hh, hl, "w02", t, two_done)

            def step(g, t, start=False, last=False):
                n, b = nxt(g, t), prv(g, t)
                if not last:
                    turn_y(*n, not (start and t == 0))
                if not (start and t == 0):
                    turn_h(*b, not (start and t < 3))
                product_y(g, t, not (start and t < 2))
                if not (start and t == 0):
                    product_h(*b, not (start and t < 3))

            turn_y(0, 0, False)
            for t in range(T):
                step(0, t, True)
            with pe.Fori(1, NG - 1) as g:
                for t in range(T):
                    step(g, t)
            for t in range(T):
                step(NG - 1, t, False, t == T - 1)
            turn_h(NG - 1, T - 1)
            product_h(NG - 1, T - 1)



class Experts:
    pass


def expert_weights(nc, a, k, c, x):
    x.w1, x.w2t = ([c.sb(f"{n}_{h}", [P, KC, FC1 * P], F32R) for h in ("hi", "lo")] for n in ("w1", "w2t"))
    x.gram = [c.sb(f"gram_{h}", [P, FC1, P], F32R) for h in ("hi", "lo")]
    x.w2g = [c.sb(f"w2g_{h}", [P, FC1, D], F32R) for h in ("hi", "lo")]
    x.route = [c.sb(f"route_{h}", [P, KC, P], F32R) for h in ("hi", "lo")]
    x.rows_x, x.rows_1 = c.sb("rows_x", [48, D], F32R), c.sb("rows_1", [48, D], F32R)
    x.b1 = c.sb("b1", [P, FC1])
    x.cross = c.sb("cross", [P, FC1])
    x.square = c.sb("square", [P, EXPERTS1])
    x.expert = c.sb("expert", [P, FC1, P], F32R)
    x.spread = c.sb("spread", [48, FC1 * P], F32R)
    x.earlier = c.sb("earlier", [P, EXPERTS1, EXPERTS1])
    with ExitStack() as stack:
        ci = Core(nc, stack, "ew")
        w1 = ci.sb("w1", [P, KC, FC1 * P])
        w2, b2r, gr = (ci.sb(n, [P, FC1, D]) for n in ("w2", "b2r", "gr"))
        scratch = ci.sb("scratch", [P, D])
        mean = ci.sb("mean", [P, 2 * FC1 + 1])
        route = ci.sb("route", [P, KC, 16])
        w2t = ci.sb("w2t", [P, KC, FC1 * P])
        gram = ci.sb("gram", [P, FC1, P])
        g48, b48, beta48, t48 = (ci.sb(n, [48, D]) for n in ("g48", "b48", "beta48", "t48"))
        lo48 = ci.sb("lo48", [48, D])
        hi48 = ci.sb("hi48", [48, D], F32R)
        is_lo, is_lo2, is_hi = (ci.sb(n, [48, 1]) for n in ("is_lo", "is_lo2", "is_hi"))
        blocks = ci.sb("blocks", [P, P // HID1, HID1])
        ex, sp1, sp2 = ci.sb("ex", [P, FC1, EXPERTS1]), ci.sb("sp1", [48, FC1 * P]), ci.sb("sp2", [48, FC1 * P])
        pt, pg, psq = ci.ps("pt"), ci.ps("pg"), ci.ps("psq")
        arrived, chain, consts, turned, evac, gram_done, square_done, zeroed = (
            ci.sem(n) for n in ("arrived", "chain", "consts", "turned", "evac", "gram_done", "square_done", "zeroed"))
        rows_arrived, hi_made = ci.sem("rows_arrived"), ci.sem("hi_made")
        block = stack.enter_context(nc.Block())
        per = P // HID1

        @block.sync
        def _(sp):
            sp.dma_start(w1[:], chunks(a["f_w1"])).then_inc(arrived, 16)
            sp.dma_start(w2[:], chunks(a["f_w2"])).then_inc(arrived, 16)
            sp.dma_start(x.b1[:], a["f_b1"]).then_inc(arrived, 16)
            with nc.allow_non_contiguous_dma(reason="router columns"):
                sp.dma_start(route[:, :, 0:8], a["f_router"].rearrange("(c p) n -> p c n", p=P)).then_inc(arrived, 16)
            for e in range(EXPERTS1):
                at = slice((e % per) * HID1, (e % per + 1) * HID1)
                for t, n in ((b2r, "f_b2"), (gr, "f_gamma")):
                    sp.dma_start(t[at, e // per, :], a[n][e:e + 1, :].broadcast_to([HID1, D])).then_inc(arrived, 16)
            sp.wait_ge(zeroed, 3)
            for r in range(3):
                at = slice(r * EXPERTS1, (r + 1) * EXPERTS1)
                sp.dma_start(g48[at, :], a["f_gamma"]).then_inc(rows_arrived, 16)
                sp.dma_start(b48[at, :], a["f_b2"]).then_inc(rows_arrived, 16)
                sp.dma_start(beta48[24 + r * EXPERTS1:24 + (r + 1) * EXPERTS1, :], a["f_beta"]).then_inc(rows_arrived, 16)
            sp.wait_ge(rows_arrived, 9 * 16)

        @block.gpsimd
        def _(pool):
            z = Steps(pool, zeroed)
            for t in (g48, b48, beta48):
                z(pool.memset(t[:], 0.0))
            s = Steps(pool, consts)
            for t in (is_lo, is_lo2, blocks, ex, sp1, sp2, x.earlier):
                s(pool.memset(t[:], 1.0))
            s.settle()

            def band(m, base, pattern, mult, width):
                s.link(pool.affine_select(out=m, in_=m, compare_op=ALU.is_ge, fill=0.0, base=base,
                                          pattern=pattern, channel_multiplier=mult))
                s.link(pool.affine_select(out=m, in_=m, compare_op=ALU.is_ge, fill=0.0, base=width - 1 - base,
                                          pattern=[[-q, n] for q, n in pattern], channel_multiplier=-mult))

            band(is_lo[:], -8, [[0, 1]], 1, 8)
            band(is_lo2[:], -32, [[0, 1]], 1, 8)
            band(blocks[:], 0, [[-HID1, per], [0, HID1]], 1, HID1)
            band(ex[:], 0, [[P, FC1], [-HID1, EXPERTS1]], 1, HID1)
            band(sp1[:], 0, [[1, FC1 * P]], -HID1, HID1)
            band(sp2[:], 16 * HID1, [[1, FC1 * P]], -HID1, HID1)
            s(pool.affine_select(out=x.earlier[:], in_=x.earlier[:], compare_op=ALU.is_gt, fill=0.0, base=0,
                                 pattern=[[1, EXPERTS1], [-1, EXPERTS1]], channel_multiplier=0))

        @block.vector
        def _(v):
            s = Steps(v, chain)
            v.wait_ge(consts, 20)
            for t in (*x.route, x.expert):
                s(v.memset(t[:].bitcast(F32), 0.0))
            s.settle()
            s(v.tensor_copy(x.expert[:, :, LOGITS:SMALL], ex[:]))
            s(v.tensor_tensor(x.spread[:], sp1[:], sp2[:], ALU.add))
            s.link(v.tensor_tensor(is_lo[:], is_lo[:], is_lo2[:], ALU.add))
            s(v.tensor_scalar(is_hi[:], is_lo[:], -1.0, 1.0, ALU.mult, ALU.add))
            v.wait_ge(arrived, 16 * 20)
            s(v.tensor_copy(x.w1[0][:], w1[:]))
            for fc in range(FC1):
                s(v.tensor_reduce(mean[:, fc:fc + 1], w2[:, fc, :], X_AXIS, ALU.add))
                s(v.tensor_reduce(mean[:, FC1 + fc:FC1 + fc + 1], b2r[:, fc, :], X_AXIS, ALU.add))
            s.settle()
            s(v.tensor_tensor(x.w1[1][:], w1[:], x.w1[0][:].bitcast(F32), ALU.subtract))
            s.link(v.tensor_scalar(mean[:, 0:2 * FC1], mean[:, 0:2 * FC1], -1.0 / D, None, ALU.mult))
            for fc in range(FC1):
                s(v.tensor_scalar(w2[:, fc, :], w2[:, fc, :], mean[:, fc:fc + 1], None, ALU.add))
                s(v.tensor_scalar(b2r[:, fc, :], b2r[:, fc, :], mean[:, FC1 + fc:FC1 + fc + 1], None, ALU.add))
            s.settle()
            for fc in range(FC1):
                s.link(v.scalar_tensor_tensor(scratch[:], w2[:, fc, :], 2.0, b2r[:, fc, :], ALU.mult, ALU.mult,
                                              accum_out=x.cross[:, fc:fc + 1]))
            s.link(v.tensor_tensor(gr[:], gr[:], w2[:], ALU.mult))
            s.link(v.tensor_copy(x.w2g[0][:], gr[:]))
            s(v.tensor_tensor(x.w2g[1][:], gr[:], x.w2g[0][:].bitcast(F32), ALU.subtract))
            v.wait_ge(rows_arrived, 9 * 16)
            s.link(v.tensor_reduce(mean[0:48, 2 * FC1:2 * FC1 + 1], b48[:], X_AXIS, ALU.add))
            s.link(v.tensor_scalar(mean[0:48, 2 * FC1:2 * FC1 + 1], mean[0:48, 2 * FC1:2 * FC1 + 1], -1.0 / D, None,
                                   ALU.mult))
            s.link(v.tensor_scalar(b48[:], b48[:], mean[0:48, 2 * FC1:2 * FC1 + 1], None, ALU.add))
            centred = s.n
            assert centred == 26, centred
            for kc in range(KC):
                v.wait_ge(turned, kc + 1)
                s(v.tensor_scalar(w2t[:, kc, :], pt[:, 0:FC1 * P], 2.0, None, ALU.mult))
                s.link(v.tensor_scalar(route[:, kc, 8:16], pt[:, FC1 * P:FC1 * P + 8], 2.0, None, ALU.mult))
            s(v.tensor_copy(x.w2t[0][:], w2t[:]))
            s.link(v.tensor_copy(x.route[0][:, :, 0:LOGITS], route[:]))
            s(v.tensor_tensor(x.w2t[1][:], w2t[:], x.w2t[0][:].bitcast(F32), ALU.subtract))
            s(v.tensor_tensor(x.route[1][:, :, 0:LOGITS], route[:], x.route[0][:, :, 0:LOGITS].bitcast(F32),
                              ALU.subtract))
            s(v.tensor_tensor(scratch[:, 0:KC * 8].rearrange("p (c n) -> p c n", c=KC), route[:, :, 8:16],
                              route[:, :, 8:16], ALU.mult))
            assert s.n == 39, s.n
            v.wait_ge(gram_done, 1)
            s.settle()
            for fc in range(FC1):
                s(v.scalar_tensor_tensor(gram[:, fc, :], pg[:, fc * P:fc * P + P], 0.25,
                                         blocks[:].rearrange("p a b -> p (a b)"), ALU.mult, ALU.mult))
            s.settle()
            s.link(v.tensor_copy(x.gram[0][:], gram[:]))
            s(v.tensor_tensor(x.gram[1][:], gram[:], x.gram[0][:].bitcast(F32), ALU.subtract))
            v.wait_ge(square_done, 1)
            s(v.tensor_scalar(x.square[:], psq[:, 0:8], 0.25, None, ALU.mult))
            s.link(v.tensor_tensor(t48[:], b48[:], g48[:], ALU.mult))
            s.link(v.tensor_tensor(t48[:], t48[:], beta48[:], ALU.add))
            for src, dst in ((g48, x.rows_x), (t48, x.rows_1)):
                s.link(v.tensor_copy(hi48[:], src[:]))
                s.link(v.tensor_tensor(lo48[:], src[:], hi48[:].bitcast(F32), ALU.subtract))
                s.link(v.tensor_scalar(lo48[:], lo48[:], is_lo[:], None, ALU.mult))
                s.link(v.scalar_tensor_tensor(dst[:], hi48[:].bitcast(F32), is_hi[:], lo48[:], ALU.mult, ALU.add))

        @block.tensor
        def _(pe):
            for kc in range(KC):
                pe.wait_ge(chain, 26 + 2 * kc)
                for fc in range(FC1):
                    pe.transpose(pt[:, fc * P:fc * P + P], w2[:, fc, kc * P:kc * P + P], k.ident[:])
                pe.matmul(pt[:, FC1 * P:FC1 * P + 8], b48[0:8, kc * P:kc * P + P], k.ident[0:8, 0:8],
                          start=True, stop=True).then_inc(turned, 1)
            pe.wait_ge(chain, 39)
            for fc in range(FC1):
                for kc in range(KC):
                    part = w2t[:, kc, fc * P:fc * P + P]
                    last = pe.matmul(pg[:, fc * P:fc * P + P], part, part, start=kc == 0, stop=kc == KC - 1)
            last.then_inc(gram_done, 1)
            for kc in range(KC):
                last = pe.matmul(psq[:, 0:8], k.ones[:], scratch[:, kc * 8:kc * 8 + 8], start=kc == 0,
                                 stop=kc == KC - 1)
            last.then_inc(square_done, 1)



def message2_phase(nc, a, k):
    with ExitStack() as stack:
        c = Core(nc, stack, "m2")
        w12 = [c.sb(f"w12_{h}", [P, KC, D], F32R) for h in ("hi", "lo")]
        split_weights(nc, k, [(chunks(a["g_w12"]), *w12)])
        messages(nc, k, "msg2", k.h, w12, k.message2)


def dense1_phase(nc, a, k, out):
    with ExitStack() as stack:
        c = Core(nc, stack, "d1")
        ex = Experts()
        expert_weights(nc, a, k, c, ex)
        x3 = [c.sb(f"x3{n}", [P, T, D]) for n in range(XS)]
        xf = [c.sb(f"xf{n}", [P, T, D]) for n in range(XS)]
        own, msg = (c.sb(n, [P, T, D]) for n in ("own", "msg"))
        at = c.sb("at", [P, T], I32)
        gain, middle = c.sb("gain", [P, T]), c.sb("middle", [P, T])
        xh, xl = ([c.sb(f"{n}{i}", [P, KC, GR], F32R) for i in range(2)] for n in ("xh", "xl"))
        hid = [c.sb(f"hid{n}", [P, FC1, GR]) for n in range(2)]
        quad, weighted = c.sb("quad", [P, FC1, GR]), c.sb("weighted", [P, FC1, GR])
        hh, hl, qh, ql, ch, cl = (c.sb(n, [P, FC1, GR], F32R) for n in ("hh", "hl", "qh", "ql", "ch", "cl"))
        st, mv = c.sb("st", [P, T, 6]), c.sb("mv", [P, T, 2])
        ve, rs, shift, power_in = (c.sb(n, [P, T]) for n in ("ve", "rs", "shift", "power_in"))
        msq = [c.sb(f"msq{n}", [P, T]) for n in range(XS)]
        S3, S4 = [P, T, EXPERTS1], [P, T, 2, EXPERTS1]
        small_t = c.sb("small_t", [SMALL, GR])
        logit = c.sb("logit", [P, T, LOGITS])
        prob, rank, var, coef = (c.sb(n, S3) for n in ("prob", "rank", "var", "coef"))
        chosen = [c.sb(f"chosen{n}", [P, T, 2, EXPERTS1]) for n in range(2)]
        spare = c.sb("spare", [P, T, 2, EXPERTS1])
        place = c.sb("place", [P, 2, EXPERTS1])
        var2, rs2 = c.sb("var2", [P, T, 2]), c.sb("rs2", [P, T, 2])
        gate = [c.sb(f"gate{n}", S3) for n in range(2)]
        top, total = c.sb("top", [P, T]), c.sb("total", [P, T])
        wins, ties = (c.sb(n, [P, T, EXPERTS1, EXPERTS1]) for n in ("wins", "ties"))
        parts = c.sb("parts", [P, T, P], F32R)
        coef_t = c.sb("coef_t", [48, GR], F32R)
        pu, pq = ([c.ps(f"{n}{i}") for i in range(2)] for n in ("pu", "pq"))
        ptr, psm, pb, px = (c.ps(n) for n in ("ptr", "psm", "pb", "px"))
        pox, po1 = [pu[0], pb, pq[0], pb], [pu[1], px, pq[1], px]

        NSTAT, NCOEF, NVAR, NROUTE, EXP_STEP = 4, 9, 7, 13, 3
        consts = c.sem("consts")
        y_in = [[c.sem(f"y_in{u}{t}") for t in range(T)] for u in range(XS)]
        own_in, msg_in, out_done = ([c.sem(f"{n}{t}") for t in range(T)] for n in ("own_in", "msg_in", "out_done"))
        at_made, msg_made, added, relu_done, halved, affine = (
            c.sem(n) for n in ("at_made", "msg_made", "added", "relu_done", "halved", "affine"))
        gains, stats, pow_done, shifted, normed = (c.sem(n) for n in ("gains", "stats", "pow_done", "shifted", "normed"))
        turned, xh_made, xl_made = (c.sem(n) for n in ("turned", "xh_made", "xl_made"))
        small_done, small_out, small_turned = (c.sem(n) for n in ("small_done", "small_out", "small_turned"))
        up_done, hid_made, hh_made, hl_made = (c.sem(n) for n in ("up_done", "hid_made", "hh_made", "hl_made"))
        cross_done, quad_made, qh_made, ql_made = (c.sem(n) for n in ("cross_done", "quad_made", "qh_made", "ql_made"))
        route, exp_done, vars_, pow2_done, coefs = (c.sem(n) for n in ("route", "exp_done", "vars", "pow2_done", "coefs"))
        coef_turned, coef_out, spread_done, scaled = (
            c.sem(n) for n in ("coef_turned", "coef_out", "spread_done", "scaled"))
        ch_made, cl_made, x_done, one_done, mul_done, finished_low, finished_high = (
            c.sem(n) for n in ("ch_made", "cl_made", "x_done", "one_done", "mul_done", "finished_low", "finished_high"))
        block = stack.enter_context(nc.Block())

        def bodies(eng, body):
            body(0, 0)
            with eng.Fori(0, (NG - XS) // XS) as i:
                for c_ in range(1, XS + 1):
                    body(i, c_)
            for c_ in range(NG - XS + 1, NG + 1):
                body(0, c_)

        def in_range(i, c_, ahead):
            return not isinstance(i, int) or 0 <= c_ + ahead < NG

        @block.sync
        def _(sp):
            def load_y(g, u, t):
                sp.dma_start(x3[u][:, t, :], k.y[ds(g * GR + t * P, P), :]).then_inc(y_in[u][t], 16)

            def load_own(g, t):
                sp.wait_ge(added, 4 * g + t + 1)
                sp.dma_start(own[:, t, :], k.own[ds(g * GR + t * P, P), :]).then_inc(own_in[t], 16)

            def body(i, c_):
                g = i * XS + c_
                if in_range(i, c_, 3):
                    for t in range(T):
                        load_own(g + 3, t)
                if not in_range(i, c_, -1):
                    return
                for t in range(T):
                    if t < 2:
                        sp.wait_ge(finished_low, 2 * (g - 1) + t + 1)
                    else:
                        sp.wait_ge(finished_high, 2 * (g - 1) + t - 1)
                    sp.dma_start(out[ds((g - 1) * GR + t * P, P), :], xf[(c_ - 1) % XS][:, t, :])\
                      .then_inc(out_done[t], 16)
                    if in_range(i, c_, 3):
                        load_y(g + 3, (c_ - 1) % XS, t)

            for t in range(T):
                load_own(0, t)
            for g in range(XS):
                for t in range(T):
                    load_y(g, g, t)
            for g in (1, 2):
                for t in range(T):
                    load_own(g, t)
            bodies(sp, body)
            for t in range(T):
                sp.wait_ge(out_done[t], 16 * XS + 16 * NG)

        @block.gpsimd
        def _(pool):
            def gather(g):
                pool.wait_ge(halved, 4 * g + 4)
                hold(pool)
                pool.tensor_copy(at[:], k.slot["d"][:, ds(T * g, T)]).then_inc(at_made, 1)
                pool.memset(msg[:], 0.0).then_inc(msg_made, 1)
                pool.wait_ge(msg_made, g + 1)
                pool.wait_ge(at_made, g + 1)
                hold(pool)
                for t in range(T):
                    pool.indirect_dma_start(msg[:, t, :], None, k.message2[:, :],
                                            bass.IndirectOffsetOnAxis(ap=at[:, t:t + 1], axis=0),
                                            bounds_check=EP - 1, oob_is_err=False).then_inc(msg_in[t], 16)

            def add(g, t):
                pool.wait_ge(own_in[t], 16 * g + 16)
                pool.wait_ge(msg_in[t], 16 * g + 16)
                pool.tensor_tensor(msg[:, t, :], msg[:, t, :], own[:, t, :], ALU.add).then_inc(added, 1)

            def power(g):
                pool.wait_ge(stats, NSTAT * g + 4)
                pool.tensor_tensor(rs[:], ve[:], k.half_neg[:, 0:T], ALU.pow).then_inc(pow_done, 1)

            def power2(g):
                pool.wait_ge(vars_, NVAR * g + NVAR)
                pool.tensor_tensor(rs2[:].rearrange("p t n -> p (t n)"), var2[:].rearrange("p t n -> p (t n)"),
                                   k.half_neg[:, 0:T * 2], ALU.pow).then_inc(pow2_done, 1)

            def low(g, fc, src, hi, lo, ready, made):
                pool.wait_ge(ready, FC1 * g + fc + 1)
                pool.tensor_tensor(lo[:, fc, :], src[:, fc, :], hi[:, fc, :].bitcast(F32), ALU.subtract)\
                    .then_inc(made, 1)

            def finish(g, u, t):
                pool.wait_ge(mul_done, 8 * g + 2 * t + 2 + 16)
                pool.tensor_tensor(xf[u][:, t, :], x3[u][:, t, :], xf[u][:, t, :], ALU.add).then_inc(finished_high, 1)

            def body(i, c_):
                g, uz = i * XS + c_, (c_ - 1) % XS
                front, main, behind = in_range(i, c_, 2), in_range(i, c_, 0), in_range(i, c_, -1)
                for fc in range(FC1):
                    if main:
                        low(g, fc, hid[c_ % 2], hh, hl, hh_made, hl_made)
                for fc in range(FC1):
                    if behind:
                        low(g - 1, fc, weighted, ch, cl, ch_made, cl_made)
                    if main:
                        low(g, fc, quad, qh, ql, qh_made, ql_made)
                if in_range(i, c_, 3):
                    gather(g + 3)
                if front:
                    power(g + 2)
                if main:
                    power2(g)
                for t in range(T):
                    if in_range(i, c_, 3):
                        add(g + 3, t)
                    if behind and t in (1, 2):
                        finish(g - 1, uz, t + 1)

            pool.sem_inc(added, 4)
            for g in range(3):
                gather(g)
                for t in range(T):
                    add(g, t)
                if g < 2:
                    power(g)
            bodies(pool, body)

        @block.scalar
        def _(act_):
            def halves(i, c_, t):
                g, u = i * XS + c_, c_ % XS
                act_.wait_ge(added, 4 * g + t + 1 + 4)
                act_.activation(msg[:, t, :], msg[:, t, :], ACT.Relu, scale=0.5).then_inc(relu_done, 1)
                act_.wait_ge(y_in[u][t], i * 16 + 16 * (c_ // XS + 1))
                act_.wait_ge(gains, 2 * g + 2)
                act_.activation(x3[u][:, t, :], x3[u][:, t, :], ACT.Identity, bias=middle[:, t:t + 1],
                                scale=gain[:, t:t + 1]).then_inc(affine, 1)

            def norm(g, u):
                act_.wait_ge(shifted, 3 * g + 1)
                for t in range(T):
                    act_.wait_ge(out_done[t], 16 * g + 16)
                    act_.activation(xf[u][:, t, :], x3[u][:, t, :], ACT.Identity, bias=shift[:, t:t + 1],
                                    scale=rs[:, t:t + 1]).then_inc(normed, 1)

            def high(g, n, t):
                act_.wait_ge(turned, 4 * g + t + 1)
                act_.activation(xh[n][:, :, t * P:t * P + P], ptr[:].rearrange("p (c n) -> p c n", n=P), ACT.Copy)\
                    .then_inc(xh_made, 1)

            def hidden(g, n, fc):
                act_.wait_ge(up_done, FC1 * g + fc + 1)
                act_.activation(hid[n][:, fc, :], pu[fc][:], ACT.Relu, bias=ex.b1[:, fc:fc + 1]).then_inc(hid_made, 1)
                act_.wait_ge(hid_made, FC1 * g + fc + 1)
                act_.activation(hh[:, fc, :], hid[n][:, fc, :], ACT.Copy).then_inc(hh_made, 1)

            def part(g, fc, src, hi, ready, made):
                act_.wait_ge(ready, FC1 * g + fc + 1)
                act_.activation(hi[:, fc, :], src[:, fc, :], ACT.Copy).then_inc(made, 1)

            def small_copy(g):
                act_.wait_ge(small_done, g + 1)
                act_.activation(small_t[:], psm[0:SMALL, :], ACT.Copy).then_inc(small_out, 1)

            def softmax_exp(g):
                act_.wait_ge(route, NROUTE * g + EXP_STEP)
                act_.activation(prob[:], prob[:], ACT.Exp).then_inc(exp_done, 1)

            def body(i, c_):
                g, n, n1 = i * XS + c_, c_ % 2, (c_ + 1) % 2
                front, mid, main, behind = (in_range(i, c_, ahead) for ahead in (2, 1, 0, -1))
                if mid:
                    norm(g + 1, (c_ + 1) % XS)
                for fc in range(FC1):
                    if main:
                        hidden(g, n, fc)
                    if mid:
                        high(g + 1, n1, fc)
                    if front:
                        halves(i, c_ + 2, fc)
                if behind:
                    act_.wait_ge(coef_turned, g + 1)
                    act_.activation(coef_t[:], px[0:48, :], ACT.Copy).then_inc(coef_out, 1)
                for fc in range(FC1):
                    if front:
                        halves(i, c_ + 2, 2 + fc)
                    if mid:
                        high(g + 1, n1, 2 + fc)
                    if behind:
                        part(g - 1, fc, weighted, ch, scaled, ch_made)
                    if main:
                        part(g, fc, quad, qh, quad_made, qh_made)
                if main:
                    small_copy(g + 1)
                if mid:
                    softmax_exp(g + 1)

            for t in range(T):
                act_.sem_inc(out_done[t], 16 * XS)
            for g in range(2):
                for t in range(T):
                    halves(0, g, t)
                if g == 0:
                    norm(0, 0)
                    for t in range(T):
                        high(0, 0, t)
                    small_copy(0)
                    softmax_exp(0)
            bodies(act_, body)

        @block.vector
        def _(v):
            v.sem_inc(halved, 4)
            v.sem_inc(mul_done, 16)
            v.memset(parts[:, :, 48:P].bitcast(F32), 0.0).then_inc(consts, 1)
            for n in range(2):
                v.memset(place[:, n, :], float(n)).then_inc(consts, 1)
            v.wait_ge(consts, 3)

            def gains_of(i, c_):
                g = i * XS + c_
                if in_range(i, c_, -1):
                    v.wait_ge(affine, 4 * g)
                hold(v)
                v.tensor_scalar(gain[:], k.dev[:, ds(T * g, T)], 0.5, None, ALU.add).then_inc(gains, 1)
                v.tensor_copy(middle[:], k.mean[:, ds(T * g, T)]).then_inc(gains, 1)

            def sum_(g, u, t):
                v.wait_ge(relu_done, 4 * g + t + 1)
                v.wait_ge(affine, 4 * g + t + 1)
                v.tensor_tensor(x3[u][:, t, :], x3[u][:, t, :], msg[:, t, :], ALU.add).then_inc(halved, 1)

            def statistics(i, c_):
                g, u = i * XS + c_, c_ % XS
                s = Steps(v, stats, NSTAT * g)
                v.wait_ge(halved, 4 * g + 4 + 4)
                if in_range(i, c_, -1):
                    v.wait_ge(normed, 4 * g)
                hold(v)
                for t in range(T):
                    ins = v.bn_stats(st[:, t, :], x3[u][:, t, :])
                s.link(ins)
                hold(v)
                for t in range(T):
                    ins = v.bn_aggr(mv[:, t, :], st[:, t, :])
                s.link(ins)
                s(v.tensor_scalar(shift[:], mv[:, :, 0], -1.0, None, ALU.mult))
                s(v.tensor_scalar(ve[:], mv[:, :, 1], 1e-5, None, ALU.add))

            def shifts(g, u):
                v.wait_ge(pow_done, g + 1)
                v.tensor_tensor(shift[:], shift[:], rs[:], ALU.mult).then_inc(shifted, 1)
                v.tensor_tensor(power_in[:], mv[:, :, 1], rs[:], ALU.mult).then_inc(shifted, 1)
                v.wait_ge(shifted, 3 * g + 2)
                v.tensor_tensor(msq[u][:], power_in[:], rs[:], ALU.mult).then_inc(shifted, 1)

            def low(g, n, t):
                v.wait_ge(xh_made, 4 * g + t + 1)
                v.tensor_tensor(xl[n][:, :, t * P:t * P + P], ptr[:].rearrange("p (c n) -> p c n", n=P),
                                xh[n][:, :, t * P:t * P + P].bitcast(F32), ALU.subtract).then_inc(xl_made, 1)

            def quadratic(g, n, fc):
                v.wait_ge(cross_done, FC1 * g + fc + 1)
                v.scalar_tensor_tensor(quad[:, fc, :], pq[fc][:], ex.cross[:, fc:fc + 1], hid[n][:, fc, :], ALU.add,
                                       ALU.mult).then_inc(quad_made, 1)

            def wide(t_):
                return t_.unsqueeze(2).broadcast_to(S3)

            def small():
                return psm[:, 0:T * SMALL].rearrange("p (t n) -> p t n", t=T)

            def routing(g, n, between):
                s = Steps(v, route, NROUTE * g)
                v.wait_ge(small_turned, g + 1)
                s.link(v.tensor_copy(logit[:], small()[:, :, 0:LOGITS]))
                choice = logit[:, :, 0:EXPERTS1]
                s.link(v.tensor_reduce(top[:], choice, X_AXIS, ALU.max))
                s(v.tensor_tensor(prob[:], choice, wide(top[:]), ALU.subtract))
                assert s.n == EXP_STEP

                def link(ins):
                    s.link(ins)
                    if s.n in between:
                        between[s.n]()
                        s.settle()

                other = choice.unsqueeze(2).broadcast_to([P, T, EXPERTS1, EXPERTS1])
                mine = choice.unsqueeze(3).broadcast_to([P, T, EXPERTS1, EXPERTS1])
                s(v.tensor_tensor(wins[:], other, mine, ALU.is_gt))
                link(v.tensor_tensor(ties[:], other, mine, ALU.is_equal))
                link(v.tensor_tensor(ties[:], ties[:],
                                     ex.earlier[:].unsqueeze(1).broadcast_to([P, T, EXPERTS1, EXPERTS1]), ALU.mult))
                link(v.tensor_tensor(wins[:], wins[:], ties[:], ALU.add))
                link(v.tensor_reduce(rank[:], wins[:], X_AXIS, ALU.add))
                s(v.tensor_tensor(chosen[n][:], rank[:].unsqueeze(2).broadcast_to(S4),
                                  place[:].unsqueeze(1).broadcast_to(S4), ALU.is_equal))
                v.wait_ge(exp_done, g + 1)
                link(v.scalar_tensor_tensor(gate[n][:], rank[:], 1.0, prob[:], ALU.is_le, ALU.mult))
                link(v.tensor_reduce(total[:], gate[n][:], X_AXIS, ALU.add))
                link(v.reciprocal(total[:], total[:]))
                link(v.tensor_tensor(gate[n][:], gate[n][:], wide(total[:]), ALU.mult))
                assert s.n == NROUTE

            def variance(g, n, u):
                s = Steps(v, vars_, NVAR * g)
                v.wait_ge(small_turned, g + 2)
                v.wait_ge(shifted, 3 * g + 3)
                s.link(v.tensor_tensor(var[:], small()[:, :, LOGITS:SMALL], logit[:, :, EXPERTS1:LOGITS], ALU.add))
                s.link(v.tensor_tensor(var[:], var[:], ex.square[:].unsqueeze(1).broadcast_to(S3), ALU.add))
                s.link(v.tensor_scalar(var[:], var[:], 1.0 / D, None, ALU.mult))
                s.link(v.tensor_tensor(var[:], var[:], wide(msq[u][:]), ALU.add))
                s.link(v.tensor_scalar(var[:], var[:], 0.0, 1e-6, ALU.max, ALU.add))
                s.link(v.tensor_tensor(spare[:], chosen[n][:], var[:].unsqueeze(2).broadcast_to(S4), ALU.mult))
                s(v.tensor_reduce(var2[:], spare[:], X_AXIS, ALU.add))
                assert s.n == NVAR

            def coefficients(g, n):
                s = Steps(v, coefs, NCOEF * g)
                v.wait_ge(pow2_done, g + 1)
                v.wait_ge(coef_turned, g + 1)
                s.link(v.tensor_tensor(spare[:], chosen[n][:], rs2[:].unsqueeze(3).broadcast_to(S4), ALU.mult))
                s.link(v.tensor_tensor(coef[:], spare[:, :, 0, :], spare[:, :, 1, :], ALU.add))
                s.link(v.tensor_tensor(coef[:], coef[:], gate[n][:], ALU.mult))
                E1 = EXPERTS1
                for at_, src in ((0, coef), (3 * E1, gate[n])):
                    s(v.tensor_copy(parts[:, :, at_:at_ + E1], src[:]))
                    s.link(v.tensor_copy(parts[:, :, at_ + E1:at_ + 2 * E1], src[:]))
                    s(v.tensor_tensor(parts[:, :, at_ + 2 * E1:at_ + 3 * E1], src[:],
                                      parts[:, :, at_:at_ + E1].bitcast(F32), ALU.subtract))
                assert s.n == NCOEF

            def scale(g, n, fc):
                v.wait_ge(spread_done, FC1 * g + fc + 1)
                v.tensor_tensor(weighted[:, fc, :], hid[n][:, fc, :], pb[:], ALU.mult).then_inc(scaled, 1)

            def finish(g, u, t):
                v.wait_ge(x_done, 4 * g + t + 1)
                v.tensor_tensor(xf[u][:, t, :], xf[u][:, t, :], pox[t][:], ALU.mult).then_inc(mul_done, 1)
                v.wait_ge(one_done, 4 * g + t + 1)
                v.tensor_tensor(x3[u][:, t, :], x3[u][:, t, :], po1[t][:], ALU.add).then_inc(mul_done, 1)
                if t < 2:
                    v.wait_ge(mul_done, 8 * g + 2 * t + 2 + 16)
                    v.tensor_tensor(xf[u][:, t, :], x3[u][:, t, :], xf[u][:, t, :], ALU.add).then_inc(finished_low, 1)

            def body(i, c_):
                g, n, n1 = i * XS + c_, c_ % 2, (c_ + 1) % 2
                u2, uz = (c_ + 2) % XS, (c_ - 1) % XS
                front, mid, main, behind = (in_range(i, c_, ahead) for ahead in (2, 1, 0, -1))
                if behind:
                    coefficients(g - 1, n1)
                for t in range(2):
                    if mid:
                        low(g + 1, n1, t)
                    if front:
                        sum_(g + 2, u2, t)
                for fc in range(FC1):
                    if behind:
                        scale(g - 1, n1, fc)
                    if mid:
                        low(g + 1, n1, 2 + fc)
                    if main:
                        quadratic(g, n, fc)
                    if front:
                        sum_(g + 2, u2, 2 + fc)
                if front:
                    statistics(i, c_ + 2)
                if in_range(i, c_, 3):
                    gains_of(i, c_ + 3)
                if behind:
                    finish(g - 1, uz, 0)
                if main:
                    variance(g, n, c_ % XS)
                if behind:
                    finish(g - 1, uz, 1)

                def between():
                    if front:
                        shifts(g + 2, u2)
                    if behind:
                        finish(g - 1, uz, 2)

                if mid:
                    routing(g + 1, n1, {7: between})
                else:
                    between()
                if behind:
                    finish(g - 1, uz, 3)

            gains_of(0, 0)
            for g in range(2):
                for t in range(T):
                    sum_(g, g, t)
                statistics(0, g)
                gains_of(0, g + 1)
                shifts(g, g)
                if g == 0:
                    for t in range(T):
                        low(0, 0, t)
                    routing(0, 0, {})
            bodies(v, body)

        @block.tensor
        def _(pe):
            pe.sem_inc(coef_turned, 1)
            pe.wait_ge(consts, 3)

            def turn(g, u, t, first=False):
                pe.wait_ge(normed, 4 * g + t + 1)
                if not first:
                    pe.wait_ge(xl_made, 4 * g + t)
                for kc in range(KC):
                    last = pe.transpose(ptr[:, kc * P:kc * P + P], xf[u][:, t, kc * P:kc * P + P], k.ident[:])
                last.then_inc(turned, 1)

            def logits(g, n, alone):
                pe.wait_ge(xl_made, 4 * g + 4)
                for kc in range(KC):
                    last = split3(pe, psm[:], (ex.route[0][:, kc, :], ex.route[1][:, kc, :]),
                                  (xh[n][:, kc, :], xl[n][:, kc, :]), kc == 0, kc == KC - 1 and alone)
                if alone:
                    last.then_inc(small_done, 1)

            def squares(g, alone):
                for fc in range(FC1):
                    pe.wait_ge(ql_made, FC1 * g + fc + 1)
                    for n, q in enumerate((qh, ql)):
                        last = pe.matmul(psm[:], ex.expert[:, fc, :], q[:, fc, :], start=alone and fc == 0 and n == 0,
                                         stop=fc == FC1 - 1 and n == 1, skip_group_check=True)
                last.then_inc(small_done, 1)

            def turn_small(g):
                pe.wait_ge(small_out, g + 1)
                for t in range(T):
                    last = pe.matmul(psm[:, t * SMALL:(t + 1) * SMALL], small_t[:, t * P:t * P + P],
                                     k.ident[0:SMALL, 0:SMALL], start=True, stop=True)
                last.then_inc(small_turned, 1)

            def up(g, n, fc):
                if fc == 0:
                    pe.wait_ge(mul_done, 8 * g + 2)
                sl = slice(fc * P, fc * P + P)
                for kc in range(KC):
                    last = split3(pe, pu[fc][:], (ex.w1[0][:, kc, sl], ex.w1[1][:, kc, sl]),
                                  (xh[n][:, kc, :], xl[n][:, kc, :]), kc == 0, kc == KC - 1)
                last.then_inc(up_done, 1)

            def cross(g, n, fc):
                if fc == 0:
                    pe.wait_ge(mul_done, 8 * g + 6)
                sl = slice(fc * P, fc * P + P)
                for kc in range(KC):
                    split3(pe, pq[fc][:], (ex.w2t[0][:, kc, sl], ex.w2t[1][:, kc, sl]),
                           (xh[n][:, kc, :], xl[n][:, kc, :]), kc == 0, False)

            def gram(g, fc):
                pe.wait_ge(hl_made, FC1 * g + fc + 1)
                split3(pe, pq[fc][:], (ex.gram[0][:, fc, :], ex.gram[1][:, fc, :]), (hh[:, fc, :], hl[:, fc, :]),
                       False, True).then_inc(cross_done, 1)

            def turn_coef(g):
                pe.wait_ge(coefs, NCOEF * g + NCOEF)
                pe.wait_ge(mul_done, 8 * g + 16)
                for t in range(T):
                    last = pe.transpose(px[:, t * P:t * P + P], parts[:, t, :].bitcast(F32), k.ident[:])
                last.then_inc(coef_turned, 1)

            def spread(g, fc):
                if fc:
                    pe.wait_ge(scaled, FC1 * g + fc)
                else:
                    pe.wait_ge(coef_out, g + 1)
                pe.matmul(pb[:], ex.spread[:, fc * P:fc * P + P], coef_t[:], start=True, stop=True)\
                  .then_inc(spread_done, 1)

            def product(g, t, main):
                sl = slice(t * P, t * P + P)
                if t == 0:
                    pe.wait_ge(cl_made, FC1 * g + FC1)
                    if main:
                        pe.wait_ge(hid_made, FC1 * g + 2 * FC1)
                if t == 3:
                    pe.wait_ge(mul_done, 8 * g + 4 + 16)
                pe.matmul(pox[t][:], coef_t[:, sl], ex.rows_x[:], start=True, stop=True).then_inc(x_done, 1)
                pe.matmul(po1[t][:], coef_t[:, sl], ex.rows_1[:], start=True, stop=False, skip_group_check=True)
                for fc in range(FC1):
                    last = split3(pe, po1[t][:], (ch[:, fc, sl], cl[:, fc, sl]),
                                  (ex.w2g[0][:, fc, :], ex.w2g[1][:, fc, :]), False, fc == FC1 - 1)
                last.then_inc(one_done, 1)

            def body(i, c_):
                g, n, n1, u1 = i * XS + c_, c_ % 2, (c_ + 1) % 2, (c_ + 1) % XS
                mid, main, behind = (in_range(i, c_, ahead) for ahead in (1, 0, -1))
                for fc in range(FC1):
                    if main:
                        up(g, n, fc)
                    if mid:
                        turn(g + 1, u1, fc)
                if behind:
                    turn_coef(g - 1)
                for fc in range(FC1):
                    if main:
                        cross(g, n, fc)
                    if mid:
                        turn(g + 1, u1, 2 + fc)
                    if behind:
                        spread(g - 1, fc)
                    if main:
                        gram(g, fc)
                if main:
                    if mid:
                        pe.wait_ge(route, NROUTE * g + 1)
                        logits(g + 1, n1, False)
                    squares(g, not mid)
                if behind:
                    product(g - 1, 0, main)
                if main:
                    turn_small(g + 1)
                if behind:
                    for t in range(1, T):
                        product(g - 1, t, main)

            for t in range(T):
                turn(0, 0, t, t == 0)
            logits(0, 0, True)
            turn_small(0)
            bodies(pe, body)




class Tables:
    pass


def program(nc, a, out):
    def dram(name, shape, dt=F32):
        return nc.dram_tensor(name, shape, dt).ap()

    with ExitStack() as stack:
        c = Core(nc, stack, "net")
        k = Tables()
        k.rec_s, k.rec_d = dram("rec_s", [EP + 1, REC_S], I32), dram("rec_d", [EP + 1, REC_D], I32)
        k.slots = {x: dram(f"slots_{x}", [NPAD, 1], I32) for x in "sd"}
        k.values, k.message1, k.message2 = (dram(n, [EP, D]) for n in ("values", "message1", "message2"))
        k.y, k.h, k.own = (dram(n, [NPAD, D]) for n in ("y", "h", "own"))
        k.ident, k.ones = c.sb("ident", [P, P]), c.sb("ones", [P, P])
        k.half_neg = c.sb("half_neg", [P, 32])
        k.slot = {x: c.sb(f"slot_{x}", [P, NT], I32) for x in "sd"}
        k.mean, k.dev = c.sb("mean", [P, NT]), c.sb("dev", [P, NT])
        with ExitStack() as edges:
            ce = Core(nc, edges, "edges")
            k.zeros, k.b12 = ce.sb("zeros", [P, D]), ce.sb("b12", [P, D])
            k.same = {x: ce.sb(f"same_{x}", [P, EP + 1], BF16) for x in "sd"}
            k.rec = {"s": ce.sb("rec_s", [P, ET, REC_S], I32), "d": ce.sb("rec_d", [P, ET, REC_D], I32)}
            sort_phase(nc, a, k)
            attention_phase(nc, a, k)
            dense0_phase(nc, a, k)
            conv_phase(nc, a, k)
            message2_phase(nc, a, k)
        dense1_phase(nc, a, k, out)


def columns(v):
    return v.reshape(-1, P, *v.shape[1:]).swapaxes(0, 1)


def kernel(x, src, dst, edge_attr_8, edge_weight, node_vec, L0_gnn_ln_g, L0_gnn_ln_b, L0_gnn_Wq, L0_gnn_bq,
           L0_gnn_Wk, L0_gnn_bk, L0_gnn_Wv, L0_gnn_bv, L0_gnn_W1, L0_gnn_b1, L0_gnn_W2, L0_gnn_b2, L0_ffn_Wr,
           L0_ffn_br, L0_ffn_Wgate, L0_ffn_bgate, L0_ffn_W1, L0_ffn_W3, L0_ffn_W2, L1_gnn_W0_1, L1_gnn_W1_1,
           L1_gnn_b1, L1_gnn_W0_2, L1_gnn_W1_2, L1_gnn_b2, L1_ffn_router_w, L1_ffn_w1, L1_ffn_b1, L1_ffn_w2,
           L1_ffn_b2, L1_ffn_gamma, L1_ffn_beta):
    import numpy as np
    import concourse.bacc as bacc
    from concourse.bass_utils import run_bass_kernel_spmd

    def padded(v, rows, fill):
        v = np.asarray(v)
        return np.concatenate([v, np.full((rows - len(v),) + v.shape[1:], fill, v.dtype)])

    def row(v):
        return np.asarray(v).reshape(1, -1)

    def column(v):
        return columns(np.asarray(v))

    src, dst = padded(src, EP, N), padded(dst, EP, N)
    arrays = {
        "x": padded(x, NPAD, 0), "key_s": row(src), "key_d": row(dst), "col_s": column(src), "col_d": column(dst),
        "attr": column(padded(edge_attr_8, EP, 0)), "edge_w": column(padded(edge_weight, EP, 0)),
        "diag": column(padded(node_vec, NPAD, 0)),
        "ln_g": column(L0_gnn_ln_g), "ln_b": column(L0_gnn_ln_b),
        "wq": L0_gnn_Wq, "wk": L0_gnn_Wk, "wv": L0_gnn_Wv,
        "bq": column(L0_gnn_bq), "bk": column(L0_gnn_bk), "bv": column(L0_gnn_bv),
        "w1t": np.asarray(L0_gnn_W1).T, "w2": L0_gnn_W2, "b1_col": column(L0_gnn_b1), "b2_row": row(L0_gnn_b2),
        "e_w1": np.asarray(L0_ffn_W1).transpose(1, 0, 2).reshape(D, -1),
        "e_w3": np.asarray(L0_ffn_W3).transpose(1, 0, 2).reshape(D, -1),
        "e_w2": np.asarray(L0_ffn_W2).reshape(-1, D),
        "e_wr": np.concatenate([L0_ffn_Wr, np.asarray(L0_ffn_Wgate).transpose(1, 0, 2).reshape(D, -1)], 1),
        "e_br": row(np.concatenate([L0_ffn_br, np.asarray(L0_ffn_bgate).reshape(-1)])),
        "g_w01": L1_gnn_W0_1, "g_w11": L1_gnn_W1_1, "g_w02": L1_gnn_W0_2, "g_w12": L1_gnn_W1_2,
        "g_b1": row(L1_gnn_b1), "g_b2": row(L1_gnn_b2),
        "f_w1": np.asarray(L1_ffn_w1).transpose(1, 0, 2).reshape(D, -1),
        "f_w2": np.asarray(L1_ffn_w2).reshape(-1, D), "f_b1": np.asarray(L1_ffn_b1).reshape(-1, P).T,
        "f_router": L1_ffn_router_w, "f_b2": L1_ffn_b2, "f_gamma": L1_ffn_gamma, "f_beta": L1_ffn_beta,
    }
    arrays = {f"in_{name}": np.ascontiguousarray(v) for name, v in arrays.items()}

    nc = bacc.Bacc("TRN2", target_bir_lowering=False, num_devices=1)
    a = {name[3:]: nc.dram_tensor(name, v.shape, mybir.dt.from_np(v.dtype), kind="ExternalInput").ap()
         for name, v in arrays.items()}
    out = nc.dram_tensor("out", [NPAD, D], F32, kind="ExternalOutput").ap()
    program(nc, a, out)
    result = run_bass_kernel_spmd(nc, [arrays], core_ids=[0])
    return result.results[0]["out"][:N]
```

```python
from contextlib import ExitStack

import concourse.bass as bass
from concourse import mybir

F32 = mybir.dt.float32
F32R = mybir.dt.float32r
BF16 = mybir.dt.bfloat16
I32 = mybir.dt.int32
ALU = mybir.AluOpType
ACT = mybir.ActivationFunctionType
X_AXIS = mybir.AxisListType.X

P = 128
D = 512
KC = D // P
N = 10000
NG = 20
T = 4
GR = T * P
NT = NG * T
NPAD = NG * GR
E = 2500
ET = 20
EG = ET // T
EP = ET * P
HEADS = 8
HD = D // HEADS
NO_SLOT = 1 << 20
REC_S = 12
REC_D = 4
EXPERTS0 = 16
XS = 4
SETS = 5
EXPERTS1 = 8
HID1 = 32
LOGITS = 2 * EXPERTS1
SMALL = 3 * EXPERTS1
FC1 = EXPERTS1 * HID1 // P


def ds(a, n):
    return bass.ds(a, n)


def split3(te, out, lhs, rhs, first=True, last=True):
    te.matmul(out, lhs[0], rhs[0], start=first, stop=False, skip_group_check=True)
    te.matmul(out, lhs[0], rhs[1], start=False, stop=False, skip_group_check=True)
    return te.matmul(out, lhs[1], rhs[0], start=False, stop=last, skip_group_check=True)


def hold(eng):
    eng.nop(nofuse=True)


class Steps:

    def __init__(self, eng, sem, base=0):
        self.eng, self.sem, self.base, self.n = eng, sem, base, 0

    def __call__(self, ins):
        ins.then_inc(self.sem, 1)
        self.n += 1
        return ins

    def settle(self):
        self.eng.wait_ge(self.sem, self.base + self.n)

    def link(self, ins):
        self(ins)
        self.settle()


class Core:

    def __init__(self, nc, stack, tag, side="left"):
        self.nc, self.stack, self.tag, self.side = nc, stack, tag, side
        self.sems = []
        stack.callback(self.release)

    def sb(self, name, shape, dt=F32):
        return self.stack.enter_context(self.nc.sbuf_tensor(f"{self.tag}_{name}", shape, dt, side=self.side))

    def ps(self, name):
        return self.stack.enter_context(self.nc.psum_tensor(f"{self.tag}_{name}", [P, D], F32))

    def sem(self, name):
        self.sems.append(self.nc.alloc_semaphore(name=f"{self.tag}_{name}"))
        return self.sems[-1]

    def release(self):
        if self.sems:
            self.nc.clear_and_free_semaphores(self.sems)
            self.nc.all_engine_barrier()



def sort_phase(nc, a, k):
    with ExitStack() as stack:
        c = Core(nc, stack, "sort")
        raw = {x: c.sb(f"raw_{x}", [P, EP], I32) for x in "sd"}
        row = {x: c.sb(f"row_{x}", [P, EP]) for x in "sd"}
        col_i = {x: c.sb(f"col_i_{x}", [P, ET], I32) for x in "sd"}
        col = {x: c.sb(f"col_{x}", [P, ET]) for x in "sd"}
        lower = {x: c.sb(f"lower_{x}", [P, ET]) for x in "sd"}
        upper = {x: c.sb(f"upper_{x}", [P, ET]) for x in "sd"}
        middle = {x: c.sb(f"middle_{x}", [P, ET]) for x in "sd"}
        tri = c.sb("tri", [P, P])
        diag = {x: c.sb(f"diag_{x}", [P, ET, P]) for x in "sd"}
        mask = {e: c.sb(f"mask_{e}", [P, 4, EP], BF16) for e in ("dve", "act")}
        ones = c.sb("ones", [P, 1], BF16)
        one = c.sb("one", [1, 1])
        rank_row = {x: c.sb(f"rank_row_{x}", [1, EP]) for x in "sd"}
        rank = {x: c.sb(f"rank_{x}", [P, ET], I32) for x in "sd"}
        rec = {"s": c.sb("rec_s", [P, ET, REC_S], I32), "d": c.sb("rec_d", [P, ET, REC_D], I32)}
        attr = c.sb("attr", [P, ET, HEADS])
        edge_w = c.sb("edge_w", [P, ET])
        no_slot = c.sb("no_slot", [P, NPAD // P], I32)
        counts = [c.ps(f"counts{n}") for n in range(EP // D)]
        rank_cols = c.ps("rank_cols")
        keys_in, tri_made = c.sem("keys_in"), c.sem("tri_made")
        rec_in, rec_made = c.sem("rec_in"), c.sem("rec_made")
        dve, act = c.sem("dve"), c.sem("act")
        mask_made = {e: c.sem(f"mask_made_{e}") for e in ("dve", "act")}
        mask_used = {e: c.sem(f"mask_used_{e}") for e in ("dve", "act")}
        maker = ["act" if j % 5 in (1, 3) else "dve" for j in range(ET)]
        SIGN_TILES = maker.count("act")

        def made_before(x, j, e):
            return (maker.count(e) if x == "d" else 0) + maker[:j].count(e)

        row_made = c.sem("row_made")
        cols_made = c.sem("cols_made")
        rank_made = c.sem("rank_made")
        tails_made, stored, scattered = c.sem("tails_made"), c.sem("stored"), c.sem("scattered")
        block = stack.enter_context(nc.Block())

        @block.sync
        def _(sp):
            for x in "sd":
                sp.dma_start(raw[x][:], a[f"key_{x}"].broadcast_to([P, EP])).then_inc(keys_in, 16)
                sp.dma_start(col_i[x][:], a[f"col_{x}"]).then_inc(keys_in, 16)
            sp.dma_start(attr[:], a["attr"]).then_inc(rec_in, 16)
            sp.dma_start(edge_w[:], a["edge_w"]).then_inc(rec_in, 16)
            sp.wait_ge(tails_made, 1)
            sp.dma_start(k.rec_s[EP:EP + 1, :], no_slot[0:1, 0:REC_S]).then_inc(stored, 16)
            sp.dma_start(k.rec_d[EP:EP + 1, :], no_slot[0:1, 0:REC_D]).then_inc(stored, 16)
            for x in "sd":
                sp.dma_start(k.slots[x].rearrange("(p n) o -> p (n o)", p=P), no_slot[:]).then_inc(stored, 16)
            sp.wait_ge(stored, 16 * 4)

        @block.gpsimd
        def _(pool):
            pool.memset(tri[:], 0.5).then_inc(tri_made, 1)
            pool.wait_ge(tri_made, 1)
            pool.affine_select(out=tri[:], in_=tri[:], compare_op=ALU.is_gt, fill=0.0, base=0,
                               pattern=[[1, P]], channel_multiplier=-1).then_inc(tri_made, 1)
            pool.memset(no_slot[:], NO_SLOT).then_inc(tails_made, 1)
            pool.memset(k.ident[:], 0.0).then_inc(tri_made, 1)
            pool.wait_ge(tri_made, 3)
            pool.affine_select(out=k.ident[:], in_=k.ident[:], compare_op=ALU.not_equal, fill=1.0,
                               base=0, pattern=[[-1, P]], channel_multiplier=1).then_inc(tri_made, 1)
            r = Steps(pool, rec_made)
            r(pool.memset(rec["s"][:, :, 2 + HEADS:REC_S], 0))
            r(pool.memset(rec["d"][:, :, 3:REC_D], 0))
            pool.wait_ge(keys_in, 64)
            pool.wait_ge(rec_in, 32)
            for x in "sd":
                r(pool.tensor_copy(rec[x][:, :, 0], col_i["s"][:]))
                r(pool.tensor_copy(rec[x][:, :, 1], col_i["d"][:]))
            r(pool.tensor_copy(rec["s"][:, :, 2:2 + HEADS].bitcast(F32), attr[:]))
            r(pool.tensor_copy(rec["d"][:, :, 2].bitcast(F32), edge_w[:]))
            r.settle()
            for n, (x, out) in enumerate((("s", k.rec_s), ("d", k.rec_d))):
                pool.wait_ge(rank_made, n + 1)
                for t in range(ET):
                    pool.indirect_dma_start(out[:, :], bass.IndirectOffsetOnAxis(ap=rank[x][:, t:t + 1], axis=0),
                                            rec[x][:, t, :], None, bounds_check=EP - 1,
                                            oob_is_err=False).then_inc(scattered, 16)
            pool.wait_ge(scattered, 2 * ET * 16)

        def mask_pieces(j):
            return (0, j * P), (j * P + P, EP), (j * P, j * P + P)

        @block.vector
        def _(v):
            s = Steps(v, dve)
            s(v.memset(ones[:], 1.0))
            s(v.memset(one[:], 1.0))
            v.wait_ge(keys_in, 64)
            for x in "sd":
                s(v.tensor_copy(row[x][:], raw[x][:]))
                s(v.tensor_copy(col[x][:], col_i[x][:]))
            s.settle()
            for x in "sd":
                s(v.tensor_scalar(lower[x][:], col[x][:], -1.0, -0.5, ALU.mult, ALU.add))
                s(v.tensor_scalar(upper[x][:], col[x][:], -1.0, 0.5, ALU.mult, ALU.add))
                s(v.tensor_scalar(middle[x][:], col[x][:], -1.0, -0.25, ALU.mult, ALU.add))
            v.wait_ge(tri_made, 2)
            for x in "sd":
                s(v.tensor_tensor(diag[x][:], row[x][:].rearrange("p (t n) -> p t n", n=P),
                                  tri[:].unsqueeze(1).broadcast_to([P, ET, P]), ALU.add))
            s.settle()
            assert s.n == 14

            def masks(x):
                for j in range(ET):
                    if maker[j] != "dve":
                        continue
                    n = made_before(x, j, "dve")
                    m = mask["dve"][:, n % 4]
                    key = col[x][:, j:j + 1]
                    before, after, own = mask_pieces(j)
                    if n >= 4:
                        v.wait_ge(mask_used["dve"], n - 3)
                    if before[1]:
                        v.tensor_scalar(m[:, before[0]:before[1]], row[x][:, before[0]:before[1]], key, 2.0,
                                        ALU.is_gt, ALU.mult)
                    if after[0] < EP:
                        v.tensor_scalar(m[:, after[0]:after[1]], row[x][:, after[0]:after[1]], key, 2.0,
                                        ALU.is_ge, ALU.mult)
                    v.tensor_scalar(m[:, own[0]:own[1]], diag[x][:, j, :], key, 2.0,
                                    ALU.is_gt, ALU.mult).then_inc(mask_made["dve"], 1)

            def ranks(n, x):
                v.wait_ge(mask_used[maker[-1]], made_before(x, ET, maker[-1]))
                for m in range(EP // D):
                    v.tensor_scalar(rank_row[x][:, m * D:m * D + D], counts[m][0:1, :], 0.5, float(P // 2 * SIGN_TILES),
                                    ALU.mult, ALU.add).then_inc(row_made, 1)

            masks("s")
            ranks(0, "s")
            masks("d")
            v.wait_ge(cols_made, 1)
            v.tensor_copy(rank["s"][:], rank_cols[:, 0:ET]).then_inc(rank_made, 1)
            ranks(1, "d")
            v.wait_ge(cols_made, 2)
            v.tensor_copy(rank["d"][:], rank_cols[:, 0:ET]).then_inc(rank_made, 1)
            v.wait_ge(rank_made, 2)

        @block.scalar
        def _(act_):
            act_.wait_ge(dve, 14)
            for x in "sd":
                for j in range(ET):
                    if maker[j] != "act":
                        continue
                    n = made_before(x, j, "act")
                    m = mask["act"][:, n % 4]
                    before, after, own = mask_pieces(j)
                    if n >= 4:
                        act_.wait_ge(mask_used["act"], n - 3)
                    if before[1]:
                        act_.activation(m[:, before[0]:before[1]], row[x][:, before[0]:before[1]],
                                        ACT.Sign, bias=lower[x][:, j:j + 1])
                    if after[0] < EP:
                        act_.activation(m[:, after[0]:after[1]], row[x][:, after[0]:after[1]],
                                        ACT.Sign, bias=upper[x][:, j:j + 1])
                    act_.activation(m[:, own[0]:own[1]], diag[x][:, j, :], ACT.Sign,
                                    bias=middle[x][:, j:j + 1]).then_inc(mask_made["act"], 1)

        @block.tensor
        def _(pe):
            pe.wait_ge(dve, 2)
            for n, x in enumerate("sd"):
                if n:
                    pe.wait_ge(row_made, 5)
                for j in range(ET):
                    e = maker[j]
                    slot = made_before(x, j, e)
                    pe.wait_ge(mask_made[e], slot + 1)
                    for m in range(EP // D):
                        last = pe.matmul(counts[m][0:1, :], ones[:], mask[e][:, slot % 4, m * D:m * D + D],
                                         start=j == 0, stop=j == ET - 1)
                    last.then_inc(mask_used[e], 1)
                pe.wait_ge(row_made, 5 * (n + 1))
                if n:
                    pe.wait_ge(rank_made, 1)
                for t in range(ET):
                    last = pe.matmul(rank_cols[:, t:t + 1], rank_row[x][:, t * P:t * P + P], one[:],
                                     start=True, stop=True)
                last.then_inc(cols_made, 1)



def edge_columns(v, s, key, next_key, places, flag, slot_at):
    s.link(v.tensor_tensor(places[:, 0:ET], key, next_key, ALU.is_equal))
    s(v.tensor_copy(flag, places[:, 0:ET]))
    s(v.tensor_scalar(places[:, ET:2 * ET], key, 7, None, ALU.logical_shift_right))
    s.link(v.tensor_scalar(places[:, 2 * ET:3 * ET], key, 127, None, ALU.bitwise_and))
    s.link(v.tensor_scalar(places[:, 2 * ET:3 * ET], places[:, 2 * ET:3 * ET], NT, None, ALU.mult))
    s.link(v.tensor_tensor(places[:, ET:2 * ET], places[:, ET:2 * ET], places[:, 2 * ET:3 * ET], ALU.add))
    s.link(v.tensor_scalar(places[:, 0:ET], places[:, 0:ET], NO_SLOT, None, ALU.mult))
    s.link(v.tensor_tensor(slot_at, places[:, ET:2 * ET], places[:, 0:ET], ALU.add))


def attention_phase(nc, a, k):
    with ExitStack() as stack:
        c = Core(nc, stack, "att")
        same, rec = k.same, k.rec
        hi = {n: c.sb(f"{n}_hi", [P, KC, D], F32R) for n in ("wq", "wk", "wv", "w12")}
        lo = {n: c.sb(f"{n}_lo", [P, KC, D], F32R) for n in ("wq", "wk", "wv", "w12")}
        ln_g, ln_b = c.sb("ln_g", [P, KC]), c.sb("ln_b", [P, KC])
        bias_in = c.sb("bias_in", [P, 3, KC])
        bias = c.sb("bias", [P, 3, KC])
        headsel = c.sb("headsel", [P, KC, HEADS])
        headsel2 = c.sb("headsel2", [HEADS, D])
        flags_ready = c.sem("flags_ready")

        recs_in, made, chain = c.sem("recs_in"), c.sem("made"), c.sem("chain")
        diagonal_summed, diagonal_made = c.sem("diagonal_summed"), c.sem("diagonal_made")
        stage_in = [c.sem(f"stage_in{n}") for n in range(2)]
        stage_free, hi_made, prep = c.sem("stage_free"), c.sem("hi_made"), c.sem("prep")
        small_in, w12_done, b12_done, bias_done = (c.sem(n) for n in ("small_in", "w12_done", "b12_done", "bias_done"))
        slots_out = c.sem("slots_out")
        w_scaled = c.sem("w_scaled")
        split_done = c.sem("split_done")
        slots_in = c.sem("slots_in")

        with ExitStack() as inner:
            ci = Core(nc, inner, "prep")
            stage = [ci.sb(f"stage{n}", [P, KC, D]) for n in range(2)]
            next_key = {x: ci.sb(f"next_key_{x}", [P, ET], I32) for x in "sd"}
            places = ci.sb("places", [P, 3 * ET], I32)
            slot_at = {x: ci.sb(f"slot_at_{x}", [P, ET], I32) for x in "sd"}
            own_place = ci.sb("own_place", [P, ET], I32)
            flag = {x: ci.sb(f"flag_{x}", [P, ET], BF16) for x in "sd"}
            flag_diag = ci.sb("flag_diag", [P, 2, T, P], BF16)
            ones_bf = ci.sb("ones_bf", [P, P], BF16)
            b1_col = ci.sb("b1_col", [P, KC])
            b1_wide = ci.sb("b1_wide", [P, KC, P])
            b2_row = ci.sb("b2_row", [1, D])
            ones_row = ci.sb("ones_row", [1, P])
            w1t = ci.sb("w1t", [P, KC, D])
            w2 = ci.sb("w2", [P, KC, D])
            w12 = ci.sb("w12", [P, KC, D])
            pk = [ci.ps(f"pk{n}") for n in range(2)]
            pb = ci.ps("pb")
            pw = [ci.ps(f"pw{n}") for n in range(2)]
            names = ("wq", "wk", "wv")
            w1_in = ci.sem("w1_in")
            rows_made = ci.sem("rows_made")
            block = inner.enter_context(nc.Block())

            @block.sync
            def _(sp):
                for x, t, w in (("s", k.rec_s, REC_S), ("d", k.rec_d, REC_D)):
                    sp.dma_start(rec[x][:], t[0:EP, :].rearrange("(t p) w -> p t w", p=P)).then_inc(recs_in, 16)
                    kk = 0 if x == "s" else 1
                    with nc.allow_non_contiguous_dma(reason="one word of each record"):
                        sp.dma_start(next_key[x][:], t[1:EP + 1, kk:kk + 1].rearrange("(t p) w -> p (t w)", p=P))\
                          .then_inc(recs_in, 16)
                for t, s in ((ln_g, "ln_g"), (ln_b, "ln_b"), (b1_col, "b1_col"), (b2_row, "b2_row")):
                    sp.dma_start(t[:], a[s]).then_inc(small_in, 16)
                for n, s in enumerate(("bq", "bk", "bv")):
                    sp.dma_start(bias_in[:, n, :], a[s]).then_inc(small_in, 16)
                sp.dma_start(w1t[:], a["w1t"].rearrange("(c p) n -> p c n", p=P)).then_inc(w1_in, 16)
                sp.dma_start(w2[:], a["w2"].rearrange("(c p) n -> p c n", p=P)).then_inc(w1_in, 16)
                for n, name in enumerate(names):
                    if n >= 2:
                        sp.wait_ge(split_done, n - 1)
                    sp.dma_start(stage[n % 2][:], a[name].rearrange("(c p) n -> p c n", p=P)).then_inc(stage_in[n % 2], 16)
                sp.wait_ge(slots_out, 2 * ET * 16)
                for x in "sd":
                    sp.dma_start(k.slot[x][:], k.slots[x].rearrange("(p n) o -> p (n o)", p=P)).then_inc(slots_in, 16)
                sp.wait_ge(slots_in, 32)

            @block.gpsimd
            def _(pool):
                s = Steps(pool, made)
                s(pool.iota(own_place[:], pattern=[[P, ET]], base=0, channel_multiplier=1))
                s(pool.memset(headsel[:], HD ** -0.5))
                s(pool.memset(headsel2[:], 1.0))
                s(pool.memset(ones_row[:], 1.0))
                s(pool.memset(k.zeros[:], 0.0))
                s(pool.memset(k.ones[:], 1.0))
                s(pool.memset(k.half_neg[:], -0.5))
                s(pool.memset(ones_bf[:], 1.0))
                s.settle()
                s.link(pool.affine_select(out=headsel[:], in_=headsel[:], compare_op=ALU.is_ge, fill=0.0, base=0,
                                          pattern=[[P, KC], [-HD, HEADS]], channel_multiplier=1))
                s.link(pool.affine_select(out=headsel[:], in_=headsel[:], compare_op=ALU.is_ge, fill=0.0, base=HD - 1,
                                          pattern=[[-P, KC], [HD, HEADS]], channel_multiplier=-1))
                s.link(pool.affine_select(out=headsel2[:], in_=headsel2[:], compare_op=ALU.is_ge, fill=0.0, base=0,
                                          pattern=[[1, D]], channel_multiplier=-HD))
                s.link(pool.affine_select(out=headsel2[:], in_=headsel2[:], compare_op=ALU.is_ge, fill=0.0,
                                          base=HD - 1, pattern=[[-1, D]], channel_multiplier=HD))
                for n, x in enumerate("sd"):
                    pool.wait_ge(chain, 8 * (n + 1))
                    for t in range(ET):
                        pool.indirect_dma_start(k.slots[x][:, :],
                                                bass.IndirectOffsetOnAxis(ap=slot_at[x][:, t:t + 1], axis=0),
                                                own_place[:, t:t + 1], None, bounds_check=NPAD - 1,
                                                oob_is_err=False).then_inc(slots_out, 16)

            @block.vector
            def _(v):
                s = Steps(v, chain)
                v.wait_ge(recs_in, 64)
                for n, x in enumerate("sd"):
                    edge_columns(v, s, rec[x][:, :, n], next_key[x][:], places, flag[x][:], slot_at[x][:])
                v.wait_ge(small_in, 7 * 16)
                for kc in range(KC):
                    s(v.tensor_copy(b1_wide[:, kc, :], b1_col[:, kc:kc + 1].broadcast_to([P, P])))
                s.settle()
                assert s.n == 20
                q = Steps(v, rows_made)
                for x in "sd":
                    q(v.memset(same[x][:, 0:1], 0.0))
                for i in range(2 * EG):
                    if i >= 2:
                        v.wait_ge(diagonal_summed, i - 1)
                    v.tensor_tensor(flag_diag[:, i % 2], k.ident[:].unsqueeze(1).broadcast_to([P, T, P]),
                                    flag["sd"[i // EG]][:, (i % EG) * T:(i % EG) * T + T].unsqueeze(2)
                                    .broadcast_to([P, T, P]), ALU.mult).then_inc(diagonal_made, 1)
                for n in range(3):
                    v.wait_ge(stage_in[n % 2], 16 * (n // 2 + 1))
                    v.wait_ge(bias_done, n + 1)
                    for kc in range(KC):
                        ins = v.tensor_scalar(stage[n % 2][:, kc, :], stage[n % 2][:, kc, :], ln_g[:, kc:kc + 1], None,
                                              ALU.mult)
                    ins.then_inc(w_scaled, 1)
                    v.wait_ge(hi_made, n + 1)
                    v.tensor_tensor(lo[names[n]][:], stage[n % 2][:], hi[names[n]][:].bitcast(F32), ALU.subtract)\
                     .then_inc(split_done, 1)
                v.wait_ge(bias_done, 3)
                q(v.tensor_tensor(bias[:], bias_in[:], pb[:, 0:3 * KC].rearrange("p (n c) -> p n c", n=3), ALU.add))
                for c4 in range(KC):
                    v.wait_ge(w12_done, c4 + 1)
                    v.tensor_copy(w12[:, c4, :], pw[c4 % 2][:]).then_inc(w_scaled, 1)
                v.wait_ge(hi_made, 4)
                v.tensor_tensor(lo["w12"][:], w12[:], hi["w12"][:].bitcast(F32), ALU.subtract).then_inc(split_done, 1)
                v.wait_ge(b12_done, 1)
                v.tensor_copy(k.b12[:], pw[0][:]).then_inc(split_done, 1)
                v.wait_ge(split_done, 5)

            @block.scalar
            def _(act_):
                for i in range(2 * EG):
                    act_.wait_ge(diagonal_summed, i + 1)
                    act_.activation(same["sd"[i // EG]][:, (i % EG) * GR + 1:(i % EG + 1) * GR + 1], pk[i % 2][:],
                                    ACT.Copy).then_inc(flags_ready, 1)
                act_.wait_ge(small_in, 7 * 16)
                for n in range(3):
                    act_.wait_ge(w_scaled, n + 1)
                    act_.activation(hi[names[n]][:], stage[n % 2][:], ACT.Copy).then_inc(hi_made, 1)
                act_.wait_ge(w_scaled, 7)
                act_.activation(hi["w12"][:], w12[:], ACT.Copy).then_inc(hi_made, 1)

            @block.tensor
            def _(pe):
                pe.wait_ge(made, 8)
                for i in range(2 * EG):
                    if i >= 2:
                        pe.wait_ge(flags_ready, i - 1)
                    pe.wait_ge(diagonal_made, i + 1)
                    pe.matmul(pk[i % 2][:], ones_bf[:], flag_diag[:, i % 2].rearrange("p t n -> p (t n)"),
                              start=True, stop=True).then_inc(diagonal_summed, 1)
                for n in range(3):
                    pe.wait_ge(stage_in[n % 2], 16 * (n // 2 + 1))
                    for dc in range(KC):
                        for kc in range(KC):
                            last = pe.matmul(pb[:, n * KC + dc:n * KC + dc + 1], stage[n % 2][:, kc, dc * P:dc * P + P],
                                             ln_b[:, kc:kc + 1], start=kc == 0, stop=kc == KC - 1)
                    last.then_inc(bias_done, 1)
                pe.wait_ge(w1_in, 32)
                for ic in range(KC):
                    if ic >= 2:
                        pe.wait_ge(w_scaled, 3 + ic - 1)
                    for kc in range(KC):
                        last = pe.matmul(pw[ic % 2][:], w1t[:, kc, ic * P:ic * P + P], w2[:, kc, :],
                                         start=kc == 0, stop=kc == KC - 1)
                    last.then_inc(w12_done, 1)
                pe.wait_ge(w_scaled, 6)
                for kc in range(KC):
                    pe.matmul(pw[0][:], b1_wide[:, kc, :], w2[:, kc, :], start=kc == 0, stop=False)
                pe.matmul(pw[0][:], ones_row[:], b2_row[:], start=False, stop=True).then_inc(b12_done, 1)

        qkv_and_softmax(nc, a, k, stack, c, hi, lo, bias, headsel, headsel2)


def qkv_and_softmax(nc, a, k, outer, co, hi, lo, bias, headsel, headsel2):
    with ExitStack() as stack:
        c = Core(nc, stack, "edge")
        scores = c.sb("scores", [HEADS, EP])
        value = c.sb("value", [P, KC, EP + 1])
        with ExitStack() as inner:
            project_edges(nc, a, k, inner, hi, lo, bias, headsel, scores, value)
        with ExitStack() as inner:
            aggregate_values(nc, a, k, inner, hi, lo, headsel2, scores, value)


def project_edges(nc, a, k, stack, hi, lo, bias, headsel, scores, value):
    c = Core(nc, stack, "qkv")
    rows = {x: c.sb(f"rows_{x}", [P, T, D]) for x in "sd"}
    at = {x: c.sb(f"at_{x}", [P, T], I32) for x in "sd"}
    st = {x: c.sb(f"st_{x}", [P, T, 6]) for x in "sd"}
    mv = {x: c.sb(f"mv_{x}", [P, T, 2]) for x in "sd"}
    ve = {x: c.sb(f"ve_{x}", [P, T]) for x in "sd"}
    r1 = {x: c.sb(f"r1_{x}", [P, T]) for x in "sd"}
    r2 = {x: c.sb(f"r2_{x}", [P, T]) for x in "sd"}
    shift = {x: c.sb(f"shift_{x}", [P, T]) for x in "sd"}
    xh = {x: c.sb(f"xh_{x}", [P, KC, GR], F32R) for x in "sd"}
    xl = {x: c.sb(f"xl_{x}", [P, KC, GR], F32R) for x in "sd"}
    qs = c.sb("qs", [P, KC, GR])
    prod = c.sb("prod", [P, 2, GR])
    attr = c.sb("attr", [P, T, 8])
    attr_t = c.sb("attr_t", [P, GR])
    pp = [c.ps(f"pp{n}") for n in range(2)]
    tr = [c.ps(f"tr{n}") for n in range(2)]
    p_score, p_attr = c.ps("p_score"), c.ps("p_attr")
    at_made = c.sem("at_made")
    rows_in = {x: [c.sem(f"rows_in_{x}{t}") for t in range(T)] for x in "sd"}
    stats = {x: c.sem(f"stats_{x}") for x in "sd"}
    pow_done = {x: c.sem(f"pow_done_{x}") for x in "sd"}
    normed = {x: c.sem(f"normed_{x}") for x in "sd"}
    turned = {x: c.sem(f"turned_{x}") for x in "sd"}
    hi_made = {x: c.sem(f"hi_made_{x}") for x in "sd"}
    lo_made = {x: c.sem(f"lo_made_{x}") for x in "sd"}
    q_done, k_done, v_done, q_out, k_out, v_out = (c.sem(n) for n in ("q_done", "k_done", "v_done", "q_out", "k_out", "v_out"))
    score_done, score_out, attr_turned, attr_out = (c.sem(n) for n in ("score_done", "score_out", "attr_turned", "attr_out"))
    value0 = c.sem("value0")
    block = stack.enter_context(nc.Block())
    NST = 9

    def gather(pool, g, x):
        n = "sd".index(x)
        pool.wait_ge(turned[x], 4 * g + 4)
        hold(pool)
        pool.tensor_copy(at[x][:], k.rec["s"][:, ds(4 * g, T), n]).then_inc(at_made, 1)
        pool.wait_ge(at_made, 3 * g + n + 1)
        hold(pool)
        for t in range(T):
            pool.indirect_dma_start(rows[x][:, t, :], None, a["x"][:, :],
                                    bass.IndirectOffsetOnAxis(ap=at[x][:, t:t + 1], axis=0),
                                    bounds_check=NPAD - 1, oob_is_err=False).then_inc(rows_in[x][t], 16)

    def powers(pool, g, x):
        for n, r in enumerate((r1, r2)):
            pool.wait_ge(stats[x], NST * g + (4 if n == 0 else 7))
            pool.tensor_tensor(r[x][:], ve[x][:], k.half_neg[:, 0:T], ALU.pow).then_inc(pow_done[x], 1)

    @block.gpsimd
    def _(pool):
        def body(g):
            gather(pool, g, "s")
            powers(pool, g, "s")
            gather(pool, g, "d")
            pool.wait_ge(attr_turned, g + 1)
            hold(pool)
            pool.tensor_copy(attr[:], k.rec["s"][:, ds(4 * g, T), 2:10].bitcast(F32)).then_inc(at_made, 1)
            powers(pool, g, "d")

        body(0)
        with pool.Fori(0, EG - 1) as g:
            body(g + 1)

    def statistics(v, g, x):
        s = Steps(v, stats[x], NST * g)
        for t in range(T):
            v.wait_ge(rows_in[x][t], 16 * g + 16)
            hold(v)
            ins = v.bn_stats(st[x][:, t, :], rows[x][:, t, :])
            if t == T - 1:
                s.link(ins)
        for t in range(T):
            if t == 0:
                hold(v)
            ins = v.bn_aggr(mv[x][:, t, :], st[x][:, t, :])
            if t == T - 1:
                s.link(ins)
        var, mean = mv[x][:, :, 1], mv[x][:, :, 0]
        s(v.tensor_scalar(shift[x][:], mean, -1.0, None, ALU.mult))
        s(v.tensor_scalar(ve[x][:], var, 1e-5, None, ALU.add))
        return s

    def statistics2(v, g, x, s):
        var = mv[x][:, :, 1]
        v.wait_ge(pow_done[x], 2 * g + 1)
        s.link(v.tensor_tensor(ve[x][:], var, r1[x][:], ALU.mult))
        s.link(v.tensor_tensor(ve[x][:], ve[x][:], r1[x][:], ALU.mult))
        s(v.tensor_scalar(ve[x][:], ve[x][:], 1e-5, None, ALU.add))

    def statistics3(v, g, x, s):
        v.wait_ge(pow_done[x], 2 * g + 2)
        s.link(v.tensor_tensor(r2[x][:], r1[x][:], r2[x][:], ALU.mult))
        s(v.tensor_tensor(shift[x][:], shift[x][:], r2[x][:], ALU.mult))
        assert s.n == NST

    def split_lo(v, g, x, t, turn):
        v.wait_ge(hi_made[x], 4 * g + t + 1)
        v.tensor_tensor(xl[x][:, :, t * P:t * P + P], tr[turn][:].rearrange("p (c n) -> p c n", n=P),
                        xh[x][:, :, t * P:t * P + P].bitcast(F32), ALU.subtract).then_inc(lo_made[x], 1)

    @block.vector
    def _(v):
        v.sem_inc(k_out, 1)
        v.sem_inc(score_out, 1)
        v.memset(value[:, :, 0:1], 0.0).then_inc(value0, 1)
        for x in "sd":
            s = statistics(v, 0, x)
            statistics2(v, 0, x, s)
            statistics3(v, 0, x, s)
        for t in range(T):
            split_lo(v, 0, "s", t, t % 2)

        def body(g, last):
            for t in range(T):
                split_lo(v, g, "d", t, t % 2)
            if not last:
                s = statistics(v, g + 1, "s")
            for cc in range(KC):
                v.wait_ge(k_done, 4 * g + cc + 1)
                v.wait_ge(q_out, 4 * g + cc + 1)
                v.wait_ge(score_done, 4 * g + cc + 1)
                v.scalar_tensor_tensor(prod[:, cc % 2, :], pp[cc % 2][:], bias[:, 1, cc:cc + 1], qs[:, cc, :],
                                       ALU.add, ALU.mult).then_inc(k_out, 1)
                if not last and cc == 1:
                    statistics2(v, g + 1, "s", s)
                if not last and cc == 2:
                    statistics3(v, g + 1, "s", s)
            v.wait_ge(attr_out, g + 1)
            v.wait_ge(score_done, 4 * g + 4 + 2)
            v.tensor_tensor(scores[:, ds(g * GR, GR)], p_score[0:HEADS, :], attr_t[0:HEADS, :], ALU.mult)\
             .then_inc(score_out, 1)
            if not last:
                s = statistics(v, g + 1, "d")
                for t in range(T):
                    split_lo(v, g + 1, "s", t, t % 2)
                    if t == 1:
                        statistics2(v, g + 1, "d", s)
                    if t == 2:
                        statistics3(v, g + 1, "d", s)

        with v.Fori(0, EG - 1) as g:
            body(g, False)
        body(EG - 1, True)
        v.wait_ge(score_out, EG + 1)

    def norm(act_, g, x, t):
        if t == 0:
            act_.wait_ge(stats[x], NST * g + NST)
        act_.activation(rows[x][:, t, :], rows[x][:, t, :], ACT.Identity, bias=shift[x][:, t:t + 1],
                        scale=r2[x][:, t:t + 1]).then_inc(normed[x], 1)

    def split_hi(act_, g, x, t, turn):
        act_.wait_ge(turned[x], 4 * g + t + 1 + 4)
        act_.activation(xh[x][:, :, t * P:t * P + P], tr[turn][:].rearrange("p (c n) -> p c n", n=P),
                        ACT.Copy).then_inc(hi_made[x], 1)

    @block.scalar
    def _(act_):
        act_.sem_inc(v_out, 4)
        for x in "sd":
            for t in range(T):
                norm(act_, 0, x, t)
        for t in range(T):
            split_hi(act_, 0, "s", t, t % 2)

        def body(g, last):
            for cc in range(KC):
                act_.wait_ge(q_done, 4 * g + cc + 1)
                if cc == 0:
                    act_.wait_ge(k_out, 4 * g + 1)
                act_.activation(qs[:, cc, :], pp[cc % 2][:], ACT.Identity, bias=bias[:, 0, cc:cc + 1])\
                    .then_inc(q_out, 1)
                split_hi(act_, g, "d", cc, cc % 2)
            act_.wait_ge(attr_turned, g + 2)
            act_.wait_ge(score_out, g + 1)
            act_.activation(attr_t[0:HEADS, :], p_attr[0:HEADS, :], ACT.Copy).then_inc(attr_out, 1)
            if not last:
                for t in range(T):
                    norm(act_, g + 1, "s", t)
            for cc in range(KC):
                if not last:
                    split_hi(act_, g + 1, "s", cc, cc % 2)
                act_.wait_ge(v_done, 4 * g + cc + 1)
                act_.activation(value[:, cc, ds(g * GR + 1, GR)], pp[cc % 2][:], ACT.Identity,
                                bias=bias[:, 2, cc:cc + 1]).then_inc(v_out, 1)
                if not last and cc >= 2:
                    norm(act_, g + 1, "d", 2 * cc - 4)
                    norm(act_, g + 1, "d", 2 * cc - 3)

        with act_.Fori(0, EG - 1) as g:
            body(g, False)
        body(EG - 1, True)

    def turn(pe, g, x, t):
        pe.wait_ge(normed[x], 4 * g + t + 1)
        for kc in range(KC):
            last = pe.transpose(tr[t % 2][:, kc * P:kc * P + P], rows[x][:, t, kc * P:kc * P + P], k.ident[:])
        last.then_inc(turned[x], 1)

    def project(pe, x, name, cc):
        for kc in range(KC):
            w = [z[name][:, kc, cc * P:cc * P + P] for z in (hi, lo)]
            last = split3(pe, pp[cc % 2][:], w, (xh[x][:, kc, :], xl[x][:, kc, :]), kc == 0, kc == KC - 1)
        return last

    @block.tensor
    def _(pe):
        pe.sem_inc(attr_turned, 1)
        pe.sem_inc(score_done, 2)
        pe.sem_inc(turned["s"], 4)
        pe.sem_inc(turned["d"], 4)
        for t in range(T):
            if t >= 2:
                pe.wait_ge(lo_made["s"], t - 1)
            turn(pe, 0, "s", t)

        def body(g, last_group):
            pe.wait_ge(lo_made["s"], 4 * g + 4)
            for cc in range(KC):
                if cc >= 2:
                    pe.wait_ge(q_out, 4 * g + cc - 1)
                else:
                    pe.wait_ge(v_out, 4 * g + cc + 1 + 2)
                project(pe, "s", "wq", cc).then_inc(q_done, 1)
                if cc >= 2:
                    pe.wait_ge(lo_made["d"], 4 * g + cc - 1)
                turn(pe, g, "d", cc)
            pe.wait_ge(at_made, 3 * g + 3)
            pe.wait_ge(score_out, g + 1)
            for t in range(T):
                last = pe.matmul(p_attr[0:HEADS, t * P:t * P + P], attr[:, t, :], k.ident[:], start=True, stop=True)
            last.then_inc(attr_turned, 1)
            pe.wait_ge(lo_made["d"], 4 * g + 4)
            for cc in range(KC):
                if cc >= 2:
                    pe.wait_ge(k_out, 4 * g + cc - 1 + 1)
                else:
                    pe.wait_ge(q_out, 4 * g + cc + 3)
                project(pe, "d", "wk", cc).then_inc(k_done, 1)
                if cc >= 1:
                    score(pe, g, cc - 1)
            for cc in range(KC):
                if cc == 1:
                    score(pe, g, KC - 1)
                if not last_group:
                    if cc >= 2:
                        pe.wait_ge(lo_made["s"], 4 * g + 4 + cc - 1)
                    turn(pe, g + 1, "s", cc)
                if cc < 2:
                    pe.wait_ge(k_out, 4 * g + cc + 4)
                else:
                    pe.wait_ge(v_out, 4 * g + cc + 3)
                project(pe, "d", "wv", cc).then_inc(v_done, 1)

        def score(pe, g, cc):
            pe.wait_ge(k_out, 4 * g + cc + 1 + 1)
            pe.matmul(p_score[0:HEADS, :], headsel[:, cc, :], prod[:, cc % 2, :], start=cc == 0,
                      stop=cc == KC - 1, skip_group_check=True).then_inc(score_done, 1)

        with pe.Fori(0, EG - 1) as g:
            body(g, False)
        body(EG - 1, True)



def aggregate_values(nc, a, k, stack, hi, lo, headsel2, scores, value):
    c = Core(nc, stack, "agg")
    pen = c.sb("pen", [HEADS, EP + 1])
    best = c.sb("best", [HEADS, EP])
    expo = c.sb("expo", [HEADS, EP])
    ah, al = c.sb("ah", [P, KC, GR], F32R), c.sb("al", [P, KC, GR], F32R)
    out = c.sb("out", [P, 2, D])
    pa = [c.ps(f"pa{n}") for n in range(KC)]
    po = [c.ps(f"po{n}") for n in range(2)]
    chain, exp_done, att_ready = c.sem("chain"), c.sem("exp_done"), c.sem("att_ready")
    spread, weighted, summed, hi_made, lo_made = (c.sem(n) for n in ("spread", "weighted", "summed", "hi_made", "lo_made"))
    row_done, row_out = c.sem("row_done"), c.sem("row_out")
    stored = [c.sem(f"stored{n}") for n in range(2)]
    same = k.same["s"]
    block = stack.enter_context(nc.Block())

    @block.vector
    def _(v):
        v.sem_inc(weighted, KC)
        s = Steps(v, chain)
        s.link(v.tensor_scalar(pen[:], same[0:HEADS, :], -1.0, 1e30, ALU.add, ALU.mult))
        s.link(v.tensor_tensor_scan(best[:], pen[:, 0:EP], scores[:], 0.0, ALU.add, ALU.max))
        s.link(v.tensor_tensor_scan(best[:, ::-1], pen[:, EP:0:-1], best[:, ::-1], -1e30, ALU.add, ALU.max))
        s(v.tensor_tensor(scores[:], scores[:], best[:], ALU.subtract))
        v.wait_ge(exp_done, 1)
        s.link(v.tensor_tensor_scan(best[:], same[0:HEADS, 0:EP], expo[:], 0.0, ALU.mult, ALU.add))
        s.link(v.tensor_tensor_scan(best[:, ::-1], same[0:HEADS, EP:0:-1], best[:, ::-1], 0.0, ALU.mult, ALU.max))
        s.link(v.tensor_scalar(best[:], best[:], 1e-16, None, ALU.add))
        s.link(v.reciprocal(best[:], best[:]))
        v.tensor_tensor(scores[:], expo[:], best[:], ALU.mult).then_inc(att_ready, 1)

        def scan(g, cc):
            v.wait_ge(spread, 4 * g + cc + 1)
            cols = value[:, cc, ds(g * GR + 1, GR)]
            v.tensor_tensor(cols, cols, pa[cc][:], ALU.mult).then_inc(weighted, 1)
            v.wait_ge(weighted, 4 * g + cc + 1 + KC)
            v.tensor_tensor_scan(cols, same[:, ds(g * GR, GR)], cols, value[:, cc, ds(g * GR, 1)],
                                 ALU.mult, ALU.add).then_inc(summed, 1)

        def low(g, cc):
            v.wait_ge(hi_made, 4 * g + cc + 1)
            v.tensor_tensor(al[:, cc, :], value[:, cc, ds(g * GR + 1, GR)], ah[:, cc, :].bitcast(F32),
                            ALU.subtract).then_inc(lo_made, 1)

        def body(g, last):
            for t in range(T):
                if not last:
                    scan(g + 1, t)
                v.wait_ge(row_done, 4 * g + t + 1)
                v.wait_ge(stored[t % 2], 32 * g + 16 * (t // 2) + 16)
                v.tensor_tensor(out[:, t % 2, :], po[t % 2][:], k.b12[:], ALU.add).then_inc(row_out, 1)
            if not last:
                for cc in range(KC):
                    low(g + 1, cc)

        for cc in range(KC):
            scan(0, cc)
        for cc in range(KC):
            low(0, cc)
        with v.Fori(0, EG - 1) as g:
            body(g, False)
        body(EG - 1, True)

    @block.scalar
    def _(act_):
        act_.wait_ge(chain, 4)
        act_.activation(expo[:], scores[:], ACT.Exp).then_inc(exp_done, 1)
        with act_.Fori(0, EG) as g:
            for cc in range(KC):
                act_.wait_ge(summed, 4 * g + cc + 1)
                if cc == 0:
                    act_.wait_ge(row_out, 4 * g + 2)
                act_.activation(ah[:, cc, :], value[:, cc, ds(g * GR + 1, GR)], ACT.Copy).then_inc(hi_made, 1)

    @block.tensor
    def _(pe):
        pe.wait_ge(att_ready, 1)

        def spread_weights(g):
            for cc in range(KC):
                pe.wait_ge(weighted, 4 * g + cc + 1)
                hold(pe)
                pe.matmul(pa[cc][:], headsel2[:, cc * P:cc * P + P], scores[:, ds(g * GR, GR)], start=True,
                          stop=True).then_inc(spread, 1)

        def body(g, last):
            if not last:
                spread_weights(g + 1)
            for t in range(T):
                pe.wait_ge(row_out, 4 * g + t + 1)
                for cc in range(KC):
                    if t == 0:
                        pe.wait_ge(lo_made, 4 * g + cc + 1)
                    sl = slice(t * P, t * P + P)
                    last = split3(pe, po[t % 2][:], (ah[:, cc, sl], al[:, cc, sl]),
                                  (hi["w12"][:, cc, :], lo["w12"][:, cc, :]), cc == 0, cc == KC - 1)
                last.then_inc(row_done, 1)

        spread_weights(0)
        with pe.Fori(0, EG - 1) as g:
            body(g, False)
        body(EG - 1, True)

    @block.sync
    def _(sp):
        for n in range(2):
            sp.sem_inc(stored[n], 16)
        sp.sem_inc(row_out, 2)
        with sp.Fori(0, EG) as g:
            for t in range(T):
                sp.wait_ge(row_out, 4 * g + t + 3)
                sp.dma_start(k.values[ds(g * GR + t * P, P), :], out[:, t % 2, :]).then_inc(stored[t % 2], 16)
        for n in range(2):
            sp.wait_ge(stored[n], 16 + 16 * ET // 2)


def chunks(source):
    return source.rearrange("(c p) n -> p c n", p=P)



def dense0_phase(nc, a, k):
    with ExitStack() as stack:
        c = Core(nc, stack, "d0")
        w = {n: [c.sb(f"{n}_{h}", [P, KC, D], F32R) for h in ("hi", "lo")] for n in ("w1", "w3", "w2")}
        wr = [c.sb(f"wr_{h}", [P, KC, P], F32R) for h in ("hi", "lo")]
        x = [c.sb(f"x{n}", [P, T, D]) for n in range(XS)]
        val = c.sb("val", [P, T, D])
        at = c.sb("at", [P, T], I32)
        xf = c.sb("xf", [P, T, D])
        xh, xl = ([c.sb(f"{n}{i}", [P, KC, GR], F32R) for i in range(2)] for n in ("xh", "xl"))
        logit_t = c.sb("logit_t", [SETS * 4, GR])
        act_out = c.sb("act_out", [P, 2, GR])
        hh, hl = (c.sb(n, [P, KC, GR], F32R) for n in ("hh", "hl"))
        wr_in = c.sb("wr_in", [P, KC, SETS * 4])
        y = c.sb("y", [P, 2, D])
        st = [c.sb(f"st{n}", [P, T, 6]) for n in range(3)]
        mv = [c.sb(f"mv{n}", [P, T, 2]) for n in range(3)]
        ve = [c.sb(f"ve{n}", [P, T]) for n in range(3)]
        rs = [c.sb(f"rs{n}", [P, T]) for n in range(3)]
        shift = [c.sb(f"shift{n}", [P, T]) for n in range(3)]
        gain = c.sb("gain", [P, T])
        rbias = c.sb("rbias", [P, SETS * 4])
        before = c.sb("before", [P, 4, 4])
        expert = c.sb("expert", [2 * EXPERTS0, D])
        expert2 = c.sb("expert2", [2 * EXPERTS0, D])
        expert_r = c.sb("expert_r", [2 * EXPERTS0, D], F32R)
        NS = T * SETS
        prob, one_hot, second, rank = (c.sb(n, [P, NS, 4]) for n in ("prob", "one_hot", "second", "rank"))
        total = c.sb("total", [P, NS])
        wins, ties = (c.sb(n, [P, NS, 4, 4]) for n in ("wins", "ties"))
        mix = c.sb("mix", [P, T, EXPERTS0])
        parts = c.sb("parts", [P, T, P], F32R)
        mix_t = c.sb("mix_t", [2 * EXPERTS0, GR], F32R)
        pa, pc, po = ([c.ps(f"{n}{i}") for i in range(2)] for n in ("pa", "pc", "po"))
        ptr, pmix = c.ps("ptr"), c.ps("pmix")

        stage = [x[n][:].rearrange("p t n -> p (t n)").rearrange("p (c n) -> p c n", c=KC) for n in (XS - 1, XS - 2)]
        weights = [(chunks(a["e_w1"]), stage[0], *w["w1"]), (chunks(a["e_w3"]), stage[1], *w["w3"]),
                   (chunks(a["e_w2"]), stage[0], *w["w2"]),
                   (chunks(a["e_wr"]), wr_in[:], wr[0][:, :, 0:SETS * 4], wr[1][:, :, 0:SETS * 4])]

        consts, routed_in = c.sem("consts"), c.sem("routed_in")
        weight_in = [c.sem(f"weight_in{n}") for n in range(4)]
        weight_high = [c.sem(f"weight_high{n}") for n in range(4)]
        weight_low = [c.sem(f"weight_low{n}") for n in range(4)]
        x_in = [c.sem(f"x_in{n}") for n in range(XS)]
        val_in = [c.sem(f"val_in{n}") for n in range(T)]
        y_out = [c.sem(f"y_out{n}") for n in range(2)]
        at_made, val_made = c.sem("at_made"), c.sem("val_made")
        stats = [c.sem(f"stats{n}") for n in range(3)]
        shift_made = [c.sem(f"shift_made{n}") for n in range(2)]
        dev_made = c.sem("dev_made")
        pow_done = [c.sem(f"pow_done{n}") for n in range(3)]
        x0_normed, x1_made, x1_normed, x2_made, y_made = (c.sem(n) for n in ("x0_normed", "x1_made", "x1_normed", "x2_made", "y_made"))
        turned, xh_made, xl_made = (c.sem(n) for n in ("turned", "xh_made", "xl_made"))
        up_done, gate_done, mixed, tanh_done = (c.sem(n) for n in ("up_done", "gate_done", "mixed", "tanh_done"))
        gated, hidden, hh_made, hl_made = (c.sem(n) for n in ("gated", "hidden", "hh_made", "hl_made"))
        down_done, logits_done, logits_out, logits_turned = (
            c.sem(n) for n in ("down_done", "logits_done", "logits_out", "logits_turned"))
        route, exp_done, mix_turned, mix_out = (c.sem(n) for n in ("route", "exp_done", "mix_turned", "mix_out"))
        block = stack.enter_context(nc.Block())
        NSTAT, NROUTE = 4, 25

        def bodies(eng, body):
            body(0, 0)
            with eng.Fori(0, (NG - XS) // XS) as i:
                for c_ in range(1, XS + 1):
                    body(i, c_)
            for c_ in range(NG - XS + 1, NG):
                body(0, c_)

        def in_range(i, c_, ahead):
            return not isinstance(i, int) or 0 <= c_ + ahead < NG

        @block.sync
        def _(sp):
            sp.sem_inc(y_out[0], 16)
            sp.sem_inc(y_out[1], 16)
            sp.dma_start(rbias[:], a["e_br"].broadcast_to([P, SETS * 4])).then_inc(routed_in, 16)

            def load(g, u):
                sp.dma_start(x[u][:], a["x"][ds(g * GR, GR), :].rearrange("(t p) n -> p t n", p=P))\
                  .then_inc(x_in[u], 16)

            def body(i, c_):
                if not in_range(i, c_, -1):
                    return
                g = i * XS + c_ - 1
                for t in range(T):
                    sp.wait_ge(y_made, 4 * g + t + 1)
                    sp.dma_start(k.y[ds(g * GR + t * P, P), :], y[:, t % 2, :]).then_inc(y_out[t % 2], 16)
                if in_range(i, c_, XS - 1):
                    load(g + XS, (c_ - 1) % XS)

            def load_weight(n):
                sp.dma_start(weights[n][1], weights[n][0]).then_inc(weight_in[n], 16)

            load(0, 0)
            for n in (0, 3, 1):
                load_weight(n)
            load(1, 1)
            sp.wait_ge(weight_low[0], 1)
            load_weight(2)
            sp.wait_ge(weight_low[1], 1)
            load(2, 2)
            sp.wait_ge(weight_low[2], 1)
            load(3, 3)
            bodies(sp, body)
            body(0, NG)
            for n in range(2):
                sp.wait_ge(y_out[n], 16 + 16 * NT // 2)

        @block.gpsimd
        def _(pool):
            s = Steps(pool, consts)
            s(pool.memset(before[:], 1.0))
            s(pool.memset(expert[:], 0.25))
            s(pool.memset(expert2[:], 0.25))
            s.settle()
            s(pool.affine_select(out=before[:], in_=before[:], compare_op=ALU.is_gt, fill=0.0, base=0,
                                 pattern=[[1, 4], [-1, 4]], channel_multiplier=0))
            for m, off in ((expert, 0), (expert2, EXPERTS0 * HID1)):
                s.link(pool.affine_select(out=m[:], in_=m[:], compare_op=ALU.is_ge, fill=0.0, base=off,
                                          pattern=[[1, D]], channel_multiplier=-HID1))
                s.link(pool.affine_select(out=m[:], in_=m[:], compare_op=ALU.is_ge, fill=0.0,
                                          base=HID1 - 1 - off, pattern=[[-1, D]], channel_multiplier=HID1))

            def power(g, n):
                pool.wait_ge(stats[n], NSTAT * g + 4 if n < 2 else 5 * g + 4)
                pool.tensor_tensor(rs[n][:], ve[n][:], k.half_neg[:, 0:T], ALU.pow).then_inc(pow_done[n], 1)

            def gather(g, t):
                if t == 0:
                    pool.wait_ge(x1_made, 4 * g + 4)
                    hold(pool)
                    pool.tensor_copy(at[:], k.slot["s"][:, ds(T * g, T)]).then_inc(at_made, 1)
                pool.tensor_tensor(val[:, t, :], k.b12[:], k.zeros[:], ALU.add).then_inc(val_made, 1)
                pool.wait_ge(val_made, 4 * g + t + 1)
                pool.wait_ge(at_made, g + 1)
                hold(pool)
                pool.indirect_dma_start(val[:, t, :], None, k.values[:, :],
                                        bass.IndirectOffsetOnAxis(ap=at[:, t:t + 1], axis=0),
                                        bounds_check=EP - 1, oob_is_err=False).then_inc(val_in[t], 16)

            def add(g, u, t):
                pool.wait_ge(x0_normed, 4 * g + t + 1)
                pool.wait_ge(val_in[t], 16 * g + 16)
                pool.tensor_tensor(x[u][:, t, :], x[u][:, t, :], val[:, t, :], ALU.add).then_inc(x1_made, 1)

            def low(g, cc):
                if cc == 0:
                    pool.wait_ge(down_done, 4 * g + 4)
                pool.wait_ge(hh_made, 4 * g + cc + 1)
                pool.tensor_tensor(hl[:, cc, :], act_out[:, cc % 2, :], hh[:, cc, :].bitcast(F32), ALU.subtract)\
                    .then_inc(hl_made, 1)

            def body(i, c_):
                g, u2 = i * XS + c_, (c_ + 2) % XS
                front = in_range(i, c_, 2)
                if in_range(i, c_, -1):
                    power(g - 1, 2)
                if front:
                    power(g + 2, 0)
                low(g, 0)
                if front:
                    add(g + 2, u2, 0)
                    add(g + 2, u2, 1)
                low(g, 1)
                if front:
                    add(g + 2, u2, 2)
                    add(g + 2, u2, 3)
                low(g, 2)
                if front:
                    power(g + 2, 1)
                if in_range(i, c_, 3):
                    gather(g + 3, 0)
                low(g, 3)
                if in_range(i, c_, 3):
                    gather(g + 3, 1)
                    gather(g + 3, 2)
                    gather(g + 3, 3)

            pool.sem_inc(hl_made, 2)
            pool.sem_inc(x1_made, 4)
            gather(0, 0)
            gather(0, 1)
            power(0, 0)
            gather(0, 2)
            gather(0, 3)
            for t in range(T):
                add(0, 0, t)
            power(1, 0)
            power(0, 1)
            for t in range(T):
                gather(1, t)
            for t in range(T):
                add(1, 1, t)
            power(1, 1)
            for t in range(T):
                gather(2, t)
            bodies(pool, body)
            power(NG - 1, 2)

        def statistics(v, g, u, n):
            s = Steps(v, stats[n], (NSTAT if n < 2 else 5) * g)
            for t in range(T):
                ins = v.bn_stats(st[n][:, t, :], x[u][:, t, :])
            s.link(ins)
            hold(v)
            for t in range(T):
                ins = v.bn_aggr(mv[n][:, t, :], st[n][:, t, :])
            s.link(ins)
            s(v.tensor_scalar(shift[n][:], mv[n][:, :, 0], -1.0, None, ALU.mult))
            s(v.tensor_scalar(ve[n][:], mv[n][:, :, 1], 1e-5, None, ALU.add))

        @block.vector
        def _(v):
            v.sem_inc(hidden, 2)
            v.sem_inc(x2_made, 2)
            v.wait_ge(consts, 8)
            v.tensor_tensor(expert_r[:], expert[:], expert2[:], ALU.add).then_inc(consts, 1)
            for part in wr:
                v.memset(part[:, :, SETS * 4:P].bitcast(F32), 0.0).then_inc(consts, 1)
            v.memset(parts[:, :, 2 * EXPERTS0:P].bitcast(F32), 0.0).then_inc(consts, 1)
            v.wait_ge(routed_in, 16)

            def split_low(n):
                v.wait_ge(weight_high[n], 1)
                v.tensor_tensor(weights[n][3][:], weights[n][1], weights[n][2][:].bitcast(F32), ALU.subtract)\
                 .then_inc(weight_low[n], 1)

            def front0(i, c_):
                g = i * XS + c_
                v.wait_ge(x_in[c_ % XS], i * 16 + 16 * (c_ // XS + 1))
                if in_range(i, c_, -1):
                    v.wait_ge(x0_normed, 4 * g)
                hold(v)
                statistics(v, g, c_ % XS, 0)

            def front0_end(g):
                v.wait_ge(pow_done[0], g + 1)
                v.tensor_scalar(gain[:], rs[0][:], 1.0, None, ALU.add).then_inc(shift_made[0], 1)
                v.tensor_tensor(shift[0][:], shift[0][:], rs[0][:], ALU.mult).then_inc(shift_made[0], 1)

            def front1(i, c_):
                g = i * XS + c_
                v.wait_ge(x1_made, 4 * g + 4 + 4)
                if in_range(i, c_, -1):
                    v.wait_ge(x1_normed, 4 * g)
                hold(v)
                statistics(v, g, c_ % XS, 1)

            def front1_end(g):
                v.wait_ge(pow_done[1], g + 1)
                v.tensor_tensor(shift[1][:], shift[1][:], rs[1][:], ALU.mult).then_inc(shift_made[1], 1)

            def low(g, n, t):
                v.wait_ge(xh_made, 4 * g + t + 1)
                v.tensor_tensor(xl[n][:, :, t * P:t * P + P], ptr[:].rearrange("p (c n) -> p c n", n=P),
                                xh[n][:, :, t * P:t * P + P].bitcast(F32), ALU.subtract).then_inc(xl_made, 1)

            def chunk(g, cc):
                h = act_out[:, cc % 2, :]
                v.wait_ge(tanh_done, 4 * g + cc + 1)
                v.scalar_tensor_tensor(h, h, 1.0, pa[cc % 2][:], ALU.add, ALU.mult).then_inc(gated, 1)
                v.wait_ge(gated, 8 * g + 2 * cc + 1)
                v.wait_ge(gate_done, 4 * g + cc + 1)
                v.tensor_tensor(h, h, pc[cc % 2][:], ALU.mult).then_inc(gated, 1)
                v.wait_ge(gated, 8 * g + 2 * cc + 2)
                v.wait_ge(mixed, 4 * g + cc + 1)
                v.tensor_tensor(h, h, pmix[:], ALU.mult).then_inc(hidden, 1)

            def back(g, u, t):
                v.wait_ge(down_done, 4 * g + t + 1 + 4)
                v.tensor_tensor(x[u][:, t, :], x[u][:, t, :], po[t % 2][:], ALU.add).then_inc(x2_made, 1)

            def back_stats(i, c_):
                g = i * XS + c_
                v.wait_ge(x2_made, 4 * g + 4 + 2)
                if in_range(i, c_, -1):
                    v.wait_ge(y_made, 4 * g)
                hold(v)
                statistics(v, g, c_ % XS, 2)
                v.tensor_copy(k.mean[:, ds(T * g, T)], mv[2][:, :, 0])

            def back_end(g):
                v.wait_ge(pow_done[2], g + 1)
                v.tensor_tensor(shift[2][:], shift[2][:], rs[2][:], ALU.mult).then_inc(stats[2], 1)
                v.tensor_tensor(k.dev[:, ds(T * g, T)], ve[2][:], rs[2][:], ALU.mult).then_inc(dev_made, 1)

            def routing(g, between):
                s = Steps(v, route, NROUTE * g)

                def link(ins):
                    s.link(ins)
                    if s.n in between:
                        between[s.n]()
                        s.settle()

                v.wait_ge(logits_turned, g + 1)
                link(v.tensor_tensor(prob[:].rearrange("p (t s) e -> p t (s e)", t=T),
                                     ptr[:, 0:T * SETS * 4].rearrange("p (t n) -> p t n", t=T),
                                     rbias[:].unsqueeze(1).broadcast_to([P, T, SETS * 4]), ALU.add))
                link(v.tensor_reduce(total[:], prob[:], X_AXIS, ALU.max))
                s(v.tensor_tensor(prob[:], prob[:], total[:].unsqueeze(2).broadcast_to([P, NS, 4]), ALU.subtract))
                v.wait_ge(exp_done, g + 1)
                link(v.tensor_reduce(total[:], prob[:], X_AXIS, ALU.add))
                link(v.reciprocal(total[:], total[:]))
                link(v.tensor_tensor(prob[:], prob[:], total[:].unsqueeze(2).broadcast_to([P, NS, 4]), ALU.mult))
                other = prob[:].unsqueeze(2).broadcast_to([P, NS, 4, 4])
                own = prob[:].unsqueeze(3).broadcast_to([P, NS, 4, 4])
                s(v.tensor_tensor(wins[:], other, own, ALU.is_gt))
                link(v.tensor_tensor(ties[:], other, own, ALU.is_equal))
                link(v.tensor_tensor(ties[:], ties[:], before[:].unsqueeze(1).broadcast_to([P, NS, 4, 4]), ALU.mult))
                link(v.tensor_tensor(wins[:], wins[:], ties[:], ALU.add))
                link(v.tensor_reduce(rank[:], wins[:], X_AXIS, ALU.add))
                s(v.scalar_tensor_tensor(one_hot[:], rank[:], 0.0, prob[:], ALU.is_equal, ALU.mult))
                link(v.scalar_tensor_tensor(second[:], rank[:], 1.0, prob[:], ALU.is_equal, ALU.mult))
                link(v.tensor_tensor(prob[:], one_hot[:], second[:], ALU.add))
                link(v.tensor_reduce(total[:], prob[:], X_AXIS, ALU.add))
                link(v.tensor_scalar(total[:], total[:], 0.9, None, ALU.is_le))
                link(v.tensor_tensor(second[:], second[:], total[:].unsqueeze(2).broadcast_to([P, NS, 4]), ALU.mult))
                link(v.tensor_tensor(prob[:], one_hot[:], second[:], ALU.add))
                link(v.tensor_reduce(total[:], prob[:], X_AXIS, ALU.add))
                link(v.tensor_scalar(total[:], total[:], 1e-9, None, ALU.add))
                link(v.reciprocal(total[:], total[:]))
                link(v.tensor_tensor(prob[:], prob[:], total[:].unsqueeze(2).broadcast_to([P, NS, 4]), ALU.mult))
                sets = prob[:].rearrange("p (t s) e -> p t s e", t=T)
                for t in range(T):
                    ins = v.tensor_tensor(mix[:, t, :].rearrange("p (s e) -> p s e", e=4), sets[:, t, 1:SETS, :],
                                          sets[:, t, 0, :].unsqueeze(2).broadcast_to([P, 4, 4]), ALU.mult)
                link(ins)
                v.wait_ge(mix_turned, g + 1)
                link(v.tensor_copy(parts[:, :, 0:EXPERTS0], mix[:]))
                s(v.tensor_tensor(parts[:, :, EXPERTS0:2 * EXPERTS0], mix[:], parts[:, :, 0:EXPERTS0].bitcast(F32),
                                  ALU.subtract))
                assert s.n == NROUTE

            def body(i, c_):
                g, u, n1 = i * XS + c_, c_ % XS, (c_ + 1) % 2
                front, mid, behind = in_range(i, c_, 2), in_range(i, c_, 1), in_range(i, c_, -1)
                if behind:
                    back_stats(i, c_ - 1)
                if behind:
                    back_end(g - 1)
                chunk(g, 0)
                if mid:
                    low(g + 1, n1, 0)
                if front:
                    front0(i, c_ + 2)
                if mid:
                    low(g + 1, n1, 1)
                if front:
                    front0_end(g + 2)
                chunk(g, 1)
                if mid:
                    low(g + 1, n1, 2)
                    low(g + 1, n1, 3)
                chunk(g, 2)
                if front:
                    front1(i, c_ + 2)
                chunk(g, 3)
                if front:
                    front1_end(g + 2)
                if mid:
                    routing(g + 1, {10: lambda: back(g, u, 0), 18: lambda: back(g, u, 1)})
                else:
                    back(g, u, 0)
                    back(g, u, 1)
                back(g, u, 2)
                back(g, u, 3)

            front0(0, 0)
            front0_end(0)
            split_low(0)
            front0(0, 1)
            front1(0, 0)
            front0_end(1)
            front1_end(0)
            split_low(3)
            for t in range(T):
                low(0, 0, t)
            split_low(1)
            split_low(2)
            front1(0, 1)
            routing(0, {})
            front1_end(1)
            bodies(v, body)
            back_stats(0, NG - 1)
            back_end(NG - 1)
            v.wait_ge(dev_made, NG)

        @block.scalar
        def _(act_):
            def split_high(n):
                act_.wait_ge(weight_in[n], 16)
                act_.activation(weights[n][2][:], weights[n][1], ACT.Copy).then_inc(weight_high[n], 1)

            def norm0(g, u, t):
                if t == 0:
                    act_.wait_ge(shift_made[0], 2 * g + 2)
                act_.activation(x[u][:, t, :], x[u][:, t, :], ACT.Identity, bias=shift[0][:, t:t + 1],
                                scale=gain[:, t:t + 1]).then_inc(x0_normed, 1)

            def norm1(g, u):
                act_.wait_ge(shift_made[1], g + 1)
                for t in range(T):
                    act_.wait_ge(turned, 4 * g + t + 1)
                    act_.activation(xf[:, t, :], x[u][:, t, :], ACT.Identity, bias=shift[1][:, t:t + 1],
                                    scale=rs[1][:, t:t + 1]).then_inc(x1_normed, 1)

            def high(g, n, t):
                act_.wait_ge(turned, 4 * g + t + 1 + 4)
                act_.activation(xh[n][:, :, t * P:t * P + P], ptr[:].rearrange("p (c n) -> p c n", n=P), ACT.Copy)\
                    .then_inc(xh_made, 1)

            def tanh(g, cc):
                act_.wait_ge(up_done, 4 * g + cc + 1)
                act_.wait_ge(hl_made, 4 * g + cc + 1)
                act_.activation(act_out[:, cc % 2, :], pa[cc % 2][:], ACT.Tanh, scale=0.5).then_inc(tanh_done, 1)

            def split(g, cc):
                act_.wait_ge(hidden, 4 * g + cc + 1 + 2)
                if cc == 0:
                    act_.wait_ge(down_done, 4 * g + 4)
                act_.activation(hh[:, cc, :], act_out[:, cc % 2, :], ACT.Copy).then_inc(hh_made, 1)

            def logits_copy(g):
                act_.wait_ge(logits_done, g + 1)
                act_.activation(logit_t[:], ptr[0:SETS * 4, :], ACT.Copy).then_inc(logits_out, 1)

            def softmax_exp(g):
                act_.wait_ge(route, NROUTE * g + 3)
                act_.activation(prob[:], prob[:], ACT.Exp).then_inc(exp_done, 1)

            def mix_copy(g):
                act_.wait_ge(mix_turned, g + 2)
                act_.activation(mix_t[:], ptr[0:2 * EXPERTS0, :], ACT.Copy).then_inc(mix_out, 1)

            def finish(g, u, t):
                if t == 0:
                    act_.wait_ge(stats[2], 5 * g + 5)
                act_.wait_ge(y_out[t % 2], 32 * g + 16 * (t // 2) + 16)
                act_.activation(y[:, t % 2, :], x[u][:, t, :], ACT.Identity, bias=shift[2][:, t:t + 1],
                                scale=rs[2][:, t:t + 1]).then_inc(y_made, 1)

            def body(i, c_):
                g, n1 = i * XS + c_, (c_ + 1) % 2
                u, u1, u2 = (c_ - 1) % XS, (c_ + 1) % XS, (c_ + 2) % XS
                front, mid, behind = in_range(i, c_, 2), in_range(i, c_, 1), in_range(i, c_, -1)
                if mid:
                    norm1(g + 1, u1)
                tanh(g, 0)
                mix_copy(g)
                if mid:
                    high(g + 1, n1, 0)
                split(g, 0)
                if behind:
                    finish(g - 1, u, 0)
                if mid:
                    high(g + 1, n1, 1)
                tanh(g, 1)
                if behind:
                    finish(g - 1, u, 1)
                if front:
                    norm0(g + 2, u2, 0)
                if mid:
                    high(g + 1, n1, 2)
                split(g, 1)
                if front:
                    norm0(g + 2, u2, 1)
                    norm0(g + 2, u2, 2)
                tanh(g, 2)
                if mid:
                    high(g + 1, n1, 3)
                if front:
                    norm0(g + 2, u2, 3)
                if behind:
                    finish(g - 1, u, 2)
                    finish(g - 1, u, 3)
                split(g, 2)
                tanh(g, 3)
                if mid:
                    logits_copy(g + 1)
                split(g, 3)
                if mid:
                    softmax_exp(g + 1)

            split_high(0)
            for g in range(2):
                for t in range(T):
                    norm0(g, g, t)
            split_high(3)
            norm1(0, 0)
            for t in range(T):
                high(0, 0, t)
            split_high(1)
            split_high(2)
            logits_copy(0)
            softmax_exp(0)
            bodies(act_, body)
            for t in range(T):
                finish(NG - 1, (NG - 1) % XS, t)

        @block.tensor
        def _(pe):
            pe.sem_inc(turned, 4)
            pe.sem_inc(down_done, 4)
            pe.sem_inc(mix_turned, 1)
            pe.wait_ge(consts, 12)

            def turn(g, t, first=False):
                pe.wait_ge(x1_normed, 4 * g + t + 1)
                if t:
                    pe.wait_ge(xl_made, 4 * g + t)
                elif not first:
                    pe.wait_ge(mix_out, g)
                for kc in range(KC):
                    last = pe.transpose(ptr[:, kc * P:kc * P + P], xf[:, t, kc * P:kc * P + P], k.ident[:])
                last.then_inc(turned, 1)

            def logits(g, n):
                pe.wait_ge(xl_made, 4 * g + 4)
                for kc in range(KC):
                    last = split3(pe, ptr[:], (wr[0][:, kc, :], wr[1][:, kc, :]), (xh[n][:, kc, :], xl[n][:, kc, :]),
                                  kc == 0, kc == KC - 1)
                last.then_inc(logits_done, 1)

            def turn_logits(g):
                pe.wait_ge(logits_out, g + 1)
                for t in range(T):
                    last = pe.matmul(ptr[:, t * SETS * 4:(t + 1) * SETS * 4], logit_t[:, t * P:t * P + P],
                                     k.ident[0:SETS * 4, 0:SETS * 4], start=True, stop=True)
                last.then_inc(logits_turned, 1)

            def up(g, n, cc, name, out, done):
                if name == "w1":
                    pe.wait_ge(hidden, 4 * g + cc + 1)
                sl = slice(cc * P, cc * P + P)
                for kc in range(KC):
                    last = split3(pe, out[cc % 2][:], (w[name][0][:, kc, sl], w[name][1][:, kc, sl]),
                                  (xh[n][:, kc, :], xl[n][:, kc, :]), kc == 0, kc == KC - 1)
                last.then_inc(done, 1)

            def spread(g, cc):
                pe.wait_ge(hidden, 4 * g + cc + 2)
                pe.matmul(pmix[:], expert_r[:, cc * P:cc * P + P], mix_t[:], start=True, stop=True).then_inc(mixed, 1)

            def turn_mix(g):
                pe.wait_ge(route, NROUTE * g + NROUTE)
                for t in range(T):
                    last = pe.transpose(ptr[:, t * P:t * P + P], parts[:, t, :].bitcast(F32), k.ident[:])
                last.then_inc(mix_turned, 1)

            def down(g, t, ccs):
                sl = slice(t * P, t * P + P)
                for cc in ccs:
                    if cc == 0:
                        pe.wait_ge(x2_made, 4 * g + t + 1)
                    pe.wait_ge(hl_made, 4 * g + cc + 1 + 2)
                    last = split3(pe, po[t % 2][:], (hh[:, cc, sl], hl[:, cc, sl]),
                                  (w["w2"][0][:, cc, :], w["w2"][1][:, cc, :]), cc == 0, cc == KC - 1)
                    if cc == KC - 1:
                        last.then_inc(down_done, 1)

            def body(i, c_):
                g, n, n1 = i * XS + c_, c_ % 2, (c_ + 1) % 2
                mid = in_range(i, c_, 1)
                up(g, n, 0, "w1", pa, up_done)
                turn_mix(g)
                up(g, n, 0, "w3", pc, gate_done)
                pe.wait_ge(mix_out, g + 1)
                spread(g, 0)
                if mid:
                    turn(g + 1, 0)
                up(g, n, 1, "w1", pa, up_done)
                if mid:
                    turn(g + 1, 1)
                up(g, n, 1, "w3", pc, gate_done)
                spread(g, 1)
                if mid:
                    turn(g + 1, 2)
                up(g, n, 2, "w1", pa, up_done)
                if mid:
                    turn(g + 1, 3)
                up(g, n, 2, "w3", pc, gate_done)
                spread(g, 2)
                up(g, n, 3, "w1", pa, up_done)
                if mid:
                    logits(g + 1, n1)
                up(g, n, 3, "w3", pc, gate_done)
                spread(g, 3)
                if mid:
                    turn_logits(g + 1)
                down(g, 0, (0, 1, 2))
                down(g, 1, (0, 1, 2))
                down(g, 0, (3,))
                down(g, 1, (3,))
                down(g, 2, range(KC))
                down(g, 3, range(KC))

            for t in range(T):
                turn(0, t, True)
            pe.wait_ge(weight_low[3], 1)
            logits(0, 0)
            turn_logits(0)
            for n in range(3):
                pe.wait_ge(weight_low[n], 1)
            bodies(pe, body)



def messages(nc, k, tag, source, jobs, table, beside=None):
    with ExitStack() as stack:
        c = Core(nc, stack, tag)
        weight = jobs[0][1:]
        stage = [c.sb(f"stage{n}", [P, KC, D]) for n in range(len(jobs))]
        loaded = [c.sem(f"loaded{n}") for n in range(len(jobs))]
        weight_high, weight_low = c.sem("weight_high"), c.sem("weight_low")
        at = c.sb("at", [P, T], I32)
        weights = c.sb("weights", [P, T])
        rows = c.sb("rows", [P, T, D])
        sums = c.sb("sums", [P, T, D])
        sh, sl = (c.sb(n, [P, 2, D], F32R) for n in ("sh", "sl"))
        out = c.sb("out", [P, 2, D])
        ptr = [c.ps(f"ptr{n}") for n in range(2)]
        po = [c.ps(f"po{n}") for n in range(2)]
        at_made = c.sem("at_made")
        rows_in = [c.sem(f"rows_in{t}") for t in range(T)]
        scaled, turned, summed, hi_made, lo_made, done, row_out = (
            c.sem(n) for n in ("scaled", "turned", "summed", "hi_made", "lo_made", "done", "row_out"))
        stored = [c.sem(f"stored{n}") for n in range(2)]
        block = stack.enter_context(nc.Block())
        same = k.same["d"]

        @block.gpsimd
        def _(pool):
            with pool.Fori(0, EG) as g:
                pool.wait_ge(scaled, 4 * g + 4)
                hold(pool)
                pool.tensor_copy(at[:], k.rec["d"][:, ds(T * g, T), 0]).then_inc(at_made, 1)
                pool.tensor_copy(weights[:], k.rec["d"][:, ds(T * g, T), 2].bitcast(F32)).then_inc(at_made, 1)
                pool.wait_ge(at_made, 2 * g + 2)
                for t in range(T):
                    pool.wait_ge(turned, 4 * g + t + 1)
                    hold(pool)
                    pool.indirect_dma_start(rows[:, t, :], None, source[:, :],
                                            bass.IndirectOffsetOnAxis(ap=at[:, t:t + 1], axis=0),
                                            bounds_check=NPAD - 1, oob_is_err=False).then_inc(rows_in[t], 16)
            if beside:
                beside.constants(pool)

        def copy_row(act_, g, t):
            act_.wait_ge(done, 4 * g + t + 1 + 2)
            act_.wait_ge(stored[t % 2], 32 * g + 16 * (t // 2) + 16)
            act_.activation(out[:, t % 2, :], po[t % 2][:], ACT.Copy).then_inc(row_out, 1)

        @block.scalar
        def _(act_):
            act_.sem_inc(row_out, 2)
            act_.sem_inc(scaled, 4)

            def scale(g, t):
                act_.wait_ge(rows_in[t], 16 * g + 16)
                act_.wait_ge(at_made, 2 * g + 2)
                act_.activation(rows[:, t, :], rows[:, t, :], ACT.Copy, scale=weights[:, t:t + 1]).then_inc(scaled, 1)

            def high(g, t):
                act_.wait_ge(summed, 4 * g + t + 1 + 4)
                act_.wait_ge(done, 4 * g + t + 1)
                act_.activation(sh[:, t % 2, :], sums[:, t, :], ACT.Copy).then_inc(hi_made, 1)

            def body(g, first, last):
                for t in range(T):
                    high(g, t)
                    if t:
                        copy_row(act_, g, t - 1)
                        if not last:
                            scale(g + 1, t - 1)
                    elif not first:
                        copy_row(act_, g - 1, T - 1)
                        scale(g, T - 1)
                if last:
                    copy_row(act_, g, T - 1)

            def split_high(n):
                act_.wait_ge(loaded[n], 16)
                act_.activation(jobs[n][1][:], stage[n][:], ACT.Copy).then_inc(weight_high, 1)

            scale(0, 0)
            scale(0, 1)
            split_high(0)
            scale(0, 2)
            scale(0, 3)
            body(0, True, False)
            with act_.Fori(1, EG - 1) as g:
                body(g, False, False)
            for n in range(1, len(jobs)):
                split_high(n)
            body(EG - 1, False, True)

        @block.vector
        def _(v):
            v.sem_inc(lo_made, 4)
            v.memset(sums[:], 0.0).then_inc(summed, 4)
            if beside:
                beside.zeros(v)

            def split_low(n):
                v.wait_ge(weight_high, n + 1)
                v.tensor_tensor(jobs[n][2][:], stage[n][:], jobs[n][1][:].bitcast(F32), ALU.subtract)\
                 .then_inc(weight_low, 1)

            split_low(0)
            with v.Fori(0, EG) as g:
                for t in range(T):
                    v.wait_ge(turned, 4 * g + t + 1 + 4)
                    v.wait_ge(summed, 4 * g + t + 4)
                    v.wait_ge(lo_made, 4 * g + t + 1)
                    hold(v)
                    for kc in range(KC):
                        own = slice(kc * P, kc * P + P)
                        last = v.tensor_tensor_scan(sums[:, t, own], same[:, ds(g * GR + t * P, P)], ptr[t % 2][:, own],
                                                    sums[:, (t - 1) % T, kc * P + P - 1:kc * P + P], ALU.mult, ALU.add)
                    last.then_inc(summed, 1)
                    v.wait_ge(hi_made, 4 * g + t + 1)
                    v.tensor_tensor(sl[:, t % 2, :], sums[:, t, :], sh[:, t % 2, :].bitcast(F32), ALU.subtract)\
                     .then_inc(lo_made, 1)
            for n in range(1, len(jobs)):
                split_low(n)
            v.wait_ge(weight_low, len(jobs))
            if beside:
                beside.arithmetic(v)

        @block.tensor
        def _(pe):
            pe.sem_inc(turned, 4)
            pe.sem_inc(done, 2)

            def turn(g, t):
                pe.wait_ge(scaled, 4 * g + t + 1 + 4)
                pe.wait_ge(summed, 4 * g + t - 1 + 4)
                for kc in range(KC):
                    own = slice(kc * P, kc * P + P)
                    last = pe.transpose(ptr[t % 2][:, own], rows[:, t, own], k.ident[:])
                last.then_inc(turned, 1)

            def product(g, t):
                pe.wait_ge(lo_made, 4 * g + t + 1 + 4)
                pe.wait_ge(row_out, 4 * g + t + 1)
                for kc in range(KC):
                    own = slice(kc * P, kc * P + P)
                    last = split3(pe, po[t % 2][:], (sh[:, t % 2, own], sl[:, t % 2, own]),
                                  (weight[0][:, kc, :], weight[1][:, kc, :]), kc == 0, kc == KC - 1)
                last.then_inc(done, 1)

            def body(g, last):
                for t in range(T):
                    if t < 2:
                        turn(g, t + 2)
                    elif not last:
                        turn(g + 1, t - 2)
                    product(g, t)

            turn(0, 0)
            turn(0, 1)
            pe.wait_ge(weight_low, 1)
            with pe.Fori(0, EG - 1) as g:
                body(g, False)
            body(EG - 1, True)
            if beside:
                beside.products(pe)

        @block.sync
        def _(sp):
            sp.sem_inc(stored[0], 16)
            sp.sem_inc(stored[1], 16)
            for n, (source_, _, _) in enumerate(jobs):
                sp.dma_start(stage[n][:], source_).then_inc(loaded[n], 16)
            if beside:
                beside.loads(sp)
            with sp.Fori(0, EG) as g:
                for t in range(T):
                    sp.wait_ge(row_out, 4 * g + t + 3)
                    sp.dma_start(table[ds(g * GR + t * P, P), :], out[:, t % 2, :]).then_inc(stored[t % 2], 16)
            for n in range(2):
                sp.wait_ge(stored[n], 16 + 16 * ET // 2)



def conv_phase(nc, a, k):
    with ExitStack() as stack:
        c = Core(nc, stack, "conv")
        w = {n: [c.sb(f"{n}_{h}", [P, KC, D], F32R) for h in ("hi", "lo")] for n in ("w11", "w01", "w02")}
        messages(nc, k, "msg1", k.y, [(chunks(a[f"g_{n}"]), *w[n]) for n in ("w11", "w01", "w02")], k.message1)
        yin = c.sb("yin", [P, T, D])
        msg = c.sb("msg", [P, T, D])
        at = c.sb("at", [P, T], I32)
        diag = c.sb("diag", [P, NT])
        dg, dg2 = c.sb("dg", [P, T]), c.sb("dg2", [P, T])
        bias = [c.sb(f"bias{n}", [P, D]) for n in range(2)]
        yh, yl, hh, hl = (c.sb(n, [P, 2, D], F32R) for n in ("yh", "yl", "hh", "hl"))
        h = c.sb("h", [P, T, D])
        own = c.sb("own", [P, 2, D])
        pty, pth, p1, p2 = ([c.ps(f"{n}{i}") for i in range(2)] for n in ("pty", "pth", "p1", "p2"))
        consts = c.sem("consts")
        y_in, msg_in, h_out = ([c.sem(f"{n}{t}") for t in range(T)] for n in ("y_in", "msg_in", "h_out"))
        own_out = [c.sem(f"own_out{n}") for n in range(2)]
        added = c.sem("added")
        at_made, msg_made, dg_made = c.sem("at_made"), c.sem("msg_made"), c.sem("dg_made")
        y_turned, yh_made, yl_made, one_done, summed, h_made = (
            c.sem(n) for n in ("y_turned", "yh_made", "yl_made", "one_done", "summed", "h_made"))
        h_turned, hh_made, hl_made, two_done, own_made = (
            c.sem(n) for n in ("h_turned", "hh_made", "hl_made", "two_done", "own_made"))
        block = stack.enter_context(nc.Block())

        @block.sync
        def _(sp):
            for t in range(T):
                sp.sem_inc(h_out[t], 16)
            for n in range(2):
                sp.sem_inc(own_out[n], 16)
            sp.dma_start(diag[:], a["diag"]).then_inc(consts, 16)
            for n in range(2):
                sp.dma_start(bias[n][:], a[f"g_b{n + 1}"].broadcast_to([P, D])).then_inc(consts, 16)

            def load(g, t):
                sp.wait_ge(y_turned, 4 * g + t + 1)
                sp.dma_start(yin[:, t, :], k.y[ds(g * GR + t * P, P), :]).then_inc(y_in[t], 16)

            def store_h(g, t):
                sp.wait_ge(h_made, 4 * g + t + 1)
                sp.dma_start(k.h[ds(g * GR + t * P, P), :], h[:, t, :]).then_inc(h_out[t], 16)

            def store_own(g, t):
                sp.wait_ge(own_made, 4 * g + t + 1 + 2)
                sp.dma_start(k.own[ds(g * GR + t * P, P), :], own[:, t % 2, :]).then_inc(own_out[t % 2], 16)

            for t in range(T):
                load(0, t)
            with sp.Fori(0, NG - 1) as g:
                for t in range(T):
                    store_h(g, t)
                    load(g + 1, t)
                    if t:
                        store_own(g, t - 1)
                store_own(g, T - 1)
            for t in range(T):
                store_h(NG - 1, t)
            for t in range(T):
                store_own(NG - 1, t)
            for t in range(T):
                sp.wait_ge(h_out[t], 16 + 16 * NG)
            for n in range(2):
                sp.wait_ge(own_out[n], 16 + 32 * NG)

        @block.gpsimd
        def _(pool):
            with pool.Fori(0, NG) as g:
                pool.wait_ge(summed, 4 * g + 4)
                hold(pool)
                pool.tensor_copy(at[:], k.slot["d"][:, ds(T * g, T)]).then_inc(at_made, 1)
                pool.memset(msg[:], 0.0).then_inc(msg_made, 1)
                pool.wait_ge(msg_made, g + 1)
                pool.wait_ge(at_made, g + 1)
                hold(pool)
                for t in range(T):
                    pool.indirect_dma_start(msg[:, t, :], None, k.message1[:, :],
                                            bass.IndirectOffsetOnAxis(ap=at[:, t:t + 1], axis=0),
                                            bounds_check=EP - 1, oob_is_err=False).then_inc(msg_in[t], 16)

        def nxt(g, t):
            return (g, t + 1) if t < T - 1 else (g + 1, 0)

        def prv(g, t):
            return (g, t - 1) if t else (g - 1, T - 1)

        def low(v, g, t, bank, hi, lo, made, ready):
            v.wait_ge(ready, 4 * g + t + 1)
            v.tensor_tensor(lo[:, t % 2, :], bank[t % 2][:], hi[:, t % 2, :].bitcast(F32), ALU.subtract)\
             .then_inc(made, 1)

        @block.vector
        def _(v):
            v.sem_inc(summed, 4)
            v.sem_inc(own_made, 2)
            v.wait_ge(consts, 48)

            def own_term(g, t):
                v.wait_ge(two_done, 4 * g + t + 1)
                v.wait_ge(own_out[t % 2], 32 * g + 16 * (t // 2) + 16)
                v.scalar_tensor_tensor(own[:, t % 2, :], p2[t % 2][:], dg2[:, t:t + 1], bias[1][:], ALU.mult, ALU.add)\
                 .then_inc(own_made, 1)

            def step(g, t, behind=2, last=False):
                if not last:
                    low(v, *nxt(g, t), pty, yh, yl, yl_made, yh_made)
                if behind >= 1:
                    low(v, *prv(g, t), pth, hh, hl, hl_made, hh_made)
                if behind >= 2:
                    own_term(*prv(*prv(g, t)))
                v.wait_ge(one_done, 4 * g + t + 1)
                v.wait_ge(msg_in[t], 16 * g + 16)
                v.wait_ge(h_out[t], 16 * g + 16)
                v.scalar_tensor_tensor(h[:, t, :], p1[t % 2][:], dg[:, t:t + 1], msg[:, t, :], ALU.mult, ALU.add)\
                 .then_inc(added, 1)
                v.wait_ge(added, 4 * g + t + 1)
                v.tensor_tensor(h[:, t, :], h[:, t, :], bias[0][:], ALU.add).then_inc(summed, 1)

            def group(g, first=False, last=False):
                for t in range(T):
                    if t == 0:
                        v.tensor_copy(dg[:], diag[:, ds(T * g, T)]).then_inc(dg_made, 1)
                        v.wait_ge(dg_made, 2 * g + 1)
                    step(g, t, t if first else 2, last and t == T - 1)
                    if t == 1:
                        v.wait_ge(own_made, 4 * g + 2)
                        hold(v)
                        v.tensor_copy(dg2[:], diag[:, ds(T * g, T)]).then_inc(dg_made, 1)
                        v.wait_ge(dg_made, 2 * g + 2)

            low(v, 0, 0, pty, yh, yl, yl_made, yh_made)
            group(0, first=True)
            with v.Fori(1, NG - 1) as g:
                group(g)
            group(NG - 1, last=True)
            low(v, NG - 1, T - 1, pth, hh, hl, hl_made, hh_made)
            own_term(NG - 1, T - 2)
            own_term(NG - 1, T - 1)
            v.wait_ge(own_made, NT + 2)

        @block.scalar
        def _(act_):
            def high(g, t, bank, hi, made, ready):
                act_.wait_ge(ready, 4 * g + t + 1)
                act_.activation(hi[:, t % 2, :], bank[t % 2][:], ACT.Copy).then_inc(made, 1)

            def step(g, t, first=False, last=False):
                if not last:
                    n = nxt(g, t)
                    act_.wait_ge(y_turned, 4 * n[0] + n[1] + 1 + 4)
                    act_.activation(yh[:, n[1] % 2, :], pty[n[1] % 2][:], ACT.Copy).then_inc(yh_made, 1)
                if not first:
                    high(*prv(g, t), pth, hh, hh_made, h_turned)
                act_.wait_ge(summed, 4 * g + t + 1 + 4)
                act_.activation(h[:, t, :], h[:, t, :], ACT.Relu).then_inc(h_made, 1)

            act_.wait_ge(y_turned, 5)
            act_.activation(yh[:, 0, :], pty[0][:], ACT.Copy).then_inc(yh_made, 1)
            for t in range(T):
                step(0, t, t == 0)
            with act_.Fori(1, NG - 1) as g:
                for t in range(T):
                    step(g, t)
            for t in range(T):
                step(NG - 1, t, False, t == T - 1)
            high(NG - 1, T - 1, pth, hh, hh_made, h_turned)

        @block.tensor
        def _(pe):
            pe.sem_inc(y_turned, 4)

            def turn(bank, src, t, done):
                for kc in range(KC):
                    own_ = slice(kc * P, kc * P + P)
                    last = pe.transpose(bank[t % 2][:, own_], src[:, t, own_], k.ident[:])
                last.then_inc(done, 1)

            def product(bank, hi, lo, name, t, done):
                for kc in range(KC):
                    own_ = slice(kc * P, kc * P + P)
                    last = split3(pe, bank[t % 2][:], (hi[:, t % 2, own_], lo[:, t % 2, own_]),
                                  (w[name][0][:, kc, :], w[name][1][:, kc, :]), kc == 0, kc == KC - 1)
                last.then_inc(done, 1)

            def turn_y(g, t, wait=True):
                pe.wait_ge(y_in[t], 16 * g + 16)
                if wait:
                    pe.wait_ge(yl_made, 4 * g + t - 1)
                turn(pty, yin, t, y_turned)

            def product_y(g, t, wait=True):
                pe.wait_ge(yl_made, 4 * g + t + 1)
                if wait:
                    pe.wait_ge(summed, 4 * g + t - 1 + 4)
                product(p1, yh, yl, "w01", t, one_done)

            def turn_h(g, t, wait=True):
                pe.wait_ge(h_made, 4 * g + t + 1)
                if wait:
                    pe.wait_ge(hl_made, 4 * g + t - 1)
                turn(pth, h, t, h_turned)

            def product_h(g, t, wait=True):
                pe.wait_ge(hl_made, 4 * g + t + 1)
                if wait:
                    pe.wait_ge(own_made, 4 * g + t - 1 + 2)
                product(p2, hh, hl, "w02", t, two_done)

            def step(g, t, start=False, last=False):
                n, b = nxt(g, t), prv(g, t)
                if not last:
                    turn_y(*n, not (start and t == 0))
                if not (start and t == 0):
                    turn_h(*b, not (start and t < 3))
                product_y(g, t, not (start and t < 2))
                if not (start and t == 0):
                    product_h(*b, not (start and t < 3))

            turn_y(0, 0, False)
            for t in range(T):
                step(0, t, True)
            with pe.Fori(1, NG - 1) as g:
                for t in range(T):
                    step(g, t)
            for t in range(T):
                step(NG - 1, t, False, t == T - 1)
            turn_h(NG - 1, T - 1)
            product_h(NG - 1, T - 1)



class Beside:
    pass


class Experts:
    pass


def expert_weights(nc, a, k, c, ci, x):
    x.w1, x.w2t = ([c.sb(f"{n}_{h}", [P, KC, FC1 * P], F32R) for h in ("hi", "lo")] for n in ("w1", "w2t"))
    x.gram = [c.sb(f"gram_{h}", [P, FC1, P], F32R) for h in ("hi", "lo")]
    x.w2g = [c.sb(f"w2g_{h}", [P, FC1, D], F32R) for h in ("hi", "lo")]
    x.route = [c.sb(f"route_{h}", [P, KC, P], F32R) for h in ("hi", "lo")]
    x.rows_x, x.rows_1 = c.sb("rows_x", [48, D], F32R), c.sb("rows_1", [48, D], F32R)
    x.b1 = c.sb("b1", [P, FC1])
    x.cross = c.sb("cross", [P, FC1])
    x.square = c.sb("square", [P, EXPERTS1])
    x.expert = c.sb("expert", [P, FC1, P], F32R)
    x.spread = c.sb("spread", [48, FC1 * P], F32R)
    x.earlier = c.sb("earlier", [P, EXPERTS1, EXPERTS1])
    w1 = ci.sb("w1", [P, KC, FC1 * P])
    w2, b2r, gr = (ci.sb(n, [P, FC1, D]) for n in ("w2", "b2r", "gr"))
    scratch = ci.sb("scratch", [P, D])
    mean = ci.sb("mean", [P, 2 * FC1 + 1])
    route = ci.sb("route", [P, KC, 16])
    w2t = ci.sb("w2t", [P, KC, FC1 * P])
    gram = ci.sb("gram", [P, FC1, P])
    g48, b48, beta48, t48 = (ci.sb(n, [48, D]) for n in ("g48", "b48", "beta48", "t48"))
    lo48 = ci.sb("lo48", [48, D])
    hi48 = ci.sb("hi48", [48, D], F32R)
    is_lo, is_lo2, is_hi = (ci.sb(n, [48, 1]) for n in ("is_lo", "is_lo2", "is_hi"))
    blocks = ci.sb("blocks", [P, P // HID1, HID1])
    ex, sp1, sp2 = ci.sb("ex", [P, FC1, EXPERTS1]), ci.sb("sp1", [48, FC1 * P]), ci.sb("sp2", [48, FC1 * P])
    pt, pg, psq = ci.ps("pt"), ci.ps("pg"), ci.ps("psq")
    arrived, chain, consts, turned, gram_done, square_done, zeroed = (
        ci.sem(n) for n in ("arrived", "chain", "consts", "turned", "gram_done", "square_done", "zeroed"))
    rows_arrived = ci.sem("rows_arrived")
    programs = Beside()
    per = P // HID1

    def loads(sp):
        sp.dma_start(w1[:], chunks(a["f_w1"])).then_inc(arrived, 16)
        sp.dma_start(w2[:], chunks(a["f_w2"])).then_inc(arrived, 16)
        sp.dma_start(x.b1[:], a["f_b1"]).then_inc(arrived, 16)
        with nc.allow_non_contiguous_dma(reason="router columns"):
            sp.dma_start(route[:, :, 0:8], a["f_router"].rearrange("(c p) n -> p c n", p=P)).then_inc(arrived, 16)
        for e in range(EXPERTS1):
            at = slice((e % per) * HID1, (e % per + 1) * HID1)
            for t, n in ((b2r, "f_b2"), (gr, "f_gamma")):
                sp.dma_start(t[at, e // per, :], a[n][e:e + 1, :].broadcast_to([HID1, D])).then_inc(arrived, 16)
        sp.wait_ge(zeroed, 3)
        for r in range(3):
            at = slice(r * EXPERTS1, (r + 1) * EXPERTS1)
            sp.dma_start(g48[at, :], a["f_gamma"]).then_inc(rows_arrived, 16)
            sp.dma_start(b48[at, :], a["f_b2"]).then_inc(rows_arrived, 16)
            sp.dma_start(beta48[24 + r * EXPERTS1:24 + (r + 1) * EXPERTS1, :], a["f_beta"]).then_inc(rows_arrived, 16)
        sp.wait_ge(rows_arrived, 9 * 16)

    def constants(pool):
        s = Steps(pool, consts)
        for t in (is_lo, is_lo2, blocks, ex, sp1, sp2, x.earlier):
            s(pool.memset(t[:], 1.0))
        s.settle()

        def band(m, base, pattern, mult, width):
            s.link(pool.affine_select(out=m, in_=m, compare_op=ALU.is_ge, fill=0.0, base=base,
                                      pattern=pattern, channel_multiplier=mult))
            s.link(pool.affine_select(out=m, in_=m, compare_op=ALU.is_ge, fill=0.0, base=width - 1 - base,
                                      pattern=[[-q, n] for q, n in pattern], channel_multiplier=-mult))

        band(is_lo[:], -8, [[0, 1]], 1, 8)
        band(is_lo2[:], -32, [[0, 1]], 1, 8)
        band(blocks[:], 0, [[-HID1, per], [0, HID1]], 1, HID1)
        band(ex[:], 0, [[P, FC1], [-HID1, EXPERTS1]], 1, HID1)
        band(sp1[:], 0, [[1, FC1 * P]], -HID1, HID1)
        band(sp2[:], 16 * HID1, [[1, FC1 * P]], -HID1, HID1)
        s(pool.affine_select(out=x.earlier[:], in_=x.earlier[:], compare_op=ALU.is_gt, fill=0.0, base=0,
                             pattern=[[1, EXPERTS1], [-1, EXPERTS1]], channel_multiplier=0))

    def zeros(v):
        for t in (g48, b48, beta48):
            v.memset(t[:], 0.0).then_inc(zeroed, 1)

    def arithmetic(v):
        s = Steps(v, chain)
        v.wait_ge(consts, 20)
        for t in (*x.route, x.expert):
            s(v.memset(t[:].bitcast(F32), 0.0))
        s.settle()
        s(v.tensor_copy(x.expert[:, :, LOGITS:SMALL], ex[:]))
        s(v.tensor_tensor(x.spread[:], sp1[:], sp2[:], ALU.add))
        s.link(v.tensor_tensor(is_lo[:], is_lo[:], is_lo2[:], ALU.add))
        s(v.tensor_scalar(is_hi[:], is_lo[:], -1.0, 1.0, ALU.mult, ALU.add))
        v.wait_ge(arrived, 16 * 20)
        s(v.tensor_copy(x.w1[0][:], w1[:]))
        for fc in range(FC1):
            s(v.tensor_reduce(mean[:, fc:fc + 1], w2[:, fc, :], X_AXIS, ALU.add))
            s(v.tensor_reduce(mean[:, FC1 + fc:FC1 + fc + 1], b2r[:, fc, :], X_AXIS, ALU.add))
        s.settle()
        s(v.tensor_tensor(x.w1[1][:], w1[:], x.w1[0][:].bitcast(F32), ALU.subtract))
        s.link(v.tensor_scalar(mean[:, 0:2 * FC1], mean[:, 0:2 * FC1], -1.0 / D, None, ALU.mult))
        for fc in range(FC1):
            s(v.tensor_scalar(w2[:, fc, :], w2[:, fc, :], mean[:, fc:fc + 1], None, ALU.add))
            s(v.tensor_scalar(b2r[:, fc, :], b2r[:, fc, :], mean[:, FC1 + fc:FC1 + fc + 1], None, ALU.add))
        s.settle()
        for fc in range(FC1):
            s.link(v.scalar_tensor_tensor(scratch[:], w2[:, fc, :], 2.0, b2r[:, fc, :], ALU.mult, ALU.mult,
                                          accum_out=x.cross[:, fc:fc + 1]))
        s.link(v.tensor_tensor(gr[:], gr[:], w2[:], ALU.mult))
        s.link(v.tensor_copy(x.w2g[0][:], gr[:]))
        s(v.tensor_tensor(x.w2g[1][:], gr[:], x.w2g[0][:].bitcast(F32), ALU.subtract))
        v.wait_ge(rows_arrived, 9 * 16)
        s.link(v.tensor_reduce(mean[0:48, 2 * FC1:2 * FC1 + 1], b48[:], X_AXIS, ALU.add))
        s.link(v.tensor_scalar(mean[0:48, 2 * FC1:2 * FC1 + 1], mean[0:48, 2 * FC1:2 * FC1 + 1], -1.0 / D, None,
                               ALU.mult))
        s.link(v.tensor_scalar(b48[:], b48[:], mean[0:48, 2 * FC1:2 * FC1 + 1], None, ALU.add))
        centred = s.n
        assert centred == 26, centred
        for kc in range(KC):
            v.wait_ge(turned, kc + 1)
            s(v.tensor_scalar(w2t[:, kc, :], pt[:, 0:FC1 * P], 2.0, None, ALU.mult))
            s.link(v.tensor_scalar(route[:, kc, 8:16], pt[:, FC1 * P:FC1 * P + 8], 2.0, None, ALU.mult))
        s(v.tensor_copy(x.w2t[0][:], w2t[:]))
        s.link(v.tensor_copy(x.route[0][:, :, 0:LOGITS], route[:]))
        s(v.tensor_tensor(x.w2t[1][:], w2t[:], x.w2t[0][:].bitcast(F32), ALU.subtract))
        s(v.tensor_tensor(x.route[1][:, :, 0:LOGITS], route[:], x.route[0][:, :, 0:LOGITS].bitcast(F32),
                          ALU.subtract))
        s(v.tensor_tensor(scratch[:, 0:KC * 8].rearrange("p (c n) -> p c n", c=KC), route[:, :, 8:16],
                          route[:, :, 8:16], ALU.mult))
        assert s.n == 39, s.n
        s.link(v.tensor_tensor(t48[:], b48[:], g48[:], ALU.mult))
        s.link(v.tensor_tensor(t48[:], t48[:], beta48[:], ALU.add))
        for src, dst in ((g48, x.rows_x), (t48, x.rows_1)):
            s.link(v.tensor_copy(hi48[:], src[:]))
            s.link(v.tensor_tensor(lo48[:], src[:], hi48[:].bitcast(F32), ALU.subtract))
            s.link(v.tensor_scalar(lo48[:], lo48[:], is_lo[:], None, ALU.mult))
            s.link(v.scalar_tensor_tensor(dst[:], hi48[:].bitcast(F32), is_hi[:], lo48[:], ALU.mult, ALU.add))
        v.wait_ge(gram_done, 1)
        s.settle()
        for fc in range(FC1):
            s(v.scalar_tensor_tensor(gram[:, fc, :], pg[:, fc * P:fc * P + P], 0.25,
                                     blocks[:].rearrange("p a b -> p (a b)"), ALU.mult, ALU.mult))
        s.settle()
        s.link(v.tensor_copy(x.gram[0][:], gram[:]))
        s(v.tensor_tensor(x.gram[1][:], gram[:], x.gram[0][:].bitcast(F32), ALU.subtract))
        v.wait_ge(square_done, 1)
        s(v.tensor_scalar(x.square[:], psq[:, 0:8], 0.25, None, ALU.mult))

    def products(pe):
        for kc in range(KC):
            pe.wait_ge(chain, 26 + 2 * kc)
            for fc in range(FC1):
                pe.transpose(pt[:, fc * P:fc * P + P], w2[:, fc, kc * P:kc * P + P], k.ident[:])
            pe.matmul(pt[:, FC1 * P:FC1 * P + 8], b48[0:8, kc * P:kc * P + P], k.ident[0:8, 0:8],
                      start=True, stop=True).then_inc(turned, 1)
        pe.wait_ge(chain, 39)
        for fc in range(FC1):
            for kc in range(KC):
                part = w2t[:, kc, fc * P:fc * P + P]
                last = pe.matmul(pg[:, fc * P:fc * P + P], part, part, start=kc == 0, stop=kc == KC - 1)
        last.then_inc(gram_done, 1)
        for kc in range(KC):
            last = pe.matmul(psq[:, 0:8], k.ones[:], scratch[:, kc * 8:kc * 8 + 8], start=kc == 0,
                             stop=kc == KC - 1)
        last.then_inc(square_done, 1)

    programs.loads, programs.zeros, programs.constants = loads, zeros, constants
    programs.arithmetic, programs.products = arithmetic, products
    return programs



def message2_phase(nc, a, k, keep):
    with ExitStack() as stack:
        c = Core(nc, stack, "m2")
        w12 = [c.sb(f"w12_{h}", [P, KC, D], F32R) for h in ("hi", "lo")]
        ex = Experts()
        beside = expert_weights(nc, a, k, Core(nc, keep, "ex", side="right"), c, ex)
        messages(nc, k, "msg2", k.h, [(chunks(a["g_w12"]), *w12)], k.message2, beside)
    return ex


def dense1_phase(nc, a, k, ex, out):
    with ExitStack() as stack:
        c = Core(nc, stack, "d1")
        x3 = [c.sb(f"x3{n}", [P, T, D]) for n in range(XS)]
        xf = [c.sb(f"xf{n}", [P, T, D]) for n in range(XS)]
        own, msg = (c.sb(n, [P, T, D]) for n in ("own", "msg"))
        at = c.sb("at", [P, T], I32)
        gain, middle = c.sb("gain", [P, T]), c.sb("middle", [P, T])
        xh, xl = ([c.sb(f"{n}{i}", [P, KC, GR], F32R) for i in range(2)] for n in ("xh", "xl"))
        hid = [c.sb(f"hid{n}", [P, FC1, GR]) for n in range(2)]
        quad, weighted = c.sb("quad", [P, FC1, GR]), c.sb("weighted", [P, FC1, GR])
        hh, hl, qh, ql, ch, cl = (c.sb(n, [P, FC1, GR], F32R) for n in ("hh", "hl", "qh", "ql", "ch", "cl"))
        st, mv = c.sb("st", [P, T, 6]), c.sb("mv", [P, T, 2])
        ve, rs, shift, power_in = (c.sb(n, [P, T]) for n in ("ve", "rs", "shift", "power_in"))
        msq = [c.sb(f"msq{n}", [P, T]) for n in range(XS)]
        S3, S4 = [P, T, EXPERTS1], [P, T, 2, EXPERTS1]
        small_t = c.sb("small_t", [SMALL, GR])
        logit = c.sb("logit", [P, T, LOGITS])
        prob, rank, var, coef = (c.sb(n, S3) for n in ("prob", "rank", "var", "coef"))
        chosen = [c.sb(f"chosen{n}", [P, T, 2, EXPERTS1]) for n in range(2)]
        spare = c.sb("spare", [P, T, 2, EXPERTS1])
        place = c.sb("place", [P, 2, EXPERTS1])
        var2, rs2 = c.sb("var2", [P, T, 2]), c.sb("rs2", [P, T, 2])
        gate = [c.sb(f"gate{n}", S3) for n in range(2)]
        top, total = c.sb("top", [P, T]), c.sb("total", [P, T])
        wins, ties = (c.sb(n, [P, T, EXPERTS1, EXPERTS1]) for n in ("wins", "ties"))
        parts = c.sb("parts", [P, T, P], F32R)
        coef_t = c.sb("coef_t", [48, GR], F32R)
        pu, pq = ([c.ps(f"{n}{i}") for i in range(2)] for n in ("pu", "pq"))
        ptr, psm, pb, px = (c.ps(n) for n in ("ptr", "psm", "pb", "px"))
        pox, po1 = [pu[0], pb, pq[0], pb], [pu[1], px, pq[1], px]

        NSTAT, NCOEF, NVAR, NROUTE, EXP_STEP = 4, 9, 7, 13, 3
        consts = c.sem("consts")
        y_in = [[c.sem(f"y_in{u}{t}") for t in range(T)] for u in range(XS)]
        own_in, msg_in, out_done = ([c.sem(f"{n}{t}") for t in range(T)] for n in ("own_in", "msg_in", "out_done"))
        at_made, msg_made, added, relu_done, halved_low, halved_high, affine = (
            c.sem(n) for n in ("at_made", "msg_made", "added", "relu_done", "halved_low", "halved_high",
                                   "affine"))
        gains, stats, pow_done, shifted, normed = (c.sem(n) for n in ("gains", "stats", "pow_done", "shifted", "normed"))
        turned, xh_made, xl_made = (c.sem(n) for n in ("turned", "xh_made", "xl_made"))
        small_done, small_out, small_turned = (c.sem(n) for n in ("small_done", "small_out", "small_turned"))
        up_done, hid_made, hh_made, hl_made = (c.sem(n) for n in ("up_done", "hid_made", "hh_made", "hl_made"))
        cross_done, quad_made, qh_made, ql_made = (c.sem(n) for n in ("cross_done", "quad_made", "qh_made", "ql_made"))
        route, exp_done, vars_, pow2_done, coefs = (c.sem(n) for n in ("route", "exp_done", "vars", "pow2_done", "coefs"))
        coef_turned, coef_out, spread_done, scaled = (
            c.sem(n) for n in ("coef_turned", "coef_out", "spread_done", "scaled"))
        ch_made, cl_made, x_done, one_done, mul_done, finished_low, finished_high = (
            c.sem(n) for n in ("ch_made", "cl_made", "x_done", "one_done", "mul_done", "finished_low", "finished_high"))
        block = stack.enter_context(nc.Block())

        def bodies(eng, body):
            body(0, 0)
            with eng.Fori(0, (NG - XS) // XS) as i:
                for c_ in range(1, XS + 1):
                    body(i, c_)
            for c_ in range(NG - XS + 1, NG + 1):
                body(0, c_)

        def in_range(i, c_, ahead):
            return not isinstance(i, int) or 0 <= c_ + ahead < NG

        @block.sync
        def _(sp):
            def load_y(g, u, t):
                sp.dma_start(x3[u][:, t, :], k.y[ds(g * GR + t * P, P), :]).then_inc(y_in[u][t], 16)

            def load_own(g, t):
                sp.wait_ge(added, 4 * g + t + 1)
                sp.dma_start(own[:, t, :], k.own[ds(g * GR + t * P, P), :]).then_inc(own_in[t], 16)

            def body(i, c_):
                g = i * XS + c_
                if in_range(i, c_, 3):
                    for t in range(T):
                        load_own(g + 3, t)
                if not in_range(i, c_, -1):
                    return
                for t in range(T):
                    if t == 0:
                        sp.wait_ge(finished_low, g)
                    else:
                        sp.wait_ge(finished_high, 3 * (g - 1) + t)
                    sp.dma_start(out[ds((g - 1) * GR + t * P, P), :], xf[(c_ - 1) % XS][:, t, :])\
                      .then_inc(out_done[t], 16)
                    if in_range(i, c_, 3):
                        load_y(g + 3, (c_ - 1) % XS, t)

            for t in range(T):
                load_own(0, t)
            for g in range(XS):
                for t in range(T):
                    load_y(g, g, t)
            for g in (1, 2):
                for t in range(T):
                    load_own(g, t)
            bodies(sp, body)
            for t in range(T):
                sp.wait_ge(out_done[t], 16 * XS + 16 * NG)

        @block.gpsimd
        def _(pool):
            def gather(g):
                pool.wait_ge(halved_low, 2 * g + 2)
                pool.wait_ge(halved_high, 2 * g + 2)
                hold(pool)
                pool.tensor_copy(at[:], k.slot["d"][:, ds(T * g, T)]).then_inc(at_made, 1)
                pool.memset(msg[:], 0.0).then_inc(msg_made, 1)
                pool.wait_ge(msg_made, g + 1)
                pool.wait_ge(at_made, g + 1)
                hold(pool)
                for t in range(T):
                    pool.indirect_dma_start(msg[:, t, :], None, k.message2[:, :],
                                            bass.IndirectOffsetOnAxis(ap=at[:, t:t + 1], axis=0),
                                            bounds_check=EP - 1, oob_is_err=False).then_inc(msg_in[t], 16)

            def add(g, t):
                pool.wait_ge(own_in[t], 16 * g + 16)
                pool.wait_ge(msg_in[t], 16 * g + 16)
                pool.tensor_tensor(msg[:, t, :], msg[:, t, :], own[:, t, :], ALU.add).then_inc(added, 1)

            def sum_(g, u, t):
                pool.wait_ge(relu_done, 4 * g + t + 1)
                pool.wait_ge(affine, 4 * g + t + 1)
                pool.tensor_tensor(x3[u][:, t, :], x3[u][:, t, :], msg[:, t, :], ALU.add).then_inc(halved_low, 1)

            def power(g):
                pool.wait_ge(stats, NSTAT * g + 4)
                pool.tensor_tensor(rs[:], ve[:], k.half_neg[:, 0:T], ALU.pow).then_inc(pow_done, 1)

            def power2(g):
                pool.wait_ge(vars_, NVAR * g + NVAR)
                pool.tensor_tensor(rs2[:].rearrange("p t n -> p (t n)"), var2[:].rearrange("p t n -> p (t n)"),
                                   k.half_neg[:, 0:T * 2], ALU.pow).then_inc(pow2_done, 1)

            def low(g, fc, src, hi, lo, ready, made):
                pool.wait_ge(ready, FC1 * g + fc + 1)
                pool.tensor_tensor(lo[:, fc, :], src[:, fc, :], hi[:, fc, :].bitcast(F32), ALU.subtract)\
                    .then_inc(made, 1)

            def finish(g, u, t):
                pool.wait_ge(mul_done, 8 * g + 2 * t + 2 + 16)
                pool.tensor_tensor(xf[u][:, t, :], x3[u][:, t, :], xf[u][:, t, :], ALU.add).then_inc(finished_high, 1)

            def body(i, c_):
                g, uz = i * XS + c_, (c_ - 1) % XS
                front, main, behind = in_range(i, c_, 2), in_range(i, c_, 0), in_range(i, c_, -1)
                for fc in range(FC1):
                    if main:
                        low(g, fc, hid[c_ % 2], hh, hl, hh_made, hl_made)
                for t in range(2):
                    if front:
                        sum_(g + 2, (c_ + 2) % XS, t)
                for fc in range(FC1):
                    if behind:
                        low(g - 1, fc, weighted, ch, cl, ch_made, cl_made)
                    if main:
                        low(g, fc, quad, qh, ql, qh_made, ql_made)
                if in_range(i, c_, 3):
                    gather(g + 3)
                if front:
                    power(g + 2)
                if main:
                    power2(g)
                for t in range(T):
                    if in_range(i, c_, 3):
                        add(g + 3, t)
                    if behind and t < 3:
                        finish(g - 1, uz, t + 1)

            pool.sem_inc(added, 4)
            pool.sem_inc(halved_low, 2)
            for g in range(3):
                gather(g)
                for t in range(T):
                    add(g, t)
                if g < 2:
                    for t in range(2):
                        sum_(g, g, t)
                    power(g)
            bodies(pool, body)

        @block.scalar
        def _(act_):
            def halves(i, c_, t):
                g, u = i * XS + c_, c_ % XS
                act_.wait_ge(added, 4 * g + t + 1 + 4)
                act_.activation(msg[:, t, :], msg[:, t, :], ACT.Relu, scale=0.5).then_inc(relu_done, 1)
                act_.wait_ge(y_in[u][t], i * 16 + 16 * (c_ // XS + 1))
                act_.wait_ge(gains, 2 * g + 2)
                act_.activation(x3[u][:, t, :], x3[u][:, t, :], ACT.Identity, bias=middle[:, t:t + 1],
                                scale=gain[:, t:t + 1]).then_inc(affine, 1)

            def norm(g, u):
                act_.wait_ge(shifted, 3 * g + 1)
                for t in range(T):
                    act_.wait_ge(out_done[t], 16 * g + 16)
                    act_.activation(xf[u][:, t, :], x3[u][:, t, :], ACT.Identity, bias=shift[:, t:t + 1],
                                    scale=rs[:, t:t + 1]).then_inc(normed, 1)

            def high(g, n, t):
                act_.wait_ge(turned, 4 * g + t + 1)
                act_.activation(xh[n][:, :, t * P:t * P + P], ptr[:].rearrange("p (c n) -> p c n", n=P), ACT.Copy)\
                    .then_inc(xh_made, 1)

            def hidden(g, n, fc):
                act_.wait_ge(up_done, FC1 * g + fc + 1)
                act_.activation(hid[n][:, fc, :], pu[fc][:], ACT.Relu, bias=ex.b1[:, fc:fc + 1]).then_inc(hid_made, 1)
                act_.wait_ge(hid_made, FC1 * g + fc + 1)
                act_.activation(hh[:, fc, :], hid[n][:, fc, :], ACT.Copy).then_inc(hh_made, 1)

            def part(g, fc, src, hi, ready, made):
                act_.wait_ge(ready, FC1 * g + fc + 1)
                act_.activation(hi[:, fc, :], src[:, fc, :], ACT.Copy).then_inc(made, 1)

            def small_copy(g):
                act_.wait_ge(small_done, g + 1)
                act_.activation(small_t[:], psm[0:SMALL, :], ACT.Copy).then_inc(small_out, 1)

            def softmax_exp(g):
                act_.wait_ge(route, NROUTE * g + EXP_STEP)
                act_.activation(prob[:], prob[:], ACT.Exp).then_inc(exp_done, 1)

            def body(i, c_):
                g, n, n1 = i * XS + c_, c_ % 2, (c_ + 1) % 2
                front, mid, main, behind = (in_range(i, c_, ahead) for ahead in (2, 1, 0, -1))
                if mid:
                    norm(g + 1, (c_ + 1) % XS)
                for fc in range(FC1):
                    if main:
                        hidden(g, n, fc)
                    if mid:
                        high(g + 1, n1, fc)
                    if front:
                        halves(i, c_ + 2, fc)
                if behind:
                    act_.wait_ge(coef_turned, g + 1)
                    act_.activation(coef_t[:], px[0:48, :], ACT.Copy).then_inc(coef_out, 1)
                for fc in range(FC1):
                    if front:
                        halves(i, c_ + 2, 2 + fc)
                    if mid:
                        high(g + 1, n1, 2 + fc)
                    if behind:
                        part(g - 1, fc, weighted, ch, scaled, ch_made)
                    if main:
                        part(g, fc, quad, qh, quad_made, qh_made)
                if main:
                    small_copy(g + 1)
                if mid:
                    softmax_exp(g + 1)

            for t in range(T):
                act_.sem_inc(out_done[t], 16 * XS)
            for t in range(T):
                halves(0, 0, t)
            norm(0, 0)
            for t in range(T):
                high(0, 0, t)
            for t in range(T):
                halves(0, 1, t)
            small_copy(0)
            softmax_exp(0)
            bodies(act_, body)

        @block.vector
        def _(v):
            v.sem_inc(halved_high, 2)
            v.sem_inc(mul_done, 16)
            v.memset(parts[:, :, 48:P].bitcast(F32), 0.0).then_inc(consts, 1)
            for n in range(2):
                v.memset(place[:, n, :], float(n)).then_inc(consts, 1)
            v.wait_ge(consts, 3)

            def gains_of(i, c_):
                g = i * XS + c_
                if in_range(i, c_, -1):
                    v.wait_ge(affine, 4 * g)
                hold(v)
                v.tensor_scalar(gain[:], k.dev[:, ds(T * g, T)], 0.5, None, ALU.add).then_inc(gains, 1)
                v.tensor_copy(middle[:], k.mean[:, ds(T * g, T)]).then_inc(gains, 1)

            def sum_(g, u, t):
                v.wait_ge(relu_done, 4 * g + t + 1)
                v.wait_ge(affine, 4 * g + t + 1)
                v.tensor_tensor(x3[u][:, t, :], x3[u][:, t, :], msg[:, t, :], ALU.add).then_inc(halved_high, 1)

            def statistics(i, c_):
                g, u = i * XS + c_, c_ % XS
                s = Steps(v, stats, NSTAT * g)
                v.wait_ge(halved_low, 2 * g + 2 + 2)
                v.wait_ge(halved_high, 2 * g + 2 + 2)
                if in_range(i, c_, -1):
                    v.wait_ge(normed, 4 * g)
                hold(v)
                for t in range(T):
                    ins = v.bn_stats(st[:, t, :], x3[u][:, t, :])
                s.link(ins)
                hold(v)
                for t in range(T):
                    ins = v.bn_aggr(mv[:, t, :], st[:, t, :])
                s.link(ins)
                s(v.tensor_scalar(shift[:], mv[:, :, 0], -1.0, None, ALU.mult))
                s(v.tensor_scalar(ve[:], mv[:, :, 1], 1e-5, None, ALU.add))

            def shifts(g, u):
                v.wait_ge(pow_done, g + 1)
                v.tensor_tensor(shift[:], shift[:], rs[:], ALU.mult).then_inc(shifted, 1)
                v.tensor_tensor(power_in[:], mv[:, :, 1], rs[:], ALU.mult).then_inc(shifted, 1)
                v.wait_ge(shifted, 3 * g + 2)
                v.tensor_tensor(msq[u][:], power_in[:], rs[:], ALU.mult).then_inc(shifted, 1)

            def low(g, n, t):
                v.wait_ge(xh_made, 4 * g + t + 1)
                v.tensor_tensor(xl[n][:, :, t * P:t * P + P], ptr[:].rearrange("p (c n) -> p c n", n=P),
                                xh[n][:, :, t * P:t * P + P].bitcast(F32), ALU.subtract).then_inc(xl_made, 1)

            def quadratic(g, n, fc):
                v.wait_ge(cross_done, FC1 * g + fc + 1)
                v.scalar_tensor_tensor(quad[:, fc, :], pq[fc][:], ex.cross[:, fc:fc + 1], hid[n][:, fc, :], ALU.add,
                                       ALU.mult).then_inc(quad_made, 1)

            def wide(t_):
                return t_.unsqueeze(2).broadcast_to(S3)

            def small():
                return psm[:, 0:T * SMALL].rearrange("p (t n) -> p t n", t=T)

            def routing(g, n, between):
                s = Steps(v, route, NROUTE * g)
                v.wait_ge(small_turned, g + 1)
                s.link(v.tensor_copy(logit[:], small()[:, :, 0:LOGITS]))
                choice = logit[:, :, 0:EXPERTS1]
                s.link(v.tensor_reduce(top[:], choice, X_AXIS, ALU.max))
                s(v.tensor_tensor(prob[:], choice, wide(top[:]), ALU.subtract))
                assert s.n == EXP_STEP

                def link(ins):
                    s.link(ins)
                    if s.n in between:
                        between[s.n]()
                        s.settle()

                other = choice.unsqueeze(2).broadcast_to([P, T, EXPERTS1, EXPERTS1])
                mine = choice.unsqueeze(3).broadcast_to([P, T, EXPERTS1, EXPERTS1])
                s(v.tensor_tensor(wins[:], other, mine, ALU.is_gt))
                link(v.tensor_tensor(ties[:], other, mine, ALU.is_equal))
                link(v.tensor_tensor(ties[:], ties[:],
                                     ex.earlier[:].unsqueeze(1).broadcast_to([P, T, EXPERTS1, EXPERTS1]), ALU.mult))
                link(v.tensor_tensor(wins[:], wins[:], ties[:], ALU.add))
                link(v.tensor_reduce(rank[:], wins[:], X_AXIS, ALU.add))
                s(v.tensor_tensor(chosen[n][:], rank[:].unsqueeze(2).broadcast_to(S4),
                                  place[:].unsqueeze(1).broadcast_to(S4), ALU.is_equal))
                v.wait_ge(exp_done, g + 1)
                link(v.scalar_tensor_tensor(gate[n][:], rank[:], 1.0, prob[:], ALU.is_le, ALU.mult))
                link(v.tensor_reduce(total[:], gate[n][:], X_AXIS, ALU.add))
                link(v.reciprocal(total[:], total[:]))
                link(v.tensor_tensor(gate[n][:], gate[n][:], wide(total[:]), ALU.mult))
                assert s.n == NROUTE

            def variance(g, n, u):
                s = Steps(v, vars_, NVAR * g)
                v.wait_ge(small_turned, g + 2)
                v.wait_ge(shifted, 3 * g + 3)
                s.link(v.tensor_tensor(var[:], small()[:, :, LOGITS:SMALL], logit[:, :, EXPERTS1:LOGITS], ALU.add))
                s.link(v.tensor_tensor(var[:], var[:], ex.square[:].unsqueeze(1).broadcast_to(S3), ALU.add))
                s.link(v.tensor_scalar(var[:], var[:], 1.0 / D, None, ALU.mult))
                s.link(v.tensor_tensor(var[:], var[:], wide(msq[u][:]), ALU.add))
                s.link(v.tensor_scalar(var[:], var[:], 0.0, 1e-6, ALU.max, ALU.add))
                s.link(v.tensor_tensor(spare[:], chosen[n][:], var[:].unsqueeze(2).broadcast_to(S4), ALU.mult))
                s(v.tensor_reduce(var2[:], spare[:], X_AXIS, ALU.add))
                assert s.n == NVAR

            def coefficients(g, n):
                s = Steps(v, coefs, NCOEF * g)
                v.wait_ge(pow2_done, g + 1)
                v.wait_ge(coef_turned, g + 1)
                s.link(v.tensor_tensor(spare[:], chosen[n][:], rs2[:].unsqueeze(3).broadcast_to(S4), ALU.mult))
                s.link(v.tensor_tensor(coef[:], spare[:, :, 0, :], spare[:, :, 1, :], ALU.add))
                s.link(v.tensor_tensor(coef[:], coef[:], gate[n][:], ALU.mult))
                E1 = EXPERTS1
                for at_, src in ((0, coef), (3 * E1, gate[n])):
                    s(v.tensor_copy(parts[:, :, at_:at_ + E1], src[:]))
                    s.link(v.tensor_copy(parts[:, :, at_ + E1:at_ + 2 * E1], src[:]))
                    s(v.tensor_tensor(parts[:, :, at_ + 2 * E1:at_ + 3 * E1], src[:],
                                      parts[:, :, at_:at_ + E1].bitcast(F32), ALU.subtract))
                assert s.n == NCOEF

            def scale(g, n, fc):
                v.wait_ge(spread_done, FC1 * g + fc + 1)
                v.tensor_tensor(weighted[:, fc, :], hid[n][:, fc, :], pb[:], ALU.mult).then_inc(scaled, 1)

            def finish(g, u, t):
                v.wait_ge(x_done, 4 * g + t + 1)
                v.tensor_tensor(xf[u][:, t, :], xf[u][:, t, :], pox[t][:], ALU.mult).then_inc(mul_done, 1)
                v.wait_ge(one_done, 4 * g + t + 1)
                v.tensor_tensor(x3[u][:, t, :], x3[u][:, t, :], po1[t][:], ALU.add).then_inc(mul_done, 1)
                if t == 0:
                    v.wait_ge(mul_done, 8 * g + 2 * t + 2 + 16)
                    v.tensor_tensor(xf[u][:, t, :], x3[u][:, t, :], xf[u][:, t, :], ALU.add).then_inc(finished_low, 1)

            def body(i, c_):
                g, n, n1 = i * XS + c_, c_ % 2, (c_ + 1) % 2
                u2, uz = (c_ + 2) % XS, (c_ - 1) % XS
                front, mid, main, behind = (in_range(i, c_, ahead) for ahead in (2, 1, 0, -1))
                if behind:
                    coefficients(g - 1, n1)
                for t in range(2):
                    if mid:
                        low(g + 1, n1, t)
                for fc in range(FC1):
                    if behind:
                        scale(g - 1, n1, fc)
                    if mid:
                        low(g + 1, n1, 2 + fc)
                    if main:
                        quadratic(g, n, fc)
                    if front:
                        sum_(g + 2, u2, 2 + fc)
                if front:
                    statistics(i, c_ + 2)
                if in_range(i, c_, 3):
                    gains_of(i, c_ + 3)
                if behind:
                    finish(g - 1, uz, 0)
                if main:
                    variance(g, n, c_ % XS)
                if behind:
                    finish(g - 1, uz, 1)

                def between():
                    if front:
                        shifts(g + 2, u2)
                    if behind:
                        finish(g - 1, uz, 2)

                if mid:
                    routing(g + 1, n1, {7: between})
                else:
                    between()
                if behind:
                    finish(g - 1, uz, 3)

            gains_of(0, 0)
            for t in range(2, T):
                sum_(0, 0, t)
            statistics(0, 0)
            gains_of(0, 1)
            shifts(0, 0)
            for t in range(T):
                low(0, 0, t)
            for t in range(2, T):
                sum_(1, 1, t)
            statistics(0, 1)
            gains_of(0, 2)
            shifts(1, 1)
            routing(0, 0, {})
            bodies(v, body)

        @block.tensor
        def _(pe):
            pe.sem_inc(coef_turned, 1)
            pe.wait_ge(consts, 3)

            def turn(g, u, t, first=False):
                pe.wait_ge(normed, 4 * g + t + 1)
                if not first:
                    pe.wait_ge(xl_made, 4 * g + t)
                for kc in range(KC):
                    last = pe.transpose(ptr[:, kc * P:kc * P + P], xf[u][:, t, kc * P:kc * P + P], k.ident[:])
                last.then_inc(turned, 1)

            def logits(g, n, alone):
                pe.wait_ge(xl_made, 4 * g + 4)
                for kc in range(KC):
                    last = split3(pe, psm[:], (ex.route[0][:, kc, :], ex.route[1][:, kc, :]),
                                  (xh[n][:, kc, :], xl[n][:, kc, :]), kc == 0, kc == KC - 1 and alone)
                if alone:
                    last.then_inc(small_done, 1)

            def squares(g, alone):
                for fc in range(FC1):
                    pe.wait_ge(ql_made, FC1 * g + fc + 1)
                    for n, q in enumerate((qh, ql)):
                        last = pe.matmul(psm[:], ex.expert[:, fc, :], q[:, fc, :], start=alone and fc == 0 and n == 0,
                                         stop=fc == FC1 - 1 and n == 1, skip_group_check=True)
                last.then_inc(small_done, 1)

            def turn_small(g):
                pe.wait_ge(small_out, g + 1)
                for t in range(T):
                    last = pe.matmul(psm[:, t * SMALL:(t + 1) * SMALL], small_t[:, t * P:t * P + P],
                                     k.ident[0:SMALL, 0:SMALL], start=True, stop=True)
                last.then_inc(small_turned, 1)

            def up(g, n, fc):
                if fc == 0:
                    pe.wait_ge(mul_done, 8 * g + 2)
                sl = slice(fc * P, fc * P + P)
                for kc in range(KC):
                    last = split3(pe, pu[fc][:], (ex.w1[0][:, kc, sl], ex.w1[1][:, kc, sl]),
                                  (xh[n][:, kc, :], xl[n][:, kc, :]), kc == 0, kc == KC - 1)
                last.then_inc(up_done, 1)

            def cross(g, n, fc):
                if fc == 0:
                    pe.wait_ge(mul_done, 8 * g + 6)
                sl = slice(fc * P, fc * P + P)
                for kc in range(KC):
                    split3(pe, pq[fc][:], (ex.w2t[0][:, kc, sl], ex.w2t[1][:, kc, sl]),
                           (xh[n][:, kc, :], xl[n][:, kc, :]), kc == 0, False)

            def gram(g, fc):
                pe.wait_ge(hl_made, FC1 * g + fc + 1)
                split3(pe, pq[fc][:], (ex.gram[0][:, fc, :], ex.gram[1][:, fc, :]), (hh[:, fc, :], hl[:, fc, :]),
                       False, True).then_inc(cross_done, 1)

            def turn_coef(g):
                pe.wait_ge(coefs, NCOEF * g + NCOEF)
                pe.wait_ge(mul_done, 8 * g + 16)
                for t in range(T):
                    last = pe.transpose(px[:, t * P:t * P + P], parts[:, t, :].bitcast(F32), k.ident[:])
                last.then_inc(coef_turned, 1)

            def spread(g, fc):
                if fc:
                    pe.wait_ge(scaled, FC1 * g + fc)
                else:
                    pe.wait_ge(coef_out, g + 1)
                pe.matmul(pb[:], ex.spread[:, fc * P:fc * P + P], coef_t[:], start=True, stop=True)\
                  .then_inc(spread_done, 1)

            def product(g, t, main):
                sl = slice(t * P, t * P + P)
                if t == 0:
                    pe.wait_ge(cl_made, FC1 * g + FC1)
                    if main:
                        pe.wait_ge(hid_made, FC1 * g + 2 * FC1)
                if t == 3:
                    pe.wait_ge(mul_done, 8 * g + 4 + 16)
                pe.matmul(pox[t][:], coef_t[:, sl], ex.rows_x[:], start=True, stop=True).then_inc(x_done, 1)
                pe.matmul(po1[t][:], coef_t[:, sl], ex.rows_1[:], start=True, stop=False, skip_group_check=True)
                for fc in range(FC1):
                    last = split3(pe, po1[t][:], (ch[:, fc, sl], cl[:, fc, sl]),
                                  (ex.w2g[0][:, fc, :], ex.w2g[1][:, fc, :]), False, fc == FC1 - 1)
                last.then_inc(one_done, 1)

            def body(i, c_):
                g, n, n1, u1 = i * XS + c_, c_ % 2, (c_ + 1) % 2, (c_ + 1) % XS
                mid, main, behind = (in_range(i, c_, ahead) for ahead in (1, 0, -1))
                for fc in range(FC1):
                    if main:
                        up(g, n, fc)
                    if behind and fc:
                        turn_coef(g - 1)
                    if mid:
                        turn(g + 1, u1, fc)
                for fc in range(FC1):
                    if main:
                        cross(g, n, fc)
                    if mid:
                        turn(g + 1, u1, 2 + fc)
                    if behind:
                        spread(g - 1, fc)
                    if main:
                        gram(g, fc)
                if main:
                    if mid:
                        pe.wait_ge(route, NROUTE * g + 1)
                        logits(g + 1, n1, False)
                    squares(g, not mid)
                if behind:
                    product(g - 1, 0, main)
                if main:
                    turn_small(g + 1)
                if behind:
                    for t in range(1, T):
                        product(g - 1, t, main)

            for t in range(T):
                turn(0, 0, t, t == 0)
            logits(0, 0, True)
            turn_small(0)
            bodies(pe, body)




class Tables:
    pass


def program(nc, a, out):
    def dram(name, shape, dt=F32):
        return nc.dram_tensor(name, shape, dt).ap()

    with ExitStack() as stack:
        c = Core(nc, stack, "net")
        k = Tables()
        k.rec_s, k.rec_d = dram("rec_s", [EP + 1, REC_S], I32), dram("rec_d", [EP + 1, REC_D], I32)
        k.slots = {x: dram(f"slots_{x}", [NPAD, 1], I32) for x in "sd"}
        k.values, k.message1, k.message2 = (dram(n, [EP, D]) for n in ("values", "message1", "message2"))
        k.y, k.h, k.own = (dram(n, [NPAD, D]) for n in ("y", "h", "own"))
        k.ident, k.ones = c.sb("ident", [P, P]), c.sb("ones", [P, P])
        k.half_neg = c.sb("half_neg", [P, 32])
        k.slot = {x: c.sb(f"slot_{x}", [P, NT], I32) for x in "sd"}
        k.mean, k.dev = c.sb("mean", [P, NT]), c.sb("dev", [P, NT])
        with ExitStack() as edges:
            ce = Core(nc, edges, "edges")
            k.zeros, k.b12 = ce.sb("zeros", [P, D]), ce.sb("b12", [P, D])
            k.same = {x: ce.sb(f"same_{x}", [P, EP + 1], BF16) for x in "sd"}
            k.rec = {"s": ce.sb("rec_s", [P, ET, REC_S], I32), "d": ce.sb("rec_d", [P, ET, REC_D], I32)}
            sort_phase(nc, a, k)
            attention_phase(nc, a, k)
            dense0_phase(nc, a, k)
            conv_phase(nc, a, k)
            ex = message2_phase(nc, a, k, stack)
        dense1_phase(nc, a, k, ex, out)


def columns(v):
    return v.reshape(-1, P, *v.shape[1:]).swapaxes(0, 1)


def kernel(x, src, dst, edge_attr_8, edge_weight, node_vec, L0_gnn_ln_g, L0_gnn_ln_b, L0_gnn_Wq, L0_gnn_bq,
           L0_gnn_Wk, L0_gnn_bk, L0_gnn_Wv, L0_gnn_bv, L0_gnn_W1, L0_gnn_b1, L0_gnn_W2, L0_gnn_b2, L0_ffn_Wr,
           L0_ffn_br, L0_ffn_Wgate, L0_ffn_bgate, L0_ffn_W1, L0_ffn_W3, L0_ffn_W2, L1_gnn_W0_1, L1_gnn_W1_1,
           L1_gnn_b1, L1_gnn_W0_2, L1_gnn_W1_2, L1_gnn_b2, L1_ffn_router_w, L1_ffn_w1, L1_ffn_b1, L1_ffn_w2,
           L1_ffn_b2, L1_ffn_gamma, L1_ffn_beta):
    import numpy as np
    import concourse.bacc as bacc
    from concourse.bass_utils import run_bass_kernel_spmd

    def padded(v, rows, fill):
        v = np.asarray(v)
        return np.concatenate([v, np.full((rows - len(v),) + v.shape[1:], fill, v.dtype)])

    def row(v):
        return np.asarray(v).reshape(1, -1)

    def column(v):
        return columns(np.asarray(v))

    src, dst = padded(src, EP, N), padded(dst, EP, N)
    arrays = {
        "x": padded(x, NPAD, 0), "key_s": row(src), "key_d": row(dst), "col_s": column(src), "col_d": column(dst),
        "attr": column(padded(edge_attr_8, EP, 0)), "edge_w": column(padded(edge_weight, EP, 0)),
        "diag": column(padded(node_vec, NPAD, 0)),
        "ln_g": column(L0_gnn_ln_g), "ln_b": column(L0_gnn_ln_b),
        "wq": L0_gnn_Wq, "wk": L0_gnn_Wk, "wv": L0_gnn_Wv,
        "bq": column(L0_gnn_bq), "bk": column(L0_gnn_bk), "bv": column(L0_gnn_bv),
        "w1t": np.asarray(L0_gnn_W1).T, "w2": L0_gnn_W2, "b1_col": column(L0_gnn_b1), "b2_row": row(L0_gnn_b2),
        "e_w1": np.asarray(L0_ffn_W1).transpose(1, 0, 2).reshape(D, -1),
        "e_w3": np.asarray(L0_ffn_W3).transpose(1, 0, 2).reshape(D, -1),
        "e_w2": np.asarray(L0_ffn_W2).reshape(-1, D),
        "e_wr": np.concatenate([L0_ffn_Wr, np.asarray(L0_ffn_Wgate).transpose(1, 0, 2).reshape(D, -1)], 1),
        "e_br": row(np.concatenate([L0_ffn_br, np.asarray(L0_ffn_bgate).reshape(-1)])),
        "g_w01": L1_gnn_W0_1, "g_w11": L1_gnn_W1_1, "g_w02": L1_gnn_W0_2, "g_w12": L1_gnn_W1_2,
        "g_b1": row(L1_gnn_b1), "g_b2": row(L1_gnn_b2),
        "f_w1": np.asarray(L1_ffn_w1).transpose(1, 0, 2).reshape(D, -1),
        "f_w2": np.asarray(L1_ffn_w2).reshape(-1, D), "f_b1": np.asarray(L1_ffn_b1).reshape(-1, P).T,
        "f_router": L1_ffn_router_w, "f_b2": L1_ffn_b2, "f_gamma": L1_ffn_gamma, "f_beta": L1_ffn_beta,
    }
    arrays = {f"in_{name}": np.ascontiguousarray(v) for name, v in arrays.items()}

    nc = bacc.Bacc("TRN2", target_bir_lowering=False, num_devices=1)
    a = {name[3:]: nc.dram_tensor(name, v.shape, mybir.dt.from_np(v.dtype), kind="ExternalInput").ap()
         for name, v in arrays.items()}
    out = nc.dram_tensor("out", [NPAD, D], F32, kind="ExternalOutput").ap()
    program(nc, a, out)
    result = run_bass_kernel_spmd(nc, [arrays], core_ids=[0])
    return result.results[0]["out"][:N]
```
